# Optimizing a Trainium2 kernel written in Bass

```python
import numpy as np
import jax
import jax.numpy as jnp

def _softmax(x, axis=-1):
    return jax.nn.softmax(x, axis=axis)

def _gelu(x):
    return jax.nn.gelu(x, approximate=True)

def _silu(x):
    return jax.nn.silu(x)

def _sigmoid(x):
    return jax.nn.sigmoid(x)

def _layernorm(x, axis=-1, eps=1e-05):
    m = jnp.mean(x, axis=axis, keepdims=True)
    v = jnp.var(x, axis=axis, keepdims=True)
    return (x - m) / jnp.sqrt(v + eps)

def _scatter_add(tgt, idx, src, axis=0):
    return tgt.at[idx].add(src)

def _segment_sum(src, seg, n):
    return jax.ops.segment_sum(src, seg, n)
kernel_name = 'mk_flamingo_gated_d4_seqx_r4_9e7516'

def setup_inputs(seed: int=0):
    np.random.seed(seed)
    _w = jnp.asarray

    def _rec_inputs():
        import jax
        import jax.numpy as jnp
        _rk = jax.random.key(seed)
        x = -0.0005207 + 1.001 * jax.random.normal(jax.random.fold_in(_rk, 1), (8, 112, 1024), jnp.float32)
        _lenS = 112 - jax.random.randint(jax.random.fold_in(_rk, 7), (8,), 0, max(1, 112 // 4) + 1, jnp.int32)
        _lenS2 = 375 - jax.random.randint(jax.random.fold_in(_rk, 8), (8,), 0, max(1, 375 // 4) + 1, jnp.int32)
        _ctx_4096P = jax.random.normal(jax.random.fold_in(_rk, 11), (8, 16, 1024), jnp.float32)
        _ctx_4096c = jax.random.dirichlet(jax.random.fold_in(_rk, 511), 0.3 * jnp.ones((16,), jnp.float32), (8, 375))
        _ctx_4096t = jnp.einsum('bsk,bkd->bsd', _ctx_4096c, _ctx_4096P)
        _ctx_4096t = _ctx_4096t * jax.lax.rsqrt(jnp.mean(jnp.square(_ctx_4096t)) + 1e-12) * 0.953939
        ctx_4096 = -0.00010331 + 0.999899 * (_ctx_4096t + 0.3 * jax.random.normal(jax.random.fold_in(_rk, 611), (8, 375, 1024), jnp.float32))
        _g = jax.random.normal(jax.random.fold_in(_rk, 9001), (2, 4), jnp.float32)
        _g = jnp.sign(_g) * jnp.maximum(jnp.abs(_g), 1.0) + (_g == 0) * 1.0
        g_xattn = _g[0]
        g_ffn = _g[1]
        return (x, ctx_4096, g_xattn, g_ffn)
    x, ctx_4096, g_xattn, g_ffn = _rec_inputs()

    def _L0_xattn_setup():
        import jax, jax.numpy as jnp
        import numpy as np
        B, Q, D = (8, 64, 1024)
        CTX = 1024
        H, KV, HD = (16, 4, 96)
        G = H // KV
        key = jax.random.key(seed)
        ks = jax.random.split(key, 6)
        s = 0.02
        return {'latents': jax.random.normal(ks[0], (B, Q, D), jnp.float32), 'context': jax.random.normal(ks[1], (B, CTX, D), jnp.float32), 'Wq': jax.random.normal(ks[2], (H * HD, D), jnp.float32) * s, 'Wk': jax.random.normal(ks[3], (KV * HD, D), jnp.float32) * s, 'Wv': jax.random.normal(ks[4], (KV * HD, D), jnp.float32) * s, 'Wo': jax.random.normal(ks[5], (D, H * HD), jnp.float32) * s}
    _L0_xattn_all = _L0_xattn_setup()
    _L0_xattn_in = {k: v for k, v in _L0_xattn_all.items() if k in ('Wq', 'Wk', 'Wv', 'Wo')}
    del _L0_xattn_all

    def _L0_ffn_setup():
        import jax, jax.numpy as jnp
        import numpy as np
        Q_MAX = 127.0
        key = jax.random.key(seed)
        k1, k2, k3, k4 = jax.random.split(key, 4)
        B, S, K, N = (4, 512, 1024, 1024)
        inp = jax.random.normal(k1, (B, S, K), dtype=jnp.float32)
        qweight = (jax.random.randint(k2, (N, K), 0, 255) - 127).astype(jnp.int8)
        wparams = jax.random.uniform(k3, (N,), dtype=jnp.float32) * 0.02 + 0.001
        bias = jax.random.normal(k4, (N,), dtype=jnp.float32) * 0.1
        return {'inp': inp, 'qweight': qweight, 'wparams': wparams, 'bias': bias}
    _L0_ffn_all = _L0_ffn_setup()
    _L0_ffn_in = {k: v for k, v in _L0_ffn_all.items() if k in ('qweight', 'wparams', 'bias')}
    del _L0_ffn_all

    def _L1_xattn_setup():
        import jax, jax.numpy as jnp
        import numpy as np
        TEXT_DIM = 1024
        FEATURE_DIM = 1024

        def _xavier_uniform(key, shape):
            fan_in, fan_out = (shape[1], shape[0])
            limit = float(np.sqrt(6.0 / (fan_in + fan_out)))
            return jax.random.uniform(key, shape, jnp.float32, -limit, limit)
        key = jax.random.key(seed)
        k1, k2, k3, k4 = jax.random.split(key, 4)
        text = jax.random.normal(k1, (8, 512, TEXT_DIM), jnp.float32)
        features = jax.random.normal(k2, (8, 144, FEATURE_DIM), jnp.float32)
        Wq = _xavier_uniform(k3, (FEATURE_DIM, TEXT_DIM))
        bq = jnp.zeros((FEATURE_DIM,), jnp.float32)
        Wk = _xavier_uniform(k4, (FEATURE_DIM, FEATURE_DIM))
        bk = jnp.zeros((FEATURE_DIM,), jnp.float32)
        return {'text': text, 'features': features, 'Wq': Wq, 'bq': bq, 'Wk': Wk, 'bk': bk}
    _L1_xattn_all = _L1_xattn_setup()
    _L1_xattn_in = {k: v for k, v in _L1_xattn_all.items() if k in ('Wq', 'bq', 'Wk', 'bk')}
    del _L1_xattn_all

    def _L1_ffn_setup():
        import jax, jax.numpy as jnp
        import numpy as np
        HID, BOT, RDIM, NSLOT, K, VB = (1024, 64, 48, 256, 8, 64)
        TAU_LOW, TAU_HIGH, EARLY_EXIT = (0.5, 2.0, 0.05)

        def _uncertainty(h, Wu1, bu1, Wu2, bu2):
            var = jnp.var(h, axis=-1)
            log_var = jnp.log1p(var)
            norm_var = log_var / (jnp.mean(log_var) + 1e-06)
            learned = (jax.nn.gelu(h @ Wu1.T + bu1) @ Wu2.T + bu2)[..., 0]
            return jnp.clip(norm_var * 0.5 + jax.nn.sigmoid(learned) * 2.5, 0.0, 5.0)
        key = jax.random.key(seed)
        ks = jax.random.split(key, 12)
        B, S = (2, 512)
        return {'hidden_states': jax.random.normal(ks[0], (B, S, HID), dtype=jnp.float32), 'Wq': jax.random.normal(ks[1], (BOT, HID), dtype=jnp.float32) / np.sqrt(HID), 'Wr': jax.random.normal(ks[2], (RDIM, BOT), dtype=jnp.float32) / np.sqrt(BOT), 'aux_keys': jax.random.normal(ks[3], (NSLOT, BOT), dtype=jnp.float32) * 0.01, 'aux_values': jax.random.normal(ks[4], (NSLOT, HID), dtype=jnp.float32) * 0.02, 'Wvd': jax.random.normal(ks[5], (VB, HID), dtype=jnp.float32) * 0.1 / np.sqrt(HID), 'Wvu': jax.random.normal(ks[6], (HID, VB), dtype=jnp.float32) * 0.1 / np.sqrt(VB), 'Wu1': jax.random.normal(ks[7], (HID // 4, HID), dtype=jnp.float32) / np.sqrt(HID), 'bu1': jnp.zeros((HID // 4,), dtype=jnp.float32), 'Wu2': jax.random.normal(ks[8], (1, HID // 4), dtype=jnp.float32) * 0.01, 'bu2': jnp.zeros((1,), dtype=jnp.float32), 'gate_w1': jnp.float32(0.5), 'gate_bias': jnp.float32(-1.0), 'log_rel': jnp.zeros((NSLOT,), dtype=jnp.float32)}
    _L1_ffn_all = _L1_ffn_setup()
    _L1_ffn_in = {k: v for k, v in _L1_ffn_all.items() if k in ('Wq', 'Wr', 'aux_keys', 'aux_values', 'Wvd', 'Wvu', 'Wu1', 'bu1', 'Wu2', 'bu2', 'gate_w1', 'gate_bias', 'log_rel')}
    del _L1_ffn_all

    def _L2_xattn_setup():
        import jax, jax.numpy as jnp
        import numpy as np
        DIM = 1024
        NUM_HEADS = 32
        NUM_KV_HEADS = 8
        HEAD_DIM = DIM // NUM_HEADS
        KV_DIM = DIM // (NUM_HEADS // NUM_KV_HEADS)
        B, S = (1, 512)
        key = jax.random.key(seed)
        ks = jax.random.split(key, 7)
        w_scale = DIM ** (-0.5)
        return {'query': jax.random.normal(ks[0], (B, S, DIM), jnp.float32), 'key': jax.random.normal(ks[1], (B, S, DIM), jnp.float32), 'value': jax.random.normal(ks[2], (B, S, DIM), jnp.float32), 'Wq': jax.random.normal(ks[3], (DIM, DIM), jnp.float32) * w_scale, 'Wk': jax.random.normal(ks[4], (DIM, KV_DIM), jnp.float32) * w_scale, 'Wv': jax.random.normal(ks[5], (DIM, KV_DIM), jnp.float32) * w_scale, 'Wo': jax.random.normal(ks[6], (DIM, DIM), jnp.float32) * w_scale}
    _L2_xattn_all = _L2_xattn_setup()
    _L2_xattn_in = {k: v for k, v in _L2_xattn_all.items() if k in ('Wq', 'Wk', 'Wv', 'Wo')}
    del _L2_xattn_all

    def _L2_ffn_setup():
        import jax, jax.numpy as jnp
        import numpy as np
        import math
        HIDDEN = 1024
        INTER = 4096
        QMAX = 7.0

        def quantize_act(x):
            scale = jnp.maximum(jnp.max(jnp.abs(x), axis=-1, keepdims=True) / QMAX, 1e-08)
            return jnp.clip(jnp.round(x / scale), -8.0, 7.0) * scale

        def quantize_weight(w):
            scale = jnp.maximum(jnp.max(jnp.abs(w), axis=-1, keepdims=True) / QMAX, 1e-08)
            return jnp.clip(jnp.round(w / scale), -8.0, 7.0) * scale

        def matmul_hadU(x, scale):
            shp = x.shape
            n = shp[-1]
            v = x.reshape(-1, n, 1)
            while v.shape[1] > 1:
                v = v.reshape(v.shape[0], v.shape[1] // 2, 2, v.shape[3] if v.ndim == 4 else v.shape[2])
                a = v[:, :, 0, :]
                b = v[:, :, 1, :]
                v = jnp.concatenate([a + b, a - b], axis=-1)
                v = v[:, :, None, :].reshape(v.shape[0], v.shape[1], 1, v.shape[2])
                v = v.reshape(v.shape[0], v.shape[1], v.shape[3])
            return v.reshape(shp) * scale
        key = jax.random.key(seed)
        k1, k2, k3 = jax.random.split(key, 3)
        x = jax.random.normal(k1, (2, 512, HIDDEN), dtype=jnp.float32)
        w_gate_up = jax.random.normal(k2, (2 * INTER, HIDDEN), dtype=jnp.float32) * 0.02
        w_down = jax.random.normal(k3, (HIDDEN, INTER), dtype=jnp.float32) * 0.02
        return {'x': x, 'w_gate_up': w_gate_up, 'w_down': w_down}
    _L2_ffn_all = _L2_ffn_setup()
    _L2_ffn_in = {k: v for k, v in _L2_ffn_all.items() if k in ('w_gate_up', 'w_down')}
    del _L2_ffn_all

    def _L3_xattn_setup():
        import jax, jax.numpy as jnp
        import numpy as np
        B, N, K, F = (8, 1024, 16, 64)
        key = jax.random.key(seed)
        k1, k2, k3, k4 = jax.random.split(key, 4)
        xyz = jax.random.normal(k1, (B, 3, N), dtype=jnp.float32)
        feat = jax.random.normal(k2, (B, F, N), dtype=jnp.float32)
        affine_w = jax.random.normal(k3, (K,), dtype=jnp.float32) / np.sqrt(K).astype(np.float32)
        affine_b = jax.random.normal(k4, (1,), dtype=jnp.float32) / np.sqrt(K).astype(np.float32)
        return {'xyz': xyz, 'feat': feat, 'affine_w': affine_w, 'affine_b': affine_b}
    _L3_xattn_all = _L3_xattn_setup()
    _L3_xattn_in = {k: v for k, v in _L3_xattn_all.items() if k in ('affine_w', 'affine_b')}
    del _L3_xattn_all

    def _L3_ffn_setup():
        import jax, jax.numpy as jnp
        import numpy as np
        N_EXPERTS = 8
        TOP_K = 2
        D_MODEL = 1024
        RANK = 64
        key = jax.random.key(seed)
        k0, k1, k2, k3 = jax.random.split(key, 4)
        inputs = jax.random.normal(k0, (4, 512, D_MODEL), dtype=jnp.float32)
        gate_w = jax.random.normal(k1, (N_EXPERTS, D_MODEL), dtype=jnp.float32) * 0.02
        lora_A = jax.random.normal(k2, (N_EXPERTS, RANK, D_MODEL), dtype=jnp.float32) * 0.02
        lora_B = jax.random.normal(k3, (N_EXPERTS, D_MODEL, RANK), dtype=jnp.float32) * 0.02
        return {'inputs': inputs, 'gate_w': gate_w, 'lora_A': lora_A, 'lora_B': lora_B}
    _L3_ffn_all = _L3_ffn_setup()
    _L3_ffn_in = {k: v for k, v in _L3_ffn_all.items() if k in ('gate_w', 'lora_A', 'lora_B')}
    del _L3_ffn_all
    return {'x': x, 'ctx_4096': ctx_4096, 'g_xattn': g_xattn, 'g_ffn': g_ffn, 'L0_xattn_Wq': _L0_xattn_in['Wq'], 'L0_xattn_Wk': _L0_xattn_in['Wk'], 'L0_xattn_Wv': _L0_xattn_in['Wv'], 'L0_xattn_Wo': _L0_xattn_in['Wo'], 'L0_ffn_qweight': _L0_ffn_in['qweight'], 'L0_ffn_wparams': _L0_ffn_in['wparams'], 'L0_ffn_bias': _L0_ffn_in['bias'], 'L1_xattn_Wq': _L1_xattn_in['Wq'], 'L1_xattn_bq': _L1_xattn_in['bq'], 'L1_xattn_Wk': _L1_xattn_in['Wk'], 'L1_xattn_bk': _L1_xattn_in['bk'], 'L1_ffn_Wq': _L1_ffn_in['Wq'], 'L1_ffn_Wr': _L1_ffn_in['Wr'], 'L1_ffn_aux_keys': _L1_ffn_in['aux_keys'], 'L1_ffn_aux_values': _L1_ffn_in['aux_values'], 'L1_ffn_Wvd': _L1_ffn_in['Wvd'], 'L1_ffn_Wvu': _L1_ffn_in['Wvu'], 'L1_ffn_Wu1': _L1_ffn_in['Wu1'], 'L1_ffn_bu1': _L1_ffn_in['bu1'], 'L1_ffn_Wu2': _L1_ffn_in['Wu2'], 'L1_ffn_bu2': _L1_ffn_in['bu2'], 'L1_ffn_gate_w1': _L1_ffn_in['gate_w1'], 'L1_ffn_gate_bias': _L1_ffn_in['gate_bias'], 'L1_ffn_log_rel': _L1_ffn_in['log_rel'], 'L2_xattn_Wq': _L2_xattn_in['Wq'], 'L2_xattn_Wk': _L2_xattn_in['Wk'], 'L2_xattn_Wv': _L2_xattn_in['Wv'], 'L2_xattn_Wo': _L2_xattn_in['Wo'], 'L2_ffn_w_gate_up': _L2_ffn_in['w_gate_up'], 'L2_ffn_w_down': _L2_ffn_in['w_down'], 'L3_xattn_affine_w': _L3_xattn_in['affine_w'], 'L3_xattn_affine_b': _L3_xattn_in['affine_b'], 'L3_ffn_gate_w': _L3_ffn_in['gate_w'], 'L3_ffn_lora_A': _L3_ffn_in['lora_A'], 'L3_ffn_lora_B': _L3_ffn_in['lora_B']}

def reference(x, ctx_4096, g_xattn, g_ffn, L0_xattn_Wq, L0_xattn_Wk, L0_xattn_Wv, L0_xattn_Wo, L0_ffn_qweight, L0_ffn_wparams, L0_ffn_bias, L1_xattn_Wq, L1_xattn_bq, L1_xattn_Wk, L1_xattn_bk, L1_ffn_Wq, L1_ffn_Wr, L1_ffn_aux_keys, L1_ffn_aux_values, L1_ffn_Wvd, L1_ffn_Wvu, L1_ffn_Wu1, L1_ffn_bu1, L1_ffn_Wu2, L1_ffn_bu2, L1_ffn_gate_w1, L1_ffn_gate_bias, L1_ffn_log_rel, L2_xattn_Wq, L2_xattn_Wk, L2_xattn_Wv, L2_xattn_Wo, L2_ffn_w_gate_up, L2_ffn_w_down, L3_xattn_affine_w, L3_xattn_affine_b, L3_ffn_gate_w, L3_ffn_lora_A, L3_ffn_lora_B):
    import jax
    import jax.numpy as jnp

    def _L0_xattn_ref(latents, context, Wq, Wk, Wv, Wo):
        import jax, jax.numpy as jnp
        import numpy as np
        B, Q, D = (8, 64, 1024)
        CTX = 1024
        H, KV, HD = (16, 4, 96)
        G = H // KV
        b, q_len, _ = latents.shape
        hidden = jnp.concatenate([context, latents], axis=1)
        s_len = hidden.shape[1]
        q = (latents @ Wq.T).reshape(b, q_len, H, HD)
        k = (hidden @ Wk.T).reshape(b, s_len, KV, HD)
        v = (hidden @ Wv.T).reshape(b, s_len, KV, HD)
        q = q.transpose(0, 2, 1, 3).reshape(b, KV, G, q_len, HD)
        k = k.transpose(0, 2, 1, 3)
        v = v.transpose(0, 2, 1, 3)
        scale = 1.0 / jnp.sqrt(jnp.asarray(HD, q.dtype))
        scores = jnp.einsum('bkgqd,bksd->bkgqs', q, k) * scale
        attn = jax.nn.softmax(scores.astype(jnp.float32), axis=-1).astype(q.dtype)
        out = jnp.einsum('bkgqs,bksd->bkgqd', attn, v)
        out = out.reshape(b, H, q_len, HD).transpose(0, 2, 1, 3).reshape(b, q_len, H * HD)
        return out @ Wo.T

    def _L0_ffn_ref(inp, qweight, wparams, bias):
        import jax, jax.numpy as jnp
        import numpy as np
        Q_MAX = 127.0
        B, S, K = inp.shape
        x = inp.reshape(B * S, K)
        a_scale = jnp.max(jnp.abs(x), axis=1, keepdims=True) / Q_MAX
        qinp = jnp.clip(jnp.round(x / a_scale), -Q_MAX, Q_MAX).astype(jnp.int8)
        d = jax.lax.dot_general(qinp, qweight.T, (((1,), (0,)), ((), ())), preferred_element_type=jnp.int32)
        out = d.astype(jnp.float32) * a_scale * wparams[None, :] + bias[None, :]
        return out.reshape(B, S, -1)

    def _L1_xattn_ref(text, features, Wq, bq, Wk, bk):
        import jax, jax.numpy as jnp
        import numpy as np
        TEXT_DIM = 1024
        FEATURE_DIM = 1024

        def _xavier_uniform(key, shape):
            fan_in, fan_out = (shape[1], shape[0])
            limit = float(np.sqrt(6.0 / (fan_in + fan_out)))
            return jax.random.uniform(key, shape, jnp.float32, -limit, limit)
        Q = jnp.einsum('btx,dx->btd', text, Wq) + bq
        K = jnp.einsum('bpx,dx->bpd', features, Wk) + bk
        scale = 1.0 / jnp.sqrt(jnp.asarray(K.shape[-1], K.dtype))
        scores = jnp.einsum('btd,bpd->btp', Q, K) * scale
        attn = jax.nn.softmax(scores, axis=-1)
        attended = jnp.einsum('btp,bpd->btd', attn, features)
        return attended

    def _L1_ffn_ref(hidden_states, Wq, Wr, aux_keys, aux_values, Wvd, Wvu, Wu1, bu1, Wu2, bu2, gate_w1, gate_bias, log_rel):
        import jax, jax.numpy as jnp
        import numpy as np
        HID, BOT, RDIM, NSLOT, K, VB = (1024, 64, 48, 256, 8, 64)
        TAU_LOW, TAU_HIGH, EARLY_EXIT = (0.5, 2.0, 0.05)

        def _uncertainty(h, Wu1, bu1, Wu2, bu2):
            var = jnp.var(h, axis=-1)
            log_var = jnp.log1p(var)
            norm_var = log_var / (jnp.mean(log_var) + 1e-06)
            learned = (jax.nn.gelu(h @ Wu1.T + bu1) @ Wu2.T + bu2)[..., 0]
            return jnp.clip(norm_var * 0.5 + jax.nn.sigmoid(learned) * 2.5, 0.0, 5.0)
        query = hidden_states @ Wq.T
        rq = query @ Wr.T
        rk = aux_keys @ Wr.T
        router_scores = jnp.einsum('bsr,nr->bsn', rq, rk) / np.sqrt(RDIM) + log_rel
        top_scores, top_idx = jax.lax.top_k(router_scores, K)
        sel_keys = aux_keys[top_idx]
        attn = jnp.einsum('bsd,bskd->bsk', query, sel_keys) / np.sqrt(BOT) + log_rel[top_idx]
        w = jax.nn.softmax(attn, axis=-1)
        sel_vals = aux_values[top_idx]
        aux_out = jnp.einsum('bsk,bskh->bsh', w, sel_vals)
        aux_out = aux_out @ Wvd.T @ Wvu.T
        u = _uncertainty(hidden_states, Wu1, bu1, Wu2, bu2)
        u_norm = jnp.clip((u - TAU_LOW) / (TAU_HIGH - TAU_LOW), 0.0, 1.0)
        gate = jax.nn.sigmoid(gate_w1 * u_norm + gate_bias)
        gate = jnp.where(gate < EARLY_EXIT, 0.0, gate)
        return hidden_states + gate[..., None] * aux_out

    def _L2_xattn_ref(query, key, value, Wq, Wk, Wv, Wo):
        import jax, jax.numpy as jnp
        import numpy as np
        DIM = 1024
        NUM_HEADS = 32
        NUM_KV_HEADS = 8
        HEAD_DIM = DIM // NUM_HEADS
        KV_DIM = DIM // (NUM_HEADS // NUM_KV_HEADS)
        B, S = (1, 512)
        b, sq, _ = query.shape
        _, sk, _ = key.shape
        rep = NUM_HEADS // NUM_KV_HEADS
        q = (query @ Wq).reshape(b, sq, NUM_HEADS, HEAD_DIM).transpose(0, 2, 1, 3)
        k = (key @ Wk).reshape(b, sk, NUM_KV_HEADS, HEAD_DIM).transpose(0, 2, 1, 3)
        v = (value @ Wv).reshape(b, sk, NUM_KV_HEADS, HEAD_DIM).transpose(0, 2, 1, 3)
        k = jnp.repeat(k, rep, axis=1)
        v = jnp.repeat(v, rep, axis=1)
        scale = HEAD_DIM ** (-0.5)
        scores = jnp.einsum('bhqd,bhkd->bhqk', q, k) * scale
        probs = jax.nn.softmax(scores, axis=-1)
        out = jnp.einsum('bhqk,bhkd->bhqd', probs, v)
        out = out.transpose(0, 2, 1, 3).reshape(b, sq, DIM)
        return out @ Wo

    def _L2_ffn_ref(x, w_gate_up, w_down):
        import jax, jax.numpy as jnp
        import numpy as np
        import math
        HIDDEN = 1024
        INTER = 4096
        QMAX = 7.0

        def quantize_act(x):
            scale = jnp.maximum(jnp.max(jnp.abs(x), axis=-1, keepdims=True) / QMAX, 1e-08)
            return jnp.clip(jnp.round(x / scale), -8.0, 7.0) * scale

        def quantize_weight(w):
            scale = jnp.maximum(jnp.max(jnp.abs(w), axis=-1, keepdims=True) / QMAX, 1e-08)
            return jnp.clip(jnp.round(w / scale), -8.0, 7.0) * scale

        def matmul_hadU(x, scale):
            shp = x.shape
            n = shp[-1]
            v = x.reshape(-1, n, 1)
            while v.shape[1] > 1:
                v = v.reshape(v.shape[0], v.shape[1] // 2, 2, v.shape[3] if v.ndim == 4 else v.shape[2])
                a = v[:, :, 0, :]
                b = v[:, :, 1, :]
                v = jnp.concatenate([a + b, a - b], axis=-1)
                v = v[:, :, None, :].reshape(v.shape[0], v.shape[1], 1, v.shape[2])
                v = v.reshape(v.shape[0], v.shape[1], v.shape[3])
            return v.reshape(shp) * scale
        had_scale = 1.0 / math.sqrt(INTER)
        xq = quantize_act(x)
        wq = quantize_weight(w_gate_up)
        gate_up = jnp.einsum('bsh,oh->bso', xq, wq)
        gate, up = (gate_up[..., :INTER], gate_up[..., INTER:])
        h = jax.nn.silu(gate) * up
        h = matmul_hadU(h, had_scale)
        hq = quantize_act(h)
        wdq = quantize_weight(w_down)
        out = jnp.einsum('bsi,oi->bso', hq, wdq)
        return out

    def _L3_xattn_ref(xyz, feat, affine_w, affine_b):
        import jax, jax.numpy as jnp
        import numpy as np
        B, N, K, F = (8, 1024, 16, 64)
        Bn, Fd, Nn = feat.shape
        xy = xyz[:, 0:2, :]
        inner = 2.0 * jnp.einsum('bcn,bcm->bnm', xy, xy)
        sq = jnp.sum(xy * xy, axis=1)
        pdist = sq[:, None, :] - inner + sq[:, :, None]
        idx = jax.lax.top_k(-pdist, K)[1]
        flat_idx = idx.reshape(Bn, Nn * K)
        gathered = jnp.take_along_axis(feat, flat_idx[:, None, :], axis=2)
        lap = gathered.reshape(Bn, K, Nn * Fd)
        out = jnp.einsum('bkm,k->bm', lap, affine_w) + affine_b[0]
        return out.reshape(Bn, Nn, Fd).transpose(0, 2, 1)

    def _L3_ffn_ref(inputs, gate_w, lora_A, lora_B):
        import jax, jax.numpy as jnp
        import numpy as np
        N_EXPERTS = 8
        TOP_K = 2
        D_MODEL = 1024
        RANK = 64
        x = inputs.reshape(-1, inputs.shape[-1])
        T = x.shape[0]
        gate_probs = jax.nn.softmax(x @ gate_w.T, axis=-1)
        weights, sel = jax.lax.top_k(gate_probs, TOP_K)
        weights = weights / jnp.sum(weights, axis=-1, keepdims=True)
        w_full = jnp.zeros((T, N_EXPERTS), dtype=x.dtype).at[jnp.arange(T)[:, None], sel].add(weights)
        out = jnp.zeros((T, D_MODEL), dtype=x.dtype)
        for e in range(N_EXPERTS):
            y = x @ lora_A[e].T @ lora_B[e].T
            out = out + w_full[:, e:e + 1] * y
        return out.reshape(inputs.shape[:-1] + (D_MODEL,))
    x = x + jnp.tanh(g_xattn[0]) * _L0_xattn_ref(_layernorm(x, axis=-1), ctx_4096, L0_xattn_Wq, L0_xattn_Wk, L0_xattn_Wv, L0_xattn_Wo)
    x = x + jnp.tanh(g_ffn[0]) * _L0_ffn_ref(_layernorm(x, axis=-1), L0_ffn_qweight, L0_ffn_wparams, L0_ffn_bias)
    x = x + jnp.tanh(g_xattn[1]) * _L1_xattn_ref(_layernorm(x, axis=-1), ctx_4096, L1_xattn_Wq, L1_xattn_bq, L1_xattn_Wk, L1_xattn_bk)
    x = x + jnp.tanh(g_ffn[1]) * _L1_ffn_ref(_layernorm(x, axis=-1), L1_ffn_Wq, L1_ffn_Wr, L1_ffn_aux_keys, L1_ffn_aux_values, L1_ffn_Wvd, L1_ffn_Wvu, L1_ffn_Wu1, L1_ffn_bu1, L1_ffn_Wu2, L1_ffn_bu2, L1_ffn_gate_w1, L1_ffn_gate_bias, L1_ffn_log_rel)
    x = x + jnp.tanh(g_xattn[2]) * _L2_xattn_ref(_layernorm(x, axis=-1), ctx_4096, ctx_4096, L2_xattn_Wq, L2_xattn_Wk, L2_xattn_Wv, L2_xattn_Wo)
    x = x + jnp.tanh(g_ffn[2]) * _L2_ffn_ref(_layernorm(x, axis=-1), L2_ffn_w_gate_up, L2_ffn_w_down)
    x = x + jnp.tanh(g_xattn[3]) * _L3_xattn_ref(ctx_4096, _layernorm(x, axis=-1), L3_xattn_affine_w, L3_xattn_affine_b)
    x = x + jnp.tanh(g_ffn[3]) * _L3_ffn_ref(_layernorm(x, axis=-1), L3_ffn_gate_w, L3_ffn_lora_A, L3_ffn_lora_B)
    return x

_drawn_inputs = setup_inputs


def setup_inputs(seed=0):
    import zlib

    import numpy as np

    out = dict(_drawn_inputs(seed))
    spreads = {'L1_xattn_bq': (0.0, 0.8),
     'L1_xattn_bk': (0.0, 2.0),
     'L1_ffn_bu1': (0.0, 2.0),
     'L1_ffn_log_rel': (0.0, 0.8)}
    factors = {'g_ffn': 8.0,
     'L0_ffn_bias': 8.0,
     'L1_xattn_Wq': 6.604,
     'L1_xattn_Wk': 6.707,
     'L1_ffn_Wq': 8.0,
     'L1_ffn_Wr': 8.0,
     'L1_ffn_aux_keys': 8.0,
     'L1_ffn_aux_values': 8.0,
     'L1_ffn_Wvd': 8.0,
     'L1_ffn_Wvu': 8.0,
     'L1_ffn_Wu1': 8.0,
     'L1_ffn_Wu2': 8.0,
     'L2_xattn_Wq': 8.0,
     'L2_xattn_Wk': 8.0,
     'L2_xattn_Wv': 3.133,
     'L2_xattn_Wo': 3.198,
     'L2_ffn_w_gate_up': 5.448,
     'L2_ffn_w_down': 5.445,
     'L3_ffn_gate_w': 8.0,
     'L3_ffn_lora_A': 8.0,
     'L3_ffn_lora_B': 8.0,
     'L3_xattn_affine_w': 5.518}
    for name, (base, spread) in spreads.items():
        noise = np.random.default_rng([zlib.crc32(name.encode()), seed]).standard_normal(out[name].shape)
        drawn = base * np.exp(spread * noise) if base else spread * noise
        out[name] = jnp.asarray(drawn.astype(out[name].dtype))
    for name, factor in factors.items():
        out[name] = (out[name] * factor).astype(out[name].dtype)
    return out
```

```python
from contextlib import ExitStack

import concourse.bass as bass
from concourse import mybir

F32 = mybir.dt.float32
BF16 = mybir.dt.bfloat16
FP8 = mybir.dt.float8e4
I8 = mybir.dt.int8
U32 = mybir.dt.uint32
ALU = mybir.AluOpType
ACT = mybir.ActivationFunctionType
AX = mybir.AxisListType.X

B, Q, D = 8, 112, 1024
CTX = 375
P = 128
KC = D // P
PAIRS = B // 2
CT = 125
CTILES = CTX // CT
EPS = 1e-5
MAGIC = 1.5 * 2.0 ** 23
LOW = -1e30


class Banks:

    def __init__(self, nc, ctx):
        self.tile = [ctx.enter_context(nc.psum_tensor(f"bank{k}", [P, 512], F32)) for k in range(8)]
        self.full = [ctx.enter_context(nc.semaphore(f"bank_full{k}")) for k in range(8)]
        self.free = [ctx.enter_context(nc.semaphore(f"bank_free{k}")) for k in range(8)]
        self.used = [0] * 8


class Turns:

    def __init__(self, banks, order, rounds):
        self.banks, self.at, self.per = banks, {}, [0] * 8
        for name, k in order:
            self.at[name] = (k, self.per[k])
            self.per[k] += 1
        self.start = list(banks.used)
        for k in range(8):
            banks.used[k] += rounds * self.per[k]

    def tile(self, name):
        return self.banks.tile[self.at[name][0]]

    def full(self, name):
        return self.banks.full[self.at[name][0]]

    def free(self, name):
        return self.banks.free[self.at[name][0]]

    def count(self, name, turn):
        k, n = self.at[name]
        return turn * self.per[k] + (self.start[k] + n + 1)


class Scope:

    def __init__(self, nc, ctx, stage):
        self.nc, self.ctx, self.stage = nc, ctx, stage
        self.sems = []
        ctx.callback(self.clear)

    def sb(self, name, shape, dt=F32):
        return self.ctx.enter_context(self.nc.sbuf_tensor(f"{self.stage}_{name}", shape, dt))

    def sem(self, name):
        self.sems.append(self.nc.alloc_semaphore(f"{self.stage}_{name}"))
        return self.sems[-1]

    def clear(self):
        if self.sems:
            self.nc.clear_and_free_semaphores(self.sems)
            self.nc.all_engine_barrier()


class Consts:

    def __init__(self, nc, ctx):
        s = Scope(nc, ctx, "const")
        self.ident = s.sb("ident", [P, P])
        self.identb = s.sb("identb", [P, P], BF16)
        self.gates = s.sb("gates", [P, 8])


def rows(v, n):
    return v.rearrange("(a d) -> a d", a=1).broadcast_to([n, v.shape[0]])


def fold(w):
    return w.rearrange("(k p) n -> p k n", p=P)


def setup(nc, C, banks, g_xattn, g_ffn, masks):
    with ExitStack() as ctx:
        s = Scope(nc, ctx, "setup")
        loaded = s.sem("loaded")
        block = ctx.enter_context(nc.Block())

        @block.sync
        def _(sp):
            sp.dma_start(C.ident[:], masks["ident"]).then_inc(loaded, 16)
            sp.dma_start(C.gates[:, 0:4], rows(g_xattn, P)).then_inc(loaded, 16)
            sp.dma_start(C.gates[:, 4:8], rows(g_ffn, P)).then_inc(loaded, 16)

        @block.scalar
        def _(act):
            act.wait_ge(loaded, 48)
            act.activation(C.gates[:], C.gates[:], ACT.Tanh)

        @block.vector
        def _(dve):
            dve.wait_ge(loaded, 48)
            dve.tensor_copy(C.identb[:], C.ident[:])

        @block.tensor
        def _(pe):
            for k in range(8):
                pe.sem_inc(banks.free[k], 1)


def stream_x(sp, x, x_in, x_out, x_loaded, x_done, x_stored):
    for s in range(2):
        sp.dma_start(x[:, s, :], x_in[s]).then_inc(x_loaded[s], 16)

    def store(b, p, s):
        sp.wait_ge(x_done, b + 1)
        sp.dma_start(x_out[b], x[:, s, :]).then_inc(x_stored[s], 16)
        sp.wait_ge(x_stored[s], p * 16 + 16)

    with sp.Fori(0, PAIRS - 1) as p:
        for s in range(2):
            store(p * 2 + s, p, s)
            sp.dma_start(x[:, s, :], x_in[p * 2 + (s + 2)]).then_inc(x_loaded[s], 16)
    for s in range(2):
        store(B - 2 + s, PAIRS - 1, s)


class Norm:

    def __init__(self, s, n):
        self.stats = s.sb("ln_stats", [Q, n, 2, 6])
        self.mv = s.sb("ln_mv", [Q, n, 2])
        self.std = s.sb("ln_std", [Q, n, 1])
        self.rstd = s.sb("ln_rstd", [Q, n, 1])
        self.var_ready = s.sem("var_ready")
        self.std_ready = s.sem("std_ready")

    def statistics(self, dve, x, i):
        for h in range(2):
            dve.bn_stats(self.stats[:, i, h, :], x[:, h * 512:(h + 1) * 512])
        dve.drain()
        dve.bn_aggr(self.mv[:, i, :], self.stats[:, i, :, :])
        dve.drain()
        dve.tensor_scalar(self.std[:, i, :], self.mv[:, i, 1:2], EPS, None, ALU.add).then_inc(self.var_ready, 1)

    def root(self, act, i, b):
        act.wait_ge(self.var_ready, b + 1)
        act.activation(self.std[:, i, :], self.std[:, i, :], ACT.Sqrt).then_inc(self.std_ready, 1)

    def scale(self, dve, x, z, i, b):
        dve.wait_ge(self.std_ready, b + 1)
        dve.reciprocal(self.rstd[:, i, :], self.std[:, i, :])
        dve.drain()
        return dve.tensor_scalar(z, x, self.mv[:, i, 0:1], self.rstd[:, i, :], ALU.subtract, ALU.mult)


def divide(dve, out, rest, n):
    dve.tensor_scalar(rest, out, 1.0 / n, None, ALU.mult)
    dve.drain()
    dve.scalar_tensor_tensor(out=out, in0=rest, scalar=-(n + 1.0), in1=out, op0=ALU.mult, op1=ALU.add)
    dve.drain()
    dve.tensor_tensor(out, out, rest, ALU.add)
    dve.drain()
    dve.scalar_tensor_tensor(out=out, in0=out, scalar=1.0 / n, in1=rest, op0=ALU.mult, op1=ALU.add)
    dve.drain()


def quantised_ffn(nc, C, banks, gate, x_in, x_out, qweightT, wparams, bias):
    QMAX = 127.0
    with ExitStack() as ctx:
        s_ = Scope(nc, ctx, "qffn")
        w8 = s_.sb("w8", [P, KC, D], I8)
        w = s_.sb("w", [P, KC, D], BF16)
        wp = s_.sb("wparams", [Q, D])
        bi = s_.sb("bias", [Q, D])
        x = s_.sb("x", [Q, 2, D])
        z = s_.sb("z", [Q, 2, D])
        q = s_.sb("q", [Q, 2, D], BF16)
        qT = s_.sb("qT", [P, 2, KC, Q], BF16)
        y = s_.sb("y", [Q, 2, D])
        ascale = s_.sb("ascale", [Q, 2, 1])
        rscale = s_.sb("rscale", [Q, 2, 1])
        norm = Norm(s_, 2)
        w_loaded = s_.sem("w_loaded")
        rows_loaded = s_.sem("rows_loaded")
        w_cast = s_.sem("w_cast")
        x_loaded = [s_.sem(f"x_loaded{i}") for i in range(2)]
        x_stored = [s_.sem(f"x_stored{i}") for i in range(2)]
        q_ready, qT_ready, y_ready, x_done = s_.sem("q_ready"), s_.sem("qT_ready"), s_.sem("y_ready"), s_.sem("x_done")
        part_done = s_.sem("part_done")
        rows_scaled = s_.sem("rows_scaled")
        turns = Turns(banks, [(("T", s), s) for s in range(2)]
                      + [(("y", s, n), 2 + 2 * s + n) for s in range(2) for n in range(2)], PAIRS)
        block = ctx.enter_context(nc.Block())

        @block.sync
        def _(sp):
            sp.dma_start(w8[:].bitcast(U32), fold(qweightT)).then_inc(w_loaded, 16)
            sp.dma_start(wp[:], rows(wparams, Q)).then_inc(rows_loaded, 16)
            sp.dma_start(bi[:], rows(bias, Q)).then_inc(rows_loaded, 16)
            stream_x(sp, x, x_in, x_out, x_loaded, x_done, x_stored)

        @block.vector
        def _(dve):
            dve.wait_ge(w_loaded, 16)
            dve.tensor_copy(w[:, 0:KC // 2, :], w8[:, 0:KC // 2, :]).then_inc(w_cast, 1)
            with dve.Fori(0, PAIRS) as p:
                for s in range(2):
                    dve.wait_ge(x_loaded[s], p * 16 + 16)
                    norm.statistics(dve, x[:, s, :], s)
                for s in range(2):
                    norm.scale(dve, x[:, s, :], z[:, s, :], s, p * 2 + s)
                for s in range(2):
                    dve.drain()
                    dve.tensor_reduce(ascale[:, s, :], z[:, s, :], AX, ALU.max, apply_absolute_value=True)
                for s in range(2):
                    dve.drain()
                    divide(dve, ascale[:, s, :], rscale[:, s, :], QMAX)
                    dve.reciprocal(rscale[:, s, :], ascale[:, s, :])
                    dve.drain()
                    dve.tensor_scalar(z[:, s, :], z[:, s, :], rscale[:, s, :], MAGIC, ALU.mult, ALU.add)
                for s in range(2):
                    dve.drain()
                    dve.tensor_scalar(q[:, s, :], z[:, s, :], MAGIC, QMAX, ALU.subtract, ALU.min).then_inc(q_ready, 1)

        @block.tensor
        def _(pe):
            pe.wait_ge(w_cast, 2)
            with pe.Fori(0, PAIRS) as p:
                for s in range(2):
                    t = ("T", s)
                    pe.wait_ge(q_ready, p * 2 + (s + 1))
                    pe.wait_ge(turns.free(t), turns.count(t, p))
                    o = turns.tile(t)[:].bitcast(BF16)
                    for k in range(KC):
                        mm = pe.transpose(o[:, k * Q:(k + 1) * Q], q[:, s, k * P:(k + 1) * P], C.identb[0:Q, 0:Q])
                    mm.then_inc(turns.full(t), 1)
                for s in range(2):
                    pe.wait_ge(qT_ready, p * 2 + (s + 1))
                    for n in range(2):
                        t = ("y", s, n)
                        pe.wait_ge(turns.free(t), turns.count(t, p))
                        for k in range(KC):
                            mm = pe.matmul(turns.tile(t)[0:Q, :], qT[:, s, k, :], w[:, k, n * 512:(n + 1) * 512],
                                           start=(k == 0), stop=(k == KC - 1))
                        mm.then_inc(turns.full(t), 1)

        @block.scalar
        def _(act):
            act.wait_ge(w_loaded, 16)
            act.copy(w[:, KC // 2:KC, :], w8[:, KC // 2:KC, :]).then_inc(w_cast, 1)
            with act.Fori(0, PAIRS) as p:
                for s in range(2):
                    norm.root(act, s, p * 2 + s)
                for s in range(2):
                    t = ("T", s)
                    act.wait_ge(turns.full(t), turns.count(t, p))
                    o = turns.tile(t)[:].bitcast(BF16)
                    act.copy(qT[:, s, :, :], o[:, 0:KC * Q].rearrange("p (k q) -> p k q", k=KC)).then_inc(turns.free(t), 1)
                    act.drain().then_inc(qT_ready, 1)
                for s in range(2):
                    for n in range(2):
                        t = ("y", s, n)
                        act.wait_ge(turns.full(t), turns.count(t, p))
                        act.activation(y[:, s, n * 512:(n + 1) * 512], turns.tile(t)[0:Q, :], ACT.Copy,
                                       scale=ascale[:, s, :]).then_inc(turns.free(t), 1)
                    act.drain().then_inc(y_ready, 1)

        @block.gpsimd
        def _(pool):
            pool.wait_ge(rows_loaded, 32)
            gp = C.gates[0:Q, gate:gate + 1]
            for v in (wp, bi):
                pool.tensor_scalar(v[:], v[:], gp, 1.0, ALU.mult, ALU.mult).then_inc(rows_scaled, 1)
            pool.wait_ge(rows_scaled, 2)
            with pool.Fori(0, PAIRS) as p:
                for s in range(2):
                    pool.wait_ge(y_ready, p * 2 + (s + 1))
                    pool.tensor_tensor(y[:, s, :], y[:, s, :], wp[:], ALU.mult)
                    pool.tensor_tensor(x[:, s, :], x[:, s, :], bi[:], ALU.add).then_inc(part_done, 1)
                    pool.wait_ge(part_done, p * 2 + (s + 1))
                    pool.tensor_tensor(x[:, s, :], x[:, s, :], y[:, s, :], ALU.add).then_inc(x_done, 1)


def turn_rows(pe, C, turns, src, name, s, p, n=2):
    for h in range(n):
        t = (name, s, h)
        pe.wait_ge(turns.free(t), turns.count(t, p))
        for k in range(4):
            c = (4 * h + k) * P
            mm = pe.transpose(turns.tile(t)[:, k * Q:(k + 1) * Q], src[:, c:c + P], C.ident[0:Q, 0:Q])
        mm.then_inc(turns.full(t), 1)


def copy_turned(act, turns, dst, name, s, p, ready, n=2):
    for h in range(n):
        t = (name, s, h)
        act.wait_ge(turns.full(t), turns.count(t, p))
        act.activation(dst[:, 4 * h:4 * h + 4, :], turns.tile(t)[:, 0:4 * Q].rearrange("p (k q) -> p k q", k=4),
                       ACT.Copy).then_inc(turns.free(t), 1)
    act.drain().then_inc(ready, 1)


def project(pe, turns, lhsT, w, name, s, p, n=2):
    for h in range(n):
        t = (name, s, h)
        pe.wait_ge(turns.free(t), turns.count(t, p))
        for k in range(w.shape[1]):
            mm = pe.matmul(turns.tile(t)[0:Q, :], lhsT[:, k, :], w[:, k, h * 512:(h + 1) * 512],
                           start=(k == 0), stop=(k == w.shape[1] - 1))
        mm.then_inc(turns.full(t), 1)


def plain_attention(nc, C, banks, gate, x_in, x_out, A):
    SCALE = float(D) ** -0.5
    with ExitStack() as ctx:
        s_ = Scope(nc, ctx, "plain")
        wq, wk = s_.sb("wq", [P, KC, D]), s_.sb("wk", [P, KC, D])
        bq, bk = s_.sb("bq", [Q, D]), s_.sb("bk", [P, KC])
        x, z = s_.sb("x", [Q, 2, D]), s_.sb("z", [Q, 2, D])
        zT, qT, tT = (s_.sb(n, [P, 2, KC, Q]) for n in ("zT", "qT", "tT"))
        q, t_ = s_.sb("q", [Q, 2, D]), z
        cT, cN = s_.sb("ctxT", [P, 2, KC, CTX]), s_.sb("ctx", [CT, 2, CTILES, D])
        pr, pT = s_.sb("probs", [Q, 2, CTX]), s_.sb("probsT", [CT, 2, CTILES, Q])
        nmax, rsum, coef = (s_.sb(n, [Q, 2, 1]) for n in ("nmax", "rsum", "coef"))
        qbk, total = s_.sb("qbk", [Q, 2, 1]), s_.sb("total", [Q, 2, 1])
        norm = Norm(s_, 2)
        wq_loaded, wk_loaded, b_loaded = s_.sem("wq_loaded"), s_.sem("wk_loaded"), s_.sem("b_loaded")
        x_loaded = [s_.sem(f"x_loaded{i}") for i in range(2)]
        x_stored = [s_.sem(f"x_stored{i}") for i in range(2)]
        ctx_loaded = [s_.sem(f"ctx_loaded{i}") for i in range(2)]
        ctx_free = [s_.sem(f"ctx_free{i}") for i in range(2)]
        z_ready, zT_ready, q_ready, qT_ready, t_ready, tT_ready = (
            s_.sem(n) for n in ("z_ready", "zT_ready", "q_ready", "qT_ready", "t_ready", "tT_ready"))
        max_ready, probs_ready, pT_ready, x_done = (
            s_.sem(n) for n in ("max_ready", "probs_ready", "pT_ready", "x_done"))
        order = []
        for st, b0, n in (("zT", 0, 2), ("q", 2, 2), ("qT", 0, 2), ("t", 2, 2), ("tT", 0, 2), ("S", 2, 1), ("pT", 3, 1),
                          ("o", 0, 2)):
            order += [((st, s, h), 4 * s + b0 + h) for s in range(2) for h in range(n)]
        turns = Turns(banks, order, PAIRS)
        block = ctx.enter_context(nc.Block())

        @block.sync
        def _(sp):
            sp.dma_start(wq[:], fold(A["L1_xattn_WqT"])).then_inc(wq_loaded, 16)
            sp.dma_start(wk[:], fold(A["L1_xattn_Wk"])).then_inc(wk_loaded, 16)
            stream_x(sp, x, x_in, x_out, x_loaded, x_done, x_stored)

        @block.gpsimd
        def _(pool):
            pool.dma_start(bq[:], rows(A["L1_xattn_bq"], Q)).then_inc(b_loaded, 16)
            pool.dma_start(bk[:], A["L1_xattn_bk"]).then_inc(b_loaded, 16)
            with pool.Fori(0, PAIRS) as p:
                for s in range(2):
                    pool.wait_ge(ctx_free[s], p + 1)
                    pool.dma_start(cT[:, s], A["ctxT"][p * 2 + s].rearrange("(k p) n -> p k n", p=P)).then_inc(ctx_loaded[s], 16)
                    pool.dma_start(cN[:, s], A["ctx_4096"][p * 2 + s].rearrange("(t p) n -> p t n", p=CT)).then_inc(ctx_loaded[s], 16)

        @block.tensor
        def _(pe):
            pe.wait_ge(wq_loaded, 16)
            pe.wait_ge(wk_loaded, 16)
            pe.wait_ge(b_loaded, 32)
            with pe.Fori(0, PAIRS) as p:
                for s in range(2):
                    pe.wait_ge(z_ready, p * 2 + (s + 1))
                    turn_rows(pe, C, turns, z[:, s], "zT", s, p)
                for s in range(2):
                    pe.wait_ge(zT_ready, p * 2 + (s + 1))
                    project(pe, turns, zT[:, s], wq, "q", s, p)
                for s in range(2):
                    pe.wait_ge(q_ready, p * 2 + (s + 1))
                    turn_rows(pe, C, turns, q[:, s], "qT", s, p)
                for s in range(2):
                    pe.wait_ge(qT_ready, p * 2 + (s + 1))
                    project(pe, turns, qT[:, s], wk, "t", s, p)
                for s in range(2):
                    pe.wait_ge(t_ready, p * 2 + (s + 1))
                    turn_rows(pe, C, turns, t_[:, s], "tT", s, p)
                for s in range(2):
                    t = ("S", s, 0)
                    pe.wait_ge(tT_ready, p * 2 + (s + 1))
                    pe.wait_ge(ctx_loaded[s], p * 32 + 32)
                    pe.wait_ge(turns.free(t), turns.count(t, p))
                    for k in range(KC):
                        pe.matmul(turns.tile(t)[0:Q, 0:CTX], tT[:, s, k, :], cT[:, s, k, :], start=(k == 0), stop=(k == KC - 1))
                    for k in range(KC):
                        mm = pe.matmul(turns.tile(t)[0:Q, 400:401], qT[:, s, k, :], bk[:, k:k + 1], start=(k == 0),
                                       stop=(k == KC - 1))
                    mm.then_inc(turns.full(t), 1)
                for s in range(2):
                    t = ("pT", s, 0)
                    pe.wait_ge(probs_ready, p * 2 + (s + 1))
                    pe.wait_ge(turns.free(t), turns.count(t, p))
                    for k in range(CTILES):
                        mm = pe.transpose(turns.tile(t)[0:CT, k * Q:(k + 1) * Q], pr[:, s, k * CT:(k + 1) * CT], C.ident[0:Q, 0:Q])
                    mm.then_inc(turns.full(t), 1)
                for s in range(2):
                    pe.wait_ge(pT_ready, p * 2 + (s + 1))
                    for h in range(2):
                        t = ("o", s, h)
                        pe.wait_ge(turns.free(t), turns.count(t, p))
                        for k in range(CTILES):
                            mm = pe.matmul(turns.tile(t)[0:Q, :], pT[:, s, k, :], cN[:, s, k, h * 512:(h + 1) * 512],
                                           start=(k == 0), stop=(k == CTILES - 1))
                        mm.then_inc(turns.full(t), 1)

        @block.scalar
        def _(act):
            with act.Fori(0, PAIRS) as p:
                for s in range(2):
                    norm.root(act, s, p * 2 + s)
                for s in range(2):
                    copy_turned(act, turns, zT[:, s], "zT", s, p, zT_ready)
                for s in range(2):
                    copy_turned(act, turns, qT[:, s], "qT", s, p, qT_ready)
                for s in range(2):
                    copy_turned(act, turns, tT[:, s], "tT", s, p, tT_ready)
                for s in range(2):
                    t = ("S", s, 0)
                    act.wait_ge(max_ready, p * 2 + (s + 1))
                    act.activation(pr[:, s, :], turns.tile(t)[0:Q, 0:CTX], ACT.Exp, bias=nmax[:, s, :], scale=SCALE,
                                   accum_out=rsum[:, s, :])
                    act.drain().then_inc(turns.free(t), 1)
                    act.drain().then_inc(probs_ready, 1)

        @block.vector
        def _(dve):
            for s in range(2):
                dve.sem_inc(ctx_free[s], 1)
            dve.wait_ge(b_loaded, 32)
            with dve.Fori(0, PAIRS) as p:
                for s in range(2):
                    dve.wait_ge(x_loaded[s], p * 16 + 16)
                    norm.statistics(dve, x[:, s, :], s)
                for s in range(2):
                    norm.scale(dve, x[:, s, :], z[:, s, :], s, p * 2 + s).then_inc(z_ready, 1)
                for s in range(2):
                    for h in range(2):
                        t = ("q", s, h)
                        c = slice(h * 512, (h + 1) * 512)
                        dve.wait_ge(turns.full(t), turns.count(t, p))
                        dve.tensor_tensor(q[:, s, c], turns.tile(t)[0:Q, :], bq[:, c], ALU.add).then_inc(turns.free(t), 1)
                    dve.drain().then_inc(q_ready, 1)
                for s in range(2):
                    for h in range(2):
                        t = ("t", s, h)
                        dve.wait_ge(turns.full(t), turns.count(t, p))
                        dve.tensor_copy(t_[:, s, h * 512:(h + 1) * 512], turns.tile(t)[0:Q, :]).then_inc(turns.free(t), 1)
                    dve.drain().then_inc(t_ready, 1)
                for s in range(2):
                    t = ("S", s, 0)
                    dve.wait_ge(turns.full(t), turns.count(t, p))
                    dve.tensor_copy(qbk[:, s, :], turns.tile(t)[0:Q, 400:401])
                    dve.tensor_reduce(nmax[:, s, :], turns.tile(t)[0:Q, 0:CTX], AX, ALU.max, negate=True)
                    dve.drain()
                    dve.tensor_tensor(total[:, s, :], nmax[:, s, :], qbk[:, s, :], ALU.subtract)
                    dve.drain()
                    dve.tensor_scalar(nmax[:, s, :], total[:, s, :], qbk[:, s, :], SCALE, ALU.add, ALU.mult).then_inc(max_ready, 1)
                for s in range(2):
                    t = ("pT", s, 0)
                    dve.wait_ge(probs_ready, p * 2 + (s + 1))
                    dve.reciprocal(coef[:, s, :], rsum[:, s, :])
                    dve.wait_ge(turns.full(t), turns.count(t, p))
                    dve.tensor_copy(pT[:, s, :, :], turns.tile(t)[0:CT, 0:CTILES * Q].rearrange("p (k q) -> p k q", q=Q))\
                       .then_inc(turns.free(t), 1)
                    dve.drain().then_inc(pT_ready, 1)
                    dve.tensor_scalar(coef[:, s, :], coef[:, s, :], C.gates[0:Q, gate:gate + 1], None, ALU.mult)
                dve.drain()
                for s in range(2):
                    for h in range(2):
                        t = ("o", s, h)
                        c = slice(h * 512, (h + 1) * 512)
                        dve.wait_ge(turns.full(t), turns.count(t, p))
                        dve.scalar_tensor_tensor(out=x[:, s, c], in0=turns.tile(t)[0:Q, :], scalar=coef[:, s, :],
                                                 in1=x[:, s, c], op0=ALU.mult, op1=ALU.add).then_inc(turns.free(t), 1)
                    dve.drain().then_inc(x_done, 1)
                    dve.drain().then_inc(ctx_free[s], 1)


def memory_ffn(nc, C, banks, gate, x_in, x_out, A):
    BOT, RDIM, NSLOT, HU = 64, 48, 256, 256
    TAU_LOW, TAU_HIGH, EARLY_EXIT = 0.5, 2.0, 0.05
    with ExitStack() as ctx:
        s_ = Scope(nc, ctx, "mem")
        wqT, wu1T, wvdT = s_.sb("wqT", [P, KC, BOT]), s_.sb("wu1T", [P, KC, HU]), s_.sb("wvdT", [P, KC, BOT])
        wu2, bu1 = s_.sb("wu2", [P, 2]), s_.sb("bu1", [P, 2])
        bu2, gw1, gbias = (s_.sb(n, [Q, 1]) for n in ("bu2", "gw1", "gbias"))
        wrT, keysT, wvuT = s_.sb("wrT", [BOT, P]), s_.sb("keysT", [BOT, NSLOT]), s_.sb("wvuT", [BOT, D])
        valuesT, rel = s_.sb("valuesT", [P, KC, NSLOT]), s_.sb("log_rel", [Q, NSLOT])
        ones = s_.sb("ones", [Q, Q])
        av, rkT = s_.sb("av", [P, 2, BOT]), s_.sb("rkT", [RDIM, NSLOT])
        x, z = s_.sb("x", [Q, 2, D]), s_.sb("z", [Q, 2, D])
        zT = s_.sb("zT", [P, KC, 2 * Q])
        queryT, hidT = s_.sb("queryT", [BOT, 2 * Q]), s_.sb("hidT", [P, 2, 2 * Q])
        rqT, vT = s_.sb("rqT", [RDIM, 2 * Q]), s_.sb("vT", [BOT, 2 * Q])
        route, attn, left = (s_.sb(n, [Q, 2, NSLOT]) for n in ("route", "attn", "left"))
        w, wT = s_.sb("w", [Q, 2, NSLOT]), s_.sb("wT", [P, 2, 2, Q])
        best = s_.sb("best", [Q, 2, 8])
        nmax, rsum, coef, var_z, log_var, learned, unsure, keep = (
            s_.sb(n, [Q, 2]) for n in ("nmax", "rsum", "coef", "var_z", "log_var", "learned", "unsure", "keep"))
        lsum, rmean = s_.sb("lsum", [Q, 1]), s_.sb("rmean", [Q, 1])
        norm = Norm(s_, 2)
        w_loaded = s_.sem("w_loaded")
        pre_loaded = [s_.sem(f"pre_loaded{i}") for i in range(2)]
        pre_free = [s_.sem(f"pre_free{i}") for i in range(2)]
        x_loaded = [s_.sem(f"x_loaded{i}") for i in range(2)]
        x_stored = [s_.sem(f"x_stored{i}") for i in range(2)]
        pre_var, pre_log, lsum_ready, tables_ready = (s_.sem(n) for n in ("pre_var", "pre_log", "lsum_ready", "tables_ready"))
        z_ready, zT_ready, proj_ready, rq_ready, sig_ready, un_ready, gate_ready = (
            s_.sem(n) for n in ("z_ready", "zT_ready", "proj_ready", "rq_ready", "sig_ready", "un_ready", "gate_ready"))
        max_ready, w_ready, wT_ready, v_ready, x_done = (
            s_.sem(n) for n in ("max_ready", "w_ready", "wT_ready", "v_ready", "x_done"))
        prep = Turns(banks, [("lsum", 0), ("rk", 1), ("av", 2)], 1)
        turns = Turns(banks, [(("zT", s, h), 2 * s + h) for s in range(2) for h in range(2)]
                      + [("query", 4), ("hid", 5), ("rq", 6), ("learned", 7)]
                      + [(("scores", s), s) for s in range(2)] + [(("wT", s), 2 + s) for s in range(2)] + [("v", 4)]
                      + [(("o", s, h), (5, 6, 7, 0)[2 * s + h]) for s in range(2) for h in range(2)], PAIRS)
        weights = [(wqT, fold(A["L1_ffn_WqT"])), (wu1T, fold(A["L1_ffn_Wu1T"])), (wvdT, fold(A["L1_ffn_WvdT"])),
                   (wu2, A["L1_ffn_Wu2"]), (bu1, A["L1_ffn_bu1"]), (bu2, rows(A["L1_ffn_bu2"], Q)),
                   (gw1, rows(A["L1_ffn_gate_w1"], Q)), (gbias, rows(A["L1_ffn_gate_bias"], Q)),
                   (wrT, A["L1_ffn_WrT"]), (keysT, A["L1_ffn_aux_keysT"]), (wvuT, A["L1_ffn_WvuT"]),
                   (valuesT, fold(A["L1_ffn_aux_valuesT"])), (rel, rows(A["L1_ffn_log_rel"], Q))]
        block = ctx.enter_context(nc.Block())

        @block.sync
        def _(sp):
            with sp.Fori(0, PAIRS) as p:
                for s in range(2):
                    sp.wait_ge(pre_free[s], p + 1)
                    sp.dma_start(x[:, s, :], x_in[p * 2 + s]).then_inc(pre_loaded[s], 16)
            for s in range(2):
                sp.wait_ge(pre_free[s], PAIRS + 1)
            stream_x(sp, x, x_in, x_out, x_loaded, x_done, x_stored)

        @block.gpsimd
        def _(pool):
            for dst, src in weights:
                pool.dma_start(dst[:], src).then_inc(w_loaded, 16)

        @block.tensor
        def _(pe):
            pe.wait_ge(w_loaded, 16 * len(weights))
            pe.wait_ge(prep.free("rk"), prep.count("rk", 0))
            pe.matmul(prep.tile("rk")[:, 0:NSLOT], wrT[:], keysT[:], start=True, stop=True).then_inc(prep.full("rk"), 1)
            pe.wait_ge(prep.free("av"), prep.count("av", 0))
            for c in range(2):
                for k in range(KC):
                    mm = pe.matmul(prep.tile("av")[:, c * BOT:(c + 1) * BOT], valuesT[:, k, c * P:(c + 1) * P], wvdT[:, k, :],
                                   start=(k == 0), stop=(k == KC - 1))
            mm.then_inc(prep.full("av"), 1)
            pe.wait_ge(lsum_ready, 1)
            pe.wait_ge(prep.free("lsum"), prep.count("lsum", 0))
            pe.matmul(prep.tile("lsum")[0:Q, 0:1], ones[:], lsum[:], start=True, stop=True).then_inc(prep.full("lsum"), 1)
            pe.wait_ge(tables_ready, 2)
            with pe.Fori(0, PAIRS) as p:
                for s in range(2):
                    pe.wait_ge(z_ready, p * 2 + (s + 1))
                    turn_rows(pe, C, turns, z[:, s], "zT", s, p)
                pe.wait_ge(zT_ready, p * 2 + 2)
                pe.wait_ge(turns.free("query"), turns.count("query", p))
                for k in range(KC):
                    mm = pe.matmul(turns.tile("query")[0:BOT, 0:2 * Q], wqT[:, k, :], zT[:, k, :], start=(k == 0), stop=(k == KC - 1))
                mm.then_inc(turns.full("query"), 1)
                pe.wait_ge(turns.free("hid"), turns.count("hid", p))
                for c in range(2):
                    for k in range(KC):
                        mm = pe.matmul(turns.tile("hid")[:, c * 2 * Q:(c + 1) * 2 * Q], wu1T[:, k, c * P:(c + 1) * P], zT[:, k, :],
                                       start=(k == 0), stop=(k == KC - 1))
                mm.then_inc(turns.full("hid"), 1)
                pe.wait_ge(proj_ready, p * 2 + 1)
                pe.wait_ge(turns.free("rq"), turns.count("rq", p))
                pe.matmul(turns.tile("rq")[:, 0:2 * Q], wrT[:], queryT[:], start=True, stop=True).then_inc(turns.full("rq"), 1)
                pe.wait_ge(proj_ready, p * 2 + 2)
                pe.wait_ge(turns.free("learned"), turns.count("learned", p))
                for s in range(2):
                    for c in range(2):
                        mm = pe.matmul(turns.tile("learned")[0:Q, s:s + 1], hidT[:, c, s * Q:(s + 1) * Q], wu2[:, c:c + 1],
                                       start=(c == 0), stop=(c == 1))
                mm.then_inc(turns.full("learned"), 1)
                pe.wait_ge(rq_ready, p + 1)
                for s in range(2):
                    t = ("scores", s)
                    pe.wait_ge(turns.free(t), turns.count(t, p))
                    pe.matmul(turns.tile(t)[0:Q, 0:NSLOT], rqT[:, s * Q:(s + 1) * Q], rkT[:], start=True, stop=True)
                    pe.matmul(turns.tile(t)[0:Q, NSLOT:2 * NSLOT], queryT[:, s * Q:(s + 1) * Q], keysT[:], start=True,
                              stop=True).then_inc(turns.full(t), 1)
                for s in range(2):
                    t = ("wT", s)
                    pe.wait_ge(w_ready, p * 2 + (s + 1))
                    pe.wait_ge(turns.free(t), turns.count(t, p))
                    for c in range(2):
                        mm = pe.transpose(turns.tile(t)[:, c * Q:(c + 1) * Q], w[:, s, c * P:(c + 1) * P], C.ident[0:Q, 0:Q])
                    mm.then_inc(turns.full(t), 1)
                pe.wait_ge(wT_ready, p * 2 + 2)
                pe.wait_ge(turns.free("v"), turns.count("v", p))
                for c in range(2):
                    mm = pe.matmul(turns.tile("v")[0:BOT, 0:2 * Q], av[:, c, :], wT[:, c, :, :], start=(c == 0), stop=(c == 1))
                mm.then_inc(turns.full("v"), 1)
                pe.wait_ge(v_ready, p + 1)
                for s in range(2):
                    for h in range(2):
                        t = ("o", s, h)
                        pe.wait_ge(turns.free(t), turns.count(t, p))
                        pe.matmul(turns.tile(t)[0:Q, :], vT[:, s * Q:(s + 1) * Q], wvuT[:, h * 512:(h + 1) * 512], start=True,
                                  stop=True).then_inc(turns.full(t), 1)

        @block.scalar
        def _(act):
            act.wait_ge(prep.full("rk"), prep.count("rk", 0))
            act.activation(rkT[:], prep.tile("rk")[0:RDIM, 0:NSLOT], ACT.Copy).then_inc(prep.free("rk"), 1)
            act.wait_ge(prep.full("av"), prep.count("av", 0))
            act.activation(av[:], prep.tile("av")[:, 0:2 * BOT].rearrange("p (c n) -> p c n", c=2), ACT.Copy)\
               .then_inc(prep.free("av"), 1)
            act.drain().then_inc(tables_ready, 1)
            with act.Fori(0, PAIRS) as p:
                act.wait_ge(pre_var, p + 1)
                act.activation(log_var[:], var_z[:], ACT.Ln, bias=1.0).then_inc(pre_log, 1)
            with act.Fori(0, PAIRS) as p:
                for s in range(2):
                    norm.root(act, s, p * 2 + s)
                for s in range(2):
                    copy_turned(act, turns, zT[:, :, s * Q:(s + 1) * Q], "zT", s, p, zT_ready)
                act.wait_ge(turns.full("query"), turns.count("query", p))
                act.activation(queryT[:], turns.tile("query")[0:BOT, 0:2 * Q], ACT.Copy).then_inc(turns.free("query"), 1)
                act.drain().then_inc(proj_ready, 1)
                act.wait_ge(turns.full("hid"), turns.count("hid", p))
                for c in range(2):
                    act.activation(hidT[:, c, :], turns.tile("hid")[:, c * 2 * Q:(c + 1) * 2 * Q], ACT.Gelu_apprx_tanh,
                                   bias=bu1[:, c:c + 1])
                act.drain().then_inc(turns.free("hid"), 1)
                act.drain().then_inc(proj_ready, 1)
                act.wait_ge(turns.full("rq"), turns.count("rq", p))
                act.activation(rqT[:], turns.tile("rq")[0:RDIM, 0:2 * Q], ACT.Copy).then_inc(turns.free("rq"), 1)
                act.drain().then_inc(rq_ready, 1)
                for s in range(2):
                    act.wait_ge(max_ready, p * 2 + (s + 1))
                    act.activation(w[:, s, :], attn[:, s, :], ACT.Exp, bias=nmax[:, s:s + 1], accum_out=rsum[:, s:s + 1])
                    act.drain().then_inc(w_ready, 1)
                act.activation(log_var[:], var_z[:], ACT.Ln, bias=1.0)
                act.wait_ge(turns.full("learned"), turns.count("learned", p))
                act.activation(learned[:], turns.tile("learned")[0:Q, 0:2], ACT.Sigmoid, bias=bu2[:]).then_inc(turns.free("learned"), 1)
                act.drain().then_inc(sig_ready, 1)
                act.wait_ge(un_ready, p + 1)
                act.activation(coef[:], unsure[:], ACT.Sigmoid, bias=gbias[:], scale=gw1[:]).then_inc(gate_ready, 1)
                act.wait_ge(turns.full("v"), turns.count("v", p))
                act.activation(vT[:], turns.tile("v")[0:BOT, 0:2 * Q], ACT.Copy).then_inc(turns.free("v"), 1)
                act.drain().then_inc(v_ready, 1)

        @block.vector
        def _(dve):
            for s in range(2):
                dve.sem_inc(pre_free[s], 1)
            dve.memset(ones[:], 1.0)
            dve.memset(lsum[:], 0.0)
            with dve.Fori(0, PAIRS) as p:
                for s in range(2):
                    dve.wait_ge(pre_loaded[s], p * 16 + 16)
                    for h in range(2):
                        dve.bn_stats(norm.stats[:, s, h, :], x[:, s, h * 512:(h + 1) * 512])
                    dve.drain()
                    dve.bn_aggr(norm.mv[:, s, :], norm.stats[:, s, :, :]).then_inc(pre_free[s], 1)
                dve.drain()
                dve.tensor_scalar(norm.rstd[:, :, 0], norm.mv[:, :, 1], EPS, None, ALU.add)
                dve.drain()
                dve.reciprocal(norm.rstd[:, :, 0], norm.rstd[:, :, 0])
                dve.drain()
                dve.tensor_tensor(var_z[:], norm.mv[:, :, 1], norm.rstd[:, :, 0], ALU.mult).then_inc(pre_var, 1)
                dve.wait_ge(pre_log, p + 1)
                for s in range(2):
                    dve.tensor_tensor(lsum[:], lsum[:], log_var[:, s:s + 1], ALU.add)
                    dve.drain()
            dve.sem_inc(lsum_ready, 1)
            dve.wait_ge(prep.full("lsum"), prep.count("lsum", 0))
            dve.tensor_scalar(rmean[:], prep.tile("lsum")[0:Q, 0:1], 1.0 / (B * Q), 1e-6, ALU.mult, ALU.add)\
               .then_inc(prep.free("lsum"), 1)
            dve.drain()
            dve.reciprocal(rmean[:], rmean[:])
            dve.drain().then_inc(tables_ready, 1)
            gc = C.gates[0:Q, gate:gate + 1]
            with dve.Fori(0, PAIRS) as p:
                for s in range(2):
                    dve.wait_ge(x_loaded[s], p * 16 + 16)
                    norm.statistics(dve, x[:, s, :], s)
                for s in range(2):
                    norm.scale(dve, x[:, s, :], z[:, s, :], s, p * 2 + s).then_inc(z_ready, 1)
                dve.tensor_tensor(var_z[:], norm.mv[:, :, 1], norm.rstd[:, :, 0], ALU.mult)
                dve.drain()
                dve.tensor_tensor(var_z[:], var_z[:], norm.rstd[:, :, 0], ALU.mult)
                for s in range(2):
                    dve.scalar_tensor_tensor(out=x[:, s, :], in0=z[:, s, :], scalar=gc, in1=x[:, s, :], op0=ALU.mult, op1=ALU.add)
                for s in range(2):
                    t = ("scores", s)
                    dve.wait_ge(turns.full(t), turns.count(t, p))
                    dve.scalar_tensor_tensor(out=route[:, s, :], in0=turns.tile(t)[0:Q, 0:NSLOT], scalar=float(RDIM) ** -0.5,
                                             in1=rel[:], op0=ALU.mult, op1=ALU.add)
                    dve.scalar_tensor_tensor(out=attn[:, s, :], in0=turns.tile(t)[0:Q, NSLOT:2 * NSLOT], scalar=float(BOT) ** -0.5,
                                             in1=rel[:], op0=ALU.mult, op1=ALU.add)
                    dve.drain().then_inc(turns.free(t), 1)
                    dve.max(best[:, s, :], route[:, s, :])
                    dve.drain()
                    dve.match_replace(left[:, s, :], best[:, s, :], route[:, s, :], -3e38)
                    dve.drain()
                    dve.tensor_tensor(left[:, s, :], left[:, s, :], route[:, s, :], ALU.is_equal)
                    dve.drain()
                    dve.scalar_tensor_tensor(out=attn[:, s, :], in0=left[:, s, :], scalar=LOW, in1=attn[:, s, :],
                                             op0=ALU.mult, op1=ALU.add)
                    dve.drain()
                    dve.tensor_reduce(nmax[:, s:s + 1], attn[:, s, :], AX, ALU.max, negate=True).then_inc(max_ready, 1)
                for s in range(2):
                    t = ("wT", s)
                    dve.wait_ge(turns.full(t), turns.count(t, p))
                    dve.tensor_copy(wT[:, :, s, :], turns.tile(t)[:, 0:2 * Q].rearrange("p (c q) -> p c q", c=2))\
                       .then_inc(turns.free(t), 1)
                    dve.drain().then_inc(wT_ready, 1)
                dve.wait_ge(sig_ready, p + 1)
                dve.tensor_scalar(unsure[:], log_var[:], rmean[:], 0.5, ALU.mult, ALU.mult)
                dve.drain()
                dve.scalar_tensor_tensor(out=unsure[:], in0=learned[:], scalar=2.5, in1=unsure[:], op0=ALU.mult, op1=ALU.add)
                dve.drain()
                dve.tensor_scalar(unsure[:], unsure[:], 0.0, 5.0, ALU.max, ALU.min)
                dve.drain()
                dve.tensor_scalar(unsure[:], unsure[:], TAU_LOW, 1.0 / (TAU_HIGH - TAU_LOW), ALU.subtract, ALU.mult)
                dve.drain()
                dve.tensor_scalar(unsure[:], unsure[:], 0.0, 1.0, ALU.max, ALU.min).then_inc(un_ready, 1)
                dve.reciprocal(rsum[:], rsum[:])
                dve.wait_ge(gate_ready, p + 1)
                dve.tensor_scalar(keep[:], coef[:], EARLY_EXIT, gc, ALU.is_ge, ALU.mult)
                dve.drain()
                dve.tensor_tensor(coef[:], coef[:], keep[:], ALU.mult)
                dve.drain()
                dve.tensor_tensor(coef[:], coef[:], rsum[:], ALU.mult)
                dve.drain()
                for s in range(2):
                    for h in range(2):
                        t = ("o", s, h)
                        c = slice(h * 512, (h + 1) * 512)
                        dve.wait_ge(turns.full(t), turns.count(t, p))
                        dve.scalar_tensor_tensor(out=x[:, s, c], in0=turns.tile(t)[0:Q, :], scalar=coef[:, s:s + 1],
                                                 in1=x[:, s, c], op0=ALU.mult, op1=ALU.add).then_inc(turns.free(t), 1)
                    dve.drain().then_inc(x_done, 1)


def experts_ffn(nc, C, banks, gate, x_in, x_out, A):
    NE, RANK = 8, 64
    R = NE * RANK
    with ExitStack() as ctx:
        s_ = Scope(nc, ctx, "moe")
        aT, bT, gT = s_.sb("aT", [P, KC, R]), s_.sb("bT", [P, R // P, D]), s_.sb("gT", [P, KC, NE])
        x, z = s_.sb("x", [Q, 2, D]), s_.sb("z", [Q, 2, D])
        zT = s_.sb("zT", [P, 2, KC, Q])
        prob, best, w8, hit = (s_.sb(n, [Q, 2, NE]) for n in ("prob", "best", "w8", "hit"))
        place, placef = s_.sb("place", [Q, 2, 8], U32), s_.sb("placef", [Q, 2, 8])
        number = s_.sb("number", [Q, NE])
        nmax, both = s_.sb("nmax", [Q, 2]), s_.sb("both", [Q, 2])
        h, hT = s_.sb("h", [Q, 2, R]), s_.sb("hT", [P, 2, R // P, Q])
        norm = Norm(s_, 2)
        w_loaded = s_.sem("w_loaded")
        x_loaded = [s_.sem(f"x_loaded{i}") for i in range(2)]
        x_stored = [s_.sem(f"x_stored{i}") for i in range(2)]
        z_ready, zT_ready, max_ready, prob_ready, h_ready, hT_ready, x_done, numbered = (
            s_.sem(n) for n in ("z_ready", "zT_ready", "max_ready", "prob_ready", "h_ready", "hT_ready", "x_done", "numbered"))
        turns = Turns(banks, [(("zT", s, i), 4 * s + i) for s in range(2) for i in range(2)]
                      + [((n, s), 4 * s + i) for n, i in (("gate", 2), ("h", 3)) for s in range(2)]
                      + [(("hT", s, 0), 4 * s) for s in range(2)]
                      + [(("o", s, i), 4 * s + 1 + i) for s in range(2) for i in range(2)], PAIRS)
        weights = [(aT, fold(A["L3_lora_AT"])), (bT, fold(A["L3_lora_BT"])), (gT, fold(A["L3_ffn_gate_wT"]))]
        block = ctx.enter_context(nc.Block())

        @block.sync
        def _(sp):
            stream_x(sp, x, x_in, x_out, x_loaded, x_done, x_stored)

        @block.gpsimd
        def _(pool):
            pool.iota(number[:], pattern=[[1, NE]], base=0, channel_multiplier=0,
                      allow_small_or_imprecise_dtypes=True).then_inc(numbered, 1)
            for dst, src in weights:
                pool.dma_start(dst[:], src).then_inc(w_loaded, 16)

        @block.tensor
        def _(pe):
            pe.wait_ge(w_loaded, 16 * len(weights))
            with pe.Fori(0, PAIRS) as p:
                for s in range(2):
                    pe.wait_ge(z_ready, p * 2 + (s + 1))
                    turn_rows(pe, C, turns, z[:, s], "zT", s, p)
                for s in range(2):
                    pe.wait_ge(zT_ready, p * 2 + (s + 1))
                    for name, w, n in (("gate", gT, NE), ("h", aT, R)):
                        t = (name, s)
                        pe.wait_ge(turns.free(t), turns.count(t, p))
                        for k in range(KC):
                            mm = pe.matmul(turns.tile(t)[0:Q, 0:n], zT[:, s, k, :], w[:, k, :], start=(k == 0), stop=(k == KC - 1))
                        mm.then_inc(turns.full(t), 1)
                for s in range(2):
                    pe.wait_ge(h_ready, p * 2 + (s + 1))
                    turn_rows(pe, C, turns, h[:, s], "hT", s, p, n=1)
                for s in range(2):
                    pe.wait_ge(hT_ready, p * 2 + (s + 1))
                    project(pe, turns, hT[:, s], bT, "o", s, p)

        @block.scalar
        def _(act):
            with act.Fori(0, PAIRS) as p:
                for s in range(2):
                    norm.root(act, s, p * 2 + s)
                for s in range(2):
                    copy_turned(act, turns, zT[:, s], "zT", s, p, zT_ready)
                for s in range(2):
                    t = ("gate", s)
                    act.wait_ge(max_ready, p * 2 + (s + 1))
                    act.activation(prob[:, s, :], turns.tile(t)[0:Q, 0:NE], ACT.Exp, bias=nmax[:, s:s + 1]).then_inc(turns.free(t), 1)
                    act.drain().then_inc(prob_ready, 1)
                for s in range(2):
                    copy_turned(act, turns, hT[:, s], "hT", s, p, hT_ready, n=1)

        @block.vector
        def _(dve):
            dve.wait_ge(numbered, 1)
            gc = C.gates[0:Q, gate:gate + 1]
            with dve.Fori(0, PAIRS) as p:
                for s in range(2):
                    dve.wait_ge(x_loaded[s], p * 16 + 16)
                    norm.statistics(dve, x[:, s, :], s)
                for s in range(2):
                    norm.scale(dve, x[:, s, :], z[:, s, :], s, p * 2 + s).then_inc(z_ready, 1)
                for s in range(2):
                    t = ("gate", s)
                    dve.wait_ge(turns.full(t), turns.count(t, p))
                    dve.tensor_reduce(nmax[:, s:s + 1], turns.tile(t)[0:Q, 0:NE], AX, ALU.max, negate=True).then_inc(max_ready, 1)
                for s in range(2):
                    dve.wait_ge(prob_ready, p * 2 + (s + 1))
                    dve.tensor_reduce(both[:, s:s + 1], prob[:, s, :], AX, ALU.add)
                    dve.drain()
                    dve.reciprocal(both[:, s:s + 1], both[:, s:s + 1])
                    dve.drain()
                    dve.tensor_scalar(prob[:, s, :], prob[:, s, :], both[:, s:s + 1], None, ALU.mult)
                    dve.drain()
                    dve.max(best[:, s, :], prob[:, s, :])
                    dve.drain()
                    dve.max_index(place[:, s, :], best[:, s, :], prob[:, s, :])
                    dve.tensor_tensor(both[:, s:s + 1], best[:, s, 0:1], best[:, s, 1:2], ALU.add)
                    dve.drain()
                    dve.tensor_copy(placef[:, s, :], place[:, s, :])
                    dve.reciprocal(both[:, s:s + 1], both[:, s:s + 1])
                    dve.drain()
                    dve.tensor_scalar(best[:, s, 0:2], best[:, s, 0:2], both[:, s:s + 1], gc, ALU.mult, ALU.mult)
                    dve.drain()
                    dve.tensor_scalar(w8[:, s, :], number[:], placef[:, s, 0:1], best[:, s, 0:1], ALU.is_equal, ALU.mult)
                    dve.tensor_scalar(hit[:, s, :], number[:], placef[:, s, 1:2], best[:, s, 1:2], ALU.is_equal, ALU.mult)
                    dve.drain()
                    dve.tensor_tensor(w8[:, s, :], w8[:, s, :], hit[:, s, :], ALU.add)
                    dve.drain()
                    t = ("h", s)
                    dve.wait_ge(turns.full(t), turns.count(t, p))
                    dve.tensor_tensor(h[:, s, :].rearrange("q (e r) -> q e r", e=NE),
                                      turns.tile(t)[0:Q, :].rearrange("q (e r) -> q e r", e=NE),
                                      w8[:, s, :].unsqueeze(2).broadcast_to([Q, NE, RANK]), ALU.mult).then_inc(turns.free(t), 1)
                    dve.drain().then_inc(h_ready, 1)
                for s in range(2):
                    for i in range(2):
                        t = ("o", s, i)
                        c = slice(i * 512, (i + 1) * 512)
                        dve.wait_ge(turns.full(t), turns.count(t, p))
                        dve.tensor_tensor(x[:, s, c], turns.tile(t)[0:Q, :], x[:, s, c], ALU.add).then_inc(turns.free(t), 1)
                    dve.drain().then_inc(x_done, 1)


def latent_attention(nc, C, banks, gate, x_in, x_out, A, nearest):
    H, KV, HD = 16, 4, 96
    G = H // KV
    S = CTX + Q
    DK, DQ = KV * HD, H * HD
    OC = DQ // P
    SCALE = float(HD) ** -0.5
    KT = [(k * CT, CT) for k in range(CTILES)] + [(CTX, Q)]
    with ExitStack() as ctx:
        s_ = Scope(nc, ctx, "latent")
        wk, wv = s_.sb("wk", [P, KC, DK]), s_.sb("wv", [P, KC, DK])
        wq, wo = s_.sb("wq", [P, KC, DQ]), s_.sb("wo", [P, OC, D])
        x, z = s_.sb("x", [Q, 2, D]), s_.sb("z", [Q, D])
        hT = s_.sb("hT", [P, KC, S])
        kT, v = s_.sb("kT", [HD, KV, S]), s_.sb("v", [P, 4, DK])
        q, qT = s_.sb("q", [Q, DQ]), s_.sb("qT", [HD, H, Q])
        pr, pT = s_.sb("probs", [Q, 2, S]), s_.sb("probsT", [P, 2, 4, Q])
        o, oT = q, s_.sb("oT", [P, OC, Q])
        y = z
        nmax, rsum = s_.sb("nmax", [Q, H]), s_.sb("rsum", [Q, H])
        xy, here = s_.sb("xy", [P, 2, D]), s_.sb("here", [P, 2, KC])
        near, far = s_.sb("near", [P, D]), s_.sb("far", [P, D])
        top, rank = s_.sb("top", [P, 2, 8]), s_.sb("rank", [P, KC, 2, 8], U32)
        norm = Norm(s_, 1)
        wk_loaded, wv_loaded, wq_loaded, wo_loaded = (s_.sem(n) for n in ("wk_loaded", "wv_loaded", "wq_loaded", "wo_loaded"))
        x_loaded = [s_.sem(f"x_loaded{i}") for i in range(2)]
        x_stored = [s_.sem(f"x_stored{i}") for i in range(2)]
        hT_free, ctx_loaded, xy_free, xy_loaded = (s_.sem(n) for n in ("hT_free", "ctx_loaded", "xy_free", "xy_loaded"))
        here_ready, sq_ready, sq_free, rank_ready, rank_stored = (
            s_.sem(n) for n in ("here_ready", "sq_ready", "sq_free", "rank_ready", "rank_stored"))
        z_ready, zT_ready, v_ready, kT_ready, q_ready, qT_ready = (
            s_.sem(n) for n in ("z_ready", "zT_ready", "v_ready", "kT_ready", "q_ready", "qT_ready"))
        max_ready, probs_ready, pT_ready, heads_done, o_ready, oT_ready, y_ready, x_done = (
            s_.sem(n) for n in ("max_ready", "probs_ready", "pT_ready", "heads_done", "o_ready", "oT_ready", "y_ready", "x_done"))
        groups = ([("v", i) for i in range(CTILES)] + [("zT", 0, i) for i in range(2)] + [("v", 3)]
                  + [("k", i) for i in range(KV)] + [("q", i) for i in range(3)] + [("qT", i) for i in range(4)])
        order = [(g, i % 4) for i, g in enumerate(groups)]
        for h in range(H + 3):
            if h < H:
                order.append((("S", h), 4 + h % 2))
            if 2 <= h < H + 2:
                order.append((("pT", h - 2), 6 + h % 2))
            if h >= 3 and (h - 3) % G == 0:
                order.append((("o", (h - 3) // G), (h - 3) // G % 2))
        order += [(("oT", i), 2 + i % 2) for i in range(3)] + [(("y", i), i) for i in range(2)]
        turns = Turns(banks, order, B)
        block = ctx.enter_context(nc.Block())

        @block.sync
        def _(sp):
            def load_x(b, s):
                sp.dma_start(x[:, s, :], x_in[b]).then_inc(x_loaded[s], 16)

            def load_rest(b):
                sp.wait_ge(hT_free, b + 1)
                sp.dma_start(hT[:, :, 0:CTX], A["ctxT"][b].rearrange("(k p) n -> p k n", p=P)).then_inc(ctx_loaded, 16)
                sp.wait_ge(xy_free, b + 1)
                sp.dma_start(xy[:], A["planes"][b].rearrange("(a n) -> a n", a=1).broadcast_to([P, 2 * D])
                             .rearrange("p (c n) -> p c n", c=2)).then_inc(xy_loaded, 16)
                sp.dma_start(here[:], A["points"][b]).then_inc(xy_loaded, 16)

            with sp.Fori(0, PAIRS) as p:
                for s in range(2):
                    sp.wait_ge(x_stored[s], p * 16 + 16)
                    load_x(p * 2 + s, s)
                    load_rest(p * 2 + s)
            for s in range(2):
                sp.wait_ge(x_stored[s], 16 * PAIRS + 16)
            sp.wait_ge(rank_stored, 16 * B + 16)

        @block.gpsimd
        def _(pool):
            for s in range(2):
                pool.sem_inc(x_stored[s], 16)
            pool.sem_inc(rank_stored, 16)
            pool.dma_start(wv[:], fold(A["L0_xattn_WvT"])).then_inc(wv_loaded, 16)
            pool.dma_start(wk[:], fold(A["L0_xattn_WkT"])).then_inc(wk_loaded, 16)
            pool.dma_start(wq[:], fold(A["L0_xattn_WqT"])).then_inc(wq_loaded, 16)
            pool.dma_start(wo[:], fold(A["L0_xattn_WoT"])).then_inc(wo_loaded, 16)
            with pool.Fori(0, PAIRS) as p:
                for s in range(2):
                    pool.wait_ge(y_ready, p * 2 + (s + 1))
                    pool.tensor_tensor(x[:, s, :], x[:, s, :], y[:], ALU.add).then_inc(x_done, 1)

        @block.tensor
        def _(pe):
            pe.wait_ge(wv_loaded, 16)

            def fill(t, b, lhsT, rhs, m, n, chunks):
                pe.wait_ge(turns.free(t), turns.count(t, b))
                for k in range(chunks):
                    mm = pe.matmul(turns.tile(t)[0:m, 0:n], lhsT(k), rhs(k), start=(k == 0), stop=(k == chunks - 1))
                mm.then_inc(turns.full(t), 1)

            def sequence(b):
                pe.wait_ge(ctx_loaded, b * 16 + 16)
                for i in range(CTILES):
                    fill(("v", i), b, lambda k: hT[:, k, i * CT:(i + 1) * CT], lambda k: wv[:, k, :], CT, DK, KC)
                pe.wait_ge(z_ready, b + 1)
                turn_rows(pe, C, turns, z, "zT", 0, b)
                pe.wait_ge(zT_ready, b + 1)
                fill(("v", 3), b, lambda k: hT[:, k, CTX:S], lambda k: wv[:, k, :], Q, DK, KC)
                pe.wait_ge(wk_loaded, 16)
                for i in range(KV):
                    fill(("k", i), b, lambda k: wk[:, k, i * HD:(i + 1) * HD], lambda k: hT[:, k, :], HD, S, KC)
                pe.wait_ge(wq_loaded, 16)
                for i in range(3):
                    fill(("q", i), b, lambda k: hT[:, k, CTX:S], lambda k: wq[:, k, i * 512:(i + 1) * 512], Q, 512, KC)
                for i in range(4):
                    t = ("qT", i)
                    pe.wait_ge(q_ready, b * 3 + min(3, (i * 4 * HD + 4 * HD - 1) // 512 + 1))
                    pe.wait_ge(turns.free(t), turns.count(t, b))
                    for j in range(4):
                        h = 4 * i + j
                        mm = pe.transpose(turns.tile(t)[0:HD, j * Q:(j + 1) * Q], q[:, h * HD:(h + 1) * HD], C.ident[0:Q, 0:Q])
                    mm.then_inc(turns.full(t), 1)
                pe.wait_ge(kT_ready, b + 1)
                pe.wait_ge(v_ready, b + 1)
                for step in range(H + 3):
                    h = step
                    if h < H:
                        t = ("S", h)
                        pe.wait_ge(qT_ready, b * 4 + (h // 4 + 1))
                        pe.wait_ge(turns.free(t), turns.count(t, b))
                        pe.matmul(turns.tile(t)[0:Q, 0:S], qT[:, h, :], kT[:, h // G, :], start=True, stop=True)\
                          .then_inc(turns.full(t), 1)
                    h = step - 2
                    if 0 <= h < H:
                        t = ("pT", h)
                        pe.wait_ge(probs_ready, b * H + (h + 1))
                        pe.wait_ge(turns.free(t), turns.count(t, b))
                        for k, (c, n) in enumerate(KT):
                            mm = pe.transpose(turns.tile(t)[0:n, k * Q:(k + 1) * Q], pr[:, h % 2, c:c + n], C.ident[0:Q, 0:Q])
                        mm.then_inc(turns.full(t), 1)
                    h = step - 3
                    if h >= 0:
                        t = ("o", h // G)
                        pe.wait_ge(pT_ready, b * H + (h + 1))
                        if h % G == 0:
                            pe.wait_ge(turns.free(t), turns.count(t, b))
                        for k, (c, n) in enumerate(KT):
                            mm = pe.matmul(turns.tile(t)[0:Q, h % G * HD:(h % G + 1) * HD], pT[0:n, h % 2, k, :],
                                           v[0:n, k, h // G * HD:(h // G + 1) * HD], start=(k == 0), stop=(k == len(KT) - 1))
                        mm.then_inc(turns.full(t) if h % G == G - 1 else heads_done, 1)
                for i in range(3):
                    t = ("oT", i)
                    pe.wait_ge(o_ready, b * KV + min(KV, (i * 512 + 511) // (G * HD) + 1))
                    pe.wait_ge(turns.free(t), turns.count(t, b))
                    for j in range(4):
                        c = (4 * i + j) * P
                        mm = pe.transpose(turns.tile(t)[:, j * Q:(j + 1) * Q], o[:, c:c + P], C.ident[0:Q, 0:Q])
                    mm.then_inc(turns.full(t), 1)
                pe.wait_ge(oT_ready, b + 1)
                pe.wait_ge(wo_loaded, 16)
                for i in range(2):
                    fill(("y", i), b, lambda k: oT[:, k, :], lambda k: wo[:, k, i * 512:(i + 1) * 512], Q, 512, OC)

            with pe.Fori(0, B) as b:
                sequence(b)

        def squares(act, t):
            act.activation(near[:], xy[:, 0, :], ACT.Square, bias=here[:, 0, t:t + 1])
            act.activation(far[:], xy[:, 1, :], ACT.Square, bias=here[:, 1, t:t + 1]).then_inc(sq_ready, 1)

        @block.scalar
        def _(act):
            with act.Fori(0, PAIRS) as p:
                for s in range(2):
                    b = p * 2 + s
                    tile = 0

                    def distances():
                        nonlocal tile
                        if tile == 0:
                            act.wait_ge(here_ready, b + 1)
                        act.wait_ge(sq_free, b * KC + (tile + 1))
                        squares(act, tile)
                        tile += 1

                    def empty(t, dst, src, scale=1.0):
                        act.wait_ge(turns.full(t), turns.count(t, b))
                        act.activation(dst, src, ACT.Copy, scale=scale).then_inc(turns.free(t), 1)

                    norm.root(act, 0, b)
                    for i in range(CTILES):
                        empty(("v", i), v[0:CT, i, :], turns.tile(("v", i))[0:CT, 0:DK])
                        if i < 2:
                            distances()
                    copy_turned(act, turns, hT[:, :, CTX:S], "zT", 0, b, zT_ready)
                    empty(("v", 3), v[0:Q, 3, :], turns.tile(("v", 3))[0:Q, 0:DK])
                    act.drain().then_inc(v_ready, 1)
                    for i in range(KV):
                        empty(("k", i), kT[:, i, :], turns.tile(("k", i))[0:HD, 0:S])
                        distances()
                    act.drain().then_inc(kT_ready, 1)
                    for i in range(3):
                        empty(("q", i), q[:, i * 512:(i + 1) * 512], turns.tile(("q", i))[0:Q, :], scale=SCALE)
                        act.drain().then_inc(q_ready, 1)
                        if i < 2:
                            distances()
                    act.sem_inc(hT_free, 1)
                    for i in range(4):
                        empty(("qT", i), qT[:, 4 * i:4 * i + 4, :],
                              turns.tile(("qT", i))[0:HD, 0:4 * Q].rearrange("p (j q) -> p j q", j=4))
                        act.drain().then_inc(qT_ready, 1)
                    for h in range(H):
                        t = ("S", h)
                        act.wait_ge(max_ready, b * H + (h + 1))
                        if h >= 2:
                            act.wait_ge(turns.full(("pT", h - 2)), turns.count(("pT", h - 2), b))
                        act.activation(pr[:, h % 2, :], turns.tile(t)[0:Q, 0:S], ACT.Exp, bias=nmax[:, h:h + 1],
                                       accum_out=rsum[:, h:h + 1]).then_inc(turns.free(t), 1)
                        act.drain().then_inc(probs_ready, 1)
                    act.wait_ge(rank_ready, b + 1)
                    act.dma_start(nearest[b].rearrange("p t k -> p (t k)"), rank[:].rearrange("p t a k -> p (t a k)"))\
                       .then_inc(rank_stored, 16)
                    for i in range(3):
                        empty(("oT", i), oT[:, 4 * i:4 * i + 4, :],
                              turns.tile(("oT", i))[:, 0:4 * Q].rearrange("p (j q) -> p j q", j=4))
                    act.drain().then_inc(oT_ready, 1)
                    for i in range(2):
                        empty(("y", i), y[:, i * 512:(i + 1) * 512], turns.tile(("y", i))[0:Q, :],
                              scale=C.gates[0:Q, gate:gate + 1])
                    act.drain().then_inc(y_ready, 1)
                    act.wait_ge(x_done, b + 1)
                    act.dma_start(x_out[b], x[:, s, :]).then_inc(x_stored[s], 16)

        @block.vector
        def _(dve):
            dve.sem_inc(hT_free, 1)
            dve.sem_inc(xy_free, 1)
            dve.sem_inc(sq_free, 1)
            with dve.Fori(0, PAIRS) as p:
                for s in range(2):
                    b = p * 2 + s
                    dve.wait_ge(x_loaded[s], p * 16 + 16)
                    norm.statistics(dve, x[:, s, :], 0)
                    norm.scale(dve, x[:, s, :], z[:], 0, b).then_inc(z_ready, 1)
                    dve.wait_ge(xy_loaded, b * 32 + 32)
                    dve.tensor_scalar(here[:], here[:], -1.0, None, ALU.mult).then_inc(here_ready, 1)
                    dve.wait_ge(rank_stored, b * 16 + 16)
                    for t in range(KC):
                        dve.wait_ge(sq_ready, b * KC + (t + 1))
                        dve.scalar_tensor_tensor(out=near[:], in0=near[:], scalar=-1.0, in1=far[:], op0=ALU.mult, op1=ALU.subtract)
                        dve.drain()
                        dve.max(top[:, 0, :], near[:])
                        dve.drain()
                        dve.max_index(rank[:, t, 0, :], top[:, 0, :], near[:])
                        dve.match_replace(far[:], top[:, 0, :], near[:], -3e38)
                        dve.drain()
                        dve.max(top[:, 1, :], far[:])
                        dve.drain()
                        dve.max_index(rank[:, t, 1, :], top[:, 1, :], far[:])
                        dve.drain().then_inc(sq_free, 1)
                    dve.sem_inc(xy_free, 1)
                    dve.sem_inc(rank_ready, 1)
                    for step in range(H + 3):
                        h = step
                        if h < H:
                            t = ("S", h)
                            dve.wait_ge(turns.full(t), turns.count(t, b))
                            dve.tensor_reduce(nmax[:, h:h + 1], turns.tile(t)[0:Q, 0:S], AX, ALU.max, negate=True)\
                               .then_inc(max_ready, 1)
                        h = step - 2
                        if 0 <= h < H:
                            t = ("pT", h)
                            dve.wait_ge(turns.full(t), turns.count(t, b))
                            if h >= 2:
                                g = h - 2
                                if g % G == G - 1:
                                    dve.wait_ge(turns.full(("o", g // G)), turns.count(("o", g // G), b))
                                else:
                                    dve.wait_ge(heads_done, b * (H - KV) + (g - g // G + 1))
                            dve.tensor_copy(pT[0:CT, h % 2, 0:3, :], turns.tile(t)[0:CT, 0:3 * Q].rearrange("p (k q) -> p k q", k=3))
                            dve.tensor_copy(pT[0:Q, h % 2, 3, :], turns.tile(t)[0:Q, 3 * Q:4 * Q]).then_inc(turns.free(t), 1)
                            dve.drain().then_inc(pT_ready, 1)
                        h = step - 3
                        if h >= 0 and h % G == G - 1:
                            g = h // G
                            t = ("o", g)
                            dve.reciprocal(rsum[:, g * G:(g + 1) * G], rsum[:, g * G:(g + 1) * G])
                            dve.drain()
                            dve.wait_ge(turns.full(t), turns.count(t, b))
                            dve.tensor_tensor(o[:, g * G * HD:(g + 1) * G * HD].rearrange("q (h d) -> q h d", h=G),
                                              turns.tile(t)[0:Q, 0:G * HD].rearrange("q (h d) -> q h d", h=G),
                                              rsum[:, g * G:(g + 1) * G].unsqueeze(2).broadcast_to([Q, G, HD]), ALU.mult)\
                               .then_inc(turns.free(t), 1)
                            dve.drain().then_inc(o_ready, 1)


def grouped_attention(nc, C, banks, gate, x_in, x_out, A):
    HD, QUADS = 32, 8
    DKV = 256
    SCALE = float(HD) ** -0.5
    with ExitStack() as ctx:
        s_ = Scope(nc, ctx, "grouped")
        wq, wo = s_.sb("wq", [P, KC, D]), s_.sb("wo", [P, KC, D])
        wk, wv = s_.sb("wk", [P, KC, DKV]), s_.sb("wv", [P, KC, DKV])
        x, z, q = s_.sb("x", [Q, 2, D]), s_.sb("z", [Q, D]), s_.sb("q", [Q, D])
        zT, qT, oT = (s_.sb(n, [P, KC, Q]) for n in ("zT", "qT", "oT"))
        cT = s_.sb("ctxT", [P, 2, KC, CTX])
        kT, v, o = s_.sb("kT", [P, 2, CTX]), s_.sb("v", [CT, CTILES, DKV]), s_.sb("o", [Q, D])
        pr, pT = s_.sb("probs", [Q, 2, 4, CTX]), s_.sb("probsT", [CT, 2, CTILES, 4, Q])
        nmax, rsum = s_.sb("nmax", [Q, QUADS, 4]), s_.sb("rsum", [Q, QUADS, 4])
        norm = Norm(s_, 1)
        wkv_loaded, wq_loaded, wo_loaded = s_.sem("wkv_loaded"), s_.sem("wq_loaded"), s_.sem("wo_loaded")
        x_loaded = [s_.sem(f"x_loaded{i}") for i in range(2)]
        x_stored = [s_.sem(f"x_stored{i}") for i in range(2)]
        ctx_loaded = [s_.sem(f"ctx_loaded{i}") for i in range(2)]
        ctx_free = [s_.sem(f"ctx_free{i}") for i in range(2)]
        z_ready, zT_ready, kv_ready, q_ready, qT_ready = (
            s_.sem(n) for n in ("z_ready", "zT_ready", "kv_ready", "q_ready", "qT_ready"))
        max_ready, probs_ready, pT_ready, heads_done, o_ready, oT_ready, x_done = (
            s_.sem(n) for n in ("max_ready", "probs_ready", "pT_ready", "heads_done", "o_ready", "oT_ready", "x_done"))
        order = [(("k", i), i) for i in range(2)] + [(("v", i), 2 + i) for i in range(CTILES)]
        order += [(("zT", 0, i), 5 + i) for i in range(2)] + [(("q", 0, i), i) for i in range(2)]
        order += [(("qT", 0, i), 2 + i) for i in range(2)]
        for m in range(QUADS + 1):
            if m < QUADS:
                order += [(("S", m, j), j) for j in range(4)]
            if m >= 1:
                order += [(("pT", m - 1, k), 4 + k) for k in range(CTILES)]
                if (m - 1) % 4 == 0:
                    order.append((("o", (m - 1) // 4), 7))
        order += [(("oT", 0, i), 4 + i) for i in range(2)] + [(("y", 0, i), 6 + i) for i in range(2)]
        turns = Turns(banks, order, B)
        block = ctx.enter_context(nc.Block())

        @block.sync
        def _(sp):
            stream_x(sp, x, x_in, x_out, x_loaded, x_done, x_stored)

        @block.gpsimd
        def _(pool):
            pool.dma_start(wk[:], fold(A["L2_xattn_Wk"])).then_inc(wkv_loaded, 16)
            pool.dma_start(wv[:], fold(A["L2_xattn_Wv"])).then_inc(wkv_loaded, 16)
            for s in range(2):
                pool.dma_start(cT[:, s], A["ctxT"][s].rearrange("(k p) n -> p k n", p=P)).then_inc(ctx_loaded[s], 16)
            pool.dma_start(wq[:], fold(A["L2_xattn_Wq"])).then_inc(wq_loaded, 16)
            pool.dma_start(wo[:], fold(A["L2_xattn_Wo"])).then_inc(wo_loaded, 16)
            with pool.Fori(1, PAIRS) as p:
                for s in range(2):
                    pool.wait_ge(ctx_free[s], p)
                    pool.dma_start(cT[:, s], A["ctxT"][p * 2 + s].rearrange("(k p) n -> p k n", p=P)).then_inc(ctx_loaded[s], 16)

        @block.tensor
        def _(pe):
            pe.wait_ge(wkv_loaded, 32)

            def fill(t, b, lhsT, rhs, m, n, chunks):
                pe.wait_ge(turns.free(t), turns.count(t, b))
                for k in range(chunks):
                    mm = pe.matmul(turns.tile(t)[0:m, 0:n], lhsT(k), rhs(k), start=(k == 0), stop=(k == chunks - 1))
                mm.then_inc(turns.full(t), 1)

            with pe.Fori(0, PAIRS) as p:
                for s in range(2):
                    b = p * 2 + s
                    pe.wait_ge(ctx_loaded[s], p * 16 + 16)
                    for i in range(2):
                        fill(("k", i), b, lambda k: wk[:, k, i * P:(i + 1) * P], lambda k: cT[:, s, k, :], P, CTX, KC)
                    for i in range(CTILES):
                        fill(("v", i), b, lambda k: cT[:, s, k, i * CT:(i + 1) * CT], lambda k: wv[:, k, :], CT, DKV, KC)
                    pe.wait_ge(z_ready, b + 1)
                    turn_rows(pe, C, turns, z, "zT", 0, b)
                    pe.wait_ge(zT_ready, b + 1)
                    pe.wait_ge(wq_loaded, 16)
                    project(pe, turns, zT, wq, "q", 0, b)
                    pe.wait_ge(q_ready, b + 1)
                    turn_rows(pe, C, turns, q, "qT", 0, b)
                    pe.wait_ge(kv_ready, b + 1)
                    pe.wait_ge(qT_ready, b + 1)
                    for step in range(QUADS + 1):
                        m = step
                        if m < QUADS:
                            for j in range(4):
                                t = ("S", m, j)
                                r = slice(j * HD, (j + 1) * HD)
                                pe.wait_ge(turns.free(t), turns.count(t, b))
                                pe.matmul(turns.tile(t)[0:Q, 0:CTX], qT[r, m, :], kT[r, m // 4, :], start=True, stop=True)\
                                  .then_inc(turns.full(t), 1)
                        m = step - 1
                        if m >= 0:
                            pe.wait_ge(probs_ready, (b * QUADS + (m + 1)) * 4)
                            for k in range(CTILES):
                                t = ("pT", m, k)
                                pe.wait_ge(turns.free(t), turns.count(t, b))
                                for j in range(4):
                                    mm = pe.transpose(turns.tile(t)[0:CT, j * Q:(j + 1) * Q], pr[:, m % 2, j, k * CT:(k + 1) * CT],
                                                      C.ident[0:Q, 0:Q])
                                mm.then_inc(turns.full(t), 1)
                            t = ("o", m // 4)
                            pe.wait_ge(pT_ready, (b * QUADS + (m + 1)) * 3)
                            if m % 4 == 0:
                                pe.wait_ge(turns.free(t), turns.count(t, b))
                            for j in range(4):
                                g = 4 * (m // 4) + j
                                c = (m % 4) * P + j * HD
                                for k in range(CTILES):
                                    mm = pe.matmul(turns.tile(t)[0:Q, c:c + HD], pT[:, m % 2, k, j, :], v[:, k, g * HD:(g + 1) * HD],
                                                   start=(k == 0), stop=(k == CTILES - 1))
                            mm.then_inc(turns.full(t) if m % 4 == 3 else heads_done, 1)
                    pe.wait_ge(o_ready, b * 2 + 2)
                    turn_rows(pe, C, turns, o, "oT", 0, b)
                    pe.wait_ge(oT_ready, b + 1)
                    pe.wait_ge(wo_loaded, 16)
                    project(pe, turns, oT, wo, "y", 0, b)

        @block.scalar
        def _(act):
            with act.Fori(0, PAIRS) as p:
                for s in range(2):
                    b = p * 2 + s

                    def empty(t, dst, src, scale=1.0):
                        act.wait_ge(turns.full(t), turns.count(t, b))
                        act.activation(dst, src, ACT.Copy, scale=scale).then_inc(turns.free(t), 1)

                    norm.root(act, 0, b)
                    for i in range(2):
                        empty(("k", i), kT[:, i, :], turns.tile(("k", i))[:, 0:CTX])
                    for i in range(CTILES):
                        empty(("v", i), v[:, i, :], turns.tile(("v", i))[0:CT, 0:DKV])
                    act.drain().then_inc(kv_ready, 1)
                    act.sem_inc(ctx_free[s], 1)
                    copy_turned(act, turns, zT, "zT", 0, b, zT_ready)
                    for i in range(2):
                        empty(("q", 0, i), q[:, i * 512:(i + 1) * 512], turns.tile(("q", 0, i))[0:Q, :], scale=SCALE)
                    act.drain().then_inc(q_ready, 1)
                    copy_turned(act, turns, qT, "qT", 0, b, qT_ready)

                    def last_tile(m):
                        t = ("pT", m, 2)
                        act.wait_ge(turns.full(t), turns.count(t, b))
                        if m >= 2:
                            if m == 5:
                                act.wait_ge(turns.full(("o", 0)), turns.count(("o", 0), b))
                            else:
                                act.wait_ge(heads_done, b * 6 + (m - 1 - (m > 5)))
                        act.activation(pT[:, m % 2, 2, :, :], turns.tile(t)[0:CT, 0:4 * Q].rearrange("p (j q) -> p j q", j=4),
                                       ACT.Copy).then_inc(turns.free(t), 1)
                        act.drain().then_inc(pT_ready, 1)

                    for m in range(QUADS):
                        for j in range(4):
                            t = ("S", m, j)
                            act.wait_ge(max_ready, (b * QUADS + m) * 4 + (j + 1))
                            if m >= 2 and j == 0:
                                u = ("pT", m - 2, 2)
                                act.wait_ge(turns.full(u), turns.count(u, b))
                            act.activation(pr[:, m % 2, j, :], turns.tile(t)[0:Q, 0:CTX], ACT.Exp, bias=nmax[:, m, j:j + 1],
                                           accum_out=rsum[:, m, j:j + 1]).then_inc(turns.free(t), 1)
                            act.drain().then_inc(probs_ready, 1)
                        if m >= 1:
                            last_tile(m - 1)
                    last_tile(QUADS - 1)
                    copy_turned(act, turns, oT, "oT", 0, b, oT_ready)

        @block.vector
        def _(dve):
            with dve.Fori(0, PAIRS) as p:
                for s in range(2):
                    b = p * 2 + s
                    dve.wait_ge(x_loaded[s], p * 16 + 16)
                    norm.statistics(dve, x[:, s, :], 0)
                    norm.scale(dve, x[:, s, :], z[:], 0, b).then_inc(z_ready, 1)
                    for step in range(QUADS + 1):
                        m = step
                        if m < QUADS:
                            for j in range(4):
                                t = ("S", m, j)
                                dve.wait_ge(turns.full(t), turns.count(t, b))
                                dve.tensor_reduce(nmax[:, m, j:j + 1], turns.tile(t)[0:Q, 0:CTX], AX, ALU.max, negate=True)\
                                   .then_inc(max_ready, 1)
                        m = step - 1
                        if m >= 0:
                            if m >= 2:
                                if m == 5:
                                    dve.wait_ge(turns.full(("o", 0)), turns.count(("o", 0), b))
                                else:
                                    dve.wait_ge(heads_done, b * 6 + (m - 1 - (m > 5)))
                            for k in range(2):
                                t = ("pT", m, k)
                                dve.wait_ge(turns.full(t), turns.count(t, b))
                                dve.tensor_copy(pT[:, m % 2, k, :, :], turns.tile(t)[0:CT, 0:4 * Q].rearrange("p (j q) -> p j q", j=4))\
                                   .then_inc(turns.free(t), 1)
                                dve.drain().then_inc(pT_ready, 1)
                            if m % 4 == 3:
                                g = m // 4
                                t = ("o", g)
                                dve.reciprocal(rsum[:, 4 * g:4 * g + 4, :], rsum[:, 4 * g:4 * g + 4, :])
                                dve.drain()
                                dve.wait_ge(turns.full(t), turns.count(t, b))
                                dve.tensor_tensor(o[:, g * 512:(g + 1) * 512].rearrange("q (h d) -> q h d", h=16),
                                                  turns.tile(t)[0:Q, :].rearrange("q (h d) -> q h d", h=16),
                                                  rsum[:, 4 * g:4 * g + 4, :].rearrange("q m j -> q (m j)").unsqueeze(2)
                                                  .broadcast_to([Q, 16, HD]), ALU.mult).then_inc(turns.free(t), 1)
                                dve.drain().then_inc(o_ready, 1)
                    for i in range(2):
                        t = ("y", 0, i)
                        c = slice(i * 512, (i + 1) * 512)
                        dve.wait_ge(turns.full(t), turns.count(t, b))
                        dve.scalar_tensor_tensor(out=x[:, s, c], in0=turns.tile(t)[0:Q, :], scalar=C.gates[0:Q, gate:gate + 1],
                                                 in1=x[:, s, c], op0=ALU.mult, op1=ALU.add).then_inc(turns.free(t), 1)
                    dve.drain().then_inc(x_done, 1)


def quantise_weights(nc, C, banks, wall, scales, codes):
    with ExitStack() as ctx:
        s_ = Scope(nc, ctx, "weights")
        W = 4096
        raw, q, code = s_.sb("raw", [P, 2, W]), s_.sb("q", [P, 2, W], BF16), s_.sb("code", [P, 2, W], FP8)
        scale, rscale = s_.sb("scale", [P, 2, 4]), s_.sb("rscale", [P, 2, 4])
        raw_loaded = [s_.sem(f"raw_loaded{i}") for i in range(2)]
        code_stored = [s_.sem(f"code_stored{i}") for i in range(2)]
        raw_free, q_ready, code_ready = s_.sem("raw_free"), s_.sem("q_ready"), s_.sem("code_ready")
        passed = s_.sem("passed")
        NGU, NU = 16, wall.shape[0]
        turns = Turns(banks, [((s, i), 4 * s + i) for s in range(2) for i in range(4)], NU // 2)
        block = ctx.enter_context(nc.Block())

        @block.sync
        def _(sp):
            with sp.Fori(0, NU // 2) as p:
                for s in range(2):
                    sp.wait_ge(raw_free, p * 2 + (s + 1))
                    sp.dma_start(raw[:, s, :], wall[p * 2 + s]).then_inc(raw_loaded[s], 16)

        @block.vector
        def _(dve):
            dve.sem_inc(raw_free, 2)

            def units(first, last, n):
                with dve.Fori(first // 2, last // 2) as p:
                    for s in range(2):
                        rows_ = raw[:, s, :].rearrange("p (r w) -> p r w", r=n)
                        dve.wait_ge(raw_loaded[s], p * 16 + 16)
                        dve.wait_ge(code_stored[s], p * 32 + 32)
                        dve.tensor_reduce(scale[:, s, 0:n], rows_, AX, ALU.max, apply_absolute_value=True)
                        dve.drain()
                        divide(dve, scale[:, s, 0:n], rscale[:, s, 0:n], 7.0)
                        dve.tensor_scalar(scale[:, s, 0:n], scale[:, s, 0:n], 1e-8, None, ALU.max)
                        dve.drain()
                        dve.reciprocal(rscale[:, s, 0:n], scale[:, s, 0:n])
                        dve.drain()
                        for r in range(n):
                            dve.tensor_scalar(rows_[:, r, :], rows_[:, r, :], rscale[:, s, r:r + 1], MAGIC, ALU.mult, ALU.add)
                        dve.drain()
                        dve.tensor_scalar(q[:, s, :], raw[:, s, :], MAGIC, 7.0, ALU.subtract, ALU.min).then_inc(q_ready, 1)
                        dve.drain().then_inc(raw_free, 1)

            dve.memset(scale[:], 1.0)
            dve.drain()
            units(0, NGU, 4)
            units(NGU, NU, 1)

        @block.tensor
        def _(pe):
            def units(first, last, n):
                with pe.Fori(first // 2, last // 2) as p:
                    for s in range(2):
                        pe.wait_ge(q_ready, p * 2 + (s + 1))
                        for i in range(4):
                            t = (s, i)
                            pe.wait_ge(turns.free(t), turns.count(t, p))
                            o = turns.tile(t)[:].bitcast(BF16)
                            for j in range(8):
                                m = 8 * i + j
                                c = (m % 4 * 8 + m // 4) * P if n == 4 else m * P
                                mm = pe.transpose(o[:, j * P:(j + 1) * P], q[:, s, c:c + P], C.identb[:])
                            mm.then_inc(turns.full(t), 1)

            units(0, NGU, 4)
            units(NGU, NU, 1)

        @block.scalar
        def _(act):
            for s in range(2):
                act.sem_inc(code_stored[s], 32)
            with act.Fori(0, NU // 2) as p:
                for s in range(2):
                    act.wait_ge(code_stored[s], p * 32 + 32)
                    for i in range(4):
                        t = (s, i)
                        act.wait_ge(turns.full(t), turns.count(t, p))
                        act.sem_inc(passed, 1)
                        act.copy(code[:, s, i * 1024:(i + 1) * 1024], turns.tile(t)[:].bitcast(BF16), saturate=False)\
                           .then_inc(turns.free(t), 1)
                    act.drain().then_inc(code_ready, 1)
                    act.wait_ge(code_ready, p * 2 + (s + 1))
                    act.dma_start(codes[p * 2 + s], code[:, s, :].bitcast(U32)).then_inc(code_stored[s], 16)
                    act.dma_start(scales[p * 2 + s], scale[:, s, :]).then_inc(code_stored[s], 16)
            for s in range(2):
                act.wait_ge(code_stored[s], 32 * (NU // 2) + 32)


def hadamard_ffn(nc, C, banks, gate, x_in, x_out, A, scales, codes):
    F, NF = 4096, 32
    N2 = 2 * Q
    SPLIT = 80
    with ExitStack() as ctx:
        s_ = Scope(nc, ctx, "ffn")
        wgu, wd = s_.sb("wgu", [P, 16, F], FP8), s_.sb("wd", [P, 8, F], FP8)
        sgu, sd = s_.sb("sgu", [P, 16, 4]), s_.sb("sd", [P, 8, 4])
        had = s_.sb("had", [P, P])
        sdb = s_.sb("sdb", [Q, D])
        x = s_.sb("x", [Q, 2, D])
        ha, hb = s_.sb("ha", [Q, F]), s_.sb("hb", [Q, F])
        hq = s_.sb("hq", [Q, F], BF16)
        z = ha[:, 0:2 * D].rearrange("q (s d) -> q s d", s=2)
        q = hq[:, 0:2 * D].rearrange("q (s d) -> q s d", s=2)
        qT = s_.sb("qT", [P, KC, N2], BF16)
        h = s_.sb("h", [P, NF, N2])
        hqT = s_.sb("hqT", [P, NF, Q], BF16)
        gs, sl, us = (s_.sb(n, [P, 2, 2, N2]) for n in ("gs", "sl", "us"))
        sxb = s_.sb("sxb", [P, N2])
        sx, rsx, sh, rsh = (s_.sb(n, [Q, 2]) for n in ("sx", "rsx", "sh", "rsh"))
        norm = Norm(s_, 2)
        w_loaded, sdb_ready = s_.sem("w_loaded"), s_.sem("sdb_ready")
        passed = s_.sem("passed")
        x_loaded = [s_.sem(f"x_loaded{i}") for i in range(2)]
        x_stored = [s_.sem(f"x_stored{i}") for i in range(2)]
        q_ready, qT_ready, gs_ready, sl_ready, us_ready, h_ready = (
            s_.sem(n) for n in ("q_ready", "qT_ready", "gs_ready", "sl_ready", "us_ready", "h_ready"))
        sum_ready, diff_ready, hq_ready, hqT_ready, x_done = (
            s_.sem(n) for n in ("sum_ready", "diff_ready", "hq_ready", "hqT_ready", "x_done"))
        prep = Turns(banks, [(("sd", i), i) for i in range(2)], 1)
        order = [(("xT", s), 4 + s) for s in range(2)] + [("sx", 6)]
        for j in range(16):
            order += [(("g", j), 2 * (j % 2)), (("u", j), 2 * (j % 2) + 1)]
        for s in range(2):
            order += [(("h", s, i), 4 + i % 4) for i in range(8)]
            order += [(("hT", s, i), i) for i in range(4)] + [(("y", s, i), 2 * s + i) for i in range(2)]
        turns = Turns(banks, order, PAIRS)
        block = ctx.enter_context(nc.Block())

        @block.sync
        def _(sp):
            sp.dma_start(had[:], A["hadamard"]).then_inc(w_loaded, 16)
            sp.dma_start(sgu[:], scales[0:16].rearrange("u p r -> p u r")).then_inc(w_loaded, 16)
            sp.dma_start(sd[:], scales[16:24].rearrange("u p r -> p u r")).then_inc(w_loaded, 16)
            for i in range(4):
                sp.dma_start(wgu[:, 4 * i:4 * i + 4, :].bitcast(U32), codes[4 * i:4 * i + 4].rearrange("u p w -> p u w"))\
                  .then_inc(w_loaded, 16)
            sp.dma_start(wd[:].bitcast(U32), codes[16:24].rearrange("u p w -> p u w")).then_inc(w_loaded, 16)
            stream_x(sp, x, x_in, x_out, x_loaded, x_done, x_stored)

        @block.tensor
        def _(pe):
            pe.wait_ge(w_loaded, 16 * 8)
            for i in range(2):
                t = ("sd", i)
                pe.wait_ge(prep.free(t), prep.count(t, 0))
                for u in range(4):
                    mm = pe.matmul(prep.tile(t)[0:Q, u * P:(u + 1) * P], sd[:, 4 * i + u, 0:1].broadcast_to([P, Q]), C.ident[:],
                                   start=True, stop=True)
                mm.then_inc(prep.full(t), 1)
            with pe.Fori(0, PAIRS) as p:
                for s in range(2):
                    t = ("xT", s)
                    pe.wait_ge(q_ready, p * 2 + (s + 1))
                    pe.wait_ge(turns.free(t), turns.count(t, p))
                    o = turns.tile(t)[:].bitcast(BF16)
                    for k in range(KC):
                        mm = pe.transpose(o[:, k * Q:(k + 1) * Q], q[:, s, k * P:(k + 1) * P], C.identb[0:Q, 0:Q])
                    mm.then_inc(turns.full(t), 1)
                pe.wait_ge(turns.free("sx"), turns.count("sx", p))
                for s in range(2):
                    mm = pe.matmul(turns.tile("sx")[:, s * Q:(s + 1) * Q], sx[:, s:s + 1].broadcast_to([Q, P]), C.ident[0:Q, 0:Q],
                                   start=True, stop=True)
                mm.then_inc(turns.full("sx"), 1)
                pe.wait_ge(qT_ready, p + 1)
                for j in range(16):
                    for name, u0 in (("g", 0), ("u", 8)):
                        t = (name, j)
                        pe.wait_ge(turns.free(t), turns.count(t, p))
                        pe.sem_inc(passed, 1)
                        for i in range(2):
                            f = 2 * j + i
                            for k in range(KC):
                                c = (k * 4 + f % 4) * P
                                mm = pe.matmul(turns.tile(t)[:, i * N2:(i + 1) * N2], wgu[:, u0 + f // 4, c:c + P], qT[:, k, :],
                                               start=(k == 0), stop=(k == KC - 1))
                        mm.then_inc(turns.full(t), 1)
                for s in range(2):
                    for i in range(8):
                        t = ("h", s, i)
                        pe.wait_ge(h_ready, p * 16 + (2 * i + 2))
                        pe.wait_ge(turns.free(t), turns.count(t, p))
                        for c in range(4):
                            mm = pe.matmul(turns.tile(t)[0:Q, c * P:(c + 1) * P], h[:, 4 * i + c, s * Q:(s + 1) * Q], had[:],
                                           start=True, stop=True)
                        mm.then_inc(turns.full(t), 1)
                for s in range(2):
                    pe.wait_ge(hq_ready, p * 2 + (s + 1))
                    for i in range(4):
                        t = ("hT", s, i)
                        pe.wait_ge(turns.free(t), turns.count(t, p))
                        o = turns.tile(t)[:].bitcast(BF16)
                        for c in range(8):
                            mm = pe.transpose(o[:, c * Q:(c + 1) * Q], hq[:, (8 * i + c) * P:(8 * i + c + 1) * P], C.identb[0:Q, 0:Q])
                        mm.then_inc(turns.full(t), 1)
                    pe.wait_ge(hqT_ready, p * 2 + (s + 1))
                    for i in range(2):
                        t = ("y", s, i)
                        pe.wait_ge(turns.free(t), turns.count(t, p))
                        pe.sem_inc(passed, 1)
                        for c in range(NF):
                            mm = pe.matmul(turns.tile(t)[0:Q, :], hqT[:, c, :], wd[:, 4 * i:4 * i + 4, c * P:(c + 1) * P],
                                           start=(c == 0), stop=(c == NF - 1))
                        mm.then_inc(turns.full(t), 1)

        @block.scalar
        def _(act):
            for i in range(2):
                t = ("sd", i)
                act.wait_ge(prep.full(t), prep.count(t, 0))
                act.activation(sdb[:, i * 512:(i + 1) * 512], prep.tile(t)[0:Q, :], ACT.Copy,
                               scale=C.gates[0:Q, gate:gate + 1]).then_inc(prep.free(t), 1)
            act.drain().then_inc(sdb_ready, 1)
            with act.Fori(0, PAIRS) as p:
                for s in range(2):
                    norm.root(act, s, p * 2 + s)
                for s in range(2):
                    t = ("xT", s)
                    act.wait_ge(turns.full(t), turns.count(t, p))
                    act.copy(qT[:, :, s * Q:(s + 1) * Q], turns.tile(t)[:].bitcast(BF16)[:, 0:KC * Q].rearrange("p (k q) -> p k q", k=KC))\
                       .then_inc(turns.free(t), 1)
                act.wait_ge(turns.full("sx"), turns.count("sx", p))
                act.activation(sxb[:], turns.tile("sx")[:, 0:N2], ACT.Copy).then_inc(turns.free("sx"), 1)
                act.drain().then_inc(qT_ready, 1)
                for j in range(16):
                    act.wait_ge(gs_ready, p * 16 + (j + 1))
                    if j >= 2:
                        act.wait_ge(h_ready, p * 16 + (j - 1))
                    for i in range(2):
                        f = 2 * j + i
                        act.activation(sl[:, j % 2, i, :], gs[:, j % 2, i, :], ACT.Silu, scale=sgu[:, f // 4, f % 4:f % 4 + 1])
                    act.drain().then_inc(sl_ready, 1)
                for s in range(2):
                    for i in range(4):
                        t = ("hT", s, i)
                        act.wait_ge(turns.full(t), turns.count(t, p))
                        act.copy(hqT[:, 8 * i:8 * i + 8, :], turns.tile(t)[:].bitcast(BF16)[:, 0:8 * Q].rearrange("p (c q) -> p c q", c=8))\
                           .then_inc(turns.free(t), 1)
                    act.drain().then_inc(hqT_ready, 1)

        def half(v, k):
            w = v.rearrange("q (m two l c) -> q m two l c", two=2, l=1 << k, c=P)
            return w[:, :, 0], w[:, :, 1]

        @block.gpsimd
        def _(pool):
            with pool.Fori(0, PAIRS) as p:
                for j in range(16):
                    pool.wait_ge(sl_ready, p * 16 + (j + 1))
                    pool.wait_ge(us_ready, p * 16 + (j + 1))
                    pool.tensor_tensor(h[:, 2 * j:2 * j + 2, :], sl[:, j % 2], us[:, j % 2], ALU.mult).then_inc(h_ready, 1)
                for s in range(2):
                    for k in range(1, 5):
                        src, dst = (ha, hb) if k % 2 else (hb, ha)
                        (a, b), (_, d) = half(src[:], k), half(dst[:], k)
                        pool.wait_ge(sum_ready, (p * 2 + s) * 4 + k)
                        for l in range(1 << k):
                            op = pool.tensor_tensor(d[:, :, l, 0:SPLIT], a[:, :, l, 0:SPLIT], b[:, :, l, 0:SPLIT], ALU.subtract)
                        op.then_inc(diff_ready, 1)

        @block.vector
        def _(dve):
            dve.wait_ge(w_loaded, 16 * 8)
            dve.wait_ge(sdb_ready, 1)

            def integers(dst, src, m, scale, rscale, unit):
                dve.tensor_reduce(scale, src, AX, ALU.max, apply_absolute_value=True)
                dve.drain()
                divide(dve, scale, rscale, 7.0)
                dve.tensor_scalar(scale, scale, unit, 1e-8, ALU.mult, ALU.max)
                dve.drain()
                dve.reciprocal(rscale, scale)
                dve.drain()
                if unit != 1.0:
                    dve.tensor_scalar(rscale, rscale, unit, None, ALU.mult)
                    dve.drain()
                dve.tensor_scalar(src, src, rscale, MAGIC, ALU.mult, ALU.add)
                dve.drain()
                return dve.tensor_scalar(dst, src, MAGIC, 7.0, ALU.subtract, ALU.min)

            with dve.Fori(0, PAIRS) as p:
                for s in range(2):
                    dve.wait_ge(x_loaded[s], p * 16 + 16)
                    norm.statistics(dve, x[:, s, :], s)
                for s in range(2):
                    norm.scale(dve, x[:, s, :], z[:, s, :], s, p * 2 + s)
                for s in range(2):
                    dve.drain()
                    integers(q[:, s, :], z[:, s, :], 1, sx[:, s:s + 1], rsx[:, s:s + 1], 1.0).then_inc(q_ready, 1)
                dve.wait_ge(qT_ready, p + 1)
                both = sxb[:].unsqueeze(1).broadcast_to([P, 2, N2])
                for j in range(16):
                    t = ("g", j)
                    dve.wait_ge(turns.full(t), turns.count(t, p))
                    if j >= 2:
                        dve.wait_ge(h_ready, p * 16 + (j - 1))
                    dve.tensor_tensor(gs[:, j % 2], turns.tile(t)[:, 0:2 * N2].rearrange("p (i n) -> p i n", i=2), both, ALU.mult)\
                       .then_inc(turns.free(t), 1)
                    dve.drain().then_inc(gs_ready, 1)
                    t = ("u", j)
                    dve.wait_ge(turns.full(t), turns.count(t, p))
                    for i in range(2):
                        f = 2 * j + i
                        op = dve.scalar_tensor_tensor(out=us[:, j % 2, i, :], in0=turns.tile(t)[:, i * N2:(i + 1) * N2],
                                                      scalar=sgu[:, 8 + f // 4, f % 4:f % 4 + 1], in1=sxb[:], op0=ALU.mult, op1=ALU.mult)
                    op.then_inc(turns.free(t), 1)
                    dve.drain().then_inc(us_ready, 1)
                for s in range(2):
                    for i in range(8):
                        t = ("h", s, i)
                        dve.wait_ge(turns.full(t), turns.count(t, p))
                        a = turns.tile(t)[0:Q, :].rearrange("q (m two c) -> q m two c", m=2, two=2)
                        o = ha[:, i * 512:(i + 1) * 512].rearrange("q (m two c) -> q m two c", m=2, two=2)
                        t1 = hb[:, i * 512:i * 512 + 256].rearrange("q (m c) -> q m c", m=2)
                        dve.tensor_copy(t1, a[:, :, 1])
                        dve.drain()
                        dve.tensor_tensor(o[:, :, 0], a[:, :, 0], t1, ALU.add)
                        dve.tensor_tensor(o[:, :, 1], a[:, :, 0], t1, ALU.subtract).then_inc(turns.free(t), 1)
                    dve.drain().then_inc(sum_ready, 1)
                    for k in range(1, 5):
                        src, dst = (ha, hb) if k % 2 else (hb, ha)
                        (a, b), (c, d) = half(src[:], k), half(dst[:], k)
                        if k > 1:
                            dve.drain()
                            dve.wait_ge(diff_ready, (p * 2 + s) * 4 + (k - 1))
                            dve.sem_inc(sum_ready, 1)
                        sa, sb, sc = (v[:].rearrange("q (m two c) -> q m two c", two=2, c=P << k) for v in (src, src, dst))
                        dve.tensor_tensor(sc[:, :, 0], sa[:, :, 0], sb[:, :, 1], ALU.add)
                        for l in range(1 << k):
                            dve.tensor_tensor(d[:, :, l, SPLIT:P], a[:, :, l, SPLIT:P], b[:, :, l, SPLIT:P], ALU.subtract)
                    dve.drain()
                    dve.wait_ge(diff_ready, (p * 2 + s) * 4 + 4)
                    if s == 1:
                        t = ("hT", 0, 3)
                        dve.wait_ge(turns.full(t), turns.count(t, p))
                    integers(hq[:], ha[:], F, sh[:, s:s + 1], rsh[:, s:s + 1], 2.0 ** -6).then_inc(hq_ready, 1)
                for s in range(2):
                    for i in range(2):
                        t = ("y", s, i)
                        c = slice(i * 512, (i + 1) * 512)
                        dve.wait_ge(turns.full(t), turns.count(t, p))
                        dve.scalar_tensor_tensor(out=hb[:, c], in0=turns.tile(t)[0:Q, :], scalar=sh[:, s:s + 1], in1=sdb[:, c],
                                                 op0=ALU.mult, op1=ALU.mult).then_inc(turns.free(t), 1)
                    dve.drain()
                    dve.tensor_tensor(x[:, s, :], x[:, s, :], hb[:, 0:D], ALU.add).then_inc(x_done, 1)
                    dve.drain()


def gather_points(nc, C, banks, gate, x_in, x_out, A, nearest):
    K, R, AR = 16, Q // 16, KC * Q // 16
    U = 2 * K
    with ExitStack() as ctx:
        s_ = Scope(nc, ctx, "points")
        x, z = s_.sb("x", [Q, 2, D]), s_.sb("z", [Q, 2, D])
        norm = Norm(s_, 2)
        wcol, sel, wsel = s_.sb("wcol", [Q, 1]), s_.sb("sel", [Q, R]), s_.sb("wsel", [Q, R])
        bias, count, eights = s_.sb("bias", [P, 1]), s_.sb("count", [P, 1]), s_.sb("eights", [P, KC])
        idx = s_.sb("idx", [P, 2, KC, K], U32)
        point, hi, lo = (s_.sb(n, [P, 2, KC, K]) for n in ("point", "hi", "lo"))
        lob = s_.sb("lob", [P, 2, KC, K], BF16)
        mask = s_.sb("mask", [P, 2, KC, K, KC])
        table, rest = s_.sb("table", [P, 2, AR]), s_.sb("rest", [P, 2, AR])
        part = [s_.sb(f"part{i}", [P, 2, AR], BF16) for i in range(3)]
        spread, onehot = s_.sb("spread", [P, 2, D], BF16), s_.sb("onehot", [P, 2, D], BF16)
        kept = s_.sb("kept", [P, 2, KC, KC, R])
        val = s_.sb("val", [P, K, R, KC])
        flat = s_.sb("flat", [AR, 2, P, K])
        back = s_.sb("back", [P, 2, KC, Q])
        flat_dram = nc.dram_tensor("flat", (2, AR, P * K), F32, kind="Internal").ap()
        consts_loaded, wsel_ready = s_.sem("consts_loaded"), s_.sem("wsel_ready")
        passed = s_.sem("passed")
        x_loaded = [s_.sem(f"x_loaded{i}") for i in range(2)]
        x_stored = [s_.sem(f"x_stored{i}") for i in range(2)]
        idx_loaded = [s_.sem(f"idx_loaded{i}") for i in range(2)]
        flat_stored, back_loaded = s_.sem("flat_stored"), s_.sem("back_loaded")
        idx_used, lo_ready, z_ready, table_ready = (s_.sem(n) for n in ("idx_used", "lo_ready", "z_ready", "table_ready"))
        spread_ready, onehot_ready, val_ready, flat_ready, x_done = (
            s_.sem(n) for n in ("spread_ready", "onehot_ready", "val_ready", "flat_ready", "x_done"))
        steps = [("spread", 0), ("spread", 1), ("table", 0)]
        for u in range(U + 2):
            if u + 2 < U:
                steps.append(("spread", u + 2))
            if u == K - 4:
                steps.append(("table", 1))
            if u < U:
                steps.append(("look", u))
            if u >= 2 and (u - 2) % 4 == 3:
                steps.append(("turn", (u - 2) // 4))
            if u == K + 10:
                steps.append(("back", 0))
        steps.append(("back", 1))
        order = []
        for name, i in steps:
            if name == "spread":
                order += [((name, i, h), 2 * (i % 2) + h) for h in range(2)]
            elif name == "look":
                order.append(((name, i), 4 + i % 2))
            elif name == "back":
                order += [((name, i, h), 6 + h) for h in range(2)]
            else:
                order.append(((name, i), 6 + i % 2))
        turns = Turns(banks, order, PAIRS)
        block = ctx.enter_context(nc.Block())

        @block.sync
        def _(sp):
            sp.dma_start(wcol[:], A["L3_xattn_affine_w"]).then_inc(consts_loaded, 16)
            sp.dma_start(sel[:], A["row_mask"]).then_inc(consts_loaded, 16)
            sp.dma_start(bias[:], rows(A["L3_xattn_affine_b"], P)).then_inc(consts_loaded, 16)
            sp.dma_start(count[:], A["count"]).then_inc(consts_loaded, 16)
            sp.dma_start(eights[:], rows(A["eights"], P)).then_inc(consts_loaded, 16)
            for s in range(2):
                sp.dma_start(x[:, s, :], x_in[s]).then_inc(x_loaded[s], 16)

            def sequence(p, s):
                b = p * 2 + s
                sp.wait_ge(flat_ready, b + 1)
                sp.dma_start(flat_dram[s], flat[:, s].rearrange("a n k -> a (n k)")).then_inc(flat_stored, 16)
                sp.wait_ge(flat_stored, b * 16 + 16)
                sp.dma_start(back[:, s].rearrange("p t f -> p (t f)"),
                             flat_dram[s].rearrange("a c -> (a c)").rearrange("(p c) -> p c", p=P)).then_inc(back_loaded, 16)
                sp.wait_ge(x_done, b + 1)
                sp.dma_start(x_out[b], x[:, s, :]).then_inc(x_stored[s], 16)
                sp.wait_ge(x_stored[s], p * 16 + 16)

            with sp.Fori(0, PAIRS - 1) as p:
                for s in range(2):
                    sequence(p, s)
                    sp.dma_start(x[:, s, :], x_in[p * 2 + (s + 2)]).then_inc(x_loaded[s], 16)
            for s in range(2):
                sequence(PAIRS - 1, s)

        @block.gpsimd
        def _(pool):
            with pool.Fori(0, PAIRS) as p:
                for s in range(2):
                    pool.wait_ge(idx_used, p * 2 + (s + 1))
                    pool.dma_start(idx[:, s], nearest[p * 2 + s]).then_inc(idx_loaded[s], 16)

        @block.tensor
        def _(pe):
            pe.wait_ge(wsel_ready, 1)
            with pe.Fori(0, PAIRS) as p:
                for name, i in steps:
                    if name == "spread":
                        s, k = i // K, i % K
                        if k == 0:
                            pe.wait_ge(lo_ready, p * 2 + (s + 1))
                        for h in range(2):
                            t = (name, i, h)
                            pe.wait_ge(turns.free(t), turns.count(t, p))
                            for j in range(4):
                                mm = pe.matmul(turns.tile(t)[:, j * P:(j + 1) * P], lob[:, s, 4 * h + j, k:k + 1].broadcast_to([P, P]),
                                               C.identb[:], start=True, stop=True)
                            mm.then_inc(turns.full(t), 1)
                    elif name == "table":
                        t = (name, i)
                        pe.wait_ge(z_ready, p * 2 + (i + 1))
                        pe.wait_ge(turns.free(t), turns.count(t, p))
                        for a in range(KC):
                            mm = pe.matmul(turns.tile(t)[:, a * R:(a + 1) * R], z[:, i, a * P:(a + 1) * P], wsel[:], start=True, stop=True)
                        mm.then_inc(turns.full(t), 1)
                    elif name == "look":
                        t = (name, i)
                        if i % K == 0:
                            pe.wait_ge(table_ready, p * 2 + (i // K + 1))
                        pe.wait_ge(onehot_ready, p * U + (i + 1))
                        pe.wait_ge(turns.free(t), turns.count(t, p))
                        for j in range(KC):
                            for n in range(3):
                                mm = pe.matmul(turns.tile(t)[:, j * AR:(j + 1) * AR], onehot[:, i % 2, j * P:(j + 1) * P],
                                               part[n][:, i // K, :], start=(n == 0), stop=(n == 2))
                        mm.then_inc(turns.full(t), 1)
                    elif name == "turn":
                        t = (name, i)
                        pe.wait_ge(val_ready, p * U + (4 * i + 4))
                        pe.wait_ge(turns.free(t), turns.count(t, p))
                        pe.sem_inc(passed, 1)
                        for j in range(4):
                            mm = pe.transpose(turns.tile(t)[0:AR, j * P:(j + 1) * P], val[:, (4 * i + j) % K].rearrange("p r t -> p (r t)"),
                                              C.ident[:])
                        mm.then_inc(turns.full(t), 1)
                    else:
                        pe.wait_ge(back_loaded, p * 32 + (16 * i + 16))
                        for h in range(2):
                            t = (name, i, h)
                            pe.wait_ge(turns.free(t), turns.count(t, p))
                            for j in range(4):
                                mm = pe.transpose(turns.tile(t)[0:Q, j * P:(j + 1) * P], back[:, i, 4 * h + j, :], C.ident[:])
                            mm.then_inc(turns.full(t), 1)

        @block.scalar
        def _(act):
            with act.Fori(0, PAIRS) as p:
                norm.root(act, 0, p * 2)
                for name, i in steps:
                    if name == "spread":
                        if i == 6:
                            norm.root(act, 1, p * 2 + 1)
                        if i >= 2:
                            act.wait_ge(onehot_ready, p * U + (i - 1))
                        for h in range(2):
                            t = (name, i, h)
                            act.wait_ge(turns.full(t), turns.count(t, p))
                            act.activation(spread[:, i % 2, h * 512:(h + 1) * 512], turns.tile(t)[:], ACT.Copy).then_inc(turns.free(t), 1)
                        act.drain().then_inc(spread_ready, 1)
                    elif name == "turn":
                        t = (name, i)
                        act.wait_ge(turns.full(t), turns.count(t, p))
                        act.activation(flat[:, i // 4, :, i % 4 * 4:i % 4 * 4 + 4],
                                       turns.tile(t)[0:AR, :].rearrange("a (j n) -> a n j", j=4), ACT.Copy).then_inc(turns.free(t), 1)
                        if i % 4 == 3:
                            act.drain().then_inc(flat_ready, 1)

        @block.vector
        def _(dve):
            dve.sem_inc(idx_used, 2)
            dve.wait_ge(consts_loaded, 80)
            dve.tensor_scalar(wsel[:], sel[:], wcol[:], None, ALU.mult).then_inc(wsel_ready, 1)

            def indices(p, s):
                dve.wait_ge(idx_loaded[s], p * 16 + 16)
                dve.tensor_copy(point[:, s], idx[:, s]).then_inc(idx_used, 1)
                dve.drain()
                dve.tensor_scalar(hi[:, s], point[:, s], 63.5, 1.0 / P, ALU.subtract, ALU.mult)
                dve.drain()
                dve.tensor_scalar(hi[:, s], hi[:, s], MAGIC, MAGIC, ALU.add, ALU.subtract)
                dve.drain()
                dve.scalar_tensor_tensor(out=lob[:, s], in0=hi[:, s], scalar=-float(P), in1=point[:, s], op0=ALU.mult, op1=ALU.add)\
                   .then_inc(lo_ready, 1)
                dve.tensor_tensor(mask[:, s].rearrange("p t k a -> p (t k) a"),
                                  hi[:, s].rearrange("p t k -> p (t k)").unsqueeze(2).broadcast_to([P, KC * K, KC]),
                                  eights[:].unsqueeze(1).broadcast_to([P, KC * K, KC]), ALU.is_equal)

            def points(p, s):
                norm.scale(dve, x[:, s, :], z[:, s, :], s, p * 2 + s).then_inc(z_ready, 1)

            def split(p, s):
                t = ("table", s)
                dve.wait_ge(turns.full(t), turns.count(t, p))
                dve.tensor_scalar(table[:, s], turns.tile(t)[:, 0:AR], bias[:], None, ALU.add).then_inc(turns.free(t), 1)
                dve.drain()
                dve.tensor_copy(part[0][:, s], table[:, s])
                dve.drain()
                dve.tensor_tensor(rest[:, s], table[:, s], part[0][:, s], ALU.subtract)
                dve.drain()
                dve.tensor_copy(part[1][:, s], rest[:, s])
                dve.drain()
                dve.tensor_tensor(part[2][:, s], rest[:, s], part[1][:, s], ALU.subtract)
                dve.drain().then_inc(table_ready, 1)

            def keep(p, i):
                t, s, k = ("look", i), i // K, i % K
                dve.wait_ge(turns.full(t), turns.count(t, p))
                dve.tensor_tensor(kept[:, i % 2], turns.tile(t)[:, 0:KC * AR].rearrange("p (t a r) -> p t a r", t=KC, a=KC),
                                  mask[:, s, :, k, :].unsqueeze(3).broadcast_to([P, KC, KC, R]), ALU.mult).then_inc(turns.free(t), 1)
                dve.drain()
                dve.tensor_reduce(val[:, k].rearrange("p r t -> p t r"), kept[:, i % 2].rearrange("p t a r -> p t r a"), AX, ALU.add)\
                   .then_inc(val_ready, 1)

            def update(p, s):
                for h in range(2):
                    t = ("back", s, h)
                    dve.wait_ge(turns.full(t), turns.count(t, p))
                    xs = x[:, s, :].rearrange("f (q j) -> f j q", j=KC)[:, 4 * h:4 * h + 4, :]
                    op = dve.scalar_tensor_tensor(out=xs, in0=turns.tile(t)[0:Q, :].rearrange("f (j q) -> f j q", j=4),
                                                  scalar=C.gates[0:Q, gate:gate + 1], in1=xs, op0=ALU.mult, op1=ALU.add)
                    op.then_inc(turns.free(t), 1)
                dve.drain().then_inc(x_done, 1)

            with dve.Fori(0, PAIRS) as p:
                indices(p, 0)
                dve.wait_ge(x_loaded[0], p * 16 + 16)
                norm.statistics(dve, x[:, 0, :], 0)
                indices(p, 1)
                points(p, 0)
                split(p, 0)
                for i in range(U + 1):
                    if i == 4:
                        dve.wait_ge(x_loaded[1], p * 16 + 16)
                        norm.statistics(dve, x[:, 1, :], 1)
                    if i == 8:
                        points(p, 1)
                    if i == K - 2:
                        split(p, 1)
                    if i < U:
                        dve.wait_ge(spread_ready, p * U + (i + 1))
                        dve.tensor_scalar(onehot[:, i % 2], spread[:, i % 2], count[:], None, ALU.is_equal).then_inc(onehot_ready, 1)
                    if i >= 1:
                        keep(p, i - 1)
                    if i == K + 12:
                        update(p, 0)
                update(p, 1)


NAMES = ["x", "ctx_4096", "g_xattn", "g_ffn", "L0_xattn_Wq", "L0_xattn_Wk", "L0_xattn_Wv", "L0_xattn_Wo",
         "L0_ffn_qweight", "L0_ffn_wparams", "L0_ffn_bias", "L1_xattn_Wq", "L1_xattn_bq", "L1_xattn_Wk",
         "L1_xattn_bk", "L1_ffn_Wq", "L1_ffn_Wr", "L1_ffn_aux_keys", "L1_ffn_aux_values", "L1_ffn_Wvd",
         "L1_ffn_Wvu", "L1_ffn_Wu1", "L1_ffn_bu1", "L1_ffn_Wu2", "L1_ffn_bu2", "L1_ffn_gate_w1",
         "L1_ffn_gate_bias", "L1_ffn_log_rel", "L2_xattn_Wq", "L2_xattn_Wk", "L2_xattn_Wv", "L2_xattn_Wo",
         "L2_ffn_w_gate_up", "L2_ffn_w_down", "L3_xattn_affine_w", "L3_xattn_affine_b", "L3_ffn_gate_w",
         "L3_ffn_lora_A", "L3_ffn_lora_B"]


def layout(a):
    import numpy as np
    out = dict(a)
    for name in ("L0_xattn_Wq", "L0_xattn_Wk", "L0_xattn_Wv", "L0_xattn_Wo", "L0_ffn_qweight", "L1_xattn_Wq",
                 "L1_ffn_Wq", "L1_ffn_Wr", "L1_ffn_aux_keys", "L1_ffn_aux_values", "L1_ffn_Wvd", "L1_ffn_Wvu",
                 "L1_ffn_Wu1", "L3_ffn_gate_w"):
        out[name + "T"] = out.pop(name).T
    out["L1_ffn_WrT"] = np.concatenate([out["L1_ffn_WrT"], np.zeros((64, P - 48), np.float32)], axis=1)
    out["L0_ffn_qweightT"] = np.ascontiguousarray(out["L0_ffn_qweightT"]).view(np.uint32)
    out["ctxT"] = a["ctx_4096"].transpose(0, 2, 1)
    gu = out.pop("L2_ffn_w_gate_up").reshape(16, 4, P, D).transpose(0, 2, 1, 3).reshape(16, P, 4 * D)
    out["L2_weights"] = np.concatenate([gu, out.pop("L2_ffn_w_down").reshape(8, P, 4 * D)])
    out["planes"] = a["ctx_4096"][:, 0:2].reshape(B, 2 * D)
    out["points"] = a["ctx_4096"][:, 0:2].reshape(B, 2, KC, P).transpose(0, 3, 1, 2)
    order = [16 * (m // 4) + 4 * j + m % 4 for m in range(8) for j in range(4)]
    out["L2_xattn_Wq"] = a["L2_xattn_Wq"].reshape(D, 32, 32)[:, order].reshape(D, D)
    out["L2_xattn_Wo"] = a["L2_xattn_Wo"].reshape(32, 32, D)[order].reshape(D, D)
    out["L3_lora_AT"] = out.pop("L3_ffn_lora_A").reshape(512, D).T
    out["L3_lora_BT"] = out.pop("L3_ffn_lora_B").transpose(0, 2, 1).reshape(512, D)
    out["L3_xattn_affine_w"] = np.repeat(a["L3_xattn_affine_w"], 7).reshape(Q, 1)
    for name in ("L1_xattn_bk", "L1_ffn_bu1", "L1_ffn_Wu2"):
        out[name] = a[name].reshape(-1, P).T
    for name in ("L1_ffn_gate_w1", "L1_ffn_gate_bias"):
        out[name] = a[name].reshape(1)
    h = np.ones((1, 1), np.float32)
    while len(h) < P:
        h = np.block([[h, h], [h, -h]]).astype(np.float32)
    out["ident"] = np.eye(P, dtype=np.float32)
    out["hadamard"] = h
    out["row_mask"] = (np.arange(Q)[:, None] % 7 == np.arange(7)[None, :]).astype(np.float32)
    out["eights"] = np.arange(KC, dtype=np.float32)
    out["count"] = np.arange(P, dtype=np.float32).reshape(P, 1)
    return {n: np.ascontiguousarray(v) for n, v in out.items()}


def program(nc, A, x_in, x_out):
    with ExitStack() as ctx:
        banks = Banks(nc, ctx)
        C = Consts(nc, ctx)
        setup(nc, C, banks, A["g_xattn"], A["g_ffn"], A)

        def dram(name, shape, dt=F32):
            return nc.dram_tensor(name, shape, dt, kind="Internal").ap()

        stages = {
            "a0": lambda i, o: latent_attention(nc, C, banks, 0, i, o, A, idx),
            "qffn": lambda i, o: quantised_ffn(nc, C, banks, 4, i, o, A["L0_ffn_qweightT"], A["L0_ffn_wparams"],
                                               A["L0_ffn_bias"]),
            "a1": lambda i, o: plain_attention(nc, C, banks, 1, i, o, A),
            "mem": lambda i, o: memory_ffn(nc, C, banks, 5, i, o, A),
            "a2": lambda i, o: grouped_attention(nc, C, banks, 2, i, o, A),
            "ffn": lambda i, o: (quantise_weights(nc, C, banks, A["L2_weights"], scales, codes),
                                 hadamard_ffn(nc, C, banks, 6, i, o, A, scales, codes)),
            "knn": lambda i, o: gather_points(nc, C, banks, 3, i, o, A, idx),
            "moe": lambda i, o: experts_ffn(nc, C, banks, 7, i, o, A),
        }
        idx = dram("nearest", (B, P, KC, 16), U32)
        scales, codes = dram("scales", (24, P, 4)), dram("codes", (24, P, 1024), U32)
        now = x_in
        for n, (name, stage) in enumerate(stages.items()):
            then = x_out if n == len(stages) - 1 else dram(f"x_after_{name}", (B, Q, D))
            stage(now, then)
            now = then


def kernel(**inputs):
    import numpy as np
    import concourse.bacc as bacc
    from concourse.bass_utils import run_bass_kernel_spmd

    nc = bacc.Bacc("TRN2", target_bir_lowering=False, num_devices=1)
    arrays = layout({name: np.asarray(inputs[name]) for name in NAMES})
    A = {n: nc.dram_tensor(n, v.shape, mybir.dt.from_np(v.dtype), kind="ExternalInput").ap() for n, v in arrays.items()}
    out = nc.dram_tensor("x_final", (B, Q, D), F32, kind="ExternalOutput").ap()
    program(nc, A, A["x"], out)
    return run_bass_kernel_spmd(nc, [arrays], core_ids=[0]).results[0]["x_final"]
```

```python
from contextlib import ExitStack

import concourse.bass as bass
from concourse import mybir

F32 = mybir.dt.float32
BF16 = mybir.dt.bfloat16
FP8 = mybir.dt.float8e4
I8 = mybir.dt.int8
U32 = mybir.dt.uint32
ALU = mybir.AluOpType
ACT = mybir.ActivationFunctionType
AX = mybir.AxisListType.X

B, Q, D = 8, 112, 1024
CTX = 375
P = 128
KC = D // P
PAIRS = B // 2
CT = 125
CTILES = CTX // CT
EPS = 1e-5
MAGIC = 1.5 * 2.0 ** 23
LOW = -1e30


class Banks:

    def __init__(self, nc, ctx):
        self.tile = [ctx.enter_context(nc.psum_tensor(f"bank{k}", [P, 512], F32)) for k in range(8)]
        self.full = [ctx.enter_context(nc.semaphore(f"bank_full{k}")) for k in range(8)]
        self.free = [ctx.enter_context(nc.semaphore(f"bank_free{k}")) for k in range(8)]
        self.used = [0] * 8


class Turns:

    def __init__(self, banks, order, rounds):
        self.banks, self.at, self.per = banks, {}, [0] * 8
        for name, k in order:
            self.at[name] = (k, self.per[k])
            self.per[k] += 1
        self.start = list(banks.used)
        for k in range(8):
            banks.used[k] += rounds * self.per[k]

    def tile(self, name):
        return self.banks.tile[self.at[name][0]]

    def full(self, name):
        return self.banks.full[self.at[name][0]]

    def free(self, name):
        return self.banks.free[self.at[name][0]]

    def count(self, name, turn):
        k, n = self.at[name]
        return turn * self.per[k] + (self.start[k] + n + 1)


class Scope:

    def __init__(self, nc, ctx, stage):
        self.nc, self.ctx, self.stage = nc, ctx, stage
        self.sems = []
        ctx.callback(self.clear)

    def sb(self, name, shape, dt=F32):
        return self.ctx.enter_context(self.nc.sbuf_tensor(f"{self.stage}_{name}", shape, dt))

    def sem(self, name):
        self.sems.append(self.nc.alloc_semaphore(f"{self.stage}_{name}"))
        return self.sems[-1]

    def clear(self):
        if self.sems:
            self.nc.clear_and_free_semaphores(self.sems)
            self.nc.all_engine_barrier()


class Consts:

    def __init__(self, nc, ctx):
        s = Scope(nc, ctx, "const")
        self.ident = s.sb("ident", [P, P])
        self.identb = s.sb("identb", [P, P], BF16)
        self.gates = s.sb("gates", [P, 8])


def rows(v, n):
    return v.rearrange("(a d) -> a d", a=1).broadcast_to([n, v.shape[0]])


def fold(w):
    return w.rearrange("(k p) n -> p k n", p=P)


def setup(nc, C, banks, g_xattn, g_ffn, masks):
    with ExitStack() as ctx:
        s = Scope(nc, ctx, "setup")
        loaded = s.sem("loaded")
        block = ctx.enter_context(nc.Block())

        @block.sync
        def _(sp):
            sp.dma_start(C.ident[:], masks["ident"]).then_inc(loaded, 16)
            sp.dma_start(C.gates[:, 0:4], rows(g_xattn, P)).then_inc(loaded, 16)
            sp.dma_start(C.gates[:, 4:8], rows(g_ffn, P)).then_inc(loaded, 16)

        @block.scalar
        def _(act):
            act.wait_ge(loaded, 48)
            act.activation(C.gates[:], C.gates[:], ACT.Tanh)

        @block.vector
        def _(dve):
            dve.wait_ge(loaded, 48)
            dve.tensor_copy(C.identb[:], C.ident[:])

        @block.tensor
        def _(pe):
            for k in range(8):
                pe.sem_inc(banks.free[k], 1)


def stream_x(sp, x, x_in, x_out, x_loaded, x_done, x_stored):
    for s in range(2):
        sp.dma_start(x[:, s, :], x_in[s]).then_inc(x_loaded[s], 16)

    def store(b, p, s):
        sp.wait_ge(x_done, b + 1)
        sp.dma_start(x_out[b], x[:, s, :]).then_inc(x_stored[s], 16)
        sp.wait_ge(x_stored[s], p * 16 + 16)

    with sp.Fori(0, PAIRS - 1) as p:
        for s in range(2):
            store(p * 2 + s, p, s)
            sp.dma_start(x[:, s, :], x_in[p * 2 + (s + 2)]).then_inc(x_loaded[s], 16)
    for s in range(2):
        store(B - 2 + s, PAIRS - 1, s)


def every_pair(eng, pair):
    with eng.Fori(0, PAIRS - 1) as p:
        pair(p, False)
    pair(PAIRS - 1, True)


def stream_ahead(sp, x, z, x_in, x_out, x_loaded, z_loaded, x_done, x_stored, z_used):
    for s in range(2):
        sp.dma_start(x[:, s, :], x_in[s]).then_inc(x_loaded[s], 16)

    def pair(p, last):
        if not last:
            for s in range(2):
                sp.wait_ge(*z_used(s, p))
                sp.dma_start(z[:, s, :], x_in[p * 2 + (s + 2)]).then_inc(z_loaded[s], 16)
        for s in range(2):
            sp.wait_ge(x_done, p * 2 + (s + 1))
            sp.dma_start(x_out[p * 2 + s], x[:, s, :]).then_inc(x_stored[s], 16)
            sp.wait_ge(x_stored[s], p * 16 + 16)
            if not last:
                sp.dma_start(x[:, s, :], x_in[p * 2 + (s + 2)]).then_inc(x_loaded[s], 16)

    every_pair(sp, pair)


class Norm:

    def __init__(self, s, n):
        self.stats = s.sb("ln_stats", [Q, n, 2, 6])
        self.mv = s.sb("ln_mv", [Q, n, 2])
        self.std = s.sb("ln_std", [Q, n, 1])
        self.rstd = s.sb("ln_rstd", [Q, n, 1])
        self.var_ready = s.sem("var_ready")
        self.std_ready = s.sem("std_ready")

    def statistics(self, dve, x, i):
        for h in range(2):
            dve.bn_stats(self.stats[:, i, h, :], x[:, h * 512:(h + 1) * 512])
        dve.drain()
        dve.bn_aggr(self.mv[:, i, :], self.stats[:, i, :, :])
        dve.drain()
        dve.tensor_scalar(self.std[:, i, :], self.mv[:, i, 1:2], EPS, None, ALU.add).then_inc(self.var_ready, 1)

    def root(self, act, i, b):
        act.wait_ge(self.var_ready, b + 1)
        act.activation(self.std[:, i, :], self.std[:, i, :], ACT.Sqrt).then_inc(self.std_ready, 1)

    def in_place(self, dve, z, z_loaded, p, z_ready):
        for s in range(2):
            dve.wait_ge(z_loaded[s], p * 16 + 16)
            self.statistics(dve, z[:, s, :], s)
        for s in range(2):
            self.scale(dve, z[:, s, :], z[:, s, :], s, p * 2 + s).then_inc(z_ready, 1)

    def scale(self, dve, x, z, i, b):
        dve.wait_ge(self.std_ready, b + 1)
        dve.reciprocal(self.rstd[:, i, :], self.std[:, i, :])
        dve.drain()
        return dve.tensor_scalar(z, x, self.mv[:, i, 0:1], self.rstd[:, i, :], ALU.subtract, ALU.mult)


class Nearest:

    def __init__(self, s, tiles, slots, ranks, A):
        self.tiles, self.slots, self.ranks, self.A = tiles, slots, ranks, A
        n = len(tiles)
        self.xy, self.here = s.sb("xy", [P, slots, 2, D]), s.sb("here", [P, slots, 2, KC])
        self.near, self.far = s.sb("near", [P, slots, D]), s.sb("far", [P, slots, D])
        self.top, self.rank = s.sb("top", [P, 2, 8]), s.sb("rank", [P, n, 2, 8], U32)
        self.xy_loaded = [s.sem(f"xy_loaded{i}") for i in range(slots)]
        self.xy_free, self.here_ready, self.sq_ready, self.sq_free, self.rank_ready, self.rank_stored = (
            s.sem(n) for n in ("xy_free", "here_ready", "sq_ready", "sq_free", "rank_ready", "rank_stored"))

    def credits(self, dve):
        dve.sem_inc(self.xy_free, self.slots)
        dve.sem_inc(self.sq_free, self.slots)
        dve.sem_inc(self.rank_stored, 16)

    def load(self, sp, b, slot):
        sp.wait_ge(self.xy_free, b + 1)
        sp.dma_start(self.xy[:, slot], self.A["planes"][b].rearrange("(a n) -> a n", a=1).broadcast_to([P, 2 * D])
                     .rearrange("p (c n) -> p c n", c=2)).then_inc(self.xy_loaded[slot], 16)
        sp.dma_start(self.here[:, slot], self.A["points"][b]).then_inc(self.xy_loaded[slot], 16)

    def begin(self, dve, b, slot, turn):
        dve.wait_ge(self.xy_loaded[slot], turn * 32 + 32)
        dve.tensor_scalar(self.here[:, slot], self.here[:, slot], -1.0, None, ALU.mult).then_inc(self.here_ready, 1)

    def squares(self, act, b, slot, i):
        n, t = len(self.tiles), self.tiles[i]
        k = (slot * n + i) % self.slots
        if i == 0:
            act.wait_ge(self.here_ready, b + 1)
        act.wait_ge(self.sq_free, b * n + (i + 1))
        act.activation(self.near[:, k], self.xy[:, slot, 0], ACT.Square, bias=self.here[:, slot, 0, t:t + 1])
        act.activation(self.far[:, k], self.xy[:, slot, 1], ACT.Square, bias=self.here[:, slot, 1, t:t + 1])\
           .then_inc(self.sq_ready, 1)

    def sort(self, dve, b, slot, i):
        n = len(self.tiles)
        k = (slot * n + i) % self.slots
        near, far, top = self.near[:, k], self.far[:, k], self.top
        dve.wait_ge(self.sq_ready, b * n + (i + 1))
        if i == 0:
            dve.wait_ge(self.rank_stored, b * 16 + 16)
        dve.scalar_tensor_tensor(out=near, in0=near, scalar=-1.0, in1=far, op0=ALU.mult, op1=ALU.subtract)
        dve.drain()
        dve.max(top[:, 0, :], near)
        dve.drain()
        dve.max_index(self.rank[:, i, 0, :], top[:, 0, :], near)
        dve.match_replace(far, top[:, 0, :], near, -3e38)
        dve.drain()
        dve.max(top[:, 1, :], far)
        dve.drain()
        dve.max_index(self.rank[:, i, 1, :], top[:, 1, :], far)
        dve.drain().then_inc(self.sq_free, 1)
        if i == n - 1:
            dve.sem_inc(self.xy_free, 1)
            dve.sem_inc(self.rank_ready, 1)

    def store(self, eng, b):
        t0, n = self.tiles[0], len(self.tiles)
        eng.wait_ge(self.rank_ready, b + 1)
        eng.dma_start(self.ranks[b][:, t0:t0 + n, :].rearrange("p t k -> p (t k)"), self.rank[:].rearrange("p t a k -> p (t a k)"))\
           .then_inc(self.rank_stored, 16)

    def stored(self, eng):
        eng.wait_ge(self.rank_stored, 16 * B + 16)


def divide(dve, out, rest, n):
    dve.tensor_scalar(rest, out, 1.0 / n, None, ALU.mult)
    dve.drain()
    dve.scalar_tensor_tensor(out=out, in0=rest, scalar=-(n + 1.0), in1=out, op0=ALU.mult, op1=ALU.add)
    dve.drain()
    dve.tensor_tensor(out, out, rest, ALU.add)
    dve.drain()
    dve.scalar_tensor_tensor(out=out, in0=out, scalar=1.0 / n, in1=rest, op0=ALU.mult, op1=ALU.add)
    dve.drain()


def quantised_ffn(nc, C, banks, gate, x_in, x_out, qweightT, wparams, bias):
    QMAX = 127.0
    with ExitStack() as ctx:
        s_ = Scope(nc, ctx, "qffn")
        w8 = s_.sb("w8", [P, KC, D], I8)
        w = s_.sb("w", [P, KC, D], BF16)
        wp = s_.sb("wparams", [Q, D])
        bi = s_.sb("bias", [Q, D])
        x = s_.sb("x", [Q, 2, D])
        z = s_.sb("z", [Q, 2, D])
        q = s_.sb("q", [Q, 2, D], BF16)
        qT = s_.sb("qT", [P, 2, KC, Q], BF16)
        y = s_.sb("y", [Q, 2, D])
        ascale, yscale = s_.sb("ascale", [Q, 2, 1]), s_.sb("yscale", [Q, 2, 1])
        rscale = s_.sb("rscale", [Q, 2, 1])
        norm = Norm(s_, 2)
        w_loaded = s_.sem("w_loaded")
        rows_loaded = s_.sem("rows_loaded")
        w_cast = s_.sem("w_cast")
        x_loaded = [s_.sem(f"x_loaded{i}") for i in range(2)]
        x_stored = [s_.sem(f"x_stored{i}") for i in range(2)]
        z_loaded = [s_.sem(f"z_loaded{i}") for i in range(2)]
        z_ready, q_free, y_free = s_.sem("z_ready"), s_.sem("q_free"), s_.sem("y_free")
        q_ready, qT_ready, y_ready, x_done = s_.sem("q_ready"), s_.sem("qT_ready"), s_.sem("y_ready"), s_.sem("x_done")
        part_done = s_.sem("part_done")
        rows_scaled = s_.sem("rows_scaled")
        turns = Turns(banks, [(("T", s), s) for s in range(2)]
                      + [(("y", s, n), 2 + 2 * s + n) for s in range(2) for n in range(2)], PAIRS)
        block = ctx.enter_context(nc.Block())

        @block.sync
        def _(sp):
            for s in range(2):
                sp.dma_start(z[:, s, :], x_in[s]).then_inc(z_loaded[s], 16)
            sp.dma_start(w8[:].bitcast(U32), fold(qweightT)).then_inc(w_loaded, 16)
            sp.dma_start(wp[:], rows(wparams, Q)).then_inc(rows_loaded, 16)
            sp.dma_start(bi[:], rows(bias, Q)).then_inc(rows_loaded, 16)
            stream_ahead(sp, x, z, x_in, x_out, x_loaded, z_loaded, x_done, x_stored, lambda s, p: (q_ready, p * 2 + (s + 1)))

        @block.vector
        def _(dve):
            dve.sem_inc(q_free, 2)
            norm.in_place(dve, z, z_loaded, 0, z_ready)
            dve.wait_ge(w_loaded, 16)
            dve.tensor_copy(w[:, 0:KC // 2, :], w8[:, 0:KC // 2, :]).then_inc(w_cast, 1)

            def pair(p, last):
                for s in range(2):
                    dve.drain()
                    dve.wait_ge(q_free, p * 2 + (s + 1))
                    dve.tensor_reduce(ascale[:, s, :], z[:, s, :], AX, ALU.max, apply_absolute_value=True)
                for s in range(2):
                    dve.drain()
                    divide(dve, ascale[:, s, :], rscale[:, s, :], QMAX)
                    dve.reciprocal(rscale[:, s, :], ascale[:, s, :])
                    dve.drain()
                    dve.tensor_scalar(z[:, s, :], z[:, s, :], rscale[:, s, :], MAGIC, ALU.mult, ALU.add)
                for s in range(2):
                    dve.drain()
                    dve.tensor_scalar(q[:, s, :], z[:, s, :], MAGIC, QMAX, ALU.subtract, ALU.min).then_inc(q_ready, 1)
                if not last:
                    norm.in_place(dve, z, z_loaded, p + 1, z_ready)

            every_pair(dve, pair)

        @block.tensor
        def _(pe):
            pe.wait_ge(w_cast, 2)
            with pe.Fori(0, PAIRS) as p:
                for s in range(2):
                    t = ("T", s)
                    pe.wait_ge(q_ready, p * 2 + (s + 1))
                    pe.wait_ge(turns.free(t), turns.count(t, p))
                    o = turns.tile(t)[:].bitcast(BF16)
                    for k in range(KC):
                        mm = pe.transpose(o[:, k * Q:(k + 1) * Q], q[:, s, k * P:(k + 1) * P], C.identb[0:Q, 0:Q])
                    mm.then_inc(turns.full(t), 1)
                for s in range(2):
                    pe.wait_ge(qT_ready, p * 2 + (s + 1))
                    for n in range(2):
                        t = ("y", s, n)
                        pe.wait_ge(turns.free(t), turns.count(t, p))
                        for k in range(KC):
                            mm = pe.matmul(turns.tile(t)[0:Q, :], qT[:, s, k, :], w[:, k, n * 512:(n + 1) * 512],
                                           start=(k == 0), stop=(k == KC - 1))
                        mm.then_inc(turns.full(t), 1)

        @block.scalar
        def _(act):
            for s in range(2):
                norm.root(act, s, s)
            act.wait_ge(w_loaded, 16)
            act.copy(w[:, KC // 2:KC, :], w8[:, KC // 2:KC, :]).then_inc(w_cast, 1)

            def pair(p, last):
                for s in range(2):
                    t = ("T", s)
                    act.wait_ge(turns.full(t), turns.count(t, p))
                    o = turns.tile(t)[:].bitcast(BF16)
                    act.copy(qT[:, s, :, :], o[:, 0:KC * Q].rearrange("p (k q) -> p k q", k=KC)).then_inc(turns.free(t), 1)
                    act.activation(yscale[:, s, :], ascale[:, s, :], ACT.Copy)
                    act.drain().then_inc(qT_ready, 1)
                    act.sem_inc(q_free, 1)
                if not last:
                    for s in range(2):
                        norm.root(act, s, p * 2 + (s + 2))
                for s in range(2):
                    act.wait_ge(y_free, p * 2 + (s + 1))
                    for n in range(2):
                        t = ("y", s, n)
                        act.wait_ge(turns.full(t), turns.count(t, p))
                        act.activation(y[:, s, n * 512:(n + 1) * 512], turns.tile(t)[0:Q, :], ACT.Copy,
                                       scale=yscale[:, s, :]).then_inc(turns.free(t), 1)
                    act.drain().then_inc(y_ready, 1)

            every_pair(act, pair)

        @block.gpsimd
        def _(pool):
            pool.wait_ge(rows_loaded, 32)
            gp = C.gates[0:Q, gate:gate + 1]
            for v in (wp, bi):
                pool.tensor_scalar(v[:], v[:], gp, 1.0, ALU.mult, ALU.mult).then_inc(rows_scaled, 1)
            pool.wait_ge(rows_scaled, 2)
            pool.sem_inc(y_free, 2)
            with pool.Fori(0, PAIRS) as p:
                for s in range(2):
                    pool.wait_ge(y_ready, p * 2 + (s + 1))
                    pool.wait_ge(x_loaded[s], p * 16 + 16)
                    pool.tensor_tensor(y[:, s, :], y[:, s, :], wp[:], ALU.mult)
                    pool.tensor_tensor(x[:, s, :], x[:, s, :], bi[:], ALU.add).then_inc(part_done, 1)
                    pool.wait_ge(part_done, p * 2 + (s + 1))
                    pool.tensor_tensor(x[:, s, :], x[:, s, :], y[:, s, :], ALU.add).then_inc(x_done, 1)
                    pool.wait_ge(x_done, p * 2 + (s + 1))
                    pool.sem_inc(y_free, 1)


def turn_rows(pe, C, turns, src, name, s, p, n=2):
    for h in range(n):
        t = (name, s, h)
        pe.wait_ge(turns.free(t), turns.count(t, p))
        for k in range(4):
            c = (4 * h + k) * P
            mm = pe.transpose(turns.tile(t)[:, k * Q:(k + 1) * Q], src[:, c:c + P], C.ident[0:Q, 0:Q])
        mm.then_inc(turns.full(t), 1)


def copy_turned(act, turns, dst, name, s, p, ready, n=2):
    for h in range(n):
        t = (name, s, h)
        act.wait_ge(turns.full(t), turns.count(t, p))
        act.activation(dst[:, 4 * h:4 * h + 4, :], turns.tile(t)[:, 0:4 * Q].rearrange("p (k q) -> p k q", k=4),
                       ACT.Copy).then_inc(turns.free(t), 1)
    act.drain().then_inc(ready, 1)


def project(pe, turns, lhsT, w, name, s, p, n=2):
    for h in range(n):
        t = (name, s, h)
        pe.wait_ge(turns.free(t), turns.count(t, p))
        for k in range(w.shape[1]):
            mm = pe.matmul(turns.tile(t)[0:Q, :], lhsT[:, k, :], w[:, k, h * 512:(h + 1) * 512],
                           start=(k == 0), stop=(k == w.shape[1] - 1))
        mm.then_inc(turns.full(t), 1)


def plain_attention(nc, C, banks, gate, x_in, x_out, A, nearest):
    SCALE = float(D) ** -0.5
    with ExitStack() as ctx:
        s_ = Scope(nc, ctx, "plain")
        wq, wk = s_.sb("wq", [P, KC, D]), s_.sb("wk", [P, KC, D])
        bq, bk = s_.sb("bq", [Q, D]), s_.sb("bk", [P, KC])
        x, z = s_.sb("x", [Q, 2, D]), s_.sb("z", [Q, 2, D])
        zT, qT, tT = (s_.sb(n, [P, 2, KC, Q]) for n in ("zT", "qT", "tT"))
        q, t_ = s_.sb("q", [Q, 2, D]), z
        cT, cN = s_.sb("ctxT", [P, 2, KC, CTX]), s_.sb("ctx", [CT, 2, CTILES, D])
        pr, pT = s_.sb("probs", [Q, 2, CTX]), s_.sb("probsT", [CT, 2, CTILES, Q])
        nmax, rsum, coef = (s_.sb(n, [Q, 2, 1]) for n in ("nmax", "rsum", "coef"))
        qbk, total = s_.sb("qbk", [Q, 2, 1]), s_.sb("total", [Q, 2, 1])
        points = Nearest(s_, [5, 6, 7], 2, nearest, A)
        norm = Norm(s_, 2)
        wq_loaded, wk_loaded, b_loaded = s_.sem("wq_loaded"), s_.sem("wk_loaded"), s_.sem("b_loaded")
        x_loaded = [s_.sem(f"x_loaded{i}") for i in range(2)]
        x_stored = [s_.sem(f"x_stored{i}") for i in range(2)]
        z_loaded = [s_.sem(f"z_loaded{i}") for i in range(2)]
        ctx_loaded = [s_.sem(f"ctx_loaded{i}") for i in range(2)]
        ctx_free = [s_.sem(f"ctx_free{i}") for i in range(2)]
        z_ready, zT_ready, q_ready, qT_ready, t_ready, tT_ready = (
            s_.sem(n) for n in ("z_ready", "zT_ready", "q_ready", "qT_ready", "t_ready", "tT_ready"))
        max_ready, probs_ready, pT_ready, x_done = (
            s_.sem(n) for n in ("max_ready", "probs_ready", "pT_ready", "x_done"))
        order = []
        for st, b0, n in (("zT", 0, 2), ("q", 2, 2), ("qT", 0, 2), ("t", 2, 2), ("tT", 0, 2), ("S", 2, 1), ("pT", 3, 1),
                          ("o", 0, 2)):
            order += [((st, s, h), 4 * s + b0 + h) for s in range(2) for h in range(n)]
        turns = Turns(banks, order, PAIRS)
        block = ctx.enter_context(nc.Block())

        @block.sync
        def _(sp):
            for s in range(2):
                sp.dma_start(z[:, s, :], x_in[s]).then_inc(z_loaded[s], 16)
            sp.dma_start(wq[:], fold(A["L1_xattn_WqT"])).then_inc(wq_loaded, 16)
            sp.dma_start(wk[:], fold(A["L1_xattn_Wk"])).then_inc(wk_loaded, 16)
            stream_ahead(sp, x, z, x_in, x_out, x_loaded, z_loaded, x_done, x_stored,
                         lambda s, p: (turns.full(("tT", s, 1)), turns.count(("tT", s, 1), p)))

        @block.gpsimd
        def _(pool):
            pool.dma_start(bq[:], rows(A["L1_xattn_bq"], Q)).then_inc(b_loaded, 16)
            pool.dma_start(bk[:], A["L1_xattn_bk"]).then_inc(b_loaded, 16)
            with pool.Fori(0, PAIRS) as p:
                for s in range(2):
                    points.load(pool, p * 2 + s, s)
                for s in range(2):
                    pool.wait_ge(ctx_free[s], p + 1)
                    pool.dma_start(cT[:, s], A["ctxT"][p * 2 + s].rearrange("(k p) n -> p k n", p=P)).then_inc(ctx_loaded[s], 16)
                    pool.dma_start(cN[:, s], A["ctx_4096"][p * 2 + s].rearrange("(t p) n -> p t n", p=CT)).then_inc(ctx_loaded[s], 16)

        @block.tensor
        def _(pe):
            pe.wait_ge(wq_loaded, 16)
            with pe.Fori(0, PAIRS) as p:
                for s in range(2):
                    pe.wait_ge(z_ready, p * 2 + (s + 1))
                    turn_rows(pe, C, turns, z[:, s], "zT", s, p)
                for s in range(2):
                    pe.wait_ge(zT_ready, p * 2 + (s + 1))
                    project(pe, turns, zT[:, s], wq, "q", s, p)
                for s in range(2):
                    pe.wait_ge(q_ready, p * 2 + (s + 1))
                    turn_rows(pe, C, turns, q[:, s], "qT", s, p)
                pe.wait_ge(wk_loaded, 16)
                pe.wait_ge(b_loaded, 32)
                for s in range(2):
                    pe.wait_ge(qT_ready, p * 2 + (s + 1))
                    project(pe, turns, qT[:, s], wk, "t", s, p)
                for s in range(2):
                    pe.wait_ge(t_ready, p * 2 + (s + 1))
                    turn_rows(pe, C, turns, t_[:, s], "tT", s, p)
                for s in range(2):
                    t = ("S", s, 0)
                    pe.wait_ge(tT_ready, p * 2 + (s + 1))
                    pe.wait_ge(ctx_loaded[s], p * 32 + 32)
                    pe.wait_ge(turns.free(t), turns.count(t, p))
                    for k in range(KC):
                        pe.matmul(turns.tile(t)[0:Q, 0:CTX], tT[:, s, k, :], cT[:, s, k, :], start=(k == 0), stop=(k == KC - 1))
                    for k in range(KC):
                        mm = pe.matmul(turns.tile(t)[0:Q, 400:401], qT[:, s, k, :], bk[:, k:k + 1], start=(k == 0),
                                       stop=(k == KC - 1))
                    mm.then_inc(turns.full(t), 1)
                for s in range(2):
                    t = ("pT", s, 0)
                    pe.wait_ge(probs_ready, p * 2 + (s + 1))
                    pe.wait_ge(turns.free(t), turns.count(t, p))
                    for k in range(CTILES):
                        mm = pe.transpose(turns.tile(t)[0:CT, k * Q:(k + 1) * Q], pr[:, s, k * CT:(k + 1) * CT], C.ident[0:Q, 0:Q])
                    mm.then_inc(turns.full(t), 1)
                for s in range(2):
                    pe.wait_ge(pT_ready, p * 2 + (s + 1))
                    for h in range(2):
                        t = ("o", s, h)
                        pe.wait_ge(turns.free(t), turns.count(t, p))
                        for k in range(CTILES):
                            mm = pe.matmul(turns.tile(t)[0:Q, :], pT[:, s, k, :], cN[:, s, k, h * 512:(h + 1) * 512],
                                           start=(k == 0), stop=(k == CTILES - 1))
                        mm.then_inc(turns.full(t), 1)

        @block.scalar
        def _(act):
            for s in range(2):
                norm.root(act, s, s)

            def pair(p, last):
                for s in range(2):
                    copy_turned(act, turns, zT[:, s], "zT", s, p, zT_ready)
                for i in range(3):
                    points.squares(act, p * 2, 0, i)
                for s in range(2):
                    copy_turned(act, turns, qT[:, s], "qT", s, p, qT_ready)
                points.store(act, p * 2)
                for i in range(3):
                    points.squares(act, p * 2 + 1, 1, i)
                for s in range(2):
                    copy_turned(act, turns, tT[:, s], "tT", s, p, tT_ready)
                for s in range(2):
                    t = ("S", s, 0)
                    act.wait_ge(max_ready, p * 2 + (s + 1))
                    act.activation(pr[:, s, :], turns.tile(t)[0:Q, 0:CTX], ACT.Exp, bias=nmax[:, s, :], scale=SCALE,
                                   accum_out=rsum[:, s, :])
                    act.drain().then_inc(turns.free(t), 1)
                    act.drain().then_inc(probs_ready, 1)
                points.store(act, p * 2 + 1)
                if not last:
                    for s in range(2):
                        norm.root(act, s, p * 2 + (s + 2))

            every_pair(act, pair)
            points.stored(act)

        @block.vector
        def _(dve):
            for s in range(2):
                dve.sem_inc(ctx_free[s], 1)
            points.credits(dve)
            norm.in_place(dve, z, z_loaded, 0, z_ready)
            dve.wait_ge(b_loaded, 32)

            def pair(p, last):
                for s in range(2):
                    points.begin(dve, p * 2 + s, s, p)
                for s in range(2):
                    for i in range(2 - s):
                        points.sort(dve, p * 2, 0, 2 * s + i)
                    for h in range(2):
                        t = ("q", s, h)
                        c = slice(h * 512, (h + 1) * 512)
                        dve.wait_ge(turns.full(t), turns.count(t, p))
                        dve.tensor_tensor(q[:, s, c], turns.tile(t)[0:Q, :], bq[:, c], ALU.add).then_inc(turns.free(t), 1)
                    dve.drain().then_inc(q_ready, 1)
                for s in range(2):
                    for i in range(2 - s):
                        points.sort(dve, p * 2 + 1, 1, 2 * s + i)
                    for h in range(2):
                        t = ("t", s, h)
                        dve.wait_ge(turns.full(t), turns.count(t, p))
                        dve.tensor_copy(t_[:, s, h * 512:(h + 1) * 512], turns.tile(t)[0:Q, :]).then_inc(turns.free(t), 1)
                    dve.drain().then_inc(t_ready, 1)
                for s in range(2):
                    t = ("S", s, 0)
                    dve.wait_ge(turns.full(t), turns.count(t, p))
                    dve.tensor_copy(qbk[:, s, :], turns.tile(t)[0:Q, 400:401])
                    dve.tensor_reduce(nmax[:, s, :], turns.tile(t)[0:Q, 0:CTX], AX, ALU.max, negate=True)
                    dve.drain()
                    dve.tensor_tensor(total[:, s, :], nmax[:, s, :], qbk[:, s, :], ALU.subtract)
                    dve.drain()
                    dve.tensor_scalar(nmax[:, s, :], total[:, s, :], qbk[:, s, :], SCALE, ALU.add, ALU.mult).then_inc(max_ready, 1)
                for s in range(2):
                    t = ("pT", s, 0)
                    dve.wait_ge(probs_ready, p * 2 + (s + 1))
                    dve.reciprocal(coef[:, s, :], rsum[:, s, :])
                    dve.wait_ge(turns.full(t), turns.count(t, p))
                    dve.tensor_copy(pT[:, s, :, :], turns.tile(t)[0:CT, 0:CTILES * Q].rearrange("p (k q) -> p k q", q=Q))\
                       .then_inc(turns.free(t), 1)
                    dve.drain().then_inc(pT_ready, 1)
                    dve.tensor_scalar(coef[:, s, :], coef[:, s, :], C.gates[0:Q, gate:gate + 1], None, ALU.mult)
                dve.drain()
                if not last:
                    norm.in_place(dve, z, z_loaded, p + 1, z_ready)
                for s in range(2):
                    dve.wait_ge(x_loaded[s], p * 16 + 16)
                    for h in range(2):
                        t = ("o", s, h)
                        c = slice(h * 512, (h + 1) * 512)
                        dve.wait_ge(turns.full(t), turns.count(t, p))
                        dve.scalar_tensor_tensor(out=x[:, s, c], in0=turns.tile(t)[0:Q, :], scalar=coef[:, s, :],
                                                 in1=x[:, s, c], op0=ALU.mult, op1=ALU.add).then_inc(turns.free(t), 1)
                    dve.drain().then_inc(x_done, 1)
                    dve.drain().then_inc(ctx_free[s], 1)

            every_pair(dve, pair)


def memory_ffn(nc, C, banks, gate, x_in, x_out, A):
    BOT, RDIM, NSLOT, HU = 64, 48, 256, 256
    TAU_LOW, TAU_HIGH, EARLY_EXIT = 0.5, 2.0, 0.05
    with ExitStack() as ctx:
        s_ = Scope(nc, ctx, "mem")
        wqT, wu1T, wvdT = s_.sb("wqT", [P, KC, BOT]), s_.sb("wu1T", [P, KC, HU]), s_.sb("wvdT", [P, KC, BOT])
        wu2, bu1 = s_.sb("wu2", [P, 2]), s_.sb("bu1", [P, 2])
        bu2, gw1, gbias = (s_.sb(n, [Q, 1]) for n in ("bu2", "gw1", "gbias"))
        wrT, keysT, wvuT = s_.sb("wrT", [BOT, P]), s_.sb("keysT", [BOT, NSLOT]), s_.sb("wvuT", [BOT, D])
        valuesT, rel = s_.sb("valuesT", [P, KC, NSLOT]), s_.sb("log_rel", [Q, NSLOT])
        ones = s_.sb("ones", [Q, Q])
        av, rkT = s_.sb("av", [P, 2, BOT]), s_.sb("rkT", [RDIM, NSLOT])
        x, z = s_.sb("x", [Q, 2, D]), s_.sb("z", [Q, 2, D])
        zT = s_.sb("zT", [P, KC, 2 * Q])
        queryT, hidT = s_.sb("queryT", [BOT, 2 * Q]), s_.sb("hidT", [P, 2, 2 * Q])
        rqT, vT = s_.sb("rqT", [RDIM, 2 * Q]), s_.sb("vT", [BOT, 2 * Q])
        route, attn, left = (s_.sb(n, [Q, 2, NSLOT]) for n in ("route", "attn", "left"))
        w, wT = s_.sb("w", [Q, 2, NSLOT]), s_.sb("wT", [P, 2, 2, Q])
        best = s_.sb("best", [Q, 2, 8])
        nmax, rsum, coef, var_z, log_var, learned, unsure, keep = (
            s_.sb(n, [Q, 2]) for n in ("nmax", "rsum", "coef", "var_z", "log_var", "learned", "unsure", "keep"))
        lsum, rmean = s_.sb("lsum", [Q, 1]), s_.sb("rmean", [Q, 1])
        norm = Norm(s_, 2)
        w_loaded = s_.sem("w_loaded")
        pre_loaded = [s_.sem(f"pre_loaded{i}") for i in range(2)]
        pre_free = [s_.sem(f"pre_free{i}") for i in range(2)]
        x_loaded = [s_.sem(f"x_loaded{i}") for i in range(2)]
        x_stored = [s_.sem(f"x_stored{i}") for i in range(2)]
        z_loaded = [s_.sem(f"z_loaded{i}") for i in range(2)]
        z_free = s_.sem("z_free")
        pre_var, pre_log, lsum_ready, tables_ready = (s_.sem(n) for n in ("pre_var", "pre_log", "lsum_ready", "tables_ready"))
        z_ready, zT_ready, proj_ready, rq_ready, sig_ready, un_ready, gate_ready = (
            s_.sem(n) for n in ("z_ready", "zT_ready", "proj_ready", "rq_ready", "sig_ready", "un_ready", "gate_ready"))
        max_ready, w_ready, wT_ready, v_ready, x_done = (
            s_.sem(n) for n in ("max_ready", "w_ready", "wT_ready", "v_ready", "x_done"))
        prep = Turns(banks, [("lsum", 0), ("rk", 1), ("av", 2)], 1)
        turns = Turns(banks, [(("zT", s, h), 2 * s + h) for s in range(2) for h in range(2)]
                      + [("query", 4), ("hid", 5), ("rq", 6), ("learned", 7)]
                      + [(("scores", s), s) for s in range(2)] + [(("wT", s), 2 + s) for s in range(2)] + [("v", 4)]
                      + [(("o", s, h), (5, 6, 7, 0)[2 * s + h]) for s in range(2) for h in range(2)], PAIRS)
        weights = [(wqT, fold(A["L1_ffn_WqT"])), (wu1T, fold(A["L1_ffn_Wu1T"])), (wvdT, fold(A["L1_ffn_WvdT"])),
                   (wu2, A["L1_ffn_Wu2"]), (bu1, A["L1_ffn_bu1"]), (bu2, rows(A["L1_ffn_bu2"], Q)),
                   (gw1, rows(A["L1_ffn_gate_w1"], Q)), (gbias, rows(A["L1_ffn_gate_bias"], Q)),
                   (wrT, A["L1_ffn_WrT"]), (keysT, A["L1_ffn_aux_keysT"]), (wvuT, A["L1_ffn_WvuT"]),
                   (valuesT, fold(A["L1_ffn_aux_valuesT"])), (rel, rows(A["L1_ffn_log_rel"], Q))]
        block = ctx.enter_context(nc.Block())

        @block.sync
        def _(sp):
            with sp.Fori(0, PAIRS) as p:
                for s in range(2):
                    sp.wait_ge(pre_free[s], p + 1)
                    sp.dma_start(x[:, s, :], x_in[p * 2 + s]).then_inc(pre_loaded[s], 16)
            for s in range(2):
                sp.wait_ge(pre_free[s], PAIRS + 1)
            for s in range(2):
                sp.dma_start(z[:, s, :], x_in[s]).then_inc(z_loaded[s], 16)
            stream_ahead(sp, x, z, x_in, x_out, x_loaded, z_loaded, x_done, x_stored,
                         lambda s, p: (z_free, p * 2 + (s + 1)))

        @block.gpsimd
        def _(pool):
            for dst, src in weights:
                pool.dma_start(dst[:], src).then_inc(w_loaded, 16)

        @block.tensor
        def _(pe):
            pe.wait_ge(w_loaded, 16 * len(weights))
            pe.wait_ge(prep.free("rk"), prep.count("rk", 0))
            pe.matmul(prep.tile("rk")[:, 0:NSLOT], wrT[:], keysT[:], start=True, stop=True).then_inc(prep.full("rk"), 1)
            pe.wait_ge(prep.free("av"), prep.count("av", 0))
            for c in range(2):
                for k in range(KC):
                    mm = pe.matmul(prep.tile("av")[:, c * BOT:(c + 1) * BOT], valuesT[:, k, c * P:(c + 1) * P], wvdT[:, k, :],
                                   start=(k == 0), stop=(k == KC - 1))
            mm.then_inc(prep.full("av"), 1)
            pe.wait_ge(lsum_ready, 1)
            pe.wait_ge(prep.free("lsum"), prep.count("lsum", 0))
            pe.matmul(prep.tile("lsum")[0:Q, 0:1], ones[:], lsum[:], start=True, stop=True).then_inc(prep.full("lsum"), 1)
            pe.wait_ge(tables_ready, 2)
            with pe.Fori(0, PAIRS) as p:
                for s in range(2):
                    pe.wait_ge(z_ready, p * 2 + (s + 1))
                    turn_rows(pe, C, turns, z[:, s], "zT", s, p)
                pe.wait_ge(zT_ready, p * 2 + 2)
                pe.wait_ge(turns.free("query"), turns.count("query", p))
                for k in range(KC):
                    mm = pe.matmul(turns.tile("query")[0:BOT, 0:2 * Q], wqT[:, k, :], zT[:, k, :], start=(k == 0), stop=(k == KC - 1))
                mm.then_inc(turns.full("query"), 1)
                pe.wait_ge(turns.free("hid"), turns.count("hid", p))
                for c in range(2):
                    for k in range(KC):
                        mm = pe.matmul(turns.tile("hid")[:, c * 2 * Q:(c + 1) * 2 * Q], wu1T[:, k, c * P:(c + 1) * P], zT[:, k, :],
                                       start=(k == 0), stop=(k == KC - 1))
                mm.then_inc(turns.full("hid"), 1)
                pe.wait_ge(proj_ready, p * 2 + 1)
                pe.wait_ge(turns.free("rq"), turns.count("rq", p))
                pe.matmul(turns.tile("rq")[:, 0:2 * Q], wrT[:], queryT[:], start=True, stop=True).then_inc(turns.full("rq"), 1)
                pe.wait_ge(proj_ready, p * 2 + 2)
                pe.wait_ge(turns.free("learned"), turns.count("learned", p))
                for s in range(2):
                    for c in range(2):
                        mm = pe.matmul(turns.tile("learned")[0:Q, s:s + 1], hidT[:, c, s * Q:(s + 1) * Q], wu2[:, c:c + 1],
                                       start=(c == 0), stop=(c == 1))
                mm.then_inc(turns.full("learned"), 1)
                pe.wait_ge(rq_ready, p + 1)
                for s in range(2):
                    t = ("scores", s)
                    pe.wait_ge(turns.free(t), turns.count(t, p))
                    pe.matmul(turns.tile(t)[0:Q, 0:NSLOT], rqT[:, s * Q:(s + 1) * Q], rkT[:], start=True, stop=True)
                    pe.matmul(turns.tile(t)[0:Q, NSLOT:2 * NSLOT], queryT[:, s * Q:(s + 1) * Q], keysT[:], start=True,
                              stop=True).then_inc(turns.full(t), 1)
                for s in range(2):
                    t = ("wT", s)
                    pe.wait_ge(w_ready, p * 2 + (s + 1))
                    pe.wait_ge(turns.free(t), turns.count(t, p))
                    for c in range(2):
                        mm = pe.transpose(turns.tile(t)[:, c * Q:(c + 1) * Q], w[:, s, c * P:(c + 1) * P], C.ident[0:Q, 0:Q])
                    mm.then_inc(turns.full(t), 1)
                pe.wait_ge(wT_ready, p * 2 + 2)
                pe.wait_ge(turns.free("v"), turns.count("v", p))
                for c in range(2):
                    mm = pe.matmul(turns.tile("v")[0:BOT, 0:2 * Q], av[:, c, :], wT[:, c, :, :], start=(c == 0), stop=(c == 1))
                mm.then_inc(turns.full("v"), 1)
                pe.wait_ge(v_ready, p + 1)
                for s in range(2):
                    for h in range(2):
                        t = ("o", s, h)
                        pe.wait_ge(turns.free(t), turns.count(t, p))
                        pe.matmul(turns.tile(t)[0:Q, :], vT[:, s * Q:(s + 1) * Q], wvuT[:, h * 512:(h + 1) * 512], start=True,
                                  stop=True).then_inc(turns.full(t), 1)

        @block.scalar
        def _(act):
            act.wait_ge(prep.full("rk"), prep.count("rk", 0))
            act.activation(rkT[:], prep.tile("rk")[0:RDIM, 0:NSLOT], ACT.Copy).then_inc(prep.free("rk"), 1)
            act.wait_ge(prep.full("av"), prep.count("av", 0))
            act.activation(av[:], prep.tile("av")[:, 0:2 * BOT].rearrange("p (c n) -> p c n", c=2), ACT.Copy)\
               .then_inc(prep.free("av"), 1)
            act.drain().then_inc(tables_ready, 1)
            with act.Fori(0, PAIRS) as p:
                act.wait_ge(pre_var, p + 1)
                act.activation(log_var[:], var_z[:], ACT.Ln, bias=1.0).then_inc(pre_log, 1)
            for s in range(2):
                norm.root(act, s, s)

            def pair(p, last):
                for s in range(2):
                    copy_turned(act, turns, zT[:, :, s * Q:(s + 1) * Q], "zT", s, p, zT_ready)
                act.wait_ge(turns.full("query"), turns.count("query", p))
                act.activation(queryT[:], turns.tile("query")[0:BOT, 0:2 * Q], ACT.Copy).then_inc(turns.free("query"), 1)
                act.drain().then_inc(proj_ready, 1)
                act.wait_ge(turns.full("hid"), turns.count("hid", p))
                for c in range(2):
                    act.activation(hidT[:, c, :], turns.tile("hid")[:, c * 2 * Q:(c + 1) * 2 * Q], ACT.Gelu_apprx_tanh,
                                   bias=bu1[:, c:c + 1])
                act.drain().then_inc(turns.free("hid"), 1)
                act.drain().then_inc(proj_ready, 1)
                act.wait_ge(turns.full("rq"), turns.count("rq", p))
                act.activation(rqT[:], turns.tile("rq")[0:RDIM, 0:2 * Q], ACT.Copy).then_inc(turns.free("rq"), 1)
                act.drain().then_inc(rq_ready, 1)
                for s in range(2):
                    act.wait_ge(max_ready, p * 2 + (s + 1))
                    act.activation(w[:, s, :], attn[:, s, :], ACT.Exp, bias=nmax[:, s:s + 1], accum_out=rsum[:, s:s + 1])
                    act.drain().then_inc(w_ready, 1)
                act.activation(log_var[:], var_z[:], ACT.Ln, bias=1.0)
                act.wait_ge(turns.full("learned"), turns.count("learned", p))
                act.activation(learned[:], turns.tile("learned")[0:Q, 0:2], ACT.Sigmoid, bias=bu2[:]).then_inc(turns.free("learned"), 1)
                act.drain().then_inc(sig_ready, 1)
                act.wait_ge(un_ready, p + 1)
                act.activation(coef[:], unsure[:], ACT.Sigmoid, bias=gbias[:], scale=gw1[:]).then_inc(gate_ready, 1)
                act.wait_ge(turns.full("v"), turns.count("v", p))
                act.activation(vT[:], turns.tile("v")[0:BOT, 0:2 * Q], ACT.Copy).then_inc(turns.free("v"), 1)
                act.drain().then_inc(v_ready, 1)
                if not last:
                    for s in range(2):
                        norm.root(act, s, p * 2 + (s + 2))

            every_pair(act, pair)

        @block.vector
        def _(dve):
            for s in range(2):
                dve.sem_inc(pre_free[s], 1)
            dve.memset(ones[:], 1.0)
            dve.memset(lsum[:], 0.0)
            with dve.Fori(0, PAIRS) as p:
                for s in range(2):
                    dve.wait_ge(pre_loaded[s], p * 16 + 16)
                    for h in range(2):
                        dve.bn_stats(norm.stats[:, s, h, :], x[:, s, h * 512:(h + 1) * 512])
                    dve.drain()
                    dve.bn_aggr(norm.mv[:, s, :], norm.stats[:, s, :, :]).then_inc(pre_free[s], 1)
                dve.drain()
                dve.tensor_scalar(norm.rstd[:, :, 0], norm.mv[:, :, 1], EPS, None, ALU.add)
                dve.drain()
                dve.reciprocal(norm.rstd[:, :, 0], norm.rstd[:, :, 0])
                dve.drain()
                dve.tensor_tensor(var_z[:], norm.mv[:, :, 1], norm.rstd[:, :, 0], ALU.mult).then_inc(pre_var, 1)
                dve.wait_ge(pre_log, p + 1)
                for s in range(2):
                    dve.tensor_tensor(lsum[:], lsum[:], log_var[:, s:s + 1], ALU.add)
                    dve.drain()
            dve.sem_inc(lsum_ready, 1)
            dve.wait_ge(prep.full("lsum"), prep.count("lsum", 0))
            dve.tensor_scalar(rmean[:], prep.tile("lsum")[0:Q, 0:1], 1.0 / (B * Q), 1e-6, ALU.mult, ALU.add)\
               .then_inc(prep.free("lsum"), 1)
            dve.drain()
            dve.reciprocal(rmean[:], rmean[:])
            dve.drain().then_inc(tables_ready, 1)
            gc = C.gates[0:Q, gate:gate + 1]
            norm.in_place(dve, z, z_loaded, 0, z_ready)

            def pair(p, last):
                dve.tensor_tensor(var_z[:], norm.mv[:, :, 1], norm.rstd[:, :, 0], ALU.mult)
                dve.drain()
                dve.tensor_tensor(var_z[:], var_z[:], norm.rstd[:, :, 0], ALU.mult)
                for s in range(2):
                    dve.wait_ge(x_loaded[s], p * 16 + 16)
                    dve.scalar_tensor_tensor(out=x[:, s, :], in0=z[:, s, :], scalar=gc, in1=x[:, s, :], op0=ALU.mult, op1=ALU.add)
                dve.drain()
                for s in range(2):
                    t = ("zT", s, 1)
                    dve.wait_ge(turns.full(t), turns.count(t, p))
                    dve.sem_inc(z_free, 1)
                for s in range(2):
                    t = ("scores", s)
                    dve.wait_ge(turns.full(t), turns.count(t, p))
                    dve.scalar_tensor_tensor(out=route[:, s, :], in0=turns.tile(t)[0:Q, 0:NSLOT], scalar=float(RDIM) ** -0.5,
                                             in1=rel[:], op0=ALU.mult, op1=ALU.add)
                    dve.scalar_tensor_tensor(out=attn[:, s, :], in0=turns.tile(t)[0:Q, NSLOT:2 * NSLOT], scalar=float(BOT) ** -0.5,
                                             in1=rel[:], op0=ALU.mult, op1=ALU.add)
                    dve.drain().then_inc(turns.free(t), 1)
                    dve.max(best[:, s, :], route[:, s, :])
                    dve.drain()
                    dve.match_replace(left[:, s, :], best[:, s, :], route[:, s, :], -3e38)
                    dve.drain()
                    dve.tensor_tensor(left[:, s, :], left[:, s, :], route[:, s, :], ALU.is_equal)
                    dve.drain()
                    dve.scalar_tensor_tensor(out=attn[:, s, :], in0=left[:, s, :], scalar=LOW, in1=attn[:, s, :],
                                             op0=ALU.mult, op1=ALU.add)
                    dve.drain()
                    dve.tensor_reduce(nmax[:, s:s + 1], attn[:, s, :], AX, ALU.max, negate=True).then_inc(max_ready, 1)
                for s in range(2):
                    t = ("wT", s)
                    dve.wait_ge(turns.full(t), turns.count(t, p))
                    dve.tensor_copy(wT[:, :, s, :], turns.tile(t)[:, 0:2 * Q].rearrange("p (c q) -> p c q", c=2))\
                       .then_inc(turns.free(t), 1)
                    dve.drain().then_inc(wT_ready, 1)
                dve.wait_ge(sig_ready, p + 1)
                dve.tensor_scalar(unsure[:], log_var[:], rmean[:], 0.5, ALU.mult, ALU.mult)
                dve.drain()
                dve.scalar_tensor_tensor(out=unsure[:], in0=learned[:], scalar=2.5, in1=unsure[:], op0=ALU.mult, op1=ALU.add)
                dve.drain()
                dve.tensor_scalar(unsure[:], unsure[:], 0.0, 5.0, ALU.max, ALU.min)
                dve.drain()
                dve.tensor_scalar(unsure[:], unsure[:], TAU_LOW, 1.0 / (TAU_HIGH - TAU_LOW), ALU.subtract, ALU.mult)
                dve.drain()
                dve.tensor_scalar(unsure[:], unsure[:], 0.0, 1.0, ALU.max, ALU.min).then_inc(un_ready, 1)
                dve.reciprocal(rsum[:], rsum[:])
                dve.wait_ge(gate_ready, p + 1)
                dve.tensor_scalar(keep[:], coef[:], EARLY_EXIT, gc, ALU.is_ge, ALU.mult)
                dve.drain()
                dve.tensor_tensor(coef[:], coef[:], keep[:], ALU.mult)
                dve.drain()
                dve.tensor_tensor(coef[:], coef[:], rsum[:], ALU.mult)
                dve.drain()
                if not last:
                    norm.in_place(dve, z, z_loaded, p + 1, z_ready)
                for s in range(2):
                    for h in range(2):
                        t = ("o", s, h)
                        c = slice(h * 512, (h + 1) * 512)
                        dve.wait_ge(turns.full(t), turns.count(t, p))
                        dve.scalar_tensor_tensor(out=x[:, s, c], in0=turns.tile(t)[0:Q, :], scalar=coef[:, s:s + 1],
                                                 in1=x[:, s, c], op0=ALU.mult, op1=ALU.add).then_inc(turns.free(t), 1)
                    dve.drain().then_inc(x_done, 1)

            every_pair(dve, pair)


def experts_ffn(nc, C, banks, gate, x_in, x_out, A):
    NE, RANK = 8, 64
    R = NE * RANK
    with ExitStack() as ctx:
        s_ = Scope(nc, ctx, "moe")
        aT, bT, gT = s_.sb("aT", [P, KC, R]), s_.sb("bT", [P, R // P, D]), s_.sb("gT", [P, KC, NE])
        x, z = s_.sb("x", [Q, 2, D]), s_.sb("z", [Q, 2, D])
        zT = s_.sb("zT", [P, 2, KC, Q])
        prob, best, w8, hit = (s_.sb(n, [Q, 2, NE]) for n in ("prob", "best", "w8", "hit"))
        place, placef = s_.sb("place", [Q, 2, 8], U32), s_.sb("placef", [Q, 2, 8])
        number = s_.sb("number", [Q, NE])
        nmax, both = s_.sb("nmax", [Q, 2]), s_.sb("both", [Q, 2])
        h, hT = s_.sb("h", [Q, 2, R]), s_.sb("hT", [P, 2, R // P, Q])
        norm = Norm(s_, 2)
        w_loaded = s_.sem("w_loaded")
        x_loaded = [s_.sem(f"x_loaded{i}") for i in range(2)]
        x_stored = [s_.sem(f"x_stored{i}") for i in range(2)]
        z_loaded = [s_.sem(f"z_loaded{i}") for i in range(2)]
        z_ready, zT_ready, max_ready, prob_ready, h_ready, hT_ready, x_done, numbered = (
            s_.sem(n) for n in ("z_ready", "zT_ready", "max_ready", "prob_ready", "h_ready", "hT_ready", "x_done", "numbered"))
        turns = Turns(banks, [(("zT", s, i), 4 * s + i) for s in range(2) for i in range(2)]
                      + [((n, s), 4 * s + i) for n, i in (("gate", 2), ("h", 3)) for s in range(2)]
                      + [(("hT", s, 0), 4 * s) for s in range(2)]
                      + [(("o", s, i), 4 * s + 1 + i) for s in range(2) for i in range(2)], PAIRS)
        weights = [(aT, fold(A["L3_lora_AT"])), (bT, fold(A["L3_lora_BT"])), (gT, fold(A["L3_ffn_gate_wT"]))]
        block = ctx.enter_context(nc.Block())

        @block.sync
        def _(sp):
            for s in range(2):
                sp.dma_start(z[:, s, :], x_in[s]).then_inc(z_loaded[s], 16)
            stream_ahead(sp, x, z, x_in, x_out, x_loaded, z_loaded, x_done, x_stored,
                         lambda s, p: (turns.full(("zT", s, 1)), turns.count(("zT", s, 1), p)))

        @block.gpsimd
        def _(pool):
            pool.iota(number[:], pattern=[[1, NE]], base=0, channel_multiplier=0,
                      allow_small_or_imprecise_dtypes=True).then_inc(numbered, 1)
            for dst, src in weights:
                pool.dma_start(dst[:], src).then_inc(w_loaded, 16)

        @block.tensor
        def _(pe):
            pe.wait_ge(w_loaded, 16 * len(weights))
            with pe.Fori(0, PAIRS) as p:
                for s in range(2):
                    pe.wait_ge(z_ready, p * 2 + (s + 1))
                    turn_rows(pe, C, turns, z[:, s], "zT", s, p)
                for s in range(2):
                    pe.wait_ge(zT_ready, p * 2 + (s + 1))
                    for name, w, n in (("gate", gT, NE), ("h", aT, R)):
                        t = (name, s)
                        pe.wait_ge(turns.free(t), turns.count(t, p))
                        for k in range(KC):
                            mm = pe.matmul(turns.tile(t)[0:Q, 0:n], zT[:, s, k, :], w[:, k, :], start=(k == 0), stop=(k == KC - 1))
                        mm.then_inc(turns.full(t), 1)
                for s in range(2):
                    pe.wait_ge(h_ready, p * 2 + (s + 1))
                    turn_rows(pe, C, turns, h[:, s], "hT", s, p, n=1)
                for s in range(2):
                    pe.wait_ge(hT_ready, p * 2 + (s + 1))
                    project(pe, turns, hT[:, s], bT, "o", s, p)

        @block.scalar
        def _(act):
            for s in range(2):
                norm.root(act, s, s)

            def pair(p, last):
                for s in range(2):
                    copy_turned(act, turns, zT[:, s], "zT", s, p, zT_ready)
                for s in range(2):
                    t = ("gate", s)
                    act.wait_ge(max_ready, p * 2 + (s + 1))
                    act.activation(prob[:, s, :], turns.tile(t)[0:Q, 0:NE], ACT.Exp, bias=nmax[:, s:s + 1]).then_inc(turns.free(t), 1)
                    act.drain().then_inc(prob_ready, 1)
                for s in range(2):
                    copy_turned(act, turns, hT[:, s], "hT", s, p, hT_ready, n=1)
                if not last:
                    for s in range(2):
                        norm.root(act, s, p * 2 + (s + 2))

            every_pair(act, pair)

        @block.vector
        def _(dve):
            dve.wait_ge(numbered, 1)
            gc = C.gates[0:Q, gate:gate + 1]
            norm.in_place(dve, z, z_loaded, 0, z_ready)

            def pair(p, last):
                for s in range(2):
                    t = ("gate", s)
                    dve.wait_ge(turns.full(t), turns.count(t, p))
                    dve.tensor_reduce(nmax[:, s:s + 1], turns.tile(t)[0:Q, 0:NE], AX, ALU.max, negate=True).then_inc(max_ready, 1)
                for s in range(2):
                    dve.wait_ge(prob_ready, p * 2 + (s + 1))
                    dve.tensor_reduce(both[:, s:s + 1], prob[:, s, :], AX, ALU.add)
                    dve.drain()
                    dve.reciprocal(both[:, s:s + 1], both[:, s:s + 1])
                    dve.drain()
                    dve.tensor_scalar(prob[:, s, :], prob[:, s, :], both[:, s:s + 1], None, ALU.mult)
                    dve.drain()
                    dve.max(best[:, s, :], prob[:, s, :])
                    dve.drain()
                    dve.max_index(place[:, s, :], best[:, s, :], prob[:, s, :])
                    dve.tensor_tensor(both[:, s:s + 1], best[:, s, 0:1], best[:, s, 1:2], ALU.add)
                    dve.drain()
                    dve.tensor_copy(placef[:, s, :], place[:, s, :])
                    dve.reciprocal(both[:, s:s + 1], both[:, s:s + 1])
                    dve.drain()
                    dve.tensor_scalar(best[:, s, 0:2], best[:, s, 0:2], both[:, s:s + 1], gc, ALU.mult, ALU.mult)
                    dve.drain()
                    dve.tensor_scalar(w8[:, s, :], number[:], placef[:, s, 0:1], best[:, s, 0:1], ALU.is_equal, ALU.mult)
                    dve.tensor_scalar(hit[:, s, :], number[:], placef[:, s, 1:2], best[:, s, 1:2], ALU.is_equal, ALU.mult)
                    dve.drain()
                    dve.tensor_tensor(w8[:, s, :], w8[:, s, :], hit[:, s, :], ALU.add)
                    dve.drain()
                    t = ("h", s)
                    dve.wait_ge(turns.full(t), turns.count(t, p))
                    dve.tensor_tensor(h[:, s, :].rearrange("q (e r) -> q e r", e=NE),
                                      turns.tile(t)[0:Q, :].rearrange("q (e r) -> q e r", e=NE),
                                      w8[:, s, :].unsqueeze(2).broadcast_to([Q, NE, RANK]), ALU.mult).then_inc(turns.free(t), 1)
                    dve.drain().then_inc(h_ready, 1)
                if not last:
                    norm.in_place(dve, z, z_loaded, p + 1, z_ready)
                for s in range(2):
                    dve.wait_ge(x_loaded[s], p * 16 + 16)
                    for i in range(2):
                        t = ("o", s, i)
                        c = slice(i * 512, (i + 1) * 512)
                        dve.wait_ge(turns.full(t), turns.count(t, p))
                        dve.tensor_tensor(x[:, s, c], turns.tile(t)[0:Q, :], x[:, s, c], ALU.add).then_inc(turns.free(t), 1)
                    dve.drain().then_inc(x_done, 1)

            every_pair(dve, pair)


def latent_attention(nc, C, banks, gate, x_in, x_out, A, nearest):
    H, KV, HD = 16, 4, 96
    G = H // KV
    S = CTX + Q
    DK, DQ = KV * HD, H * HD
    OC = DQ // P
    SCALE = float(HD) ** -0.5
    KT = [(k * CT, CT) for k in range(CTILES)] + [(CTX, Q)]
    with ExitStack() as ctx:
        s_ = Scope(nc, ctx, "latent")
        wk, wv = s_.sb("wk", [P, KC, DK]), s_.sb("wv", [P, KC, DK])
        wq, wo = s_.sb("wq", [P, KC, DQ]), s_.sb("wo", [P, OC, D])
        x, z = s_.sb("x", [Q, 2, D]), s_.sb("z", [Q, D])
        hT = s_.sb("hT", [P, KC, S])
        kT, v = s_.sb("kT", [HD, KV, S]), s_.sb("v", [P, 4, DK])
        q, qT = s_.sb("q", [Q, DQ]), s_.sb("qT", [HD, H, Q])
        pr, pT = s_.sb("probs", [Q, 2, S]), s_.sb("probsT", [P, 2, 4, Q])
        o, oT = q, s_.sb("oT", [P, OC, Q])
        y = z
        nmax, rsum = s_.sb("nmax", [Q, H]), s_.sb("rsum", [Q, H])
        points = Nearest(s_, [0, 1, 2, 3, 4], 1, nearest, A)
        norm = Norm(s_, 1)
        wk_loaded, wv_loaded, wq_loaded, wo_loaded = (s_.sem(n) for n in ("wk_loaded", "wv_loaded", "wq_loaded", "wo_loaded"))
        x_loaded = [s_.sem(f"x_loaded{i}") for i in range(2)]
        x_stored = [s_.sem(f"x_stored{i}") for i in range(2)]
        hT_free, ctx_loaded = s_.sem("hT_free"), s_.sem("ctx_loaded")
        z_ready, zT_ready, v_ready, kT_ready, q_ready, qT_ready = (
            s_.sem(n) for n in ("z_ready", "zT_ready", "v_ready", "kT_ready", "q_ready", "qT_ready"))
        max_ready, probs_ready, pT_ready, heads_done, o_ready, oT_ready, y_ready, x_done = (
            s_.sem(n) for n in ("max_ready", "probs_ready", "pT_ready", "heads_done", "o_ready", "oT_ready", "y_ready", "x_done"))
        groups = ([("v", i) for i in range(CTILES)] + [("zT", 0, i) for i in range(2)] + [("v", 3)]
                  + [("k", i) for i in range(KV)] + [("q", i) for i in range(3)] + [("qT", i) for i in range(4)])
        order = [(g, i % 4) for i, g in enumerate(groups)]
        for h in range(H + 3):
            if h < H:
                order.append((("S", h), 4 + h % 2))
            if 2 <= h < H + 2:
                order.append((("pT", h - 2), 6 + h % 2))
            if h >= 3 and (h - 3) % G == 0:
                order.append((("o", (h - 3) // G), (h - 3) // G % 2))
        order += [(("oT", i), 2 + i % 2) for i in range(3)] + [(("y", i), i) for i in range(2)]
        turns = Turns(banks, order, B)
        block = ctx.enter_context(nc.Block())

        @block.sync
        def _(sp):
            def load_x(b, s):
                sp.dma_start(x[:, s, :], x_in[b]).then_inc(x_loaded[s], 16)

            def load_rest(b):
                sp.wait_ge(hT_free, b + 1)
                sp.dma_start(hT[:, :, 0:CTX], A["ctxT"][b].rearrange("(k p) n -> p k n", p=P)).then_inc(ctx_loaded, 16)
                points.load(sp, b, 0)

            with sp.Fori(0, PAIRS) as p:
                for s in range(2):
                    sp.wait_ge(x_stored[s], p * 16 + 16)
                    load_x(p * 2 + s, s)
                    load_rest(p * 2 + s)
            for s in range(2):
                sp.wait_ge(x_stored[s], 16 * PAIRS + 16)
            points.stored(sp)

        @block.gpsimd
        def _(pool):
            for s in range(2):
                pool.sem_inc(x_stored[s], 16)
            pool.dma_start(wv[:], fold(A["L0_xattn_WvT"])).then_inc(wv_loaded, 16)
            pool.dma_start(wk[:], fold(A["L0_xattn_WkT"])).then_inc(wk_loaded, 16)
            pool.dma_start(wq[:], fold(A["L0_xattn_WqT"])).then_inc(wq_loaded, 16)
            pool.dma_start(wo[:], fold(A["L0_xattn_WoT"])).then_inc(wo_loaded, 16)
            with pool.Fori(0, PAIRS) as p:
                for s in range(2):
                    pool.wait_ge(y_ready, p * 2 + (s + 1))
                    pool.tensor_tensor(x[:, s, :], x[:, s, :], y[:], ALU.add).then_inc(x_done, 1)

        @block.tensor
        def _(pe):
            pe.wait_ge(wv_loaded, 16)

            def fill(t, b, lhsT, rhs, m, n, chunks):
                pe.wait_ge(turns.free(t), turns.count(t, b))
                for k in range(chunks):
                    mm = pe.matmul(turns.tile(t)[0:m, 0:n], lhsT(k), rhs(k), start=(k == 0), stop=(k == chunks - 1))
                mm.then_inc(turns.full(t), 1)

            def sequence(b):
                pe.wait_ge(ctx_loaded, b * 16 + 16)
                for i in range(CTILES):
                    fill(("v", i), b, lambda k: hT[:, k, i * CT:(i + 1) * CT], lambda k: wv[:, k, :], CT, DK, KC)
                pe.wait_ge(z_ready, b + 1)
                turn_rows(pe, C, turns, z, "zT", 0, b)
                pe.wait_ge(zT_ready, b + 1)
                fill(("v", 3), b, lambda k: hT[:, k, CTX:S], lambda k: wv[:, k, :], Q, DK, KC)
                pe.wait_ge(wk_loaded, 16)
                for i in range(KV):
                    fill(("k", i), b, lambda k: wk[:, k, i * HD:(i + 1) * HD], lambda k: hT[:, k, :], HD, S, KC)
                pe.wait_ge(wq_loaded, 16)
                for i in range(3):
                    fill(("q", i), b, lambda k: hT[:, k, CTX:S], lambda k: wq[:, k, i * 512:(i + 1) * 512], Q, 512, KC)
                for i in range(4):
                    t = ("qT", i)
                    pe.wait_ge(q_ready, b * 3 + min(3, (i * 4 * HD + 4 * HD - 1) // 512 + 1))
                    pe.wait_ge(turns.free(t), turns.count(t, b))
                    for j in range(4):
                        h = 4 * i + j
                        mm = pe.transpose(turns.tile(t)[0:HD, j * Q:(j + 1) * Q], q[:, h * HD:(h + 1) * HD], C.ident[0:Q, 0:Q])
                    mm.then_inc(turns.full(t), 1)
                pe.wait_ge(kT_ready, b + 1)
                pe.wait_ge(v_ready, b + 1)
                for step in range(H + 3):
                    h = step
                    if h < H:
                        t = ("S", h)
                        pe.wait_ge(qT_ready, b * 4 + (h // 4 + 1))
                        pe.wait_ge(turns.free(t), turns.count(t, b))
                        pe.matmul(turns.tile(t)[0:Q, 0:S], qT[:, h, :], kT[:, h // G, :], start=True, stop=True)\
                          .then_inc(turns.full(t), 1)
                    h = step - 2
                    if 0 <= h < H:
                        t = ("pT", h)
                        pe.wait_ge(probs_ready, b * H + (h + 1))
                        pe.wait_ge(turns.free(t), turns.count(t, b))
                        for k, (c, n) in enumerate(KT):
                            mm = pe.transpose(turns.tile(t)[0:n, k * Q:(k + 1) * Q], pr[:, h % 2, c:c + n], C.ident[0:Q, 0:Q])
                        mm.then_inc(turns.full(t), 1)
                    h = step - 3
                    if h >= 0:
                        t = ("o", h // G)
                        pe.wait_ge(pT_ready, b * H + (h + 1))
                        if h % G == 0:
                            pe.wait_ge(turns.free(t), turns.count(t, b))
                        for k, (c, n) in enumerate(KT):
                            mm = pe.matmul(turns.tile(t)[0:Q, h % G * HD:(h % G + 1) * HD], pT[0:n, h % 2, k, :],
                                           v[0:n, k, h // G * HD:(h // G + 1) * HD], start=(k == 0), stop=(k == len(KT) - 1))
                        mm.then_inc(turns.full(t) if h % G == G - 1 else heads_done, 1)
                for i in range(3):
                    t = ("oT", i)
                    pe.wait_ge(o_ready, b * KV + min(KV, (i * 512 + 511) // (G * HD) + 1))
                    pe.wait_ge(turns.free(t), turns.count(t, b))
                    for j in range(4):
                        c = (4 * i + j) * P
                        mm = pe.transpose(turns.tile(t)[:, j * Q:(j + 1) * Q], o[:, c:c + P], C.ident[0:Q, 0:Q])
                    mm.then_inc(turns.full(t), 1)
                pe.wait_ge(oT_ready, b + 1)
                pe.wait_ge(wo_loaded, 16)
                for i in range(2):
                    fill(("y", i), b, lambda k: oT[:, k, :], lambda k: wo[:, k, i * 512:(i + 1) * 512], Q, 512, OC)

            with pe.Fori(0, B) as b:
                sequence(b)

        @block.scalar
        def _(act):
            with act.Fori(0, PAIRS) as p:
                for s in range(2):
                    b = p * 2 + s

                    def empty(t, dst, src, scale=1.0):
                        act.wait_ge(turns.full(t), turns.count(t, b))
                        act.activation(dst, src, ACT.Copy, scale=scale).then_inc(turns.free(t), 1)

                    norm.root(act, 0, b)
                    for i in range(CTILES):
                        empty(("v", i), v[0:CT, i, :], turns.tile(("v", i))[0:CT, 0:DK])
                        if i == 1:
                            points.squares(act, b, 0, 0)
                    copy_turned(act, turns, hT[:, :, CTX:S], "zT", 0, b, zT_ready)
                    empty(("v", 3), v[0:Q, 3, :], turns.tile(("v", 3))[0:Q, 0:DK])
                    act.drain().then_inc(v_ready, 1)
                    for i in range(KV):
                        empty(("k", i), kT[:, i, :], turns.tile(("k", i))[0:HD, 0:S])
                        points.squares(act, b, 0, i + 1)
                    act.drain().then_inc(kT_ready, 1)
                    for i in range(3):
                        empty(("q", i), q[:, i * 512:(i + 1) * 512], turns.tile(("q", i))[0:Q, :], scale=SCALE)
                        act.drain().then_inc(q_ready, 1)
                    act.sem_inc(hT_free, 1)
                    for i in range(4):
                        empty(("qT", i), qT[:, 4 * i:4 * i + 4, :],
                              turns.tile(("qT", i))[0:HD, 0:4 * Q].rearrange("p (j q) -> p j q", j=4))
                        act.drain().then_inc(qT_ready, 1)
                    for h in range(H):
                        t = ("S", h)
                        act.wait_ge(max_ready, b * H + (h + 1))
                        if h >= 2:
                            act.wait_ge(turns.full(("pT", h - 2)), turns.count(("pT", h - 2), b))
                        act.activation(pr[:, h % 2, :], turns.tile(t)[0:Q, 0:S], ACT.Exp, bias=nmax[:, h:h + 1],
                                       accum_out=rsum[:, h:h + 1]).then_inc(turns.free(t), 1)
                        act.drain().then_inc(probs_ready, 1)
                    points.store(act, b)
                    for i in range(3):
                        empty(("oT", i), oT[:, 4 * i:4 * i + 4, :],
                              turns.tile(("oT", i))[:, 0:4 * Q].rearrange("p (j q) -> p j q", j=4))
                    act.drain().then_inc(oT_ready, 1)
                    for i in range(2):
                        empty(("y", i), y[:, i * 512:(i + 1) * 512], turns.tile(("y", i))[0:Q, :],
                              scale=C.gates[0:Q, gate:gate + 1])
                    act.drain().then_inc(y_ready, 1)
                    act.wait_ge(x_done, b + 1)
                    act.dma_start(x_out[b], x[:, s, :]).then_inc(x_stored[s], 16)

        @block.vector
        def _(dve):
            dve.sem_inc(hT_free, 1)
            points.credits(dve)
            with dve.Fori(0, PAIRS) as p:
                for s in range(2):
                    b = p * 2 + s
                    dve.wait_ge(x_loaded[s], p * 16 + 16)
                    norm.statistics(dve, x[:, s, :], 0)
                    norm.scale(dve, x[:, s, :], z[:], 0, b).then_inc(z_ready, 1)
                    points.begin(dve, b, 0, b)
                    for i in range(5):
                        points.sort(dve, b, 0, i)
                    for step in range(H + 3):
                        h = step
                        if h < H:
                            t = ("S", h)
                            dve.wait_ge(turns.full(t), turns.count(t, b))
                            dve.tensor_reduce(nmax[:, h:h + 1], turns.tile(t)[0:Q, 0:S], AX, ALU.max, negate=True)\
                               .then_inc(max_ready, 1)
                        h = step - 2
                        if 0 <= h < H:
                            t = ("pT", h)
                            dve.wait_ge(turns.full(t), turns.count(t, b))
                            if h >= 2:
                                g = h - 2
                                if g % G == G - 1:
                                    dve.wait_ge(turns.full(("o", g // G)), turns.count(("o", g // G), b))
                                else:
                                    dve.wait_ge(heads_done, b * (H - KV) + (g - g // G + 1))
                            dve.tensor_copy(pT[0:CT, h % 2, 0:3, :], turns.tile(t)[0:CT, 0:3 * Q].rearrange("p (k q) -> p k q", k=3))
                            dve.tensor_copy(pT[0:Q, h % 2, 3, :], turns.tile(t)[0:Q, 3 * Q:4 * Q]).then_inc(turns.free(t), 1)
                            dve.drain().then_inc(pT_ready, 1)
                        h = step - 3
                        if h >= 0 and h % G == G - 1:
                            g = h // G
                            t = ("o", g)
                            dve.reciprocal(rsum[:, g * G:(g + 1) * G], rsum[:, g * G:(g + 1) * G])
                            dve.drain()
                            dve.wait_ge(turns.full(t), turns.count(t, b))
                            dve.tensor_tensor(o[:, g * G * HD:(g + 1) * G * HD].rearrange("q (h d) -> q h d", h=G),
                                              turns.tile(t)[0:Q, 0:G * HD].rearrange("q (h d) -> q h d", h=G),
                                              rsum[:, g * G:(g + 1) * G].unsqueeze(2).broadcast_to([Q, G, HD]), ALU.mult)\
                               .then_inc(turns.free(t), 1)
                            dve.drain().then_inc(o_ready, 1)


def grouped_attention(nc, C, banks, gate, x_in, x_out, A, wall, scales, codes):
    HD, QUADS = 32, 8
    DKV = 256
    SCALE = float(HD) ** -0.5
    with ExitStack() as ctx:
        s_ = Scope(nc, ctx, "grouped")
        wq, wo = s_.sb("wq", [P, KC, D]), s_.sb("wo", [P, KC, D])
        wk, wv = s_.sb("wk", [P, KC, DKV]), s_.sb("wv", [P, KC, DKV])
        x, z = s_.sb("x", [Q, 2, D]), s_.sb("z", [Q, D])
        zT, qT = (s_.sb(n, [P, KC, Q]) for n in ("zT", "qT"))
        oT = zT
        cT = s_.sb("ctxT", [P, 2, KC, CTX])
        kT, v = s_.sb("kT", [P, 2, CTX]), s_.sb("v", [CT, CTILES, DKV])
        pr, pT = s_.sb("probs", [Q, 3, 4, CTX]), s_.sb("probsT", [CT, 2, CTILES, 4, Q])
        q = pr[:, 0].rearrange("q j n -> q (j n)")[:, 0:D]
        nmax, rsum = s_.sb("nmax", [Q, QUADS, 4]), s_.sb("rsum", [Q, QUADS, 4])
        raw, rounded, code = s_.sb("raw", [P, 2, 4 * D]), s_.sb("rounded", [P, 2, D], BF16), s_.sb("code", [P, 2, 4 * D], FP8)
        scale, rscale = s_.sb("scale", [P, 2, 4]), s_.sb("rscale", [P, 2, 4])
        raw_loaded = [s_.sem(f"raw_loaded{i}") for i in range(2)]
        code_stored = [s_.sem(f"code_stored{i}") for i in range(2)]
        raw_free, rounded_ready, code_ready = s_.sem("raw_free"), s_.sem("rounded_ready"), s_.sem("code_ready")
        norm = Norm(s_, 1)
        wkv_loaded, wq_loaded, wo_loaded = s_.sem("wkv_loaded"), s_.sem("wq_loaded"), s_.sem("wo_loaded")
        x_loaded = [s_.sem(f"x_loaded{i}") for i in range(2)]
        x_stored = [s_.sem(f"x_stored{i}") for i in range(2)]
        ctx_loaded = [s_.sem(f"ctx_loaded{i}") for i in range(2)]
        ctx_free = [s_.sem(f"ctx_free{i}") for i in range(2)]
        z_ready, zT_ready, v_ready, q_ready, qT_ready = (
            s_.sem(n) for n in ("z_ready", "zT_ready", "v_ready", "q_ready", "qT_ready"))
        last_ready = s_.sem("last_ready")
        passed = s_.sem("passed")
        max_ready, exp_ready, sum_ready, probs_ready, pT_ready, heads_done, oT_ready, x_done = (
            s_.sem(n) for n in ("max_ready", "exp_ready", "sum_ready", "probs_ready", "pT_ready", "heads_done", "oT_ready", "x_done"))
        order = [(("k", i), i) for i in range(2)] + [(("zT", 0, i), 5 + i) for i in range(2)] + [(("v", 0), 4)]
        order += [(("w", 0, 0), 3), (("w", 0, 1), 7), (("q", 0, 0), 0), (("w", 0, 2), 3), (("w", 0, 3), 7), (("q", 0, 1), 1)]
        order += [(("w", 1, 0), 3), (("w", 1, 1), 7), (("v", 1), 5), (("w", 1, 2), 6), (("w", 1, 3), 7)]
        order += [(("qT", 0, i), 2 + i) for i in range(2)] + [(("v", 2), 6)]
        order += [(("w", 2, i), (4, 7, 5, 7)[i]) for i in range(4)]
        for m in range(QUADS + 3):
            if m < QUADS:
                order += [(("S", m, j), j) for j in range(4)]
            if 2 <= m < QUADS + 2:
                order += [(("pT", m - 2, k), 4 + k) for k in range(CTILES)]
            if m >= 3 and (m - 3) % 4 == 0:
                order.append((("o", (m - 3) // 4), 7))
        order += [(("y", 0, i), 6 - i) for i in range(2)]
        turns = Turns(banks, order, B)
        block = ctx.enter_context(nc.Block())

        def unit(p, s, n):
            i = 3 * s + n
            return i % 2, p * 3 + i // 2, (p * 4 + (2 * s + n) if n < 2 else p * 2 + (16 + s))

        def every(eng, sequence):
            with eng.Fori(0, PAIRS - 1) as p:
                for s in range(2):
                    sequence(p, s, False)
            for s in range(2):
                sequence(PAIRS - 1, s, s == 1)

        @block.sync
        def _(sp):
            sp.dma_start(wk[:], fold(A["L2_xattn_Wk"])).then_inc(wkv_loaded, 16)
            sp.dma_start(cT[:, 0], A["ctxT"][0].rearrange("(k p) n -> p k n", p=P)).then_inc(ctx_loaded[0], 16)
            sp.dma_start(wv[:], fold(A["L2_xattn_Wv"])).then_inc(wkv_loaded, 16)
            for s in range(2):
                sp.dma_start(x[:, s, :], x_in[s]).then_inc(x_loaded[s], 16)
            sp.dma_start(wq[:], fold(A["L2_xattn_Wq"])).then_inc(wq_loaded, 16)
            sp.dma_start(cT[:, 1], A["ctxT"][1].rearrange("(k p) n -> p k n", p=P)).then_inc(ctx_loaded[1], 16)
            sp.dma_start(wo[:], fold(A["L2_xattn_Wo"])).then_inc(wo_loaded, 16)

            def sequence(p, s, last):
                for n in range(3):
                    slot, turn, u = unit(p, s, n)
                    sp.wait_ge(code_ready, p * 6 + (3 * s + n + 1))
                    sp.dma_start(codes[u], code[:, slot, :].bitcast(U32)).then_inc(code_stored[slot], 16)
                    sp.dma_start(scales[u], scale[:, slot, :]).then_inc(code_stored[slot], 16)
                more = not isinstance(p, int)
                if more:
                    sp.wait_ge(ctx_free[s], p + 1)
                    sp.dma_start(cT[:, s], A["ctxT"][p * 2 + (s + 2)].rearrange("(k p) n -> p k n", p=P)).then_inc(ctx_loaded[s], 16)
                sp.wait_ge(x_done, p * 2 + (s + 1))
                sp.dma_start(x_out[p * 2 + s], x[:, s, :]).then_inc(x_stored[s], 16)
                sp.wait_ge(x_stored[s], p * 16 + 16)
                if more:
                    sp.dma_start(x[:, s, :], x_in[p * 2 + (s + 2)]).then_inc(x_loaded[s], 16)

            every(sp, sequence)
            for i in range(2):
                sp.wait_ge(code_stored[i], 32 * 3 * PAIRS + 32)

        @block.tensor
        def _(pe):
            pe.wait_ge(wkv_loaded, 32)

            def fill(t, b, lhsT, rhs, m, n, chunks):
                pe.wait_ge(turns.free(t), turns.count(t, b))
                for k in range(chunks):
                    mm = pe.matmul(turns.tile(t)[0:m, 0:n], lhsT(k), rhs(k), start=(k == 0), stop=(k == chunks - 1))
                mm.then_inc(turns.full(t), 1)

            def turned(p, s, n, first, last):
                for i in range(first, last):
                    t = ("w", n, i)
                    pe.wait_ge(rounded_ready, (p * 6 + (3 * s + n)) * 4 + (i + 1))
                    pe.wait_ge(turns.free(t), turns.count(t, p * 2 + s))
                    o = turns.tile(t)[:].bitcast(BF16)
                    for k in range(KC):
                        mm = pe.transpose(o[:, k * P:(k + 1) * P], rounded[:, i % 2, k * P:(k + 1) * P], C.identb[:])
                    mm.then_inc(turns.full(t), 1)

            with pe.Fori(0, PAIRS) as p:
                for s in range(2):
                    b = p * 2 + s
                    pe.wait_ge(ctx_loaded[s], p * 16 + 16)
                    for i in range(2):
                        fill(("k", i), b, lambda k: wk[:, k, i * P:(i + 1) * P], lambda k: cT[:, s, k, :], P, CTX, KC)

                    def values(i):
                        fill(("v", i), b, lambda k: cT[:, s, k, i * CT:(i + 1) * CT], lambda k: wv[:, k, :], CT, DKV, KC)

                    pe.wait_ge(z_ready, b + 1)
                    turn_rows(pe, C, turns, z, "zT", 0, b)
                    values(0)
                    turned(p, s, 0, 0, 2)
                    pe.wait_ge(zT_ready, b + 1)
                    pe.wait_ge(wq_loaded, 16)
                    for i in range(2):
                        fill(("q", 0, i), b, lambda k: zT[:, k, :], lambda k: wq[:, k, i * 512:(i + 1) * 512], Q, 512, KC)
                        turned(p, s, i, 2 * (1 - i), 2 * (1 - i) + 2)
                    values(1)
                    turned(p, s, 1, 2, 4)
                    pe.wait_ge(q_ready, b + 1)
                    turn_rows(pe, C, turns, q, "qT", 0, b)
                    values(2)
                    turned(p, s, 2, 0, 4)
                    pe.wait_ge(qT_ready, b + 1)
                    for step in range(QUADS + 3):
                        m = step
                        if m < QUADS:
                            for j in range(4):
                                t = ("S", m, j)
                                r = slice(j * HD, (j + 1) * HD)
                                pe.wait_ge(turns.free(t), turns.count(t, b))
                                pe.matmul(turns.tile(t)[0:Q, 0:CTX], qT[r, m, :], kT[r, m // 4, :], start=True, stop=True)\
                                  .then_inc(turns.full(t), 1)
                        m = step - 2
                        if 0 <= m < QUADS:
                            pe.wait_ge(probs_ready, (b * QUADS + (m + 1)) * 4)
                            for k in range(CTILES):
                                t = ("pT", m, k)
                                pe.wait_ge(turns.free(t), turns.count(t, b))
                                for j in range(4):
                                    mm = pe.transpose(turns.tile(t)[0:CT, j * Q:(j + 1) * Q], pr[:, m % 3, j, k * CT:(k + 1) * CT],
                                                      C.ident[0:Q, 0:Q])
                                mm.then_inc(turns.full(t), 1)
                        m = step - 3
                        if m >= 0:
                            t = ("o", m // 4)
                            pe.wait_ge(pT_ready, b * QUADS + (m + 1))
                            pe.wait_ge(last_ready, b * QUADS + (m + 1))
                            if m == 0:
                                pe.wait_ge(v_ready, b + 1)
                            if m % 4 == 0:
                                pe.wait_ge(turns.free(t), turns.count(t, b))
                            for k in range(CTILES):
                                for j in range(4):
                                    g = 4 * (m // 4) + j
                                    mm = pe.matmul(turns.tile(t)[j * HD:(j + 1) * HD, (m % 4) * Q:(m % 4 + 1) * Q],
                                                   v[:, k, g * HD:(g + 1) * HD], pT[:, m % 2, k, j, :],
                                                   start=(k == 0), stop=(k == CTILES - 1))
                            mm.then_inc(turns.full(t) if m % 4 == 3 else heads_done, 1)
                    pe.wait_ge(oT_ready, b * 2 + 2)
                    pe.wait_ge(wo_loaded, 16)
                    project(pe, turns, oT, wo, "y", 0, b)

        @block.scalar
        def _(act):
            for i in range(2):
                act.sem_inc(code_stored[i], 32)
            norm.root(act, 0, 0)

            def sequence(p, s, last):
                b = p * 2 + s

                def coded(n, first, last):
                    slot, turn, _ = unit(p, s, n)
                    if first == 0:
                        act.wait_ge(code_stored[slot], turn * 32 + 32)
                    for i in range(first, last):
                        t = ("w", n, i)
                        act.wait_ge(turns.full(t), turns.count(t, b))
                        act.sem_inc(passed, 1)
                        o = code[:, slot, :].rearrange("p (k i c) -> p k i c", i=4, c=P)[:, :, i, :] if n < 2 else \
                            code[:, slot, i * D:(i + 1) * D].rearrange("p (k c) -> p k c", c=P)
                        act.copy(o, turns.tile(t)[:].bitcast(BF16).rearrange("p (k c) -> p k c", c=P), saturate=False)\
                           .then_inc(turns.free(t), 1)
                    if last == 4:
                        act.drain().then_inc(code_ready, 1)

                def empty(t, dst, src, scale=1.0):
                    act.wait_ge(turns.full(t), turns.count(t, b))
                    act.activation(dst, src, ACT.Copy, scale=scale).then_inc(turns.free(t), 1)

                for i in range(2):
                    empty(("k", i), kT[:, i, :], turns.tile(("k", i))[:, 0:CTX])
                copy_turned(act, turns, zT, "zT", 0, b, zT_ready)

                def values(i):
                    empty(("v", i), v[:, i, :], turns.tile(("v", i))[0:CT, 0:DKV])

                values(0)
                coded(0, 0, 2)
                for i in range(2):
                    empty(("q", 0, i), q[:, i * 512:(i + 1) * 512], turns.tile(("q", 0, i))[0:Q, :], scale=SCALE)
                    if i == 1:
                        act.drain().then_inc(q_ready, 1)
                    coded(i, 2 * (1 - i), 2 * (1 - i) + 2)
                values(1)
                coded(1, 2, 4)
                copy_turned(act, turns, qT, "qT", 0, b, qT_ready)
                values(2)
                act.drain().then_inc(v_ready, 1)
                act.sem_inc(ctx_free[s], 1)
                coded(2, 0, 4)

                def last_tile(m):
                    t = ("pT", m, 2)
                    act.wait_ge(turns.full(t), turns.count(t, b))
                    if m >= 2:
                        if m == 5:
                            act.wait_ge(turns.full(("o", 0)), turns.count(("o", 0), b))
                        else:
                            act.wait_ge(heads_done, b * 6 + (m - 1 - (m > 5)))
                    act.activation(pT[:, m % 2, 2, :, :], turns.tile(t)[0:CT, 0:4 * Q].rearrange("p (j q) -> p j q", j=4),
                                   ACT.Copy).then_inc(turns.free(t), 1)
                    act.drain().then_inc(last_ready, 1)

                def outputs(g):
                    empty(("o", g), oT[:, 4 * g:4 * g + 4, :],
                          turns.tile(("o", g))[:, 0:4 * Q].rearrange("p (m q) -> p m q", m=4))
                    act.drain().then_inc(oT_ready, 1)

                for m in range(QUADS + 2):
                    if m < QUADS:
                        for j in range(4):
                            t = ("S", m, j)
                            act.wait_ge(max_ready, (b * QUADS + m) * 4 + (j + 1))
                            if m >= 3 and j == 0:
                                u = ("pT", m - 3, 2)
                                act.wait_ge(turns.full(u), turns.count(u, b))
                            act.activation(pr[:, m % 3, j, :], turns.tile(t)[0:Q, 0:CTX], ACT.Exp, bias=nmax[:, m, j:j + 1],
                                           accum_out=rsum[:, m, j:j + 1]).then_inc(turns.free(t), 1)
                        act.drain().then_inc(exp_ready, 1)
                    if m >= 2:
                        last_tile(m - 2)
                    if m == 7:
                        outputs(0)
                if not last:
                    norm.root(act, 0, b + 1)
                outputs(1)

            every(act, sequence)

        @block.gpsimd
        def _(pool):
            for i in range(2):
                pool.dma_start(raw[:, i], wall[i]).then_inc(raw_loaded[i], 16)

            def sequence(p, s, last):
                b = p * 2 + s
                for n in range(3):
                    after = 3 * s + n + 2
                    if isinstance(p, int) and after >= 6:
                        continue
                    slot, _, u = unit(p + after // 6, after // 3 % 2, after % 3)
                    pool.wait_ge(raw_free, p * 6 + (3 * s + n + 1))
                    pool.dma_start(raw[:, slot], wall[u]).then_inc(raw_loaded[slot], 16)
                for m in range(QUADS):
                    pool.wait_ge(sum_ready, b * QUADS + (m + 1))
                    pool.sem_inc(passed, 1)
                    for j in range(4):
                        pool.tensor_scalar(pr[:, m % 3, j, :], pr[:, m % 3, j, :], rsum[:, m, j:j + 1], 1.0, ALU.mult, ALU.mult)\
                            .then_inc(probs_ready, 1)

            every(pool, sequence)

        @block.vector
        def _(dve):
            def rounding(p, s, n):
                slot, turn, _ = unit(p, s, n)
                m = 4 if n < 2 else 1
                sc, rs = scale[:, slot, 0:m], rscale[:, slot, 0:m]
                dve.wait_ge(raw_loaded[slot], turn * 16 + 16)
                dve.wait_ge(code_stored[slot], turn * 32 + 32)
                dve.tensor_reduce(sc, raw[:, slot, :].rearrange("p (r w) -> p r w", r=m), AX, ALU.max, apply_absolute_value=True)
                dve.drain()
                divide(dve, sc, rs, 7.0)
                dve.tensor_scalar(sc, sc, 1e-8, None, ALU.max)
                dve.drain()
                dve.reciprocal(rs, sc)
                dve.drain()
                for i in range(4):
                    v = raw[:, slot, i * D:(i + 1) * D]
                    dve.tensor_scalar(v, v, rscale[:, slot, i % m:i % m + 1], MAGIC, ALU.mult, ALU.add)
                dve.drain()
                for i in range(4):
                    if i >= 2 or n >= 1:
                        t = ("w", n, i - 2) if i >= 2 else ("w", n - 1, i + 2)
                        dve.wait_ge(turns.full(t), turns.count(t, p * 2 + s))
                    op = dve.tensor_scalar(rounded[:, i % 2, :], raw[:, slot, i * D:(i + 1) * D], MAGIC, 7.0, ALU.subtract, ALU.min)
                    op.then_inc(rounded_ready, 1)
                dve.drain().then_inc(raw_free, 1)

            def normalised(p, s, b):
                dve.wait_ge(x_loaded[s], p * 16 + 16)
                norm.statistics(dve, x[:, s, :], 0)
                norm.scale(dve, x[:, s, :], z[:], 0, b).then_inc(z_ready, 1)

            dve.memset(scale[:], 1.0)
            dve.drain()
            normalised(0, 0, 0)

            def sequence(p, s, last):
                b = p * 2 + s
                for n in range(3):
                    rounding(p, s, n)
                for step in range(QUADS + 2):
                    m = step
                    if m < QUADS:
                        for j in range(4):
                            t = ("S", m, j)
                            dve.wait_ge(turns.full(t), turns.count(t, b))
                            dve.tensor_reduce(nmax[:, m, j:j + 1], turns.tile(t)[0:Q, 0:CTX], AX, ALU.max, negate=True)\
                               .then_inc(max_ready, 1)
                        dve.wait_ge(exp_ready, b * QUADS + (m + 1))
                        dve.reciprocal(rsum[:, m, :], rsum[:, m, :]).then_inc(sum_ready, 1)
                    m = step - 2
                    if m >= 0:
                        if m >= 2:
                            if m == 5:
                                dve.wait_ge(turns.full(("o", 0)), turns.count(("o", 0), b))
                            else:
                                dve.wait_ge(heads_done, b * 6 + (m - 1 - (m > 5)))
                        for k in range(2):
                            t = ("pT", m, k)
                            dve.wait_ge(turns.full(t), turns.count(t, b))
                            dve.tensor_copy(pT[:, m % 2, k, :, :], turns.tile(t)[0:CT, 0:4 * Q].rearrange("p (j q) -> p j q", j=4))\
                               .then_inc(turns.free(t), 1)
                        dve.drain().then_inc(pT_ready, 1)
                if not last:
                    normalised(p + s, 1 - s, b + 1)
                for i in range(2):
                    t = ("y", 0, i)
                    c = slice(i * 512, (i + 1) * 512)
                    dve.wait_ge(turns.full(t), turns.count(t, b))
                    dve.scalar_tensor_tensor(out=x[:, s, c], in0=turns.tile(t)[0:Q, :], scalar=C.gates[0:Q, gate:gate + 1],
                                             in1=x[:, s, c], op0=ALU.mult, op1=ALU.add).then_inc(turns.free(t), 1)
                dve.drain().then_inc(x_done, 1)

            every(dve, sequence)


def hadamard_ffn(nc, C, banks, gate, x_in, x_out, A, scales, codes):
    F, NF, STEPS = 4096, 32, 8
    G = NF // STEPS
    SPLIT = 80
    with ExitStack() as ctx:
        s_ = Scope(nc, ctx, "ffn")
        wgu, wd = s_.sb("wgu", [P, 16, F], FP8), s_.sb("wd", [P, 8, F], FP8)
        sgu, sd = s_.sb("sgu", [P, 16, 4]), s_.sb("sd", [P, 8, 4])
        had = s_.sb("had", [P, P])
        sdb = s_.sb("sdb", [Q, D])
        x, z = s_.sb("x", [Q, 2, D]), s_.sb("z", [Q, D])
        ha, hb = s_.sb("ha", [Q, F]), s_.sb("hb", [Q, F])
        y = s_.sb("y", [Q, 512])
        q, hq = s_.sb("q", [Q, D], BF16), s_.sb("hq", [Q, F], BF16)
        qT, hqT = s_.sb("qT", [P, KC, Q], BF16), s_.sb("hqT", [P, NF, Q], BF16)
        h = s_.sb("h", [P, NF, Q])
        gs, sl, us = (s_.sb(n, [P, 2, G, Q]) for n in ("gs", "sl", "us"))
        sxb = s_.sb("sxb", [P, Q])
        sx, rsx, rsh, sh = (*(s_.sb(n, [Q, 1]) for n in ("sx", "rsx", "rsh")), s_.sb("sh", [Q, 2]))
        norm = Norm(s_, 1)
        gu_loaded, wd_loaded, sdb_ready, z_loaded = (s_.sem(n) for n in ("gu_loaded", "wd_loaded", "sdb_ready", "z_loaded"))
        passed = s_.sem("passed")
        x_loaded = [s_.sem(f"x_loaded{i}") for i in range(2)]
        x_stored = [s_.sem(f"x_stored{i}") for i in range(2)]
        q_ready, qT_ready, gs_ready, sl_ready, us_ready, h_ready = (
            s_.sem(n) for n in ("q_ready", "qT_ready", "gs_ready", "sl_ready", "us_ready", "h_ready"))
        ha_ready, ha_free, sum_ready, diff_ready, hq_ready, hqT_ready, x_done = (
            s_.sem(n) for n in ("ha_ready", "ha_free", "sum_ready", "diff_ready", "hq_ready", "hqT_ready", "x_done"))
        prep = Turns(banks, [(("sd", i), 6 + i) for i in range(2)], 1)
        order = [("xT", 0), ("sx", 1)]
        for j in range(STEPS):
            order += [(("g", j), 2 * (j % 2)), (("u", j), 2 * (j % 2) + 1)]
        ahead = Turns(banks, order, B)
        turns = Turns(banks, [(("h", i), 4 + i % 2) for i in range(8)], B)
        behind = Turns(banks, [(("hT", i), 6 + i % 2) for i in range(4)] + [(("y", i), 6 + i) for i in range(2)], B)
        block = ctx.enter_context(nc.Block())

        def rounds(eng, sequence):
            sequence(0, 0, 0, True, True, True)
            with eng.Fori(0, PAIRS - 2) as p:
                for s in range(2):
                    sequence(p * 2 + (1 + s), 1 - s, p + s, False, True, True)
            for b in range(B - 3, B):
                sequence(b, b % 2, b // 2, False, b + 1 < B, b + 2 < B)

        @block.sync
        def _(sp):
            sp.dma_start(z[:], x_in[0]).then_inc(z_loaded, 16)
            sp.dma_start(sgu[:], scales[0:16].rearrange("u p r -> p u r")).then_inc(gu_loaded, 16)
            for i in range(4):
                sp.dma_start(wgu[:, 4 * i:4 * i + 4, :].bitcast(U32), codes[4 * i:4 * i + 4].rearrange("u p w -> p u w"))\
                  .then_inc(gu_loaded, 16)
            sp.dma_start(had[:], A["hadamard"]).then_inc(wd_loaded, 16)
            sp.dma_start(sd[:], scales[16:24].rearrange("u p r -> p u r")).then_inc(wd_loaded, 16)
            sp.dma_start(wd[:].bitcast(U32), codes[16:24].rearrange("u p w -> p u w")).then_inc(wd_loaded, 16)
            for s in range(2):
                sp.dma_start(x[:, s, :], x_in[s]).then_inc(x_loaded[s], 16)
            sp.wait_ge(q_ready, 1)
            sp.dma_start(z[:], x_in[1]).then_inc(z_loaded, 16)

            def store(b, slot, turn):
                sp.wait_ge(x_done, b + 1)
                sp.dma_start(x_out[b], x[:, slot, :]).then_inc(x_stored[slot], 16)
                sp.wait_ge(x_stored[slot], turn * 16 + 16)

            def sequence(b, slot, turn, first, gate_up, quantise):
                if quantise:
                    sp.wait_ge(q_ready, b + 2)
                    sp.dma_start(z[:], x_in[b + 2]).then_inc(z_loaded, 16)
                if not first:
                    store(b - 1, 1 - slot, turn + (slot - 1))
                    if gate_up:
                        sp.dma_start(x[:, 1 - slot, :], x_in[b + 1]).then_inc(x_loaded[1 - slot], 16)

            rounds(sp, sequence)
            store(B - 1, 1, PAIRS - 1)

        @block.tensor
        def _(pe):
            def entered(b):
                t = "xT"
                pe.wait_ge(q_ready, b + 1)
                pe.wait_ge(ahead.free(t), ahead.count(t, b))
                o = ahead.tile(t)[:].bitcast(BF16)
                for k in range(KC):
                    mm = pe.transpose(o[:, k * Q:(k + 1) * Q], q[:, k * P:(k + 1) * P], C.identb[0:Q, 0:Q])
                mm.then_inc(ahead.full(t), 1)
                t = "sx"
                pe.wait_ge(ahead.free(t), ahead.count(t, b))
                pe.matmul(ahead.tile(t)[:, 0:Q], sx[:].broadcast_to([Q, P]), C.ident[0:Q, 0:Q], start=True, stop=True)\
                  .then_inc(ahead.full(t), 1)

            def gate_and_up(b, between=lambda j: None):
                pe.wait_ge(qT_ready, b + 1)
                for j in range(STEPS):
                    between(j)
                    for name, u0 in (("g", 0), ("u", 8)):
                        t = (name, j)
                        pe.wait_ge(ahead.free(t), ahead.count(t, b))
                        pe.sem_inc(passed, 1)
                        for i in range(G):
                            f = G * j + i
                            for k in range(KC):
                                c = (k * 4 + f % 4) * P
                                mm = pe.matmul(ahead.tile(t)[:, i * Q:(i + 1) * Q], wgu[:, u0 + f // 4, c:c + P], qT[:, k, :],
                                               start=(k == 0), stop=(k == KC - 1))
                        mm.then_inc(ahead.full(t), 1)

            pe.wait_ge(gu_loaded, 16 * 5)
            entered(0)
            gate_and_up(0)
            pe.wait_ge(wd_loaded, 16 * 3)
            for i in range(2):
                t = ("sd", i)
                pe.wait_ge(prep.free(t), prep.count(t, 0))
                for u in range(4):
                    mm = pe.matmul(prep.tile(t)[0:Q, u * P:(u + 1) * P], sd[:, 4 * i + u, 0:1].broadcast_to([P, Q]), C.ident[:],
                                   start=True, stop=True)
                mm.then_inc(prep.full(t), 1)

            def turned(b):
                pe.wait_ge(hq_ready, b + 1)
                for i in range(4):
                    t = ("hT", i)
                    pe.wait_ge(behind.free(t), behind.count(t, b))
                    o = behind.tile(t)[:].bitcast(BF16)
                    for c in range(8):
                        mm = pe.transpose(o[:, c * Q:(c + 1) * Q], hq[:, (8 * i + c) * P:(8 * i + c + 1) * P], C.identb[0:Q, 0:Q])
                    mm.then_inc(behind.full(t), 1)

            def down(b, i):
                if i == 0:
                    pe.wait_ge(hqT_ready, b + 1)
                t = ("y", i)
                pe.wait_ge(behind.free(t), behind.count(t, b))
                pe.sem_inc(passed, 1)
                for c in range(NF):
                    mm = pe.matmul(behind.tile(t)[0:Q, :], hqT[:, c, :], wd[:, 4 * i:4 * i + 4, c * P:(c + 1) * P],
                                   start=(c == 0), stop=(c == NF - 1))
                mm.then_inc(behind.full(t), 1)

            def sequence(b, slot, turn, first, gate_up, quantise):
                for i in range(8):
                    t = ("h", i)
                    pe.wait_ge(h_ready, b * STEPS + (i + 1))
                    pe.wait_ge(turns.free(t), turns.count(t, b))
                    for c in range(4):
                        mm = pe.matmul(turns.tile(t)[0:Q, c * P:(c + 1) * P], h[:, 4 * i + c, :], had[:], start=True, stop=True)
                    mm.then_inc(turns.full(t), 1)
                if gate_up:
                    entered(b + 1)
                if not first:
                    turned(b - 1)
                if gate_up:
                    gate_and_up(b + 1, lambda j: down(b - 1, j // 3 - 1) if j in (3, 6) and not first else None)
                else:
                    for i in range(2):
                        down(b - 1, i)

            rounds(pe, sequence)
            turned(B - 1)
            for i in range(2):
                down(B - 1, i)

        @block.scalar
        def _(act):
            def entered(b):
                act.wait_ge(ahead.full("xT"), ahead.count("xT", b))
                act.copy(qT[:], ahead.tile("xT")[:].bitcast(BF16)[:, 0:KC * Q].rearrange("p (k q) -> p k q", k=KC))\
                   .then_inc(ahead.free("xT"), 1)
                act.wait_ge(ahead.full("sx"), ahead.count("sx", b))
                if not isinstance(b, int) or b > 0:
                    act.wait_ge(us_ready, b * STEPS)
                act.activation(sxb[:], ahead.tile("sx")[:, 0:Q], ACT.Copy).then_inc(ahead.free("sx"), 1)
                act.drain().then_inc(qT_ready, 1)

            def gate_and_up(b, quantise):
                for j in range(STEPS):
                    if j == STEPS - 1 and quantise:
                        norm.root(act, 0, b + 1)
                    act.wait_ge(gs_ready, b * STEPS + (j + 1))
                    if j >= 2 or not isinstance(b, int) or b > 0:
                        act.wait_ge(h_ready, b * STEPS + (j - 1))
                    for i in range(G):
                        f = G * j + i
                        act.activation(sl[:, j % 2, i, :], gs[:, j % 2, i, :], ACT.Silu, scale=sgu[:, f // 4, f % 4:f % 4 + 1])
                    act.drain().then_inc(sl_ready, 1)

            norm.root(act, 0, 0)
            entered(0)
            gate_and_up(0, True)
            for i in range(2):
                t = ("sd", i)
                act.wait_ge(prep.full(t), prep.count(t, 0))
                act.activation(sdb[:, i * 512:(i + 1) * 512], prep.tile(t)[0:Q, :], ACT.Copy,
                               scale=C.gates[0:Q, gate:gate + 1]).then_inc(prep.free(t), 1)
            act.drain().then_inc(sdb_ready, 1)

            def turned(b):
                for i in range(4):
                    t = ("hT", i)
                    act.wait_ge(behind.full(t), behind.count(t, b))
                    act.copy(hqT[:, 8 * i:8 * i + 8, :], behind.tile(t)[:].bitcast(BF16)[:, 0:8 * Q].rearrange("p (c q) -> p c q", c=8))\
                       .then_inc(behind.free(t), 1)
                act.drain().then_inc(hqT_ready, 1)

            def sequence(b, slot, turn, first, gate_up, quantise):
                act.wait_ge(ha_free, b + 1)
                for i in range(8):
                    t = ("h", i)
                    act.wait_ge(turns.full(t), turns.count(t, b))
                    act.activation(ha[:, i * 512:(i + 1) * 512], turns.tile(t)[0:Q, :], ACT.Copy).then_inc(turns.free(t), 1)
                act.drain().then_inc(ha_ready, 1)
                if gate_up:
                    entered(b + 1)
                if not first:
                    turned(b - 1)
                if gate_up:
                    gate_and_up(b + 1, quantise)

            rounds(act, sequence)
            turned(B - 1)

        def half(v, k):
            w = v.rearrange("q (m two l c) -> q m two l c", two=2, l=1 << k, c=P)
            return w[:, :, 0], w[:, :, 1]

        def sides(k):
            return (ha, hb) if k % 2 == 0 else (hb, ha)

        @block.gpsimd
        def _(pool):
            def product(b, j):
                pool.wait_ge(sl_ready, b * STEPS + (j + 1))
                pool.wait_ge(us_ready, b * STEPS + (j + 1))
                pool.tensor_tensor(h[:, G * j:G * j + G, :], sl[:, j % 2], us[:, j % 2], ALU.mult).then_inc(h_ready, 1)

            for j in range(STEPS):
                product(0, j)

            def sequence(b, slot, turn, first, gate_up, quantise):
                for k in range(5):
                    src, dst = sides(k)
                    (a, c), (_, d) = half(src[:], k), half(dst[:], k)
                    pool.wait_ge(sum_ready, b * 5 + (k + 1))
                    for l in range(1 << k):
                        op = pool.tensor_tensor(d[:, :, l, 0:SPLIT], a[:, :, l, 0:SPLIT], c[:, :, l, 0:SPLIT], ALU.subtract)
                    op.then_inc(diff_ready, 1)
                    if gate_up:
                        product(b + 1, k)
                if gate_up:
                    for j in range(5, STEPS):
                        product(b + 1, j)

            rounds(pool, sequence)

        @block.vector
        def _(dve):
            def reduced(src, scale, rscale, unit):
                dve.tensor_reduce(scale, src, AX, ALU.max, apply_absolute_value=True)
                dve.drain()
                divide(dve, scale, rscale, 7.0)
                dve.tensor_scalar(scale, scale, unit, 1e-8, ALU.mult, ALU.max)
                dve.drain()
                dve.reciprocal(rscale, scale)
                dve.drain()
                if unit != 1.0:
                    dve.tensor_scalar(rscale, rscale, unit, None, ALU.mult)
                    dve.drain()

            def integers(dst, src, rscale):
                dve.tensor_scalar(src, src, rscale, MAGIC, ALU.mult, ALU.add)
                dve.drain()
                return dve.tensor_scalar(dst, src, MAGIC, 7.0, ALU.subtract, ALU.min)

            def statistics(b):
                dve.wait_ge(z_loaded, b * 16 + 16)
                norm.statistics(dve, z[:], 0)

            def quantised(b):
                norm.scale(dve, z[:], z[:], 0, b)
                dve.drain()
                if not isinstance(b, int) or b > 0:
                    dve.wait_ge(ahead.full("sx"), ahead.count("sx", b - 1))
                reduced(z[:], sx[:], rsx[:], 1.0)
                integers(q[:], z[:], rsx[:]).then_inc(q_ready, 1)

            def step(b, j):
                t = ("g", j)
                if j == 0:
                    dve.wait_ge(qT_ready, b + 1)
                dve.wait_ge(ahead.full(t), ahead.count(t, b))
                if j >= 2 or not isinstance(b, int) or b > 0:
                    dve.wait_ge(h_ready, b * STEPS + (j - 1))
                dve.tensor_tensor(gs[:, j % 2], ahead.tile(t)[:, 0:G * Q].rearrange("p (i n) -> p i n", i=G),
                                  sxb[:].unsqueeze(1).broadcast_to([P, G, Q]), ALU.mult).then_inc(ahead.free(t), 1)
                dve.drain().then_inc(gs_ready, 1)
                t = ("u", j)
                dve.wait_ge(ahead.full(t), ahead.count(t, b))
                for i in range(G):
                    f = G * j + i
                    op = dve.scalar_tensor_tensor(out=us[:, j % 2, i, :], in0=ahead.tile(t)[:, i * Q:(i + 1) * Q],
                                                  scalar=sgu[:, 8 + f // 4, f % 4:f % 4 + 1], in1=sxb[:], op0=ALU.mult, op1=ALU.mult)
                op.then_inc(ahead.free(t), 1)
                dve.drain().then_inc(us_ready, 1)

            def butterfly(b, k):
                src, dst = sides(k)
                (a, c), (_, d) = half(src[:], k), half(dst[:], k)
                sa, sb, sc = (v[:].rearrange("q (m two c) -> q m two c", two=2, c=P << k) for v in (src, src, dst))
                dve.tensor_tensor(sc[:, :, 0], sa[:, :, 0], sb[:, :, 1], ALU.add)
                for l in range(1 << k):
                    dve.tensor_tensor(d[:, :, l, SPLIT:P], a[:, :, l, SPLIT:P], c[:, :, l, SPLIT:P], ALU.subtract)

            dve.sem_inc(ha_free, 1)
            statistics(0)
            quantised(0)
            dve.wait_ge(gu_loaded, 16 * 5)
            for j in range(STEPS):
                if j == STEPS - 1:
                    statistics(1)
                step(0, j)
            quantised(1)
            dve.wait_ge(sdb_ready, 1)

            def finished(b, slot, turn, i):
                if i == 0:
                    dve.wait_ge(x_loaded[slot], turn * 16 + 16)
                t = ("y", i)
                c = slice(i * 512, (i + 1) * 512)
                dve.wait_ge(behind.full(t), behind.count(t, b))
                dve.scalar_tensor_tensor(out=y[:], in0=behind.tile(t)[0:Q, :], scalar=sh[:, slot:slot + 1], in1=sdb[:, c],
                                         op0=ALU.mult, op1=ALU.mult).then_inc(behind.free(t), 1)
                dve.drain()
                dve.tensor_tensor(x[:, slot, c], x[:, slot, c], y[:], ALU.add)
                dve.drain()
                if i == 1:
                    dve.sem_inc(x_done, 1)

            def sequence(b, slot, turn, first, gate_up, quantise):
                dve.wait_ge(ha_ready, b + 1)
                dve.sem_inc(sum_ready, 1)
                for k in range(5):
                    butterfly(b, k)
                    if k == 4 and not first:
                        finished(b - 1, 1 - slot, turn + (slot - 1), 0)
                    if gate_up:
                        step(b + 1, k)
                    dve.drain()
                    dve.wait_ge(diff_ready, b * 5 + (k + 1))
                    if k < 4:
                        dve.sem_inc(sum_ready, 1)
                dve.sem_inc(ha_free, 1)
                reduced(hb[:], sh[:, slot:slot + 1], rsh[:], 2.0 ** -6)
                if gate_up:
                    step(b + 1, 5)
                if not first:
                    t = ("hT", 3)
                    dve.wait_ge(behind.full(t), behind.count(t, b - 1))
                integers(hq[:], hb[:], rsh[:]).then_inc(hq_ready, 1)
                if gate_up:
                    step(b + 1, 6)
                if quantise:
                    statistics(b + 2)
                if gate_up:
                    step(b + 1, 7)
                if quantise:
                    quantised(b + 2)
                if not first:
                    finished(b - 1, 1 - slot, turn + (slot - 1), 1)

            rounds(dve, sequence)
            for i in range(2):
                finished(B - 1, 1, PAIRS - 1, i)


def gather_points(nc, C, banks, gate, x_in, x_out, A, nearest):
    K, R, AR = 16, Q // 16, KC * Q // 16
    U = 2 * K
    with ExitStack() as ctx:
        s_ = Scope(nc, ctx, "points")
        x, z = s_.sb("x", [Q, 2, D]), s_.sb("z", [Q, 2, D])
        norm = Norm(s_, 2)
        wcol, sel, wsel = s_.sb("wcol", [Q, 1]), s_.sb("sel", [Q, R]), s_.sb("wsel", [Q, R])
        bias, count, eights = s_.sb("bias", [P, 1]), s_.sb("count", [P, 1]), s_.sb("eights", [P, KC])
        idx = s_.sb("idx", [P, 2, KC, K], U32)
        point, hi, lo = (s_.sb(n, [P, 2, KC, K]) for n in ("point", "hi", "lo"))
        lob = s_.sb("lob", [P, 2, KC, K], BF16)
        mask = s_.sb("mask", [P, 2, KC, K, KC])
        table, rest = s_.sb("table", [P, 2, AR]), s_.sb("rest", [P, 2, AR])
        part = [s_.sb(f"part{i}", [P, 2, AR], BF16) for i in range(3)]
        spread, onehot = s_.sb("spread", [P, 2, D], BF16), s_.sb("onehot", [P, 2, D], BF16)
        kept = s_.sb("kept", [P, 2, KC, KC, R])
        val = s_.sb("val", [P, K, R, KC])
        flat = s_.sb("flat", [AR, 2, P, K])
        back = s_.sb("back", [P, 2, KC, Q])
        flat_dram = nc.dram_tensor("flat", (2, AR, P * K), F32, kind="Internal").ap()
        consts_loaded, wsel_ready = s_.sem("consts_loaded"), s_.sem("wsel_ready")
        passed = s_.sem("passed")
        x_loaded = [s_.sem(f"x_loaded{i}") for i in range(2)]
        x_stored = [s_.sem(f"x_stored{i}") for i in range(2)]
        idx_loaded = [s_.sem(f"idx_loaded{i}") for i in range(2)]
        flat_stored, back_loaded = s_.sem("flat_stored"), s_.sem("back_loaded")
        idx_used, lo_ready, z_ready, table_ready = (s_.sem(n) for n in ("idx_used", "lo_ready", "z_ready", "table_ready"))
        spread_ready, onehot_ready, val_ready, flat_ready, x_done = (
            s_.sem(n) for n in ("spread_ready", "onehot_ready", "val_ready", "flat_ready", "x_done"))
        steps = [("spread", 0), ("spread", 1), ("table", 0)]
        for u in range(U + 2):
            if u + 2 < U:
                steps.append(("spread", u + 2))
            if u == K - 4:
                steps.append(("table", 1))
            if u < U:
                steps.append(("look", u))
            if u >= 2 and (u - 2) % 4 == 3:
                steps.append(("turn", (u - 2) // 4))
            if u == K + 10:
                steps.append(("back", 0))
        steps.append(("back", 1))
        order = []
        for name, i in steps:
            if name == "spread":
                order += [((name, i, h), 2 * (i % 2) + h) for h in range(2)]
            elif name == "look":
                order.append(((name, i), 4 + i % 2))
            elif name == "back":
                order += [((name, i, h), 6 + h) for h in range(2)]
            else:
                order.append(((name, i), 6 + i % 2))
        turns = Turns(banks, order, PAIRS)
        block = ctx.enter_context(nc.Block())

        @block.sync
        def _(sp):
            sp.dma_start(wcol[:], A["L3_xattn_affine_w"]).then_inc(consts_loaded, 16)
            sp.dma_start(sel[:], A["row_mask"]).then_inc(consts_loaded, 16)
            sp.dma_start(bias[:], rows(A["L3_xattn_affine_b"], P)).then_inc(consts_loaded, 16)
            sp.dma_start(count[:], A["count"]).then_inc(consts_loaded, 16)
            sp.dma_start(eights[:], rows(A["eights"], P)).then_inc(consts_loaded, 16)
            for s in range(2):
                sp.dma_start(x[:, s, :], x_in[s]).then_inc(x_loaded[s], 16)

            def sequence(p, s):
                b = p * 2 + s
                sp.wait_ge(flat_ready, b + 1)
                sp.dma_start(flat_dram[s], flat[:, s].rearrange("a n k -> a (n k)")).then_inc(flat_stored, 16)
                sp.wait_ge(flat_stored, b * 16 + 16)
                sp.dma_start(back[:, s].rearrange("p t f -> p (t f)"),
                             flat_dram[s].rearrange("a c -> (a c)").rearrange("(p c) -> p c", p=P)).then_inc(back_loaded, 16)
                sp.wait_ge(x_done, b + 1)
                sp.dma_start(x_out[b], x[:, s, :]).then_inc(x_stored[s], 16)
                sp.wait_ge(x_stored[s], p * 16 + 16)

            with sp.Fori(0, PAIRS - 1) as p:
                for s in range(2):
                    sequence(p, s)
                    sp.dma_start(x[:, s, :], x_in[p * 2 + (s + 2)]).then_inc(x_loaded[s], 16)
            for s in range(2):
                sequence(PAIRS - 1, s)

        @block.gpsimd
        def _(pool):
            with pool.Fori(0, PAIRS) as p:
                for s in range(2):
                    pool.wait_ge(idx_used, p * 2 + (s + 1))
                    pool.dma_start(idx[:, s], nearest[p * 2 + s]).then_inc(idx_loaded[s], 16)

        @block.tensor
        def _(pe):
            pe.wait_ge(wsel_ready, 1)
            with pe.Fori(0, PAIRS) as p:
                for name, i in steps:
                    if name == "spread":
                        s, k = i // K, i % K
                        if k == 0:
                            pe.wait_ge(lo_ready, p * 2 + (s + 1))
                        for h in range(2):
                            t = (name, i, h)
                            pe.wait_ge(turns.free(t), turns.count(t, p))
                            for j in range(4):
                                mm = pe.matmul(turns.tile(t)[:, j * P:(j + 1) * P], lob[:, s, 4 * h + j, k:k + 1].broadcast_to([P, P]),
                                               C.identb[:], start=True, stop=True)
                            mm.then_inc(turns.full(t), 1)
                    elif name == "table":
                        t = (name, i)
                        pe.wait_ge(z_ready, p * 2 + (i + 1))
                        pe.wait_ge(turns.free(t), turns.count(t, p))
                        for a in range(KC):
                            mm = pe.matmul(turns.tile(t)[:, a * R:(a + 1) * R], z[:, i, a * P:(a + 1) * P], wsel[:], start=True, stop=True)
                        mm.then_inc(turns.full(t), 1)
                    elif name == "look":
                        t = (name, i)
                        if i % K == 0:
                            pe.wait_ge(table_ready, p * 2 + (i // K + 1))
                        pe.wait_ge(onehot_ready, p * U + (i + 1))
                        pe.wait_ge(turns.free(t), turns.count(t, p))
                        for j in range(KC):
                            for n in range(3):
                                mm = pe.matmul(turns.tile(t)[:, j * AR:(j + 1) * AR], onehot[:, i % 2, j * P:(j + 1) * P],
                                               part[n][:, i // K, :], start=(n == 0), stop=(n == 2))
                        mm.then_inc(turns.full(t), 1)
                    elif name == "turn":
                        t = (name, i)
                        pe.wait_ge(val_ready, p * U + (4 * i + 4))
                        pe.wait_ge(turns.free(t), turns.count(t, p))
                        pe.sem_inc(passed, 1)
                        for j in range(4):
                            mm = pe.transpose(turns.tile(t)[0:AR, j * P:(j + 1) * P], val[:, (4 * i + j) % K].rearrange("p r t -> p (r t)"),
                                              C.ident[:])
                        mm.then_inc(turns.full(t), 1)
                    else:
                        pe.wait_ge(back_loaded, p * 32 + (16 * i + 16))
                        for h in range(2):
                            t = (name, i, h)
                            pe.wait_ge(turns.free(t), turns.count(t, p))
                            for j in range(4):
                                mm = pe.transpose(turns.tile(t)[0:Q, j * P:(j + 1) * P], back[:, i, 4 * h + j, :], C.ident[:])
                            mm.then_inc(turns.full(t), 1)

        @block.scalar
        def _(act):
            with act.Fori(0, PAIRS) as p:
                norm.root(act, 0, p * 2)
                for name, i in steps:
                    if name == "spread":
                        if i == 6:
                            norm.root(act, 1, p * 2 + 1)
                        if i >= 2:
                            act.wait_ge(onehot_ready, p * U + (i - 1))
                        for h in range(2):
                            t = (name, i, h)
                            act.wait_ge(turns.full(t), turns.count(t, p))
                            act.activation(spread[:, i % 2, h * 512:(h + 1) * 512], turns.tile(t)[:], ACT.Copy).then_inc(turns.free(t), 1)
                        act.drain().then_inc(spread_ready, 1)
                    elif name == "turn":
                        t = (name, i)
                        act.wait_ge(turns.full(t), turns.count(t, p))
                        act.activation(flat[:, i // 4, :, i % 4 * 4:i % 4 * 4 + 4],
                                       turns.tile(t)[0:AR, :].rearrange("a (j n) -> a n j", j=4), ACT.Copy).then_inc(turns.free(t), 1)
                        if i % 4 == 3:
                            act.drain().then_inc(flat_ready, 1)

        @block.vector
        def _(dve):
            dve.sem_inc(idx_used, 2)
            dve.wait_ge(consts_loaded, 80)
            dve.tensor_scalar(wsel[:], sel[:], wcol[:], None, ALU.mult).then_inc(wsel_ready, 1)

            def indices(p, s):
                dve.wait_ge(idx_loaded[s], p * 16 + 16)
                dve.tensor_copy(point[:, s], idx[:, s]).then_inc(idx_used, 1)
                dve.drain()
                dve.tensor_scalar(hi[:, s], point[:, s], 63.5, 1.0 / P, ALU.subtract, ALU.mult)
                dve.drain()
                dve.tensor_scalar(hi[:, s], hi[:, s], MAGIC, MAGIC, ALU.add, ALU.subtract)
                dve.drain()
                dve.scalar_tensor_tensor(out=lob[:, s], in0=hi[:, s], scalar=-float(P), in1=point[:, s], op0=ALU.mult, op1=ALU.add)\
                   .then_inc(lo_ready, 1)
                dve.tensor_tensor(mask[:, s].rearrange("p t k a -> p (t k) a"),
                                  hi[:, s].rearrange("p t k -> p (t k)").unsqueeze(2).broadcast_to([P, KC * K, KC]),
                                  eights[:].unsqueeze(1).broadcast_to([P, KC * K, KC]), ALU.is_equal)

            def points(p, s):
                norm.scale(dve, x[:, s, :], z[:, s, :], s, p * 2 + s).then_inc(z_ready, 1)

            def split(p, s):
                t = ("table", s)
                dve.wait_ge(turns.full(t), turns.count(t, p))
                dve.tensor_scalar(table[:, s], turns.tile(t)[:, 0:AR], bias[:], None, ALU.add).then_inc(turns.free(t), 1)
                dve.drain()
                dve.tensor_copy(part[0][:, s], table[:, s])
                dve.drain()
                dve.tensor_tensor(rest[:, s], table[:, s], part[0][:, s], ALU.subtract)
                dve.drain()
                dve.tensor_copy(part[1][:, s], rest[:, s])
                dve.drain()
                dve.tensor_tensor(part[2][:, s], rest[:, s], part[1][:, s], ALU.subtract)
                dve.drain().then_inc(table_ready, 1)

            def keep(p, i):
                t, s, k = ("look", i), i // K, i % K
                dve.wait_ge(turns.full(t), turns.count(t, p))
                dve.tensor_tensor(kept[:, i % 2], turns.tile(t)[:, 0:KC * AR].rearrange("p (t a r) -> p t a r", t=KC, a=KC),
                                  mask[:, s, :, k, :].unsqueeze(3).broadcast_to([P, KC, KC, R]), ALU.mult).then_inc(turns.free(t), 1)
                dve.drain()
                dve.tensor_reduce(val[:, k].rearrange("p r t -> p t r"), kept[:, i % 2].rearrange("p t a r -> p t r a"), AX, ALU.add)\
                   .then_inc(val_ready, 1)

            def update(p, s):
                for h in range(2):
                    t = ("back", s, h)
                    dve.wait_ge(turns.full(t), turns.count(t, p))
                    xs = x[:, s, :].rearrange("f (q j) -> f j q", j=KC)[:, 4 * h:4 * h + 4, :]
                    op = dve.scalar_tensor_tensor(out=xs, in0=turns.tile(t)[0:Q, :].rearrange("f (j q) -> f j q", j=4),
                                                  scalar=C.gates[0:Q, gate:gate + 1], in1=xs, op0=ALU.mult, op1=ALU.add)
                    op.then_inc(turns.free(t), 1)
                dve.drain().then_inc(x_done, 1)

            with dve.Fori(0, PAIRS) as p:
                indices(p, 0)
                dve.wait_ge(x_loaded[0], p * 16 + 16)
                norm.statistics(dve, x[:, 0, :], 0)
                indices(p, 1)
                points(p, 0)
                split(p, 0)
                for i in range(U + 1):
                    if i == 4:
                        dve.wait_ge(x_loaded[1], p * 16 + 16)
                        norm.statistics(dve, x[:, 1, :], 1)
                    if i == 8:
                        points(p, 1)
                    if i == K - 2:
                        split(p, 1)
                    if i < U:
                        dve.wait_ge(spread_ready, p * U + (i + 1))
                        dve.tensor_scalar(onehot[:, i % 2], spread[:, i % 2], count[:], None, ALU.is_equal).then_inc(onehot_ready, 1)
                    if i >= 1:
                        keep(p, i - 1)
                    if i == K + 12:
                        update(p, 0)
                update(p, 1)


NAMES = ["x", "ctx_4096", "g_xattn", "g_ffn", "L0_xattn_Wq", "L0_xattn_Wk", "L0_xattn_Wv", "L0_xattn_Wo",
         "L0_ffn_qweight", "L0_ffn_wparams", "L0_ffn_bias", "L1_xattn_Wq", "L1_xattn_bq", "L1_xattn_Wk",
         "L1_xattn_bk", "L1_ffn_Wq", "L1_ffn_Wr", "L1_ffn_aux_keys", "L1_ffn_aux_values", "L1_ffn_Wvd",
         "L1_ffn_Wvu", "L1_ffn_Wu1", "L1_ffn_bu1", "L1_ffn_Wu2", "L1_ffn_bu2", "L1_ffn_gate_w1",
         "L1_ffn_gate_bias", "L1_ffn_log_rel", "L2_xattn_Wq", "L2_xattn_Wk", "L2_xattn_Wv", "L2_xattn_Wo",
         "L2_ffn_w_gate_up", "L2_ffn_w_down", "L3_xattn_affine_w", "L3_xattn_affine_b", "L3_ffn_gate_w",
         "L3_ffn_lora_A", "L3_ffn_lora_B"]


def layout(a):
    import numpy as np
    out = dict(a)
    for name in ("L0_xattn_Wq", "L0_xattn_Wk", "L0_xattn_Wv", "L0_xattn_Wo", "L0_ffn_qweight", "L1_xattn_Wq",
                 "L1_ffn_Wq", "L1_ffn_Wr", "L1_ffn_aux_keys", "L1_ffn_aux_values", "L1_ffn_Wvd", "L1_ffn_Wvu",
                 "L1_ffn_Wu1", "L3_ffn_gate_w"):
        out[name + "T"] = out.pop(name).T
    out["L1_ffn_WrT"] = np.concatenate([out["L1_ffn_WrT"], np.zeros((64, P - 48), np.float32)], axis=1)
    out["L0_ffn_qweightT"] = np.ascontiguousarray(out["L0_ffn_qweightT"]).view(np.uint32)
    out["ctxT"] = a["ctx_4096"].transpose(0, 2, 1)
    gu = out.pop("L2_ffn_w_gate_up").reshape(16, 4, P, D).transpose(0, 2, 1, 3).reshape(16, P, 4 * D)
    out["L2_weights"] = np.concatenate([gu, out.pop("L2_ffn_w_down").reshape(8, P, 4 * D)])
    out["planes"] = a["ctx_4096"][:, 0:2].reshape(B, 2 * D)
    out["points"] = a["ctx_4096"][:, 0:2].reshape(B, 2, KC, P).transpose(0, 3, 1, 2)
    order = [16 * (m // 4) + 4 * j + m % 4 for m in range(8) for j in range(4)]
    out["L2_xattn_Wq"] = a["L2_xattn_Wq"].reshape(D, 32, 32)[:, order].reshape(D, D)
    out["L2_xattn_Wo"] = a["L2_xattn_Wo"].reshape(32, 32, D)[order].reshape(D, D)
    out["L3_lora_AT"] = out.pop("L3_ffn_lora_A").reshape(512, D).T
    out["L3_lora_BT"] = out.pop("L3_ffn_lora_B").transpose(0, 2, 1).reshape(512, D)
    out["L3_xattn_affine_w"] = np.repeat(a["L3_xattn_affine_w"], 7).reshape(Q, 1)
    for name in ("L1_xattn_bk", "L1_ffn_bu1", "L1_ffn_Wu2"):
        out[name] = a[name].reshape(-1, P).T
    for name in ("L1_ffn_gate_w1", "L1_ffn_gate_bias"):
        out[name] = a[name].reshape(1)
    h = np.ones((1, 1), np.float32)
    while len(h) < P:
        h = np.block([[h, h], [h, -h]]).astype(np.float32)
    out["ident"] = np.eye(P, dtype=np.float32)
    out["hadamard"] = h
    out["row_mask"] = (np.arange(Q)[:, None] % 7 == np.arange(7)[None, :]).astype(np.float32)
    out["eights"] = np.arange(KC, dtype=np.float32)
    out["count"] = np.arange(P, dtype=np.float32).reshape(P, 1)
    return {n: np.ascontiguousarray(v) for n, v in out.items()}


def program(nc, A, x_in, x_out):
    with ExitStack() as ctx:
        banks = Banks(nc, ctx)
        C = Consts(nc, ctx)
        setup(nc, C, banks, A["g_xattn"], A["g_ffn"], A)

        def dram(name, shape, dt=F32):
            return nc.dram_tensor(name, shape, dt, kind="Internal").ap()

        stages = {
            "a0": lambda i, o: latent_attention(nc, C, banks, 0, i, o, A, idx),
            "qffn": lambda i, o: quantised_ffn(nc, C, banks, 4, i, o, A["L0_ffn_qweightT"], A["L0_ffn_wparams"],
                                               A["L0_ffn_bias"]),
            "a1": lambda i, o: plain_attention(nc, C, banks, 1, i, o, A, idx),
            "mem": lambda i, o: memory_ffn(nc, C, banks, 5, i, o, A),
            "a2": lambda i, o: grouped_attention(nc, C, banks, 2, i, o, A, A["L2_weights"], scales, codes),
            "ffn": lambda i, o: hadamard_ffn(nc, C, banks, 6, i, o, A, scales, codes),
            "knn": lambda i, o: gather_points(nc, C, banks, 3, i, o, A, idx),
            "moe": lambda i, o: experts_ffn(nc, C, banks, 7, i, o, A),
        }
        idx = dram("nearest", (B, P, KC, 16), U32)
        scales, codes = dram("scales", (24, P, 4)), dram("codes", (24, P, 1024), U32)
        now = x_in
        for n, (name, stage) in enumerate(stages.items()):
            then = x_out if n == len(stages) - 1 else dram(f"x_after_{name}", (B, Q, D))
            stage(now, then)
            now = then


def kernel(**inputs):
    import numpy as np
    import concourse.bacc as bacc
    from concourse.bass_utils import run_bass_kernel_spmd

    nc = bacc.Bacc("TRN2", target_bir_lowering=False, num_devices=1)
    arrays = layout({name: np.asarray(inputs[name]) for name in NAMES})
    A = {n: nc.dram_tensor(n, v.shape, mybir.dt.from_np(v.dtype), kind="ExternalInput").ap() for n, v in arrays.items()}
    out = nc.dram_tensor("x_final", (B, Q, D), F32, kind="ExternalOutput").ap()
    program(nc, A, A["x"], out)
    return run_bass_kernel_spmd(nc, [arrays], core_ids=[0]).results[0]["x_final"]
```

```python
from contextlib import ExitStack

import concourse.bass as bass
from concourse import mybir

F32 = mybir.dt.float32
BF16 = mybir.dt.bfloat16
FP8 = mybir.dt.float8e4
I8 = mybir.dt.int8
U32 = mybir.dt.uint32
ALU = mybir.AluOpType
ACT = mybir.ActivationFunctionType
AX = mybir.AxisListType.X

B, Q, D = 8, 112, 1024
CTX = 375
P = 128
KC = D // P
PAIRS = B // 2
CT = 125
CTILES = CTX // CT
EPS = 1e-5
MAGIC = 1.5 * 2.0 ** 23
LOW = -1e30


class Banks:

    def __init__(self, nc, ctx):
        self.tile = [ctx.enter_context(nc.psum_tensor(f"bank{k}", [P, 512], F32)) for k in range(8)]
        self.full = [ctx.enter_context(nc.semaphore(f"bank_full{k}")) for k in range(8)]
        self.free = [ctx.enter_context(nc.semaphore(f"bank_free{k}")) for k in range(8)]
        self.used = [0] * 8


class Turns:

    def __init__(self, banks, order, rounds):
        self.banks, self.at, self.per = banks, {}, [0] * 8
        for name, k in order:
            self.at[name] = (k, self.per[k])
            self.per[k] += 1
        self.start = list(banks.used)
        for k in range(8):
            banks.used[k] += rounds * self.per[k]

    def tile(self, name):
        return self.banks.tile[self.at[name][0]]

    def full(self, name):
        return self.banks.full[self.at[name][0]]

    def free(self, name):
        return self.banks.free[self.at[name][0]]

    def count(self, name, turn):
        k, n = self.at[name]
        return turn * self.per[k] + (self.start[k] + n + 1)


class Scope:

    def __init__(self, nc, ctx, stage):
        self.nc, self.ctx, self.stage = nc, ctx, stage
        self.sems = []
        ctx.callback(self.clear)

    def sb(self, name, shape, dt=F32):
        return self.ctx.enter_context(self.nc.sbuf_tensor(f"{self.stage}_{name}", shape, dt))

    def sem(self, name):
        self.sems.append(self.nc.alloc_semaphore(f"{self.stage}_{name}"))
        return self.sems[-1]

    def clear(self):
        if self.sems:
            self.nc.clear_and_free_semaphores(self.sems)
            self.nc.all_engine_barrier()


class Early:

    def __init__(self, nc, ctx, stage, weights):
        self.weights = weights
        self.sb = {n: ctx.enter_context(nc.sbuf_tensor(f"{stage}_{n}", shape, F32)) for n, (shape, _) in weights.items()}
        self.loaded = {n: nc.alloc_semaphore(f"{stage}_{n}_loaded") for n in weights}

    def load(self, eng):
        for n, (_, source) in self.weights.items():
            eng.dma_start(self.sb[n][:], source).then_inc(self.loaded[n], 16)


class Consts:

    def __init__(self, nc, ctx):
        s = Scope(nc, ctx, "const")
        self.ident = s.sb("ident", [P, P])
        self.identb = s.sb("identb", [P, P], BF16)
        self.gates = s.sb("gates", [P, 8])


def rows(v, n):
    return v.rearrange("(a d) -> a d", a=1).broadcast_to([n, v.shape[0]])


def fold(w):
    return w.rearrange("(k p) n -> p k n", p=P)


def setup(nc, C, banks, g_xattn, g_ffn, masks):
    with ExitStack() as ctx:
        s = Scope(nc, ctx, "setup")
        loaded = s.sem("loaded")
        block = ctx.enter_context(nc.Block())

        @block.sync
        def _(sp):
            sp.dma_start(C.ident[:], masks["ident"]).then_inc(loaded, 16)
            sp.dma_start(C.gates[:, 0:4], rows(g_xattn, P)).then_inc(loaded, 16)
            sp.dma_start(C.gates[:, 4:8], rows(g_ffn, P)).then_inc(loaded, 16)

        @block.scalar
        def _(act):
            act.wait_ge(loaded, 48)
            act.activation(C.gates[:], C.gates[:], ACT.Tanh)

        @block.vector
        def _(dve):
            dve.wait_ge(loaded, 48)
            dve.tensor_copy(C.identb[:], C.ident[:])

        @block.tensor
        def _(pe):
            for k in range(8):
                pe.sem_inc(banks.free[k], 1)


def stream_x(sp, x, x_in, x_out, x_loaded, x_done, x_stored):
    for s in range(2):
        sp.dma_start(x[:, s, :], x_in[s]).then_inc(x_loaded[s], 16)

    def store(b, p, s):
        sp.wait_ge(x_done, b + 1)
        sp.dma_start(x_out[b], x[:, s, :]).then_inc(x_stored[s], 16)
        sp.wait_ge(x_stored[s], p * 16 + 16)

    with sp.Fori(0, PAIRS - 1) as p:
        for s in range(2):
            store(p * 2 + s, p, s)
            sp.dma_start(x[:, s, :], x_in[p * 2 + (s + 2)]).then_inc(x_loaded[s], 16)
    for s in range(2):
        store(B - 2 + s, PAIRS - 1, s)


def every_pair(eng, pair):
    with eng.Fori(0, PAIRS - 1) as p:
        pair(p, False)
    pair(PAIRS - 1, True)


def stream_ahead(sp, x, z, x_in, x_out, x_loaded, z_loaded, x_done, x_stored, z_used):
    for s in range(2):
        sp.dma_start(x[:, s, :], x_in[s]).then_inc(x_loaded[s], 16)

    def pair(p, last):
        if not last:
            for s in range(2):
                sp.wait_ge(*z_used(s, p))
                sp.dma_start(z[:, s, :], x_in[p * 2 + (s + 2)]).then_inc(z_loaded[s], 16)
        for s in range(2):
            sp.wait_ge(x_done, p * 2 + (s + 1))
            sp.dma_start(x_out[p * 2 + s], x[:, s, :]).then_inc(x_stored[s], 16)
            sp.wait_ge(x_stored[s], p * 16 + 16)
            if not last:
                sp.dma_start(x[:, s, :], x_in[p * 2 + (s + 2)]).then_inc(x_loaded[s], 16)

    every_pair(sp, pair)


class Norm:

    def __init__(self, s, n):
        self.stats = s.sb("ln_stats", [Q, n, 2, 6])
        self.mv = s.sb("ln_mv", [Q, n, 2])
        self.std = s.sb("ln_std", [Q, n, 1])
        self.rstd = s.sb("ln_rstd", [Q, n, 1])
        self.var_ready = s.sem("var_ready")
        self.std_ready = s.sem("std_ready")

    def statistics(self, dve, x, i):
        for h in range(2):
            dve.bn_stats(self.stats[:, i, h, :], x[:, h * 512:(h + 1) * 512])
        dve.drain()
        dve.bn_aggr(self.mv[:, i, :], self.stats[:, i, :, :])
        dve.drain()
        dve.tensor_scalar(self.std[:, i, :], self.mv[:, i, 1:2], EPS, None, ALU.add).then_inc(self.var_ready, 1)

    def root(self, act, i, b):
        act.wait_ge(self.var_ready, b + 1)
        act.activation(self.std[:, i, :], self.std[:, i, :], ACT.Sqrt).then_inc(self.std_ready, 1)

    def in_place(self, dve, z, z_loaded, p, z_ready):
        for s in range(2):
            dve.wait_ge(z_loaded[s], p * 16 + 16)
            self.statistics(dve, z[:, s, :], s)
        for s in range(2):
            self.scale(dve, z[:, s, :], z[:, s, :], s, p * 2 + s).then_inc(z_ready, 1)

    def scale(self, dve, x, z, i, b):
        dve.wait_ge(self.std_ready, b + 1)
        dve.reciprocal(self.rstd[:, i, :], self.std[:, i, :])
        dve.drain()
        return dve.tensor_scalar(z, x, self.mv[:, i, 0:1], self.rstd[:, i, :], ALU.subtract, ALU.mult)


class Nearest:

    def __init__(self, s, tiles, slots, ranks, A):
        self.tiles, self.slots, self.ranks, self.A = tiles, slots, ranks, A
        n = len(tiles)
        self.xy, self.here = s.sb("xy", [P, slots, 2, D]), s.sb("here", [P, slots, 2, KC])
        self.near, self.far = s.sb("near", [P, slots, D]), s.sb("far", [P, slots, D])
        self.top, self.rank = s.sb("top", [P, 2, 8]), s.sb("rank", [P, n, 2, 8], U32)
        self.xy_loaded = [s.sem(f"xy_loaded{i}") for i in range(slots)]
        self.xy_free, self.here_ready, self.sq_ready, self.sq_free, self.rank_ready, self.rank_stored = (
            s.sem(n) for n in ("xy_free", "here_ready", "sq_ready", "sq_free", "rank_ready", "rank_stored"))

    def credits(self, dve):
        dve.sem_inc(self.xy_free, self.slots)
        dve.sem_inc(self.sq_free, self.slots)
        dve.sem_inc(self.rank_stored, 16)

    def load(self, sp, b, slot):
        sp.wait_ge(self.xy_free, b + 1)
        sp.dma_start(self.xy[:, slot], self.A["planes"][b].rearrange("(a n) -> a n", a=1).broadcast_to([P, 2 * D])
                     .rearrange("p (c n) -> p c n", c=2)).then_inc(self.xy_loaded[slot], 16)
        sp.dma_start(self.here[:, slot], self.A["points"][b]).then_inc(self.xy_loaded[slot], 16)

    def begin(self, dve, b, slot, turn):
        dve.wait_ge(self.xy_loaded[slot], turn * 32 + 32)
        dve.tensor_scalar(self.here[:, slot], self.here[:, slot], -1.0, None, ALU.mult).then_inc(self.here_ready, 1)

    def squares(self, act, b, slot, i):
        n, t = len(self.tiles), self.tiles[i]
        k = (slot * n + i) % self.slots
        if i == 0:
            act.wait_ge(self.here_ready, b + 1)
        act.wait_ge(self.sq_free, b * n + (i + 1))
        act.activation(self.near[:, k], self.xy[:, slot, 0], ACT.Square, bias=self.here[:, slot, 0, t:t + 1])
        act.activation(self.far[:, k], self.xy[:, slot, 1], ACT.Square, bias=self.here[:, slot, 1, t:t + 1])\
           .then_inc(self.sq_ready, 1)

    def sort(self, dve, b, slot, i):
        n = len(self.tiles)
        k = (slot * n + i) % self.slots
        near, far, top = self.near[:, k], self.far[:, k], self.top
        dve.wait_ge(self.sq_ready, b * n + (i + 1))
        if i == 0:
            dve.wait_ge(self.rank_stored, b * 16 + 16)
        dve.scalar_tensor_tensor(out=near, in0=near, scalar=-1.0, in1=far, op0=ALU.mult, op1=ALU.subtract)
        dve.drain()
        dve.max(top[:, 0, :], near)
        dve.drain()
        dve.max_index(self.rank[:, i, 0, :], top[:, 0, :], near)
        dve.match_replace(far, top[:, 0, :], near, -3e38)
        dve.drain()
        dve.max(top[:, 1, :], far)
        dve.drain()
        dve.max_index(self.rank[:, i, 1, :], top[:, 1, :], far)
        dve.drain().then_inc(self.sq_free, 1)
        if i == n - 1:
            dve.sem_inc(self.xy_free, 1)
            dve.sem_inc(self.rank_ready, 1)

    def store(self, eng, b):
        t0, n = self.tiles[0], len(self.tiles)
        eng.wait_ge(self.rank_ready, b + 1)
        eng.dma_start(self.ranks[b][:, t0:t0 + n, :].rearrange("p t k -> p (t k)"), self.rank[:].rearrange("p t a k -> p (t a k)"))\
           .then_inc(self.rank_stored, 16)

    def stored(self, eng):
        eng.wait_ge(self.rank_stored, 16 * B + 16)


def divide(dve, out, rest, n):
    dve.tensor_scalar(rest, out, 1.0 / n, None, ALU.mult)
    dve.drain()
    dve.scalar_tensor_tensor(out=out, in0=rest, scalar=-(n + 1.0), in1=out, op0=ALU.mult, op1=ALU.add)
    dve.drain()
    dve.tensor_tensor(out, out, rest, ALU.add)
    dve.drain()
    dve.scalar_tensor_tensor(out=out, in0=out, scalar=1.0 / n, in1=rest, op0=ALU.mult, op1=ALU.add)
    dve.drain()


def quantised_ffn(nc, C, banks, gate, x_in, x_out, qweightT, wparams, bias, early):
    QMAX = 127.0
    with ExitStack() as ctx:
        s_ = Scope(nc, ctx, "qffn")
        w8 = s_.sb("w8", [P, KC, D], I8)
        w = s_.sb("w", [P, KC, D], BF16)
        wp = s_.sb("wparams", [Q, D])
        bi = s_.sb("bias", [Q, D])
        x = s_.sb("x", [Q, 2, D])
        z = s_.sb("z", [Q, 2, D])
        q = s_.sb("q", [Q, 2, D], BF16)
        qT = s_.sb("qT", [P, 2, KC, Q], BF16)
        y = s_.sb("y", [Q, 2, D])
        ascale, yscale = s_.sb("ascale", [Q, 2, 1]), s_.sb("yscale", [Q, 2, 1])
        rscale = s_.sb("rscale", [Q, 2, 1])
        norm = Norm(s_, 2)
        w_loaded = s_.sem("w_loaded")
        rows_loaded = s_.sem("rows_loaded")
        w_cast = s_.sem("w_cast")
        x_loaded = [s_.sem(f"x_loaded{i}") for i in range(2)]
        x_stored = [s_.sem(f"x_stored{i}") for i in range(2)]
        z_loaded = [s_.sem(f"z_loaded{i}") for i in range(2)]
        z_ready, q_free, y_free = s_.sem("z_ready"), s_.sem("q_free"), s_.sem("y_free")
        q_ready, qT_ready, y_ready, x_done = s_.sem("q_ready"), s_.sem("qT_ready"), s_.sem("y_ready"), s_.sem("x_done")
        part_done = s_.sem("part_done")
        rows_scaled = s_.sem("rows_scaled")
        turns = Turns(banks, [(("T", s), s) for s in range(2)]
                      + [(("y", s, n), 2 + 2 * s + n) for s in range(2) for n in range(2)], PAIRS)
        block = ctx.enter_context(nc.Block())

        @block.sync
        def _(sp):
            for s in range(2):
                sp.dma_start(z[:, s, :], x_in[s]).then_inc(z_loaded[s], 16)
            sp.dma_start(w8[:].bitcast(U32), fold(qweightT)).then_inc(w_loaded, 16)
            sp.dma_start(wp[:], rows(wparams, Q)).then_inc(rows_loaded, 16)
            sp.dma_start(bi[:], rows(bias, Q)).then_inc(rows_loaded, 16)
            sp.wait_ge(w_loaded, 16)
            early.load(sp)
            stream_x(sp, x, x_in, x_out, x_loaded, x_done, x_stored)

        @block.vector
        def _(dve):
            dve.sem_inc(q_free, 2)
            norm.in_place(dve, z, z_loaded, 0, z_ready)

            def pair(p, last):
                for s in range(2):
                    dve.drain()
                    dve.wait_ge(q_free, p * 2 + (s + 1))
                    dve.tensor_reduce(ascale[:, s, :], z[:, s, :], AX, ALU.max, apply_absolute_value=True)
                for s in range(2):
                    dve.drain()
                    divide(dve, ascale[:, s, :], rscale[:, s, :], QMAX)
                    dve.reciprocal(rscale[:, s, :], ascale[:, s, :])
                    dve.drain()
                    dve.tensor_scalar(z[:, s, :], z[:, s, :], rscale[:, s, :], MAGIC, ALU.mult, ALU.add)
                for s in range(2):
                    dve.drain()
                    dve.tensor_scalar(q[:, s, :], z[:, s, :], MAGIC, QMAX, ALU.subtract, ALU.min).then_inc(q_ready, 1)
                if not last:
                    norm.in_place(dve, z, z_loaded, p + 1, z_ready)

            every_pair(dve, pair)

        @block.tensor
        def _(pe):
            pe.wait_ge(w_cast, 1)
            with pe.Fori(0, PAIRS) as p:
                for s in range(2):
                    t = ("T", s)
                    pe.wait_ge(q_ready, p * 2 + (s + 1))
                    pe.wait_ge(turns.free(t), turns.count(t, p))
                    o = turns.tile(t)[:].bitcast(BF16)
                    for k in range(KC):
                        mm = pe.transpose(o[:, k * Q:(k + 1) * Q], q[:, s, k * P:(k + 1) * P], C.identb[0:Q, 0:Q])
                    mm.then_inc(turns.full(t), 1)
                for s in range(2):
                    pe.wait_ge(qT_ready, p * 2 + (s + 1))
                    for n in range(2):
                        t = ("y", s, n)
                        pe.wait_ge(turns.free(t), turns.count(t, p))
                        for k in range(KC):
                            mm = pe.matmul(turns.tile(t)[0:Q, :], qT[:, s, k, :], w[:, k, n * 512:(n + 1) * 512],
                                           start=(k == 0), stop=(k == KC - 1))
                        mm.then_inc(turns.full(t), 1)

        @block.scalar
        def _(act):
            for s in range(2):
                norm.root(act, s, s)
            act.wait_ge(w_loaded, 16)
            act.copy(w[:], w8[:]).then_inc(w_cast, 1)

            def pair(p, last):
                for s in range(2):
                    t = ("T", s)
                    act.wait_ge(turns.full(t), turns.count(t, p))
                    o = turns.tile(t)[:].bitcast(BF16)
                    act.copy(qT[:, s, :, :], o[:, 0:KC * Q].rearrange("p (k q) -> p k q", k=KC)).then_inc(turns.free(t), 1)
                    act.activation(yscale[:, s, :], ascale[:, s, :], ACT.Copy)
                    act.drain().then_inc(qT_ready, 1)
                    act.sem_inc(q_free, 1)
                    if not last:
                        act.dma_start(z[:, s, :], x_in[p * 2 + (s + 2)]).then_inc(z_loaded[s], 16)
                if not last:
                    for s in range(2):
                        norm.root(act, s, p * 2 + (s + 2))
                for s in range(2):
                    act.wait_ge(y_free, p * 2 + (s + 1))
                    for n in range(2):
                        t = ("y", s, n)
                        act.wait_ge(turns.full(t), turns.count(t, p))
                        act.activation(y[:, s, n * 512:(n + 1) * 512], turns.tile(t)[0:Q, :], ACT.Copy,
                                       scale=yscale[:, s, :]).then_inc(turns.free(t), 1)
                    act.drain().then_inc(y_ready, 1)

            every_pair(act, pair)

        @block.gpsimd
        def _(pool):
            pool.wait_ge(rows_loaded, 32)
            gp = C.gates[0:Q, gate:gate + 1]
            for v in (wp, bi):
                pool.tensor_scalar(v[:], v[:], gp, 1.0, ALU.mult, ALU.mult).then_inc(rows_scaled, 1)
            pool.wait_ge(rows_scaled, 2)
            pool.sem_inc(y_free, 2)
            with pool.Fori(0, PAIRS) as p:
                for s in range(2):
                    pool.wait_ge(y_ready, p * 2 + (s + 1))
                    pool.wait_ge(x_loaded[s], p * 16 + 16)
                    pool.tensor_tensor(y[:, s, :], y[:, s, :], wp[:], ALU.mult)
                    pool.tensor_tensor(x[:, s, :], x[:, s, :], bi[:], ALU.add).then_inc(part_done, 1)
                    pool.wait_ge(part_done, p * 2 + (s + 1))
                    pool.tensor_tensor(x[:, s, :], x[:, s, :], y[:, s, :], ALU.add).then_inc(x_done, 1)
                    pool.wait_ge(x_done, p * 2 + (s + 1))
                    pool.sem_inc(y_free, 1)


def turn_rows(pe, C, turns, src, name, s, p, n=2):
    for h in range(n):
        t = (name, s, h)
        pe.wait_ge(turns.free(t), turns.count(t, p))
        for k in range(4):
            c = (4 * h + k) * P
            mm = pe.transpose(turns.tile(t)[:, k * Q:(k + 1) * Q], src[:, c:c + P], C.ident[0:Q, 0:Q])
        mm.then_inc(turns.full(t), 1)


def copy_turned(act, turns, dst, name, s, p, ready, n=2):
    for h in range(n):
        t = (name, s, h)
        act.wait_ge(turns.full(t), turns.count(t, p))
        act.activation(dst[:, 4 * h:4 * h + 4, :], turns.tile(t)[:, 0:4 * Q].rearrange("p (k q) -> p k q", k=4),
                       ACT.Copy).then_inc(turns.free(t), 1)
    act.drain().then_inc(ready, 1)


def project(pe, turns, lhsT, w, name, s, p, n=2):
    for h in range(n):
        t = (name, s, h)
        pe.wait_ge(turns.free(t), turns.count(t, p))
        for k in range(w.shape[1]):
            mm = pe.matmul(turns.tile(t)[0:Q, :], lhsT[:, k, :], w[:, k, h * 512:(h + 1) * 512],
                           start=(k == 0), stop=(k == w.shape[1] - 1))
        mm.then_inc(turns.full(t), 1)


def plain_attention(nc, C, banks, gate, x_in, x_out, A, nearest, early):
    SCALE = float(D) ** -0.5
    with ExitStack() as ctx:
        s_ = Scope(nc, ctx, "plain")
        s_.sems += early.loaded.values()
        wq, wk = early.sb["wq"], early.sb["wk"]
        bq, bk = s_.sb("bq", [P, KC]), s_.sb("bk", [P, KC])
        x, z = s_.sb("x", [Q, 2, D]), s_.sb("z", [Q, 2, D])
        zT, qT, tT = (s_.sb(n, [P, 2, KC, Q]) for n in ("zT", "qT", "tT"))
        cT, cN = s_.sb("ctxT", [P, 2, KC, CTX]), s_.sb("ctx", [CT, 2, CTILES, D])
        pr, pT = s_.sb("probs", [Q, 2, CTX]), s_.sb("probsT", [CT, 2, CTILES, Q])
        nmax, rsum, coef = (s_.sb(n, [Q, 2, 1]) for n in ("nmax", "rsum", "coef"))
        qbk, total = s_.sb("qbk", [Q, 2, 1]), s_.sb("total", [Q, 2, 1])
        points = Nearest(s_, [5, 6, 7], 2, nearest, A)
        norm = Norm(s_, 2)
        wq_loaded, wk_loaded, b_loaded = early.loaded["wq"], early.loaded["wk"], s_.sem("b_loaded")
        x_loaded = [s_.sem(f"x_loaded{i}") for i in range(2)]
        x_stored = [s_.sem(f"x_stored{i}") for i in range(2)]
        z_loaded = [s_.sem(f"z_loaded{i}") for i in range(2)]
        ctx_loaded = [s_.sem(f"ctx_loaded{i}") for i in range(2)]
        ctx_free = [s_.sem(f"ctx_free{i}") for i in range(2)]
        z_ready, zT_ready, qT_ready, tT_ready = (s_.sem(n) for n in ("z_ready", "zT_ready", "qT_ready", "tT_ready"))
        max_ready, probs_ready, pT_ready, x_done = (
            s_.sem(n) for n in ("max_ready", "probs_ready", "pT_ready", "x_done"))
        order = [(("zT", s, h), 4 * s + h) for s in range(2) for h in range(2)]
        order += [(("qT", i), (2, 3, 6, 7)[i]) for i in range(4)] + [(("tT", i), (0, 1, 4, 5)[i]) for i in range(4)]
        for st, b0, n in (("S", 2, 1), ("pT", 3, 1), ("o", 0, 2)):
            order += [((st, s, h), 4 * s + b0 + h) for s in range(2) for h in range(n)]
        turns = Turns(banks, order, PAIRS)
        block = ctx.enter_context(nc.Block())

        @block.sync
        def _(sp):
            for s in range(2):
                sp.dma_start(z[:, s, :], x_in[s]).then_inc(z_loaded[s], 16)
            stream_ahead(sp, x, z, x_in, x_out, x_loaded, z_loaded, x_done, x_stored,
                         lambda s, p: (turns.full(("zT", s, 1)), turns.count(("zT", s, 1), p)))

        @block.gpsimd
        def _(pool):
            pool.dma_start(bq[:], A["L1_xattn_bq"]).then_inc(b_loaded, 16)
            pool.dma_start(bk[:], A["L1_xattn_bk"]).then_inc(b_loaded, 16)
            with pool.Fori(0, PAIRS) as p:
                for s in range(2):
                    points.load(pool, p * 2 + s, s)
                for s in range(2):
                    pool.wait_ge(ctx_free[s], p + 1)
                    pool.dma_start(cT[:, s], A["ctxT"][p * 2 + s].rearrange("(k p) n -> p k n", p=P)).then_inc(ctx_loaded[s], 16)
                    pool.dma_start(cN[:, s], A["ctx_4096"][p * 2 + s].rearrange("(t p) n -> p t n", p=CT)).then_inc(ctx_loaded[s], 16)

        @block.tensor
        def _(pe):
            pe.wait_ge(wq_loaded, 16)
            with pe.Fori(0, PAIRS) as p:
                for s in range(2):
                    pe.wait_ge(z_ready, p * 2 + (s + 1))
                    turn_rows(pe, C, turns, z[:, s], "zT", s, p)

                def projected(name, w, src, ready):
                    for i in range(4):
                        t = (name, i)
                        pe.wait_ge(turns.free(t), turns.count(t, p))
                        for c in range(2):
                            for k in range(KC):
                                if ready and (i, c) == (0, 0) and k % 2 == 0:
                                    pe.wait_ge(ready, p * 4 + (k // 2 + 1))
                                mm = pe.matmul(turns.tile(t)[:, c * 2 * Q:(c + 1) * 2 * Q], w[:, k, (2 * i + c) * P:(2 * i + c + 1) * P],
                                               src[:, :, k, :], start=(k == 0), stop=(k == KC - 1))
                        mm.then_inc(turns.full(t), 1)

                pe.wait_ge(zT_ready, p * 2 + 2)
                projected("qT", wq, zT, None)
                pe.wait_ge(wk_loaded, 16)
                pe.wait_ge(b_loaded, 32)
                projected("tT", wk, qT, qT_ready)
                for s in range(2):
                    t = ("S", s, 0)
                    pe.wait_ge(tT_ready, p * 4 + 4)
                    pe.wait_ge(ctx_loaded[s], p * 32 + 32)
                    pe.wait_ge(turns.free(t), turns.count(t, p))
                    for k in range(KC):
                        pe.matmul(turns.tile(t)[0:Q, 0:CTX], tT[:, s, k, :], cT[:, s, k, :], start=(k == 0), stop=(k == KC - 1))
                    for k in range(KC):
                        mm = pe.matmul(turns.tile(t)[0:Q, 400:401], qT[:, s, k, :], bk[:, k:k + 1], start=(k == 0),
                                       stop=(k == KC - 1))
                    mm.then_inc(turns.full(t), 1)
                for s in range(2):
                    t = ("pT", s, 0)
                    pe.wait_ge(probs_ready, p * 2 + (s + 1))
                    pe.wait_ge(turns.free(t), turns.count(t, p))
                    for k in range(CTILES):
                        mm = pe.transpose(turns.tile(t)[0:CT, k * Q:(k + 1) * Q], pr[:, s, k * CT:(k + 1) * CT], C.ident[0:Q, 0:Q])
                    mm.then_inc(turns.full(t), 1)
                for s in range(2):
                    pe.wait_ge(pT_ready, p * 2 + (s + 1))
                    for h in range(2):
                        t = ("o", s, h)
                        pe.wait_ge(turns.free(t), turns.count(t, p))
                        for k in range(CTILES):
                            mm = pe.matmul(turns.tile(t)[0:Q, :], pT[:, s, k, :], cN[:, s, k, h * 512:(h + 1) * 512],
                                           start=(k == 0), stop=(k == CTILES - 1))
                        mm.then_inc(turns.full(t), 1)

        @block.scalar
        def _(act):
            for s in range(2):
                norm.root(act, s, s)
            act.wait_ge(b_loaded, 32)

            def pair(p, last):
                for s in range(2):
                    copy_turned(act, turns, zT[:, s], "zT", s, p, zT_ready)
                for i in range(4):
                    if i < 3:
                        points.squares(act, p * 2, 0, i)
                    t = ("qT", i)
                    act.wait_ge(turns.full(t), turns.count(t, p))
                    for c in range(2):
                        k = 2 * i + c
                        op = act.activation(qT[:, :, k, :], turns.tile(t)[:, c * 2 * Q:(c + 1) * 2 * Q].rearrange("p (s q) -> p s q", s=2),
                                            ACT.Identity, bias=bq[:, k:k + 1])
                    op.then_inc(turns.free(t), 1)
                    act.drain().then_inc(qT_ready, 1)
                points.store(act, p * 2)
                for i in range(4):
                    if i < 3:
                        points.squares(act, p * 2 + 1, 1, i)
                    t = ("tT", i)
                    act.wait_ge(turns.full(t), turns.count(t, p))
                    for s in range(2):
                        op = act.activation(tT[:, s, 2 * i:2 * i + 2, :],
                                            turns.tile(t)[:, 0:4 * Q].rearrange("p (c s q) -> p s c q", c=2, s=2)[:, s], ACT.Copy)
                    op.then_inc(turns.free(t), 1)
                    act.drain().then_inc(tT_ready, 1)
                for s in range(2):
                    t = ("S", s, 0)
                    act.wait_ge(max_ready, p * 2 + (s + 1))
                    act.activation(pr[:, s, :], turns.tile(t)[0:Q, 0:CTX], ACT.Exp, bias=nmax[:, s, :], scale=SCALE,
                                   accum_out=rsum[:, s, :])
                    act.drain().then_inc(turns.free(t), 1)
                    act.drain().then_inc(probs_ready, 1)
                points.store(act, p * 2 + 1)
                if not last:
                    for s in range(2):
                        norm.root(act, s, p * 2 + (s + 2))

            every_pair(act, pair)
            points.stored(act)

        @block.vector
        def _(dve):
            for s in range(2):
                dve.sem_inc(ctx_free[s], 1)
            points.credits(dve)
            norm.in_place(dve, z, z_loaded, 0, z_ready)

            def pair(p, last):
                for s in range(2):
                    points.begin(dve, p * 2 + s, s, p)
                for s in range(2):
                    for i in range(3):
                        points.sort(dve, p * 2 + s, s, i)
                for s in range(2):
                    t = ("S", s, 0)
                    dve.wait_ge(turns.full(t), turns.count(t, p))
                    dve.tensor_copy(qbk[:, s, :], turns.tile(t)[0:Q, 400:401])
                    dve.tensor_reduce(nmax[:, s, :], turns.tile(t)[0:Q, 0:CTX], AX, ALU.max, negate=True)
                    dve.drain()
                    dve.tensor_tensor(total[:, s, :], nmax[:, s, :], qbk[:, s, :], ALU.subtract)
                    dve.drain()
                    dve.tensor_scalar(nmax[:, s, :], total[:, s, :], qbk[:, s, :], SCALE, ALU.add, ALU.mult).then_inc(max_ready, 1)
                for s in range(2):
                    t = ("pT", s, 0)
                    dve.wait_ge(probs_ready, p * 2 + (s + 1))
                    dve.reciprocal(coef[:, s, :], rsum[:, s, :])
                    dve.wait_ge(turns.full(t), turns.count(t, p))
                    dve.tensor_copy(pT[:, s, :, :], turns.tile(t)[0:CT, 0:CTILES * Q].rearrange("p (k q) -> p k q", q=Q))\
                       .then_inc(turns.free(t), 1)
                    dve.drain().then_inc(pT_ready, 1)
                    dve.tensor_scalar(coef[:, s, :], coef[:, s, :], C.gates[0:Q, gate:gate + 1], None, ALU.mult)
                dve.drain()
                if not last:
                    norm.in_place(dve, z, z_loaded, p + 1, z_ready)
                for s in range(2):
                    dve.wait_ge(x_loaded[s], p * 16 + 16)
                    for h in range(2):
                        t = ("o", s, h)
                        c = slice(h * 512, (h + 1) * 512)
                        dve.wait_ge(turns.full(t), turns.count(t, p))
                        dve.scalar_tensor_tensor(out=x[:, s, c], in0=turns.tile(t)[0:Q, :], scalar=coef[:, s, :],
                                                 in1=x[:, s, c], op0=ALU.mult, op1=ALU.add).then_inc(turns.free(t), 1)
                    dve.drain().then_inc(x_done, 1)
                    dve.drain().then_inc(ctx_free[s], 1)

            every_pair(dve, pair)


def memory_ffn(nc, C, banks, gate, x_in, x_out, A, early):
    BOT, RDIM, NSLOT, HU = 64, 48, 256, 256
    TAU_LOW, TAU_HIGH, EARLY_EXIT = 0.5, 2.0, 0.05
    with ExitStack() as ctx:
        s_ = Scope(nc, ctx, "mem")
        wqT, wu1T, wvdT = s_.sb("wqT", [P, KC, BOT]), s_.sb("wu1T", [P, KC, HU]), s_.sb("wvdT", [P, KC, BOT])
        wu2, bu1 = s_.sb("wu2", [P, 2]), s_.sb("bu1", [P, 2])
        bu2, gw1, gbias = (s_.sb(n, [Q, 1]) for n in ("bu2", "gw1", "gbias"))
        wrT, keysT, wvuT = s_.sb("wrT", [BOT, P]), s_.sb("keysT", [BOT, NSLOT]), s_.sb("wvuT", [BOT, D])
        valuesT, rel = s_.sb("valuesT", [P, KC, NSLOT]), s_.sb("log_rel", [Q, NSLOT])
        ones = s_.sb("ones", [Q, Q])
        av, rkT = s_.sb("av", [P, 2, BOT]), s_.sb("rkT", [RDIM, NSLOT])
        x, z = s_.sb("x", [Q, 2, D]), s_.sb("z", [Q, 2, D])
        zT = s_.sb("zT", [P, KC, 2 * Q])
        queryT, hidT = s_.sb("queryT", [BOT, 2 * Q]), s_.sb("hidT", [P, 2, 2 * Q])
        rqT, vT = s_.sb("rqT", [RDIM, 2 * Q]), s_.sb("vT", [BOT, 2 * Q])
        route, attn, left = (s_.sb(n, [Q, 2, NSLOT]) for n in ("route", "attn", "left"))
        w, wT = s_.sb("w", [Q, 2, NSLOT]), s_.sb("wT", [P, 2, 2, Q])
        best = s_.sb("best", [Q, 2, 8])
        nmax, rsum, coef, var_z, log_var, learned, unsure, keep = (
            s_.sb(n, [Q, 2]) for n in ("nmax", "rsum", "coef", "var_z", "log_var", "learned", "unsure", "keep"))
        lsum, rmean = s_.sb("lsum", [Q, 1]), s_.sb("rmean", [Q, 1])
        PRE = 4
        early_x, stats = s_.sb("early_x", [Q, PRE, D]), s_.sb("stats", [Q, B, 2, 6])
        mv, var_all, rvar = s_.sb("mv", [Q, B, 2]), s_.sb("var_all", [Q, B]), s_.sb("rvar", [Q, B])
        norm = Norm(s_, 2)
        w_loaded = s_.sem("w_loaded")
        pre_loaded = [s_.sem(f"pre_loaded{i}") for i in range(PRE)]
        pre_free = s_.sem("pre_free")
        x_loaded = [s_.sem(f"x_loaded{i}") for i in range(2)]
        x_stored = [s_.sem(f"x_stored{i}") for i in range(2)]
        z_loaded = [s_.sem(f"z_loaded{i}") for i in range(2)]
        z_free = s_.sem("z_free")
        pre_var, lsum_ready, tables_ready = (s_.sem(n) for n in ("pre_var", "lsum_ready", "tables_ready"))
        z_ready, zT_ready, proj_ready, rq_ready, sig_ready, un_ready, gate_ready = (
            s_.sem(n) for n in ("z_ready", "zT_ready", "proj_ready", "rq_ready", "sig_ready", "un_ready", "gate_ready"))
        max_ready, w_ready, wT_ready, v_ready, x_done = (
            s_.sem(n) for n in ("max_ready", "w_ready", "wT_ready", "v_ready", "x_done"))
        prep = Turns(banks, [("lsum", 0), ("rk", 1), ("av", 2)], 1)
        turns = Turns(banks, [(("zT", s, h), 2 * s + h) for s in range(2) for h in range(2)]
                      + [("query", 4), ("hid", 5), ("rq", 6), ("learned", 7)]
                      + [(("scores", s), s) for s in range(2)] + [(("wT", s), 2 + s) for s in range(2)] + [("v", 4)]
                      + [(("o", s, h), (5, 6, 7, 0)[2 * s + h]) for s in range(2) for h in range(2)], PAIRS)
        weights = [(wqT, fold(A["L1_ffn_WqT"])), (wu1T, fold(A["L1_ffn_Wu1T"])), (wvdT, fold(A["L1_ffn_WvdT"])),
                   (wu2, A["L1_ffn_Wu2"]), (bu1, A["L1_ffn_bu1"]), (bu2, rows(A["L1_ffn_bu2"], Q)),
                   (gw1, rows(A["L1_ffn_gate_w1"], Q)), (gbias, rows(A["L1_ffn_gate_bias"], Q)),
                   (wrT, A["L1_ffn_WrT"]), (keysT, A["L1_ffn_aux_keysT"]), (wvuT, A["L1_ffn_WvuT"]),
                   (valuesT, fold(A["L1_ffn_aux_valuesT"])), (rel, rows(A["L1_ffn_log_rel"], Q))]
        block = ctx.enter_context(nc.Block())

        @block.sync
        def _(sp):
            for s in range(2):
                sp.dma_start(z[:, s, :], x_in[s]).then_inc(z_loaded[s], 16)
            for b in range(B):
                if b == PRE:
                    sp.wait_ge(w_loaded, 16 * len(weights))
                if b >= PRE:
                    sp.wait_ge(pre_free, b - PRE + 1)
                sp.dma_start(early_x[:, b % PRE, :], x_in[b]).then_inc(pre_loaded[b % PRE], 16)
            early.load(sp)
            stream_ahead(sp, x, z, x_in, x_out, x_loaded, z_loaded, x_done, x_stored,
                         lambda s, p: (z_free, p * 2 + (s + 1)))

        @block.gpsimd
        def _(pool):
            for dst, src in weights:
                pool.dma_start(dst[:], src).then_inc(w_loaded, 16)

        @block.tensor
        def _(pe):
            pe.wait_ge(w_loaded, 16 * len(weights))
            pe.wait_ge(prep.free("rk"), prep.count("rk", 0))
            pe.matmul(prep.tile("rk")[:, 0:NSLOT], wrT[:], keysT[:], start=True, stop=True).then_inc(prep.full("rk"), 1)
            pe.wait_ge(prep.free("av"), prep.count("av", 0))
            for c in range(2):
                for k in range(KC):
                    mm = pe.matmul(prep.tile("av")[:, c * BOT:(c + 1) * BOT], valuesT[:, k, c * P:(c + 1) * P], wvdT[:, k, :],
                                   start=(k == 0), stop=(k == KC - 1))
            mm.then_inc(prep.full("av"), 1)
            pe.wait_ge(lsum_ready, 1)
            pe.wait_ge(prep.free("lsum"), prep.count("lsum", 0))
            pe.matmul(prep.tile("lsum")[0:Q, 0:1], ones[:], lsum[:], start=True, stop=True).then_inc(prep.full("lsum"), 1)
            pe.wait_ge(tables_ready, 2)
            with pe.Fori(0, PAIRS) as p:
                for s in range(2):
                    pe.wait_ge(z_ready, p * 2 + (s + 1))
                    turn_rows(pe, C, turns, z[:, s], "zT", s, p)
                pe.wait_ge(zT_ready, p * 2 + 2)
                pe.wait_ge(turns.free("query"), turns.count("query", p))
                for k in range(KC):
                    mm = pe.matmul(turns.tile("query")[0:BOT, 0:2 * Q], wqT[:, k, :], zT[:, k, :], start=(k == 0), stop=(k == KC - 1))
                mm.then_inc(turns.full("query"), 1)
                pe.wait_ge(turns.free("hid"), turns.count("hid", p))
                for c in range(2):
                    for k in range(KC):
                        mm = pe.matmul(turns.tile("hid")[:, c * 2 * Q:(c + 1) * 2 * Q], wu1T[:, k, c * P:(c + 1) * P], zT[:, k, :],
                                       start=(k == 0), stop=(k == KC - 1))
                mm.then_inc(turns.full("hid"), 1)
                pe.wait_ge(proj_ready, p * 2 + 1)
                pe.wait_ge(turns.free("rq"), turns.count("rq", p))
                pe.matmul(turns.tile("rq")[:, 0:2 * Q], wrT[:], queryT[:], start=True, stop=True).then_inc(turns.full("rq"), 1)
                pe.wait_ge(proj_ready, p * 2 + 2)
                pe.wait_ge(turns.free("learned"), turns.count("learned", p))
                for s in range(2):
                    for c in range(2):
                        mm = pe.matmul(turns.tile("learned")[0:Q, s:s + 1], hidT[:, c, s * Q:(s + 1) * Q], wu2[:, c:c + 1],
                                       start=(c == 0), stop=(c == 1))
                mm.then_inc(turns.full("learned"), 1)
                pe.wait_ge(rq_ready, p + 1)
                for s in range(2):
                    t = ("scores", s)
                    pe.wait_ge(turns.free(t), turns.count(t, p))
                    pe.matmul(turns.tile(t)[0:Q, 0:NSLOT], rqT[:, s * Q:(s + 1) * Q], rkT[:], start=True, stop=True)
                    pe.matmul(turns.tile(t)[0:Q, NSLOT:2 * NSLOT], queryT[:, s * Q:(s + 1) * Q], keysT[:], start=True,
                              stop=True).then_inc(turns.full(t), 1)
                for s in range(2):
                    t = ("wT", s)
                    pe.wait_ge(w_ready, p * 2 + (s + 1))
                    pe.wait_ge(turns.free(t), turns.count(t, p))
                    for c in range(2):
                        mm = pe.transpose(turns.tile(t)[:, c * Q:(c + 1) * Q], w[:, s, c * P:(c + 1) * P], C.ident[0:Q, 0:Q])
                    mm.then_inc(turns.full(t), 1)
                pe.wait_ge(wT_ready, p * 2 + 2)
                pe.wait_ge(turns.free("v"), turns.count("v", p))
                for c in range(2):
                    mm = pe.matmul(turns.tile("v")[0:BOT, 0:2 * Q], av[:, c, :], wT[:, c, :, :], start=(c == 0), stop=(c == 1))
                mm.then_inc(turns.full("v"), 1)
                pe.wait_ge(v_ready, p + 1)
                for s in range(2):
                    for h in range(2):
                        t = ("o", s, h)
                        pe.wait_ge(turns.free(t), turns.count(t, p))
                        pe.matmul(turns.tile(t)[0:Q, :], vT[:, s * Q:(s + 1) * Q], wvuT[:, h * 512:(h + 1) * 512], start=True,
                                  stop=True).then_inc(turns.full(t), 1)

        @block.scalar
        def _(act):
            for s in range(2):
                norm.root(act, s, s)
            act.wait_ge(pre_var, 1)
            act.activation(rvar[:], var_all[:], ACT.Ln, bias=1.0, accum_out=lsum[:])
            act.drain().then_inc(lsum_ready, 1)
            act.wait_ge(prep.full("rk"), prep.count("rk", 0))
            act.activation(rkT[:], prep.tile("rk")[0:RDIM, 0:NSLOT], ACT.Copy).then_inc(prep.free("rk"), 1)
            act.wait_ge(prep.full("av"), prep.count("av", 0))
            act.activation(av[:], prep.tile("av")[:, 0:2 * BOT].rearrange("p (c n) -> p c n", c=2), ACT.Copy)\
               .then_inc(prep.free("av"), 1)
            act.drain().then_inc(tables_ready, 1)

            def pair(p, last):
                for s in range(2):
                    copy_turned(act, turns, zT[:, :, s * Q:(s + 1) * Q], "zT", s, p, zT_ready)
                act.wait_ge(turns.full("query"), turns.count("query", p))
                act.activation(queryT[:], turns.tile("query")[0:BOT, 0:2 * Q], ACT.Copy).then_inc(turns.free("query"), 1)
                act.drain().then_inc(proj_ready, 1)
                act.wait_ge(turns.full("hid"), turns.count("hid", p))
                for c in range(2):
                    act.activation(hidT[:, c, :], turns.tile("hid")[:, c * 2 * Q:(c + 1) * 2 * Q], ACT.Gelu_apprx_tanh,
                                   bias=bu1[:, c:c + 1])
                act.drain().then_inc(turns.free("hid"), 1)
                act.drain().then_inc(proj_ready, 1)
                act.wait_ge(turns.full("rq"), turns.count("rq", p))
                act.activation(rqT[:], turns.tile("rq")[0:RDIM, 0:2 * Q], ACT.Copy).then_inc(turns.free("rq"), 1)
                act.drain().then_inc(rq_ready, 1)
                for s in range(2):
                    act.wait_ge(max_ready, p * 2 + (s + 1))
                    act.activation(w[:, s, :], attn[:, s, :], ACT.Exp, bias=nmax[:, s:s + 1], accum_out=rsum[:, s:s + 1])
                    act.drain().then_inc(w_ready, 1)
                act.activation(log_var[:], var_z[:], ACT.Ln, bias=1.0)
                act.wait_ge(turns.full("learned"), turns.count("learned", p))
                act.activation(learned[:], turns.tile("learned")[0:Q, 0:2], ACT.Sigmoid, bias=bu2[:]).then_inc(turns.free("learned"), 1)
                act.drain().then_inc(sig_ready, 1)
                act.wait_ge(un_ready, p + 1)
                act.activation(coef[:], unsure[:], ACT.Sigmoid, bias=gbias[:], scale=gw1[:]).then_inc(gate_ready, 1)
                act.wait_ge(turns.full("v"), turns.count("v", p))
                act.activation(vT[:], turns.tile("v")[0:BOT, 0:2 * Q], ACT.Copy).then_inc(turns.free("v"), 1)
                act.drain().then_inc(v_ready, 1)
                if not last:
                    for s in range(2):
                        norm.root(act, s, p * 2 + (s + 2))

            every_pair(act, pair)

        @block.vector
        def _(dve):
            dve.memset(ones[:], 1.0)
            norm.in_place(dve, z, z_loaded, 0, z_ready)
            for b in range(B):
                dve.wait_ge(pre_loaded[b % PRE], b // PRE * 16 + 16)
                for h in range(2):
                    op = dve.bn_stats(stats[:, b, h, :], early_x[:, b % PRE, h * 512:(h + 1) * 512])
                op.then_inc(pre_free, 1)
            dve.drain()
            for b in range(B):
                dve.bn_aggr(mv[:, b, :], stats[:, b, :, :])
            dve.drain()
            dve.tensor_scalar(rvar[:], mv[:, :, 1], EPS, None, ALU.add)
            dve.drain()
            dve.reciprocal(rvar[:], rvar[:])
            dve.drain()
            dve.tensor_tensor(var_all[:], mv[:, :, 1], rvar[:], ALU.mult)
            dve.drain().then_inc(pre_var, 1)
            dve.wait_ge(prep.full("lsum"), prep.count("lsum", 0))
            dve.tensor_scalar(rmean[:], prep.tile("lsum")[0:Q, 0:1], 1.0 / (B * Q), 1e-6, ALU.mult, ALU.add)\
               .then_inc(prep.free("lsum"), 1)
            dve.drain()
            dve.reciprocal(rmean[:], rmean[:])
            dve.drain().then_inc(tables_ready, 1)
            gc = C.gates[0:Q, gate:gate + 1]
            def pair(p, last):
                dve.tensor_tensor(var_z[:], norm.mv[:, :, 1], norm.rstd[:, :, 0], ALU.mult)
                dve.drain()
                dve.tensor_tensor(var_z[:], var_z[:], norm.rstd[:, :, 0], ALU.mult)
                for s in range(2):
                    dve.wait_ge(x_loaded[s], p * 16 + 16)
                    dve.scalar_tensor_tensor(out=x[:, s, :], in0=z[:, s, :], scalar=gc, in1=x[:, s, :], op0=ALU.mult, op1=ALU.add)
                dve.drain()
                for s in range(2):
                    t = ("zT", s, 1)
                    dve.wait_ge(turns.full(t), turns.count(t, p))
                    dve.sem_inc(z_free, 1)
                for s in range(2):
                    t = ("scores", s)
                    dve.wait_ge(turns.full(t), turns.count(t, p))
                    dve.scalar_tensor_tensor(out=route[:, s, :], in0=turns.tile(t)[0:Q, 0:NSLOT], scalar=float(RDIM) ** -0.5,
                                             in1=rel[:], op0=ALU.mult, op1=ALU.add)
                    dve.scalar_tensor_tensor(out=attn[:, s, :], in0=turns.tile(t)[0:Q, NSLOT:2 * NSLOT], scalar=float(BOT) ** -0.5,
                                             in1=rel[:], op0=ALU.mult, op1=ALU.add)
                    dve.drain().then_inc(turns.free(t), 1)
                    dve.max(best[:, s, :], route[:, s, :])
                    dve.drain()
                    dve.match_replace(left[:, s, :], best[:, s, :], route[:, s, :], -3e38)
                    dve.drain()
                    dve.tensor_tensor(left[:, s, :], left[:, s, :], route[:, s, :], ALU.is_equal)
                    dve.drain()
                    dve.scalar_tensor_tensor(out=attn[:, s, :], in0=left[:, s, :], scalar=LOW, in1=attn[:, s, :],
                                             op0=ALU.mult, op1=ALU.add)
                    dve.drain()
                    dve.tensor_reduce(nmax[:, s:s + 1], attn[:, s, :], AX, ALU.max, negate=True).then_inc(max_ready, 1)
                for s in range(2):
                    t = ("wT", s)
                    dve.wait_ge(turns.full(t), turns.count(t, p))
                    dve.tensor_copy(wT[:, :, s, :], turns.tile(t)[:, 0:2 * Q].rearrange("p (c q) -> p c q", c=2))\
                       .then_inc(turns.free(t), 1)
                    dve.drain().then_inc(wT_ready, 1)
                dve.wait_ge(sig_ready, p + 1)
                dve.tensor_scalar(unsure[:], log_var[:], rmean[:], 0.5, ALU.mult, ALU.mult)
                dve.drain()
                dve.scalar_tensor_tensor(out=unsure[:], in0=learned[:], scalar=2.5, in1=unsure[:], op0=ALU.mult, op1=ALU.add)
                dve.drain()
                dve.tensor_scalar(unsure[:], unsure[:], 0.0, 5.0, ALU.max, ALU.min)
                dve.drain()
                dve.tensor_scalar(unsure[:], unsure[:], TAU_LOW, 1.0 / (TAU_HIGH - TAU_LOW), ALU.subtract, ALU.mult)
                dve.drain()
                dve.tensor_scalar(unsure[:], unsure[:], 0.0, 1.0, ALU.max, ALU.min).then_inc(un_ready, 1)
                dve.reciprocal(rsum[:], rsum[:])
                dve.wait_ge(gate_ready, p + 1)
                dve.tensor_scalar(keep[:], coef[:], EARLY_EXIT, gc, ALU.is_ge, ALU.mult)
                dve.drain()
                dve.tensor_tensor(coef[:], coef[:], keep[:], ALU.mult)
                dve.drain()
                dve.tensor_tensor(coef[:], coef[:], rsum[:], ALU.mult)
                dve.drain()
                if not last:
                    norm.in_place(dve, z, z_loaded, p + 1, z_ready)
                for s in range(2):
                    for h in range(2):
                        t = ("o", s, h)
                        c = slice(h * 512, (h + 1) * 512)
                        dve.wait_ge(turns.full(t), turns.count(t, p))
                        dve.scalar_tensor_tensor(out=x[:, s, c], in0=turns.tile(t)[0:Q, :], scalar=coef[:, s:s + 1],
                                                 in1=x[:, s, c], op0=ALU.mult, op1=ALU.add).then_inc(turns.free(t), 1)
                    dve.drain().then_inc(x_done, 1)

            every_pair(dve, pair)


def experts_ffn(nc, C, banks, gate, x_in, x_out, A, early):
    NE, RANK = 8, 64
    R = NE * RANK
    with ExitStack() as ctx:
        s_ = Scope(nc, ctx, "moe")
        s_.sems += early.loaded.values()
        gT, aT, bT = (early.sb[n] for n in ("gT", "aT", "bT"))
        x, z = s_.sb("x", [Q, 2, D]), s_.sb("z", [Q, 2, D])
        zT = s_.sb("zT", [P, 2, KC, Q])
        prob, best, w8, hit = (s_.sb(n, [Q, 2, NE]) for n in ("prob", "best", "w8", "hit"))
        place, placef = s_.sb("place", [Q, 2, 8], U32), s_.sb("placef", [Q, 2, 8])
        number = s_.sb("number", [Q, NE])
        nmax, both = s_.sb("nmax", [Q, 2]), s_.sb("both", [Q, 2])
        h, hT = s_.sb("h", [Q, 2, R]), s_.sb("hT", [P, 2, R // P, Q])
        norm = Norm(s_, 2)
        x_loaded = [s_.sem(f"x_loaded{i}") for i in range(2)]
        x_stored = [s_.sem(f"x_stored{i}") for i in range(2)]
        z_loaded = [s_.sem(f"z_loaded{i}") for i in range(2)]
        z_ready, zT_ready, max_ready, prob_ready, h_ready, hT_ready, x_done, numbered = (
            s_.sem(n) for n in ("z_ready", "zT_ready", "max_ready", "prob_ready", "h_ready", "hT_ready", "x_done", "numbered"))
        turns = Turns(banks, [(("zT", s, i), 4 * s + i) for s in range(2) for i in range(2)]
                      + [((n, s), 4 * s + i) for n, i in (("gate", 2), ("h", 3)) for s in range(2)]
                      + [(("hT", s, 0), 4 * s) for s in range(2)]
                      + [(("o", s, i), 4 * s + 1 + i) for s in range(2) for i in range(2)], PAIRS)
        block = ctx.enter_context(nc.Block())

        @block.sync
        def _(sp):
            for s in range(2):
                sp.dma_start(z[:, s, :], x_in[s]).then_inc(z_loaded[s], 16)
            stream_ahead(sp, x, z, x_in, x_out, x_loaded, z_loaded, x_done, x_stored,
                         lambda s, p: (turns.full(("zT", s, 1)), turns.count(("zT", s, 1), p)))

        @block.gpsimd
        def _(pool):
            pool.iota(number[:], pattern=[[1, NE]], base=0, channel_multiplier=0,
                      allow_small_or_imprecise_dtypes=True).then_inc(numbered, 1)

        @block.tensor
        def _(pe):
            for n in ("gT", "aT", "bT"):
                pe.wait_ge(early.loaded[n], 16)
            with pe.Fori(0, PAIRS) as p:
                for s in range(2):
                    pe.wait_ge(z_ready, p * 2 + (s + 1))
                    turn_rows(pe, C, turns, z[:, s], "zT", s, p)
                for s in range(2):
                    pe.wait_ge(zT_ready, p * 2 + (s + 1))
                    for name, w, n in (("gate", gT, NE), ("h", aT, R)):
                        t = (name, s)
                        pe.wait_ge(turns.free(t), turns.count(t, p))
                        for k in range(KC):
                            mm = pe.matmul(turns.tile(t)[0:Q, 0:n], zT[:, s, k, :], w[:, k, :], start=(k == 0), stop=(k == KC - 1))
                        mm.then_inc(turns.full(t), 1)
                for s in range(2):
                    pe.wait_ge(h_ready, p * 2 + (s + 1))
                    turn_rows(pe, C, turns, h[:, s], "hT", s, p, n=1)
                for s in range(2):
                    pe.wait_ge(hT_ready, p * 2 + (s + 1))
                    project(pe, turns, hT[:, s], bT, "o", s, p)

        @block.scalar
        def _(act):
            for s in range(2):
                norm.root(act, s, s)

            def pair(p, last):
                for s in range(2):
                    copy_turned(act, turns, zT[:, s], "zT", s, p, zT_ready)
                for s in range(2):
                    t = ("gate", s)
                    act.wait_ge(max_ready, p * 2 + (s + 1))
                    act.activation(prob[:, s, :], turns.tile(t)[0:Q, 0:NE], ACT.Exp, bias=nmax[:, s:s + 1]).then_inc(turns.free(t), 1)
                    act.drain().then_inc(prob_ready, 1)
                for s in range(2):
                    copy_turned(act, turns, hT[:, s], "hT", s, p, hT_ready, n=1)
                if not last:
                    for s in range(2):
                        norm.root(act, s, p * 2 + (s + 2))

            every_pair(act, pair)

        @block.vector
        def _(dve):
            dve.wait_ge(numbered, 1)
            gc = C.gates[0:Q, gate:gate + 1]
            norm.in_place(dve, z, z_loaded, 0, z_ready)

            def pair(p, last):
                for s in range(2):
                    t = ("gate", s)
                    dve.wait_ge(turns.full(t), turns.count(t, p))
                    dve.tensor_reduce(nmax[:, s:s + 1], turns.tile(t)[0:Q, 0:NE], AX, ALU.max, negate=True).then_inc(max_ready, 1)
                for s in range(2):
                    dve.wait_ge(prob_ready, p * 2 + (s + 1))
                    dve.tensor_reduce(both[:, s:s + 1], prob[:, s, :], AX, ALU.add)
                    dve.drain()
                    dve.reciprocal(both[:, s:s + 1], both[:, s:s + 1])
                    dve.drain()
                    dve.tensor_scalar(prob[:, s, :], prob[:, s, :], both[:, s:s + 1], None, ALU.mult)
                    dve.drain()
                    dve.max(best[:, s, :], prob[:, s, :])
                    dve.drain()
                    dve.max_index(place[:, s, :], best[:, s, :], prob[:, s, :])
                    dve.tensor_tensor(both[:, s:s + 1], best[:, s, 0:1], best[:, s, 1:2], ALU.add)
                    dve.drain()
                    dve.tensor_copy(placef[:, s, :], place[:, s, :])
                    dve.reciprocal(both[:, s:s + 1], both[:, s:s + 1])
                    dve.drain()
                    dve.tensor_scalar(best[:, s, 0:2], best[:, s, 0:2], both[:, s:s + 1], gc, ALU.mult, ALU.mult)
                    dve.drain()
                    dve.tensor_scalar(w8[:, s, :], number[:], placef[:, s, 0:1], best[:, s, 0:1], ALU.is_equal, ALU.mult)
                    dve.tensor_scalar(hit[:, s, :], number[:], placef[:, s, 1:2], best[:, s, 1:2], ALU.is_equal, ALU.mult)
                    dve.drain()
                    dve.tensor_tensor(w8[:, s, :], w8[:, s, :], hit[:, s, :], ALU.add)
                    dve.drain()
                    t = ("h", s)
                    dve.wait_ge(turns.full(t), turns.count(t, p))
                    dve.tensor_tensor(h[:, s, :].rearrange("q (e r) -> q e r", e=NE),
                                      turns.tile(t)[0:Q, :].rearrange("q (e r) -> q e r", e=NE),
                                      w8[:, s, :].unsqueeze(2).broadcast_to([Q, NE, RANK]), ALU.mult).then_inc(turns.free(t), 1)
                    dve.drain().then_inc(h_ready, 1)
                if not last:
                    norm.in_place(dve, z, z_loaded, p + 1, z_ready)
                for s in range(2):
                    dve.wait_ge(x_loaded[s], p * 16 + 16)
                    for i in range(2):
                        t = ("o", s, i)
                        c = slice(i * 512, (i + 1) * 512)
                        dve.wait_ge(turns.full(t), turns.count(t, p))
                        dve.tensor_tensor(x[:, s, c], turns.tile(t)[0:Q, :], x[:, s, c], ALU.add).then_inc(turns.free(t), 1)
                    dve.drain().then_inc(x_done, 1)

            every_pair(dve, pair)


def latent_attention(nc, C, banks, gate, x_in, x_out, A, nearest):
    H, KV, HD = 16, 4, 96
    G = H // KV
    S = CTX + Q
    DK, DQ = KV * HD, H * HD
    OC = DQ // P
    SCALE = float(HD) ** -0.5
    KT = [(k * CT, CT) for k in range(CTILES)] + [(CTX, Q)]
    with ExitStack() as ctx:
        s_ = Scope(nc, ctx, "latent")
        wk, wv = s_.sb("wk", [P, KC, DK]), s_.sb("wv", [P, KC, DK])
        wq, wo = s_.sb("wq", [P, KC, DQ]), s_.sb("wo", [P, OC, D])
        x, z = s_.sb("x", [Q, 2, D]), s_.sb("z", [Q, D])
        hT = s_.sb("hT", [P, KC, S])
        kT, v = s_.sb("kT", [HD, KV, S]), s_.sb("v", [P, 4, DK])
        qT = s_.sb("qT", [HD, H, Q])
        pr, pT = s_.sb("probs", [Q, 2, S]), s_.sb("probsT", [P, 2, 4, Q])
        o, oT = s_.sb("o", [Q, DQ]), s_.sb("oT", [P, OC, Q])
        y = z
        nmax, rsum = s_.sb("nmax", [Q, H]), s_.sb("rsum", [Q, H])
        points = Nearest(s_, [0, 1, 2, 3, 4], 1, nearest, A)
        norm = Norm(s_, 1)
        wk_loaded, wv_loaded, wq_loaded, wo_loaded = (s_.sem(n) for n in ("wk_loaded", "wv_loaded", "wq_loaded", "wo_loaded"))
        x_loaded = [s_.sem(f"x_loaded{i}") for i in range(2)]
        x_stored = [s_.sem(f"x_stored{i}") for i in range(2)]
        hT_free, ctx_loaded = s_.sem("hT_free"), s_.sem("ctx_loaded")
        z_ready, zT_ready, v_ready, kT_ready, qT_ready = (
            s_.sem(n) for n in ("z_ready", "zT_ready", "v_ready", "kT_ready", "qT_ready"))
        max_ready, probs_ready, pT_ready, heads_done, o_ready, oT_ready, y_ready, x_done = (
            s_.sem(n) for n in ("max_ready", "probs_ready", "pT_ready", "heads_done", "o_ready", "oT_ready", "y_ready", "x_done"))
        groups = ([("v", i) for i in range(CTILES)] + [("zT", 0, i) for i in range(2)] + [("v", 3)]
                  + [("k", i) for i in range(KV)] + [("qT", i) for i in range(4)])
        order = [(g, i % 4) for i, g in enumerate(groups)]
        for h in range(H + 3):
            if h < H:
                order.append((("S", h), 4 + h % 2))
            if 2 <= h < H + 2:
                order.append((("pT", h - 2), 6 + h % 2))
            if h >= 3 and (h - 3) % G == 0:
                order.append((("o", (h - 3) // G), (h - 3) // G % 2))
        order += [(("oT", i), 2 + i % 2) for i in range(3)] + [(("y", i), i) for i in range(2)]
        turns = Turns(banks, order, B)
        block = ctx.enter_context(nc.Block())

        @block.sync
        def _(sp):
            def load_x(b, s):
                sp.dma_start(x[:, s, :], x_in[b]).then_inc(x_loaded[s], 16)

            def load_rest(b):
                sp.wait_ge(hT_free, b + 1)
                sp.dma_start(hT[:, :, 0:CTX], A["ctxT"][b].rearrange("(k p) n -> p k n", p=P)).then_inc(ctx_loaded, 16)
                points.load(sp, b, 0)

            with sp.Fori(0, PAIRS) as p:
                for s in range(2):
                    sp.wait_ge(x_stored[s], p * 16 + 16)
                    load_x(p * 2 + s, s)
                    load_rest(p * 2 + s)
            for s in range(2):
                sp.wait_ge(x_stored[s], 16 * PAIRS + 16)
            points.stored(sp)

        @block.gpsimd
        def _(pool):
            for s in range(2):
                pool.sem_inc(x_stored[s], 16)
            pool.dma_start(wv[:], fold(A["L0_xattn_WvT"])).then_inc(wv_loaded, 16)
            pool.dma_start(wk[:], fold(A["L0_xattn_WkT"])).then_inc(wk_loaded, 16)
            pool.dma_start(wq[:], fold(A["L0_xattn_WqT"])).then_inc(wq_loaded, 16)
            pool.dma_start(wo[:], fold(A["L0_xattn_WoT"])).then_inc(wo_loaded, 16)
            with pool.Fori(0, PAIRS) as p:
                for s in range(2):
                    pool.wait_ge(y_ready, p * 2 + (s + 1))
                    pool.tensor_tensor(x[:, s, :], x[:, s, :], y[:], ALU.add).then_inc(x_done, 1)

        @block.tensor
        def _(pe):
            pe.wait_ge(wv_loaded, 16)

            def fill(t, b, lhsT, rhs, m, n, chunks):
                pe.wait_ge(turns.free(t), turns.count(t, b))
                for k in range(chunks):
                    mm = pe.matmul(turns.tile(t)[0:m, 0:n], lhsT(k), rhs(k), start=(k == 0), stop=(k == chunks - 1))
                mm.then_inc(turns.full(t), 1)

            def sequence(b):
                pe.wait_ge(ctx_loaded, b * 16 + 16)
                for i in range(CTILES):
                    fill(("v", i), b, lambda k: hT[:, k, i * CT:(i + 1) * CT], lambda k: wv[:, k, :], CT, DK, KC)
                pe.wait_ge(z_ready, b + 1)
                turn_rows(pe, C, turns, z, "zT", 0, b)
                pe.wait_ge(zT_ready, b + 1)
                fill(("v", 3), b, lambda k: hT[:, k, CTX:S], lambda k: wv[:, k, :], Q, DK, KC)
                pe.wait_ge(wk_loaded, 16)
                for i in range(KV):
                    fill(("k", i), b, lambda k: wk[:, k, i * HD:(i + 1) * HD], lambda k: hT[:, k, :], HD, S, KC)
                pe.wait_ge(wq_loaded, 16)
                for i in range(4):
                    t = ("qT", i)
                    pe.wait_ge(turns.free(t), turns.count(t, b))
                    for c in range(3):
                        for k in range(KC):
                            mm = pe.matmul(turns.tile(t)[:, c * Q:(c + 1) * Q], wq[:, k, (3 * i + c) * P:(3 * i + c + 1) * P],
                                           hT[:, k, CTX:S], start=(k == 0), stop=(k == KC - 1))
                    mm.then_inc(turns.full(t), 1)
                pe.wait_ge(kT_ready, b + 1)
                pe.wait_ge(v_ready, b + 1)
                for step in range(H + 3):
                    h = step
                    if h < H:
                        t = ("S", h)
                        pe.wait_ge(qT_ready, b * 4 + (h // 4 + 1))
                        pe.wait_ge(turns.free(t), turns.count(t, b))
                        pe.matmul(turns.tile(t)[0:Q, 0:S], qT[:, h, :], kT[:, h // G, :], start=True, stop=True)\
                          .then_inc(turns.full(t), 1)
                    h = step - 2
                    if 0 <= h < H:
                        t = ("pT", h)
                        pe.wait_ge(probs_ready, b * H + (h + 1))
                        pe.wait_ge(turns.free(t), turns.count(t, b))
                        for k, (c, n) in enumerate(KT):
                            mm = pe.transpose(turns.tile(t)[0:n, k * Q:(k + 1) * Q], pr[:, h % 2, c:c + n], C.ident[0:Q, 0:Q])
                        mm.then_inc(turns.full(t), 1)
                    h = step - 3
                    if h >= 0:
                        t = ("o", h // G)
                        pe.wait_ge(pT_ready, b * H + (h + 1))
                        if h % G == 0:
                            pe.wait_ge(turns.free(t), turns.count(t, b))
                        for k, (c, n) in enumerate(KT):
                            mm = pe.matmul(turns.tile(t)[0:Q, h % G * HD:(h % G + 1) * HD], pT[0:n, h % 2, k, :],
                                           v[0:n, k, h // G * HD:(h // G + 1) * HD], start=(k == 0), stop=(k == len(KT) - 1))
                        mm.then_inc(turns.full(t) if h % G == G - 1 else heads_done, 1)
                for i in range(3):
                    t = ("oT", i)
                    pe.wait_ge(o_ready, b * KV + min(KV, (i * 512 + 511) // (G * HD) + 1))
                    pe.wait_ge(turns.free(t), turns.count(t, b))
                    for j in range(4):
                        c = (4 * i + j) * P
                        mm = pe.transpose(turns.tile(t)[:, j * Q:(j + 1) * Q], o[:, c:c + P], C.ident[0:Q, 0:Q])
                    mm.then_inc(turns.full(t), 1)
                pe.wait_ge(oT_ready, b + 1)
                pe.wait_ge(wo_loaded, 16)
                for i in range(2):
                    fill(("y", i), b, lambda k: oT[:, k, :], lambda k: wo[:, k, i * 512:(i + 1) * 512], Q, 512, OC)

            with pe.Fori(0, B) as b:
                sequence(b)

        @block.scalar
        def _(act):
            with act.Fori(0, PAIRS) as p:
                for s in range(2):
                    b = p * 2 + s

                    def empty(t, dst, src, scale=1.0):
                        act.wait_ge(turns.full(t), turns.count(t, b))
                        act.activation(dst, src, ACT.Copy, scale=scale).then_inc(turns.free(t), 1)

                    norm.root(act, 0, b)
                    for i in range(CTILES):
                        empty(("v", i), v[0:CT, i, :], turns.tile(("v", i))[0:CT, 0:DK])
                        if i == 1:
                            points.squares(act, b, 0, 0)
                    copy_turned(act, turns, hT[:, :, CTX:S], "zT", 0, b, zT_ready)
                    empty(("v", 3), v[0:Q, 3, :], turns.tile(("v", 3))[0:Q, 0:DK])
                    act.drain().then_inc(v_ready, 1)
                    for i in range(KV):
                        empty(("k", i), kT[:, i, :], turns.tile(("k", i))[0:HD, 0:S])
                        points.squares(act, b, 0, i + 1)
                    act.drain().then_inc(kT_ready, 1)
                    for i in range(4):
                        t = ("qT", i)
                        act.wait_ge(turns.full(t), turns.count(t, b))
                        act.activation(qT[:, 4 * i:4 * i + 3, :], turns.tile(t)[0:HD, 0:3 * Q].rearrange("p (j q) -> p j q", j=3),
                                       ACT.Copy, scale=SCALE)
                        for c in range(3):
                            op = act.activation(qT[c * (P - HD):(c + 1) * (P - HD), 4 * i + 3, :], turns.tile(t)[HD:P, c * Q:(c + 1) * Q],
                                                ACT.Copy, scale=SCALE)
                        op.then_inc(turns.free(t), 1)
                        act.drain().then_inc(qT_ready, 1)
                    act.sem_inc(hT_free, 1)
                    for h in range(H):
                        t = ("S", h)
                        act.wait_ge(max_ready, b * H + (h + 1))
                        if h >= 2:
                            act.wait_ge(turns.full(("pT", h - 2)), turns.count(("pT", h - 2), b))
                        act.activation(pr[:, h % 2, :], turns.tile(t)[0:Q, 0:S], ACT.Exp, bias=nmax[:, h:h + 1],
                                       accum_out=rsum[:, h:h + 1]).then_inc(turns.free(t), 1)
                        act.drain().then_inc(probs_ready, 1)
                    points.store(act, b)
                    for i in range(3):
                        empty(("oT", i), oT[:, 4 * i:4 * i + 4, :],
                              turns.tile(("oT", i))[:, 0:4 * Q].rearrange("p (j q) -> p j q", j=4))
                    act.drain().then_inc(oT_ready, 1)
                    for i in range(2):
                        empty(("y", i), y[:, i * 512:(i + 1) * 512], turns.tile(("y", i))[0:Q, :],
                              scale=C.gates[0:Q, gate:gate + 1])
                    act.drain().then_inc(y_ready, 1)
                    act.wait_ge(x_done, b + 1)
                    act.dma_start(x_out[b], x[:, s, :]).then_inc(x_stored[s], 16)

        @block.vector
        def _(dve):
            dve.sem_inc(hT_free, 1)
            points.credits(dve)
            with dve.Fori(0, PAIRS) as p:
                for s in range(2):
                    b = p * 2 + s
                    dve.wait_ge(x_loaded[s], p * 16 + 16)
                    norm.statistics(dve, x[:, s, :], 0)
                    norm.scale(dve, x[:, s, :], z[:], 0, b).then_inc(z_ready, 1)
                    points.begin(dve, b, 0, b)
                    for i in range(5):
                        points.sort(dve, b, 0, i)
                    for step in range(H + 3):
                        h = step
                        if h < H:
                            t = ("S", h)
                            dve.wait_ge(turns.full(t), turns.count(t, b))
                            dve.tensor_reduce(nmax[:, h:h + 1], turns.tile(t)[0:Q, 0:S], AX, ALU.max, negate=True)\
                               .then_inc(max_ready, 1)
                        h = step - 2
                        if 0 <= h < H:
                            t = ("pT", h)
                            dve.wait_ge(turns.full(t), turns.count(t, b))
                            if h >= 2:
                                g = h - 2
                                if g % G == G - 1:
                                    dve.wait_ge(turns.full(("o", g // G)), turns.count(("o", g // G), b))
                                else:
                                    dve.wait_ge(heads_done, b * (H - KV) + (g - g // G + 1))
                            dve.tensor_copy(pT[0:CT, h % 2, 0:3, :], turns.tile(t)[0:CT, 0:3 * Q].rearrange("p (k q) -> p k q", k=3))
                            dve.tensor_copy(pT[0:Q, h % 2, 3, :], turns.tile(t)[0:Q, 3 * Q:4 * Q]).then_inc(turns.free(t), 1)
                            dve.drain().then_inc(pT_ready, 1)
                        h = step - 3
                        if h >= 0 and h % G == G - 1:
                            g = h // G
                            t = ("o", g)
                            dve.reciprocal(rsum[:, g * G:(g + 1) * G], rsum[:, g * G:(g + 1) * G])
                            dve.drain()
                            dve.wait_ge(turns.full(t), turns.count(t, b))
                            dve.tensor_tensor(o[:, g * G * HD:(g + 1) * G * HD].rearrange("q (h d) -> q h d", h=G),
                                              turns.tile(t)[0:Q, 0:G * HD].rearrange("q (h d) -> q h d", h=G),
                                              rsum[:, g * G:(g + 1) * G].unsqueeze(2).broadcast_to([Q, G, HD]), ALU.mult)\
                               .then_inc(turns.free(t), 1)
                            dve.drain().then_inc(o_ready, 1)


def grouped_attention(nc, C, banks, gate, x_in, x_out, A, wall, scales, codes, early):
    HD, QUADS = 32, 8
    DKV = 256
    SCALE = float(HD) ** -0.5
    with ExitStack() as ctx:
        s_ = Scope(nc, ctx, "grouped")
        s_.sems += early.loaded.values()
        wk, wv, wq, wo = (early.sb[n] for n in ("wk", "wv", "wq", "wo"))
        x = s_.sb("x", [Q, 2, D])
        zT, qT = (s_.sb(n, [P, KC, Q]) for n in ("zT", "qT"))
        oT = zT
        cT = s_.sb("ctxT", [P, 2, KC, CTX])
        kT, v = s_.sb("kT", [P, 4, 2, CTX]), s_.sb("v", [CT, CTILES, DKV])
        pr, pT = s_.sb("probs", [Q, 3, 4, CTX]), s_.sb("probsT", [CT, 2, CTILES, 4, Q])
        q = pr[:, 0].rearrange("q j n -> q (j n)")[:, 0:D]
        z = pr[:, 2].rearrange("q j n -> q (j n)")[:, 0:D]
        nmax, rsum = s_.sb("nmax", [Q, QUADS, 4]), s_.sb("rsum", [Q, QUADS, 4])
        raw, rounded, code = s_.sb("raw", [P, 2, 4 * D]), s_.sb("rounded", [P, 2, D], BF16), s_.sb("code", [P, 2, 4 * D], FP8)
        scale, rscale = s_.sb("scale", [P, 2, 4]), s_.sb("rscale", [P, 2, 4])
        raw_loaded = [s_.sem(f"raw_loaded{i}") for i in range(2)]
        code_stored = [s_.sem(f"code_stored{i}") for i in range(2)]
        raw_free, rounded_ready, code_ready = s_.sem("raw_free"), s_.sem("rounded_ready"), s_.sem("code_ready")
        norm = Norm(s_, 1)
        x_loaded = [s_.sem(f"x_loaded{i}") for i in range(2)]
        x_stored = [s_.sem(f"x_stored{i}") for i in range(2)]
        ctx_loaded = [s_.sem(f"ctx_loaded{i}") for i in range(2)]
        ctx_free = [s_.sem(f"ctx_free{i}") for i in range(2)]
        z_ready, zT_ready, v_ready, q_ready, qT_ready = (
            s_.sem(n) for n in ("z_ready", "zT_ready", "v_ready", "q_ready", "qT_ready"))
        last_ready, zeroed = s_.sem("last_ready"), s_.sem("zeroed")
        passed = s_.sem("passed")
        max_ready, exp_ready, sum_ready, probs_ready, pT_ready, heads_done, oT_ready, x_done = (
            s_.sem(n) for n in ("max_ready", "exp_ready", "sum_ready", "probs_ready", "pT_ready", "heads_done", "oT_ready", "x_done"))
        order = [(("k", i), i) for i in range(2)] + [(("zT", 0, i), 5 + i) for i in range(2)] + [(("v", 0), 4)]
        order += [(("w", 0, 0), 3), (("w", 0, 1), 7), (("q", 0, 0), 0), (("w", 0, 2), 3), (("w", 0, 3), 7), (("q", 0, 1), 1)]
        order += [(("w", 1, 0), 3), (("w", 1, 1), 7), (("v", 1), 5), (("w", 1, 2), 6), (("w", 1, 3), 7)]
        order += [(("qT", 0, i), 2 + i) for i in range(2)] + [(("v", 2), 6)]
        order += [(("w", 2, i), (4, 7, 5, 7)[i]) for i in range(4)]
        for m in range(QUADS + 3):
            if m < QUADS:
                order += [(("S", m, j), j) for j in range(4)]
            if 2 <= m < QUADS + 2:
                order += [(("pT", m - 2, k), 4 + k) for k in range(CTILES)]
            if m >= 3 and (m - 3) % 4 == 0:
                order.append((("o", (m - 3) // 4), 7))
        order += [(("y", 0, i), 6 - i) for i in range(2)]
        turns = Turns(banks, order, B)
        block = ctx.enter_context(nc.Block())

        def unit(p, s, n):
            i = 3 * s + n
            return i % 2, p * 3 + i // 2, (p * 4 + (2 * s + n) if n < 2 else p * 2 + (16 + s))

        def every(eng, sequence):
            with eng.Fori(0, PAIRS - 1) as p:
                for s in range(2):
                    sequence(p, s, False)
            for s in range(2):
                sequence(PAIRS - 1, s, s == 1)

        @block.sync
        def _(sp):
            for s in range(2):
                sp.dma_start(x[:, s, :], x_in[s]).then_inc(x_loaded[s], 16)
                sp.dma_start(cT[:, s], A["ctxT"][s].rearrange("(k p) n -> p k n", p=P)).then_inc(ctx_loaded[s], 16)

            def sequence(p, s, last):
                for n in range(3):
                    slot, turn, u = unit(p, s, n)
                    sp.wait_ge(code_ready, p * 6 + (3 * s + n + 1))
                    sp.dma_start(codes[u], code[:, slot, :].bitcast(U32)).then_inc(code_stored[slot], 16)
                    sp.dma_start(scales[u], scale[:, slot, :]).then_inc(code_stored[slot], 16)
                more = not isinstance(p, int)
                if more:
                    sp.wait_ge(ctx_free[s], p + 1)
                    sp.dma_start(cT[:, s], A["ctxT"][p * 2 + (s + 2)].rearrange("(k p) n -> p k n", p=P)).then_inc(ctx_loaded[s], 16)
                sp.wait_ge(x_done, p * 2 + (s + 1))
                sp.dma_start(x_out[p * 2 + s], x[:, s, :]).then_inc(x_stored[s], 16)
                sp.wait_ge(x_stored[s], p * 16 + 16)
                if more:
                    sp.dma_start(x[:, s, :], x_in[p * 2 + (s + 2)]).then_inc(x_loaded[s], 16)

            every(sp, sequence)
            for i in range(2):
                sp.wait_ge(code_stored[i], 32 * 3 * PAIRS + 32)

        @block.tensor
        def _(pe):
            for n in ("wk", "wv", "wq", "wo"):
                pe.wait_ge(early.loaded[n], 16)

            def fill(t, b, lhsT, rhs, m, n, chunks):
                pe.wait_ge(turns.free(t), turns.count(t, b))
                for k in range(chunks):
                    mm = pe.matmul(turns.tile(t)[0:m, 0:n], lhsT(k), rhs(k), start=(k == 0), stop=(k == chunks - 1))
                mm.then_inc(turns.full(t), 1)

            def turned(p, s, n, first, last):
                for i in range(first, last):
                    t = ("w", n, i)
                    pe.wait_ge(rounded_ready, (p * 6 + (3 * s + n)) * 4 + (i + 1))
                    pe.wait_ge(turns.free(t), turns.count(t, p * 2 + s))
                    o = turns.tile(t)[:].bitcast(BF16)
                    for k in range(KC):
                        mm = pe.transpose(o[:, k * P:(k + 1) * P], rounded[:, i % 2, k * P:(k + 1) * P], C.identb[:])
                    mm.then_inc(turns.full(t), 1)

            with pe.Fori(0, PAIRS) as p:
                for s in range(2):
                    b = p * 2 + s
                    pe.wait_ge(ctx_loaded[s], p * 16 + 16)
                    for i in range(2):
                        fill(("k", i), b, lambda k: wk[:, k, i * P:(i + 1) * P], lambda k: cT[:, s, k, :], P, CTX, KC)

                    def values(i):
                        fill(("v", i), b, lambda k: cT[:, s, k, i * CT:(i + 1) * CT], lambda k: wv[:, k, :], CT, DKV, KC)

                    pe.wait_ge(z_ready, b + 1)
                    turn_rows(pe, C, turns, z, "zT", 0, b)
                    values(0)
                    turned(p, s, 0, 0, 2)
                    pe.wait_ge(zT_ready, b + 1)
                    for i in range(2):
                        fill(("q", 0, i), b, lambda k: zT[:, k, :], lambda k: wq[:, k, i * 512:(i + 1) * 512], Q, 512, KC)
                        turned(p, s, i, 2 * (1 - i), 2 * (1 - i) + 2)
                    values(1)
                    turned(p, s, 1, 2, 4)
                    pe.wait_ge(q_ready, b + 1)
                    turn_rows(pe, C, turns, q, "qT", 0, b)
                    values(2)
                    turned(p, s, 2, 0, 4)
                    pe.wait_ge(qT_ready, b + 1)
                    for step in range(QUADS + 3):
                        m = step
                        if m < QUADS:
                            for j in range(4):
                                t = ("S", m, j)
                                pe.wait_ge(turns.free(t), turns.count(t, b))
                                pe.matmul(turns.tile(t)[0:Q, 0:CTX], qT[:, m, :], kT[:, j, m // 4, :], start=True, stop=True)\
                                  .then_inc(turns.full(t), 1)
                        m = step - 2
                        if 0 <= m < QUADS:
                            pe.wait_ge(probs_ready, (b * QUADS + (m + 1)) * 4)
                            for k in range(CTILES):
                                t = ("pT", m, k)
                                pe.wait_ge(turns.free(t), turns.count(t, b))
                                for j in range(4):
                                    mm = pe.transpose(turns.tile(t)[0:CT, j * Q:(j + 1) * Q], pr[:, m % 3, j, k * CT:(k + 1) * CT],
                                                      C.ident[0:Q, 0:Q])
                                mm.then_inc(turns.full(t), 1)
                        m = step - 3
                        if m >= 0:
                            t = ("o", m // 4)
                            pe.wait_ge(pT_ready, b * QUADS + (m + 1))
                            pe.wait_ge(last_ready, b * QUADS + (m + 1))
                            if m == 0:
                                pe.wait_ge(v_ready, b + 1)
                            if m % 4 == 0:
                                pe.wait_ge(turns.free(t), turns.count(t, b))
                            for k in range(CTILES):
                                for j in range(4):
                                    g = 4 * (m // 4) + j
                                    mm = pe.matmul(turns.tile(t)[j * HD:(j + 1) * HD, (m % 4) * Q:(m % 4 + 1) * Q],
                                                   v[:, k, g * HD:(g + 1) * HD], pT[:, m % 2, k, j, :],
                                                   start=(k == 0), stop=(k == CTILES - 1))
                            mm.then_inc(turns.full(t) if m % 4 == 3 else heads_done, 1)
                    pe.wait_ge(oT_ready, b * 2 + 2)
                    project(pe, turns, oT, wo, "y", 0, b)

        @block.scalar
        def _(act):
            for i in range(2):
                act.sem_inc(code_stored[i], 32)
            norm.root(act, 0, 0)

            def sequence(p, s, last):
                b = p * 2 + s

                def coded(n, first, last):
                    slot, turn, _ = unit(p, s, n)
                    if first == 0:
                        act.wait_ge(code_stored[slot], turn * 32 + 32)
                    for i in range(first, last):
                        t = ("w", n, i)
                        act.wait_ge(turns.full(t), turns.count(t, b))
                        act.sem_inc(passed, 1)
                        o = code[:, slot, :].rearrange("p (k i c) -> p k i c", i=4, c=P)[:, :, i, :] if n < 2 else \
                            code[:, slot, i * D:(i + 1) * D].rearrange("p (k c) -> p k c", c=P)
                        act.copy(o, turns.tile(t)[:].bitcast(BF16).rearrange("p (k c) -> p k c", c=P), saturate=False)\
                           .then_inc(turns.free(t), 1)
                    if last == 4:
                        act.drain().then_inc(code_ready, 1)

                def empty(t, dst, src, scale=1.0):
                    act.wait_ge(turns.full(t), turns.count(t, b))
                    act.activation(dst, src, ACT.Copy, scale=scale).then_inc(turns.free(t), 1)

                for i in range(2):
                    t = ("k", i)
                    act.wait_ge(turns.full(t), turns.count(t, b))
                    if i == 0:
                        act.wait_ge(zeroed, 1)
                    for j in range(4):
                        r = slice(j * HD, (j + 1) * HD)
                        op = act.activation(kT[r, j, i, :], turns.tile(t)[r, 0:CTX], ACT.Copy)
                    op.then_inc(turns.free(t), 1)
                copy_turned(act, turns, zT, "zT", 0, b, zT_ready)

                def values(i):
                    empty(("v", i), v[:, i, :], turns.tile(("v", i))[0:CT, 0:DKV])

                values(0)
                coded(0, 0, 2)
                for i in range(2):
                    empty(("q", 0, i), q[:, i * 512:(i + 1) * 512], turns.tile(("q", 0, i))[0:Q, :], scale=SCALE)
                    if i == 1:
                        act.drain().then_inc(q_ready, 1)
                    coded(i, 2 * (1 - i), 2 * (1 - i) + 2)
                values(1)
                coded(1, 2, 4)
                copy_turned(act, turns, qT, "qT", 0, b, qT_ready)
                values(2)
                act.drain().then_inc(v_ready, 1)
                act.sem_inc(ctx_free[s], 1)
                coded(2, 0, 4)

                def last_tile(m):
                    t = ("pT", m, 2)
                    act.wait_ge(turns.full(t), turns.count(t, b))
                    if m >= 2:
                        if m == 5:
                            act.wait_ge(turns.full(("o", 0)), turns.count(("o", 0), b))
                        else:
                            act.wait_ge(heads_done, b * 6 + (m - 1 - (m > 5)))
                    act.activation(pT[:, m % 2, 2, :, :], turns.tile(t)[0:CT, 0:4 * Q].rearrange("p (j q) -> p j q", j=4),
                                   ACT.Copy).then_inc(turns.free(t), 1)
                    act.drain().then_inc(last_ready, 1)

                def outputs(g):
                    empty(("o", g), oT[:, 4 * g:4 * g + 4, :],
                          turns.tile(("o", g))[:, 0:4 * Q].rearrange("p (m q) -> p m q", m=4))
                    act.drain().then_inc(oT_ready, 1)

                for m in range(QUADS + 2):
                    if m < QUADS:
                        for j in range(4):
                            t = ("S", m, j)
                            act.wait_ge(max_ready, (b * QUADS + m) * 4 + (j + 1))
                            if m >= 3 and j == 0:
                                u = ("pT", m - 3, 2)
                                act.wait_ge(turns.full(u), turns.count(u, b))
                            act.activation(pr[:, m % 3, j, :], turns.tile(t)[0:Q, 0:CTX], ACT.Exp, bias=nmax[:, m, j:j + 1],
                                           accum_out=rsum[:, m, j:j + 1]).then_inc(turns.free(t), 1)
                        act.drain().then_inc(exp_ready, 1)
                    if m >= 2:
                        last_tile(m - 2)
                    if m == 7:
                        outputs(0)
                if not last:
                    norm.root(act, 0, b + 1)
                outputs(1)

            every(act, sequence)

        @block.gpsimd
        def _(pool):
            for i in range(2):
                pool.dma_start(raw[:, i], wall[i]).then_inc(raw_loaded[i], 16)

            def sequence(p, s, last):
                b = p * 2 + s
                for n in range(3):
                    after = 3 * s + n + 2
                    if isinstance(p, int) and after >= 6:
                        continue
                    slot, _, u = unit(p + after // 6, after // 3 % 2, after % 3)
                    pool.wait_ge(raw_free, p * 6 + (3 * s + n + 1))
                    pool.dma_start(raw[:, slot], wall[u]).then_inc(raw_loaded[slot], 16)
                for m in range(QUADS):
                    pool.wait_ge(sum_ready, b * QUADS + (m + 1))
                    pool.sem_inc(passed, 1)
                    for j in range(4):
                        pool.tensor_scalar(pr[:, m % 3, j, :], pr[:, m % 3, j, :], rsum[:, m, j:j + 1], 1.0, ALU.mult, ALU.mult)\
                            .then_inc(probs_ready, 1)

            every(pool, sequence)

        @block.vector
        def _(dve):
            def rounding(p, s, n):
                slot, turn, _ = unit(p, s, n)
                m = 4 if n < 2 else 1
                sc, rs = scale[:, slot, 0:m], rscale[:, slot, 0:m]
                dve.wait_ge(raw_loaded[slot], turn * 16 + 16)
                dve.wait_ge(code_stored[slot], turn * 32 + 32)
                dve.tensor_reduce(sc, raw[:, slot, :].rearrange("p (r w) -> p r w", r=m), AX, ALU.max, apply_absolute_value=True)
                dve.drain()
                divide(dve, sc, rs, 7.0)
                dve.tensor_scalar(sc, sc, 1e-8, None, ALU.max)
                dve.drain()
                dve.reciprocal(rs, sc)
                dve.drain()
                for i in range(4):
                    v = raw[:, slot, i * D:(i + 1) * D]
                    dve.tensor_scalar(v, v, rscale[:, slot, i % m:i % m + 1], MAGIC, ALU.mult, ALU.add)
                dve.drain()
                for i in range(4):
                    if i >= 2 or n >= 1:
                        t = ("w", n, i - 2) if i >= 2 else ("w", n - 1, i + 2)
                        dve.wait_ge(turns.full(t), turns.count(t, p * 2 + s))
                    op = dve.tensor_scalar(rounded[:, i % 2, :], raw[:, slot, i * D:(i + 1) * D], MAGIC, 7.0, ALU.subtract, ALU.min)
                    op.then_inc(rounded_ready, 1)
                dve.drain().then_inc(raw_free, 1)

            def normalised(p, s, b):
                dve.wait_ge(x_loaded[s], p * 16 + 16)
                norm.statistics(dve, x[:, s, :], 0)
                norm.scale(dve, x[:, s, :], z[:], 0, b).then_inc(z_ready, 1)

            dve.memset(kT[:], 0.0)
            dve.drain().then_inc(zeroed, 1)
            dve.memset(scale[:], 1.0)
            dve.drain()
            normalised(0, 0, 0)

            def sequence(p, s, last):
                b = p * 2 + s
                for n in range(3):
                    rounding(p, s, n)
                for step in range(QUADS + 2):
                    m = step
                    if m < QUADS:
                        for j in range(4):
                            t = ("S", m, j)
                            dve.wait_ge(turns.full(t), turns.count(t, b))
                            dve.tensor_reduce(nmax[:, m, j:j + 1], turns.tile(t)[0:Q, 0:CTX], AX, ALU.max, negate=True)\
                               .then_inc(max_ready, 1)
                        dve.wait_ge(exp_ready, b * QUADS + (m + 1))
                        dve.reciprocal(rsum[:, m, :], rsum[:, m, :]).then_inc(sum_ready, 1)
                    m = step - 2
                    if m >= 0:
                        if m >= 2:
                            if m == 5:
                                dve.wait_ge(turns.full(("o", 0)), turns.count(("o", 0), b))
                            else:
                                dve.wait_ge(heads_done, b * 6 + (m - 1 - (m > 5)))
                        for k in range(2):
                            t = ("pT", m, k)
                            dve.wait_ge(turns.full(t), turns.count(t, b))
                            dve.tensor_copy(pT[:, m % 2, k, :, :], turns.tile(t)[0:CT, 0:4 * Q].rearrange("p (j q) -> p j q", j=4))\
                               .then_inc(turns.free(t), 1)
                        dve.drain().then_inc(pT_ready, 1)
                if not last:
                    normalised(p + s, 1 - s, b + 1)
                for i in range(2):
                    t = ("y", 0, i)
                    c = slice(i * 512, (i + 1) * 512)
                    dve.wait_ge(turns.full(t), turns.count(t, b))
                    dve.scalar_tensor_tensor(out=x[:, s, c], in0=turns.tile(t)[0:Q, :], scalar=C.gates[0:Q, gate:gate + 1],
                                             in1=x[:, s, c], op0=ALU.mult, op1=ALU.add).then_inc(turns.free(t), 1)
                dve.drain().then_inc(x_done, 1)

            every(dve, sequence)


def hadamard_ffn(nc, C, banks, gate, x_in, x_out, A, scales, codes):
    F, NF, STEPS = 4096, 32, 8
    G = NF // STEPS
    SPLIT = 96
    with ExitStack() as ctx:
        s_ = Scope(nc, ctx, "ffn")
        wgu, wd = s_.sb("wgu", [P, 16, F], FP8), s_.sb("wd", [P, 8, F], FP8)
        sgu, sd = s_.sb("sgu", [P, 16, 4]), s_.sb("sd", [P, 8, 4])
        had = s_.sb("had", [P, P])
        sdb = s_.sb("sdb", [Q, D])
        x, z = s_.sb("x", [Q, 2, D]), s_.sb("z", [Q, D])
        ha, hb = s_.sb("ha", [Q, F]), s_.sb("hb", [Q, F])
        y = s_.sb("y", [Q, 512])
        q, hq = s_.sb("q", [Q, D], BF16), s_.sb("hq", [Q, F], BF16)
        qT, hqT = s_.sb("qT", [P, KC, Q], BF16), s_.sb("hqT", [P, NF, Q], BF16)
        h = s_.sb("h", [P, NF, Q])
        gs, sl, us = (s_.sb(n, [P, 2, G, Q]) for n in ("gs", "sl", "us"))
        sxb = s_.sb("sxb", [P, Q])
        sx, rsx, rsh, sh = (*(s_.sb(n, [Q, 1]) for n in ("sx", "rsx", "rsh")), s_.sb("sh", [Q, 2]))
        norm = Norm(s_, 1)
        sgu_loaded, wd_loaded, sdb_ready, z_loaded = (s_.sem(n) for n in ("sgu_loaded", "wd_loaded", "sdb_ready", "z_loaded"))
        gu_loaded = [s_.sem(f"gu_loaded{i}") for i in range(4)]
        passed = s_.sem("passed")
        x_loaded = [s_.sem(f"x_loaded{i}") for i in range(2)]
        x_stored = [s_.sem(f"x_stored{i}") for i in range(2)]
        q_ready, qT_ready, gs_ready, sl_ready, us_ready, h_ready = (
            s_.sem(n) for n in ("q_ready", "qT_ready", "gs_ready", "sl_ready", "us_ready", "h_ready"))
        ha_ready, ha_free, sum_ready, diff_ready, hq_ready, hqT_ready, x_done = (
            s_.sem(n) for n in ("ha_ready", "ha_free", "sum_ready", "diff_ready", "hq_ready", "hqT_ready", "x_done"))
        prep = Turns(banks, [(("sd", i), 6 + i) for i in range(2)], 1)
        order = [("xT", 0), ("sx", 1)]
        for j in range(STEPS):
            order += [(("g", j), 2 * (j % 2)), (("u", j), 2 * (j % 2) + 1)]
        ahead = Turns(banks, order, B)
        turns = Turns(banks, [(("h", i), 4 + i % 2) for i in range(8)], B)
        behind = Turns(banks, [(("hT", i), 6 + i % 2) for i in range(4)] + [(("y", i), 6 + i) for i in range(2)], B)
        block = ctx.enter_context(nc.Block())

        def rounds(eng, sequence):
            sequence(0, 0, 0, True, True, True)
            with eng.Fori(0, PAIRS - 2) as p:
                for s in range(2):
                    sequence(p * 2 + (1 + s), 1 - s, p + s, False, True, True)
            for b in range(B - 3, B):
                sequence(b, b % 2, b // 2, False, b + 1 < B, b + 2 < B)

        @block.sync
        def _(sp):
            sp.dma_start(z[:], x_in[0]).then_inc(z_loaded, 16)
            sp.dma_start(sgu[:], scales[0:16].rearrange("u p r -> p u r")).then_inc(sgu_loaded, 16)
            for i in range(4):
                for u in (2 * i, 8 + 2 * i):
                    sp.dma_start(wgu[:, u:u + 2, :].bitcast(U32), codes[u:u + 2].rearrange("u p w -> p u w"))\
                      .then_inc(gu_loaded[i], 16)
            sp.dma_start(had[:], A["hadamard"]).then_inc(wd_loaded, 16)
            sp.dma_start(sd[:], scales[16:24].rearrange("u p r -> p u r")).then_inc(wd_loaded, 16)
            sp.dma_start(wd[:].bitcast(U32), codes[16:24].rearrange("u p w -> p u w")).then_inc(wd_loaded, 16)
            for s in range(2):
                sp.dma_start(x[:, s, :], x_in[s]).then_inc(x_loaded[s], 16)
            sp.wait_ge(q_ready, 1)
            sp.dma_start(z[:], x_in[1]).then_inc(z_loaded, 16)

            def store(b, slot, turn):
                sp.wait_ge(x_done, b + 1)
                sp.dma_start(x_out[b], x[:, slot, :]).then_inc(x_stored[slot], 16)
                sp.wait_ge(x_stored[slot], turn * 16 + 16)

            def sequence(b, slot, turn, first, gate_up, quantise):
                if quantise:
                    sp.wait_ge(q_ready, b + 2)
                    sp.dma_start(z[:], x_in[b + 2]).then_inc(z_loaded, 16)
                if not first:
                    store(b - 1, 1 - slot, turn + (slot - 1))
                    if gate_up:
                        sp.dma_start(x[:, 1 - slot, :], x_in[b + 1]).then_inc(x_loaded[1 - slot], 16)

            rounds(sp, sequence)
            store(B - 1, 1, PAIRS - 1)

        @block.tensor
        def _(pe):
            def entered(b):
                t = "xT"
                pe.wait_ge(q_ready, b + 1)
                pe.wait_ge(ahead.free(t), ahead.count(t, b))
                o = ahead.tile(t)[:].bitcast(BF16)
                for k in range(KC):
                    mm = pe.transpose(o[:, k * Q:(k + 1) * Q], q[:, k * P:(k + 1) * P], C.identb[0:Q, 0:Q])
                mm.then_inc(ahead.full(t), 1)
                t = "sx"
                pe.wait_ge(ahead.free(t), ahead.count(t, b))
                pe.matmul(ahead.tile(t)[:, 0:Q], sx[:].broadcast_to([Q, P]), C.ident[0:Q, 0:Q], start=True, stop=True)\
                  .then_inc(ahead.full(t), 1)

            def gate_and_up(b, between=lambda j: None):
                pe.wait_ge(qT_ready, b + 1)
                for j in range(STEPS):
                    between(j)
                    for name, u0 in (("g", 0), ("u", 8)):
                        t = (name, j)
                        pe.wait_ge(ahead.free(t), ahead.count(t, b))
                        pe.sem_inc(passed, 1)
                        for i in range(G):
                            f = G * j + i
                            for k in range(KC):
                                c = (k * 4 + f % 4) * P
                                mm = pe.matmul(ahead.tile(t)[:, i * Q:(i + 1) * Q], wgu[:, u0 + f // 4, c:c + P], qT[:, k, :],
                                               start=(k == 0), stop=(k == KC - 1))
                        mm.then_inc(ahead.full(t), 1)

            entered(0)
            gate_and_up(0, lambda j: pe.wait_ge(gu_loaded[j // 2], 32) if j % 2 == 0 else None)
            pe.wait_ge(wd_loaded, 16 * 3)
            for i in range(2):
                t = ("sd", i)
                pe.wait_ge(prep.free(t), prep.count(t, 0))
                for u in range(4):
                    mm = pe.matmul(prep.tile(t)[0:Q, u * P:(u + 1) * P], sd[:, 4 * i + u, 0:1].broadcast_to([P, Q]), C.ident[:],
                                   start=True, stop=True)
                mm.then_inc(prep.full(t), 1)

            def turned(b):
                pe.wait_ge(hq_ready, b + 1)
                for i in range(4):
                    t = ("hT", i)
                    pe.wait_ge(behind.free(t), behind.count(t, b))
                    o = behind.tile(t)[:].bitcast(BF16)
                    for c in range(8):
                        mm = pe.transpose(o[:, c * Q:(c + 1) * Q], hq[:, (8 * i + c) * P:(8 * i + c + 1) * P], C.identb[0:Q, 0:Q])
                    mm.then_inc(behind.full(t), 1)

            def down(b, i):
                if i == 0:
                    pe.wait_ge(hqT_ready, b + 1)
                t = ("y", i)
                pe.wait_ge(behind.free(t), behind.count(t, b))
                pe.sem_inc(passed, 1)
                for c in range(NF):
                    mm = pe.matmul(behind.tile(t)[0:Q, :], hqT[:, c, :], wd[:, 4 * i:4 * i + 4, c * P:(c + 1) * P],
                                   start=(c == 0), stop=(c == NF - 1))
                mm.then_inc(behind.full(t), 1)

            def sequence(b, slot, turn, first, gate_up, quantise):
                for i in range(8):
                    t = ("h", i)
                    pe.wait_ge(h_ready, b * STEPS + (i + 1))
                    pe.wait_ge(turns.free(t), turns.count(t, b))
                    for c in range(4):
                        mm = pe.matmul(turns.tile(t)[0:Q, c * P:(c + 1) * P], h[:, 4 * i + c, :], had[:], start=True, stop=True)
                    mm.then_inc(turns.full(t), 1)
                if not first:
                    turned(b - 1)
                if gate_up:
                    entered(b + 1)
                    gate_and_up(b + 1, lambda j: down(b - 1, j // 3 - 1) if j in (3, 6) and not first else None)
                else:
                    for i in range(2):
                        down(b - 1, i)

            rounds(pe, sequence)
            turned(B - 1)
            for i in range(2):
                down(B - 1, i)

        @block.scalar
        def _(act):
            def entered(b):
                act.wait_ge(ahead.full("xT"), ahead.count("xT", b))
                act.copy(qT[:], ahead.tile("xT")[:].bitcast(BF16)[:, 0:KC * Q].rearrange("p (k q) -> p k q", k=KC))\
                   .then_inc(ahead.free("xT"), 1)
                act.wait_ge(ahead.full("sx"), ahead.count("sx", b))
                if not isinstance(b, int) or b > 0:
                    act.wait_ge(us_ready, b * STEPS)
                act.activation(sxb[:], ahead.tile("sx")[:, 0:Q], ACT.Copy).then_inc(ahead.free("sx"), 1)
                act.drain().then_inc(qT_ready, 1)

            def gate_and_up(b, quantise):
                for j in range(STEPS):
                    if j == STEPS - 1 and quantise:
                        norm.root(act, 0, b + 1)
                    act.wait_ge(gs_ready, b * STEPS + (j + 1))
                    if j >= 2 or not isinstance(b, int) or b > 0:
                        act.wait_ge(h_ready, b * STEPS + (j - 1))
                    for i in range(G):
                        f = G * j + i
                        act.activation(sl[:, j % 2, i, :], gs[:, j % 2, i, :], ACT.Silu, scale=sgu[:, f // 4, f % 4:f % 4 + 1])
                    act.drain().then_inc(sl_ready, 1)

            norm.root(act, 0, 0)
            entered(0)
            gate_and_up(0, True)
            for i in range(2):
                t = ("sd", i)
                act.wait_ge(prep.full(t), prep.count(t, 0))
                act.activation(sdb[:, i * 512:(i + 1) * 512], prep.tile(t)[0:Q, :], ACT.Copy,
                               scale=C.gates[0:Q, gate:gate + 1]).then_inc(prep.free(t), 1)
            act.drain().then_inc(sdb_ready, 1)

            def turned(b):
                for i in range(4):
                    t = ("hT", i)
                    act.wait_ge(behind.full(t), behind.count(t, b))
                    act.copy(hqT[:, 8 * i:8 * i + 8, :], behind.tile(t)[:].bitcast(BF16)[:, 0:8 * Q].rearrange("p (c q) -> p c q", c=8))\
                       .then_inc(behind.free(t), 1)
                act.drain().then_inc(hqT_ready, 1)

            def sequence(b, slot, turn, first, gate_up, quantise):
                act.wait_ge(ha_free, b + 1)
                for i in range(8):
                    t = ("h", i)
                    act.wait_ge(turns.full(t), turns.count(t, b))
                    act.activation(ha[:, i * 512:(i + 1) * 512], turns.tile(t)[0:Q, :], ACT.Copy).then_inc(turns.free(t), 1)
                act.drain().then_inc(ha_ready, 1)
                if not first:
                    turned(b - 1)
                if gate_up:
                    entered(b + 1)
                    gate_and_up(b + 1, quantise)

            rounds(act, sequence)
            turned(B - 1)

        def half(v, k):
            w = v.rearrange("q (m two l c) -> q m two l c", two=2, l=1 << k, c=P)
            return w[:, :, 0], w[:, :, 1]

        def sides(k):
            return (ha, hb) if k % 2 == 0 else (hb, ha)

        @block.gpsimd
        def _(pool):
            def product(b, j):
                pool.wait_ge(sl_ready, b * STEPS + (j + 1))
                pool.wait_ge(us_ready, b * STEPS + (j + 1))
                pool.tensor_tensor(h[:, G * j:G * j + G, :], sl[:, j % 2], us[:, j % 2], ALU.mult).then_inc(h_ready, 1)

            for j in range(STEPS):
                product(0, j)

            def sequence(b, slot, turn, first, gate_up, quantise):
                for k in range(5):
                    src, dst = sides(k)
                    (a, c), (_, d) = half(src[:], k), half(dst[:], k)
                    pool.wait_ge(sum_ready, b * 5 + (k + 1))
                    for l in range(1 << k):
                        op = pool.tensor_tensor(d[:, :, l, 0:SPLIT], a[:, :, l, 0:SPLIT], c[:, :, l, 0:SPLIT], ALU.subtract)
                    op.then_inc(diff_ready, 1)
                    if gate_up:
                        product(b + 1, k)
                if gate_up:
                    for j in range(5, STEPS):
                        product(b + 1, j)

            rounds(pool, sequence)

        @block.vector
        def _(dve):
            def reduced(src, scale, rscale, unit):
                dve.tensor_reduce(scale, src, AX, ALU.max, apply_absolute_value=True)
                dve.drain()
                divide(dve, scale, rscale, 7.0)
                dve.tensor_scalar(scale, scale, unit, 1e-8, ALU.mult, ALU.max)
                dve.drain()
                dve.reciprocal(rscale, scale)
                dve.drain()
                if unit != 1.0:
                    dve.tensor_scalar(rscale, rscale, unit, None, ALU.mult)
                    dve.drain()

            def integers(dst, src, rscale):
                dve.tensor_scalar(src, src, rscale, MAGIC, ALU.mult, ALU.add)
                dve.drain()
                return dve.tensor_scalar(dst, src, MAGIC, 7.0, ALU.subtract, ALU.min)

            def statistics(b):
                dve.wait_ge(z_loaded, b * 16 + 16)
                norm.statistics(dve, z[:], 0)

            def quantised(b):
                norm.scale(dve, z[:], z[:], 0, b)
                dve.drain()
                if not isinstance(b, int) or b > 0:
                    dve.wait_ge(ahead.full("sx"), ahead.count("sx", b - 1))
                reduced(z[:], sx[:], rsx[:], 1.0)
                integers(q[:], z[:], rsx[:]).then_inc(q_ready, 1)

            def step(b, j):
                t = ("g", j)
                if j == 0:
                    dve.wait_ge(qT_ready, b + 1)
                dve.wait_ge(ahead.full(t), ahead.count(t, b))
                if j >= 2 or not isinstance(b, int) or b > 0:
                    dve.wait_ge(h_ready, b * STEPS + (j - 1))
                dve.tensor_tensor(gs[:, j % 2], ahead.tile(t)[:, 0:G * Q].rearrange("p (i n) -> p i n", i=G),
                                  sxb[:].unsqueeze(1).broadcast_to([P, G, Q]), ALU.mult).then_inc(ahead.free(t), 1)
                dve.drain().then_inc(gs_ready, 1)
                t = ("u", j)
                dve.wait_ge(ahead.full(t), ahead.count(t, b))
                for i in range(G):
                    f = G * j + i
                    op = dve.scalar_tensor_tensor(out=us[:, j % 2, i, :], in0=ahead.tile(t)[:, i * Q:(i + 1) * Q],
                                                  scalar=sgu[:, 8 + f // 4, f % 4:f % 4 + 1], in1=sxb[:], op0=ALU.mult, op1=ALU.mult)
                op.then_inc(ahead.free(t), 1)
                dve.drain().then_inc(us_ready, 1)

            def butterfly(b, k):
                src, dst = sides(k)
                (a, c), (_, d) = half(src[:], k), half(dst[:], k)
                sa, sb, sc = (v[:].rearrange("q (m two c) -> q m two c", two=2, c=P << k) for v in (src, src, dst))
                dve.tensor_tensor(sc[:, :, 0], sa[:, :, 0], sb[:, :, 1], ALU.add)
                for l in range(1 << k):
                    dve.tensor_tensor(d[:, :, l, SPLIT:P], a[:, :, l, SPLIT:P], c[:, :, l, SPLIT:P], ALU.subtract)

            dve.sem_inc(ha_free, 1)
            statistics(0)
            quantised(0)
            dve.wait_ge(sgu_loaded, 16)
            for j in range(STEPS):
                if j == STEPS - 1:
                    statistics(1)
                step(0, j)
            quantised(1)
            dve.wait_ge(sdb_ready, 1)

            def finished(b, slot, turn, i):
                if i == 0:
                    dve.wait_ge(x_loaded[slot], turn * 16 + 16)
                t = ("y", i)
                c = slice(i * 512, (i + 1) * 512)
                dve.wait_ge(behind.full(t), behind.count(t, b))
                dve.scalar_tensor_tensor(out=y[:], in0=behind.tile(t)[0:Q, :], scalar=sh[:, slot:slot + 1], in1=sdb[:, c],
                                         op0=ALU.mult, op1=ALU.mult).then_inc(behind.free(t), 1)
                dve.drain()
                dve.tensor_tensor(x[:, slot, c], x[:, slot, c], y[:], ALU.add)
                dve.drain()
                if i == 1:
                    dve.sem_inc(x_done, 1)

            def sequence(b, slot, turn, first, gate_up, quantise):
                dve.wait_ge(ha_ready, b + 1)
                dve.sem_inc(sum_ready, 1)
                for k in range(5):
                    butterfly(b, k)
                    if k == 4 and not first:
                        finished(b - 1, 1 - slot, turn + (slot - 1), 0)
                    if gate_up:
                        step(b + 1, k)
                    dve.drain()
                    dve.wait_ge(diff_ready, b * 5 + (k + 1))
                    if k < 4:
                        dve.sem_inc(sum_ready, 1)
                dve.sem_inc(ha_free, 1)
                reduced(hb[:], sh[:, slot:slot + 1], rsh[:], 2.0 ** -6)
                if gate_up:
                    step(b + 1, 5)
                    step(b + 1, 6)
                if quantise:
                    statistics(b + 2)
                if gate_up:
                    step(b + 1, 7)
                if not first:
                    t = ("hT", 3)
                    dve.wait_ge(behind.full(t), behind.count(t, b - 1))
                integers(hq[:], hb[:], rsh[:]).then_inc(hq_ready, 1)
                if not first:
                    finished(b - 1, 1 - slot, turn + (slot - 1), 1)
                if quantise:
                    quantised(b + 2)

            rounds(dve, sequence)
            for i in range(2):
                finished(B - 1, 1, PAIRS - 1, i)


def gather_points(nc, C, banks, gate, x_in, x_out, A, nearest, early):
    K, R, AR = 16, Q // 16, KC * Q // 16
    U = 2 * K
    with ExitStack() as ctx:
        s_ = Scope(nc, ctx, "points")
        x, z = s_.sb("x", [Q, 2, D]), s_.sb("z", [Q, 2, D])
        norm = Norm(s_, 2)
        wcol, sel, wsel = s_.sb("wcol", [Q, 1]), s_.sb("sel", [Q, R]), s_.sb("wsel", [Q, R])
        bias, count, eights = s_.sb("bias", [P, 1]), s_.sb("count", [P, 1]), s_.sb("eights", [P, KC])
        idx = s_.sb("idx", [P, 2, KC, K], U32)
        point, hi, lo = (s_.sb(n, [P, 2, KC, K]) for n in ("point", "hi", "lo"))
        lob = s_.sb("lob", [P, 2, KC, K], BF16)
        mask = s_.sb("mask", [P, 2, KC, K, KC])
        table, rest = s_.sb("table", [P, 2, AR]), s_.sb("rest", [P, 2, AR])
        part = [s_.sb(f"part{i}", [P, 2, AR], BF16) for i in range(3)]
        spread, onehot = s_.sb("spread", [P, 2, D], BF16), s_.sb("onehot", [P, 2, D], BF16)
        kept = s_.sb("kept", [P, 2, KC, KC, R])
        val = s_.sb("val", [P, K, R, KC])
        flat = s_.sb("flat", [AR, 2, P, K])
        back = s_.sb("back", [P, 2, KC, Q])
        flat_dram = nc.dram_tensor("flat", (2, AR, P * K), F32, kind="Internal").ap()
        consts_loaded, wsel_ready = s_.sem("consts_loaded"), s_.sem("wsel_ready")
        passed = s_.sem("passed")
        x_loaded = [s_.sem(f"x_loaded{i}") for i in range(2)]
        x_stored = [s_.sem(f"x_stored{i}") for i in range(2)]
        idx_loaded = [s_.sem(f"idx_loaded{i}") for i in range(2)]
        flat_stored, back_loaded = s_.sem("flat_stored"), s_.sem("back_loaded")
        z_loaded = [s_.sem(f"z_loaded{i}") for i in range(2)]
        idx_used, z_used, lo_ready, z_ready, table_ready = (
            s_.sem(n) for n in ("idx_used", "z_used", "lo_ready", "z_ready", "table_ready"))
        spread_ready, onehot_ready, val_ready, flat_ready, x_done = (
            s_.sem(n) for n in ("spread_ready", "onehot_ready", "val_ready", "flat_ready", "x_done"))
        def events(first, last):
            out = []
            for u in range(U):
                if u + 2 < U or not last:
                    out.append(("spread", u + 2))
                if u == K - 4:
                    out.append(("table", 1))
                if u == U - 5 and not last:
                    out.append(("table", 2))
                out.append(("look", u))
                if u % 4 == 1 and (u > 1 or not first):
                    out.append(("turn", (u - 2) // 4))
                if u == K + 7:
                    out.append(("back", 0))
                if u == 6 and not first:
                    out.append(("back", -1))
            return out + ([("turn", 7), ("back", 1)] if last else [])

        def uses(steps):
            out = []
            for name, i in steps:
                if name == "spread":
                    out += [((name, i, h), 2 * (i % 2) + h) for h in range(2)]
                elif name == "look":
                    out.append(((name, i), 4 + i % 2))
                elif name == "back":
                    out += [((name, i, h), 6 + h) for h in range(2)]
                else:
                    out.append(((name, i), 6 + i % 2))
            return out

        ahead = [("table", 0), ("spread", 0), ("spread", 1)]
        turns = [Turns(banks, uses(ahead), 1), Turns(banks, uses(events(True, False)), 1),
                 Turns(banks, uses(events(False, False)), PAIRS - 2), Turns(banks, uses(events(False, True)), 1)]

        def rounds(eng, round_):
            round_(0, turns[1], 0, True, False)
            with eng.Fori(0, PAIRS - 2) as q:
                round_(q + 1, turns[2], q, False, False)
            round_(PAIRS - 1, turns[3], 0, False, True)

        block = ctx.enter_context(nc.Block())

        @block.sync
        def _(sp):
            sp.dma_start(wcol[:], A["L3_xattn_affine_w"]).then_inc(consts_loaded, 16)
            sp.dma_start(sel[:], A["row_mask"]).then_inc(consts_loaded, 16)
            sp.dma_start(bias[:], rows(A["L3_xattn_affine_b"], P)).then_inc(consts_loaded, 16)
            sp.dma_start(count[:], A["count"]).then_inc(consts_loaded, 16)
            sp.dma_start(eights[:], rows(A["eights"], P)).then_inc(consts_loaded, 16)
            for s in range(2):
                sp.dma_start(x[:, s, :], x_in[s]).then_inc(x_loaded[s], 16)
            early.load(sp)

            def sequence(p, s):
                b = p * 2 + s
                sp.wait_ge(flat_ready, b + 1)
                sp.dma_start(flat_dram[s], flat[:, s].rearrange("a n k -> a (n k)")).then_inc(flat_stored, 16)
                sp.wait_ge(flat_stored, b * 16 + 16)
                sp.dma_start(back[:, s].rearrange("p t f -> p (t f)"),
                             flat_dram[s].rearrange("a c -> (a c)").rearrange("(p c) -> p c", p=P)).then_inc(back_loaded, 16)
                sp.wait_ge(x_done, b + 1)
                sp.dma_start(x_out[b], x[:, s, :]).then_inc(x_stored[s], 16)
                sp.wait_ge(x_stored[s], p * 16 + 16)

            with sp.Fori(0, PAIRS - 1) as p:
                for s in range(2):
                    sequence(p, s)
                    sp.dma_start(x[:, s, :], x_in[p * 2 + (s + 2)]).then_inc(x_loaded[s], 16)
            for s in range(2):
                sequence(PAIRS - 1, s)

        @block.gpsimd
        def _(pool):
            with pool.Fori(0, PAIRS) as p:
                for s in range(2):
                    pool.wait_ge(idx_used, p * 2 + (s + 1))
                    pool.dma_start(idx[:, s], nearest[p * 2 + s]).then_inc(idx_loaded[s], 16)
                    pool.wait_ge(z_used, p * 2 + (s + 1))
                    pool.dma_start(z[:, s, :], x_in[p * 2 + s]).then_inc(z_loaded[s], 16)

        @block.tensor
        def _(pe):
            pe.wait_ge(wsel_ready, 1)

            def spreading(p, t_, turn, i):
                s, k = i // K, i % K
                if k == 0:
                    pe.wait_ge(lo_ready, p * 2 + (s + 1))
                for h in range(2):
                    t = ("spread", i, h)
                    pe.wait_ge(t_.free(t), t_.count(t, turn))
                    for j in range(4):
                        mm = pe.matmul(t_.tile(t)[:, j * P:(j + 1) * P], lob[:, s % 2, 4 * h + j, k:k + 1].broadcast_to([P, P]),
                                       C.identb[:], start=True, stop=True)
                    mm.then_inc(t_.full(t), 1)

            def tabled(p, t_, turn, i):
                t = ("table", i)
                pe.wait_ge(z_ready, p * 2 + (i + 1))
                pe.wait_ge(t_.free(t), t_.count(t, turn))
                for a in range(KC):
                    mm = pe.matmul(t_.tile(t)[:, a * R:(a + 1) * R], z[:, i % 2, a * P:(a + 1) * P], wsel[:], start=True, stop=True)
                mm.then_inc(t_.full(t), 1)

            def looked(p, t_, turn, i):
                t = ("look", i)
                if i % K == 0:
                    pe.wait_ge(table_ready, p * 2 + (i // K + 1))
                pe.wait_ge(onehot_ready, p * U + (i + 1))
                pe.wait_ge(t_.free(t), t_.count(t, turn))
                for j in range(KC):
                    for n in range(3):
                        mm = pe.matmul(t_.tile(t)[:, j * AR:(j + 1) * AR], onehot[:, i % 2, j * P:(j + 1) * P],
                                       part[n][:, i // K, :], start=(n == 0), stop=(n == 2))
                mm.then_inc(t_.full(t), 1)

            def turned(p, t_, turn, i):
                t = ("turn", i)
                pe.wait_ge(val_ready, p * U + (4 * i + 4))
                pe.wait_ge(t_.free(t), t_.count(t, turn))
                pe.sem_inc(passed, 1)
                for j in range(4):
                    mm = pe.transpose(t_.tile(t)[0:AR, j * P:(j + 1) * P], val[:, (4 * i + j) % K].rearrange("p r t -> p (r t)"),
                                      C.ident[:])
                mm.then_inc(t_.full(t), 1)

            def returned(p, t_, turn, i):
                pe.wait_ge(back_loaded, p * 32 + (16 * i + 16))
                for h in range(2):
                    t = ("back", i, h)
                    pe.wait_ge(t_.free(t), t_.count(t, turn))
                    for j in range(4):
                        mm = pe.transpose(t_.tile(t)[0:Q, j * P:(j + 1) * P], back[:, i % 2, 4 * h + j, :], C.ident[:])
                    mm.then_inc(t_.full(t), 1)

            does = {"spread": spreading, "table": tabled, "look": looked, "turn": turned, "back": returned}

            def round_(p, t_, turn, first, last):
                for name, i in events(first, last):
                    does[name](p, t_, turn, i)

            for name, i in ahead:
                does[name](0, turns[0], 0, i)
            rounds(pe, round_)

        @block.scalar
        def _(act):
            def spreading(p, t_, turn, i):
                if i >= 2 or not isinstance(p, int) or p > 0:
                    act.wait_ge(onehot_ready, p * U + (i - 1))
                for h in range(2):
                    t = ("spread", i, h)
                    act.wait_ge(t_.full(t), t_.count(t, turn))
                    act.activation(spread[:, i % 2, h * 512:(h + 1) * 512], t_.tile(t)[:], ACT.Copy).then_inc(t_.free(t), 1)
                act.drain().then_inc(spread_ready, 1)

            def turned(p, t_, turn, i):
                t = ("turn", i)
                act.wait_ge(t_.full(t), t_.count(t, turn))
                act.activation(flat[:, i // 4 % 2, :, i % 4 * 4:i % 4 * 4 + 4],
                               t_.tile(t)[0:AR, :].rearrange("a (j n) -> a n j", j=4), ACT.Copy).then_inc(t_.free(t), 1)
                if i % 4 == 3:
                    act.drain().then_inc(flat_ready, 1)

            def round_(p, t_, turn, first, last):
                for name, i in events(first, last):
                    if (name, i) == ("spread", 6):
                        norm.root(act, 1, p * 2 + 1)
                    if (name, i) == ("spread", K + 8) and not last:
                        norm.root(act, 0, p * 2 + 2)
                    if name == "spread":
                        spreading(p, t_, turn, i)
                    elif name == "turn":
                        turned(p, t_, turn, i)

            norm.root(act, 0, 0)
            for name, i in ahead:
                if name == "spread":
                    spreading(0, turns[0], 0, i)
            rounds(act, round_)

        @block.vector
        def _(dve):
            dve.sem_inc(idx_used, 2)
            dve.sem_inc(z_used, 2)
            dve.wait_ge(consts_loaded, 80)
            dve.tensor_scalar(wsel[:], sel[:], wcol[:], None, ALU.mult).then_inc(wsel_ready, 1)

            def indices(p, s):
                dve.wait_ge(idx_loaded[s % 2], p * 16 + 16 * (s // 2 + 1))
                s %= 2
                dve.tensor_copy(point[:, s], idx[:, s]).then_inc(idx_used, 1)
                dve.drain()
                dve.tensor_scalar(hi[:, s], point[:, s], 63.5, 1.0 / P, ALU.subtract, ALU.mult)
                dve.drain()
                dve.tensor_scalar(hi[:, s], hi[:, s], MAGIC, MAGIC, ALU.add, ALU.subtract)
                dve.drain()
                dve.scalar_tensor_tensor(out=lob[:, s], in0=hi[:, s], scalar=-float(P), in1=point[:, s], op0=ALU.mult, op1=ALU.add)\
                   .then_inc(lo_ready, 1)
                dve.tensor_tensor(mask[:, s].rearrange("p t k a -> p (t k) a"),
                                  hi[:, s].rearrange("p t k -> p (t k)").unsqueeze(2).broadcast_to([P, KC * K, KC]),
                                  eights[:].unsqueeze(1).broadcast_to([P, KC * K, KC]), ALU.is_equal)

            def statistics(p, s):
                dve.wait_ge(z_loaded[s % 2], p * 16 + 16 * (s // 2 + 1))
                norm.statistics(dve, z[:, s % 2, :], s % 2)

            def points(p, s):
                norm.scale(dve, z[:, s % 2, :], z[:, s % 2, :], s % 2, p * 2 + s).then_inc(z_ready, 1)

            def split(t_, turn, s):
                t = ("table", s)
                dve.wait_ge(t_.full(t), t_.count(t, turn))
                dve.sem_inc(z_used, 1)
                s %= 2
                dve.tensor_scalar(table[:, s], t_.tile(t)[:, 0:AR], bias[:], None, ALU.add).then_inc(t_.free(t), 1)
                dve.drain()
                dve.tensor_copy(part[0][:, s], table[:, s])
                dve.drain()
                dve.tensor_tensor(rest[:, s], table[:, s], part[0][:, s], ALU.subtract)
                dve.drain()
                dve.tensor_copy(part[1][:, s], rest[:, s])
                dve.drain()
                dve.tensor_tensor(part[2][:, s], rest[:, s], part[1][:, s], ALU.subtract)
                dve.drain().then_inc(table_ready, 1)

            def keep(t_, turn, i):
                t, s, k = ("look", i), i // K, i % K
                dve.wait_ge(t_.full(t), t_.count(t, turn))
                dve.tensor_tensor(kept[:, i % 2], t_.tile(t)[:, 0:KC * AR].rearrange("p (t a r) -> p t a r", t=KC, a=KC),
                                  mask[:, s, :, k, :].unsqueeze(3).broadcast_to([P, KC, KC, R]), ALU.mult).then_inc(t_.free(t), 1)
                dve.drain()
                dve.tensor_reduce(val[:, k].rearrange("p r t -> p t r"), kept[:, i % 2].rearrange("p t a r -> p t r a"), AX, ALU.add)\
                   .then_inc(val_ready, 1)

            def update(p, t_, turn, s):
                dve.wait_ge(x_loaded[s % 2], p * 16 + 16 * (s // 2 + 1))
                for h in range(2):
                    t = ("back", s, h)
                    dve.wait_ge(t_.full(t), t_.count(t, turn))
                    xs = x[:, s % 2, :].rearrange("f (q j) -> f j q", j=KC)[:, 4 * h:4 * h + 4, :]
                    op = dve.scalar_tensor_tensor(out=xs, in0=t_.tile(t)[0:Q, :].rearrange("f (j q) -> f j q", j=4),
                                                  scalar=C.gates[0:Q, gate:gate + 1], in1=xs, op0=ALU.mult, op1=ALU.add)
                    op.then_inc(t_.free(t), 1)
                dve.drain().then_inc(x_done, 1)

            def round_(p, t_, turn, first, last):
                for i in range(U):
                    dve.wait_ge(spread_ready, p * U + (i + 1))
                    dve.tensor_scalar(onehot[:, i % 2], spread[:, i % 2], count[:], None, ALU.is_equal).then_inc(onehot_ready, 1)
                    if i == 0 and not first:
                        keep(t_, turn - 1, U - 1)
                    if i >= 1:
                        keep(t_, turn, i - 1)
                    if i == 2:
                        indices(p, 1)
                    if i == 4:
                        statistics(p, 1)
                    if i == 7 and not first:
                        update(p, t_, turn, -1)
                    if i == 8:
                        points(p, 1)
                    if i == K - 2:
                        split(t_, turn, 1)
                    if i == K + 4 and not last:
                        indices(p, 2)
                    if i == K + 6 and not last:
                        statistics(p, 2)
                    if i == K + 8:
                        update(p, t_, turn, 0)
                    if i == K + 9 and not last:
                        points(p, 2)
                    if i == U - 3 and not last:
                        split(t_, turn, 2)
                if last:
                    keep(t_, turn, U - 1)
                    update(p, t_, turn, 1)

            indices(0, 0)
            statistics(0, 0)
            points(0, 0)
            split(turns[0], 0, 0)
            rounds(dve, round_)


NAMES = ["x", "ctx_4096", "g_xattn", "g_ffn", "L0_xattn_Wq", "L0_xattn_Wk", "L0_xattn_Wv", "L0_xattn_Wo",
         "L0_ffn_qweight", "L0_ffn_wparams", "L0_ffn_bias", "L1_xattn_Wq", "L1_xattn_bq", "L1_xattn_Wk",
         "L1_xattn_bk", "L1_ffn_Wq", "L1_ffn_Wr", "L1_ffn_aux_keys", "L1_ffn_aux_values", "L1_ffn_Wvd",
         "L1_ffn_Wvu", "L1_ffn_Wu1", "L1_ffn_bu1", "L1_ffn_Wu2", "L1_ffn_bu2", "L1_ffn_gate_w1",
         "L1_ffn_gate_bias", "L1_ffn_log_rel", "L2_xattn_Wq", "L2_xattn_Wk", "L2_xattn_Wv", "L2_xattn_Wo",
         "L2_ffn_w_gate_up", "L2_ffn_w_down", "L3_xattn_affine_w", "L3_xattn_affine_b", "L3_ffn_gate_w",
         "L3_ffn_lora_A", "L3_ffn_lora_B"]


def layout(a):
    import numpy as np
    out = dict(a)
    for name in ("L0_xattn_Wq", "L0_xattn_Wk", "L0_xattn_Wv", "L0_xattn_Wo", "L0_ffn_qweight", "L1_xattn_Wq",
                 "L1_ffn_Wq", "L1_ffn_Wr", "L1_ffn_aux_keys", "L1_ffn_aux_values", "L1_ffn_Wvd", "L1_ffn_Wvu",
                 "L1_ffn_Wu1", "L3_ffn_gate_w"):
        out[name + "T"] = out.pop(name).T
    four = [96 * c + i if i < 96 else 288 + 32 * c + i - 96 for c in range(3) for i in range(128)]
    out["L0_xattn_WqT"] = out["L0_xattn_WqT"][:, [384 * g + i for g in range(4) for i in four]]
    out["L1_ffn_WrT"] = np.concatenate([out["L1_ffn_WrT"], np.zeros((64, P - 48), np.float32)], axis=1)
    out["L0_ffn_qweightT"] = np.ascontiguousarray(out["L0_ffn_qweightT"]).view(np.uint32)
    out["ctxT"] = a["ctx_4096"].transpose(0, 2, 1)
    gu = out.pop("L2_ffn_w_gate_up").reshape(16, 4, P, D).transpose(0, 2, 1, 3).reshape(16, P, 4 * D)
    out["L2_weights"] = np.concatenate([gu, out.pop("L2_ffn_w_down").reshape(8, P, 4 * D)])
    out["planes"] = a["ctx_4096"][:, 0:2].reshape(B, 2 * D)
    out["points"] = a["ctx_4096"][:, 0:2].reshape(B, 2, KC, P).transpose(0, 3, 1, 2)
    order = [16 * (m // 4) + 4 * j + m % 4 for m in range(8) for j in range(4)]
    out["L2_xattn_Wq"] = a["L2_xattn_Wq"].reshape(D, 32, 32)[:, order].reshape(D, D)
    out["L2_xattn_Wo"] = a["L2_xattn_Wo"].reshape(32, 32, D)[order].reshape(D, D)
    out["L3_lora_AT"] = out.pop("L3_ffn_lora_A").reshape(512, D).T
    out["L3_lora_BT"] = out.pop("L3_ffn_lora_B").transpose(0, 2, 1).reshape(512, D)
    out["L3_xattn_affine_w"] = np.repeat(a["L3_xattn_affine_w"], 7).reshape(Q, 1)
    for name in ("L1_xattn_bq", "L1_xattn_bk", "L1_ffn_bu1", "L1_ffn_Wu2"):
        out[name] = a[name].reshape(-1, P).T
    for name in ("L1_ffn_gate_w1", "L1_ffn_gate_bias"):
        out[name] = a[name].reshape(1)
    h = np.ones((1, 1), np.float32)
    while len(h) < P:
        h = np.block([[h, h], [h, -h]]).astype(np.float32)
    out["ident"] = np.eye(P, dtype=np.float32)
    out["hadamard"] = h
    out["row_mask"] = (np.arange(Q)[:, None] % 7 == np.arange(7)[None, :]).astype(np.float32)
    out["eights"] = np.arange(KC, dtype=np.float32)
    out["count"] = np.arange(P, dtype=np.float32).reshape(P, 1)
    return {n: np.ascontiguousarray(v) for n, v in out.items()}


def program(nc, A, x_in, x_out):
    with ExitStack() as ctx:
        banks = Banks(nc, ctx)
        C = Consts(nc, ctx)
        setup(nc, C, banks, A["g_xattn"], A["g_ffn"], A)

        def dram(name, shape, dt=F32):
            return nc.dram_tensor(name, shape, dt, kind="Internal").ap()

        def early(ctx, stage, **weights):
            return Early(nc, ctx, stage, {n: ([P, A[w].shape[0] // P, A[w].shape[1]], fold(A[w])) for n, w in weights.items()})

        idx = dram("nearest", (B, P, KC, 16), U32)
        scales, codes = dram("scales", (24, P, 4)), dram("codes", (24, P, 1024), U32)
        x = [x_in] + [dram(f"x_{n}", (B, Q, D)) for n in range(1, 8)] + [x_out]
        latent_attention(nc, C, banks, 0, x[0], x[1], A, idx)
        with ExitStack() as two:
            plain = early(two, "plain", wq="L1_xattn_WqT", wk="L1_xattn_Wk")
            quantised_ffn(nc, C, banks, 4, x[1], x[2], A["L0_ffn_qweightT"], A["L0_ffn_wparams"], A["L0_ffn_bias"], plain)
            plain_attention(nc, C, banks, 1, x[2], x[3], A, idx, plain)
        with ExitStack() as two:
            grouped = early(two, "grouped", wk="L2_xattn_Wk", wv="L2_xattn_Wv", wq="L2_xattn_Wq", wo="L2_xattn_Wo")
            memory_ffn(nc, C, banks, 5, x[3], x[4], A, grouped)
            grouped_attention(nc, C, banks, 2, x[4], x[5], A, A["L2_weights"], scales, codes, grouped)
        hadamard_ffn(nc, C, banks, 6, x[5], x[6], A, scales, codes)
        with ExitStack() as two:
            experts = early(two, "moe", gT="L3_ffn_gate_wT", aT="L3_lora_AT", bT="L3_lora_BT")
            gather_points(nc, C, banks, 3, x[6], x[7], A, idx, experts)
            experts_ffn(nc, C, banks, 7, x[7], x[8], A, experts)


def kernel(**inputs):
    import numpy as np
    import concourse.bacc as bacc
    from concourse.bass_utils import run_bass_kernel_spmd

    nc = bacc.Bacc("TRN2", target_bir_lowering=False, num_devices=1)
    arrays = layout({name: np.asarray(inputs[name]) for name in NAMES})
    A = {n: nc.dram_tensor(n, v.shape, mybir.dt.from_np(v.dtype), kind="ExternalInput").ap() for n, v in arrays.items()}
    out = nc.dram_tensor("x_final", (B, Q, D), F32, kind="ExternalOutput").ap()
    program(nc, A, A["x"], out)
    return run_bass_kernel_spmd(nc, [arrays], core_ids=[0]).results[0]["x_final"]
```
